# Optimizing a Trainium2 kernel written in Bass

```python
import numpy as np
import jax
import jax.numpy as jnp

def _softmax(x, axis=-1):
    return jax.nn.softmax(x, axis=axis)

def _gelu(x):
    return jax.nn.gelu(x, approximate=True)

def _silu(x):
    return jax.nn.silu(x)

def _sigmoid(x):
    return jax.nn.sigmoid(x)

def _layernorm(x, axis=-1, eps=1e-05):
    m = jnp.mean(x, axis=axis, keepdims=True)
    v = jnp.var(x, axis=axis, keepdims=True)
    return (x - m) / jnp.sqrt(v + eps)

def _scatter_add(tgt, idx, src, axis=0):
    return tgt.at[idx].add(src)

def _segment_sum(src, seg, n):
    return jax.ops.segment_sum(src, seg, n)
kernel_name = 'mk_decoder_postln_d4_seqx_r4_888b8f'

def setup_inputs(seed: int=0):
    np.random.seed(seed)
    _w = jnp.asarray

    def _rec_inputs():
        import jax
        import jax.numpy as jnp
        _rk = jax.random.key(seed)
        x = -0.0003929 + 0.9999 * jax.random.normal(jax.random.fold_in(_rk, 1), (4, 512, 256), jnp.float32)
        _lenS = 512 - jax.random.randint(jax.random.fold_in(_rk, 7), (4,), 0, max(1, 512 // 4) + 1, jnp.int32)
        _lenS2 = 1024 - jax.random.randint(jax.random.fold_in(_rk, 8), (4,), 0, max(1, 1024 // 4) + 1, jnp.int32)
        _ctx_1024P = jax.random.normal(jax.random.fold_in(_rk, 11), (4, 16, 256), jnp.float32)
        _ctx_1024c = jax.random.dirichlet(jax.random.fold_in(_rk, 511), 0.3 * jnp.ones((16,), jnp.float32), (4, 1024))
        _ctx_1024t = jnp.einsum('bsk,bkd->bsd', _ctx_1024c, _ctx_1024P)
        _ctx_1024t = _ctx_1024t * jax.lax.rsqrt(jnp.mean(jnp.square(_ctx_1024t)) + 1e-12) * 0.953939
        ctx_1024 = 2.81802e-05 + 1.00001 * (_ctx_1024t + 0.3 * jax.random.normal(jax.random.fold_in(_rk, 611), (4, 1024, 256), jnp.float32))
        _validS = jnp.arange(512)[None, :] < _lenS[:, None]
        _validS2 = jnp.arange(1024)[None, :] < _lenS2[:, None]
        _causal = jnp.tril(jnp.ones((512, 512), dtype=bool))
        mask_BxS2_ff1 = jnp.where(jnp.ones((4, 1024), dtype=bool), 1.0, 0.0).astype(jnp.float32)
        mask_Bx1xSxS2_ff0 = jnp.where(jnp.ones((4, 1, 512, 1024), dtype=bool), 0.0, -1000000000.0).astype(jnp.float32)
        return (x, ctx_1024, mask_BxS2_ff1, mask_Bx1xSxS2_ff0)
    x, ctx_1024, mask_BxS2_ff1, mask_Bx1xSxS2_ff0 = _rec_inputs()

    def _L0_attn_setup():
        import jax, jax.numpy as jnp
        import numpy as np
        NUM_HEADS = 16
        LEVELS = 4

        def _mha(x, w_in, b_in, w_out, b_out):
            B, S, E = x.shape
            H = NUM_HEADS
            hd = E // H
            qkv = x @ w_in.T + b_in
            q, k, v = jnp.split(qkv, 3, axis=-1)
            split = lambda t: t.reshape(B, S, H, hd).transpose(0, 2, 1, 3)
            q, k, v = (split(q), split(k), split(v))
            scores = jnp.einsum('bhqd,bhkd->bhqk', q, k) / jnp.sqrt(jnp.asarray(hd, x.dtype))
            attn = jax.nn.softmax(scores, axis=-1)
            out = jnp.einsum('bhqk,bhkd->bhqd', attn, v)
            out = out.transpose(0, 2, 1, 3).reshape(B, S, E)
            return out @ w_out.T + b_out

        def _upsample_linear(x, target):
            B, L, E = x.shape
            src = (jnp.arange(target, dtype=jnp.float32) + 0.5) * (L / target) - 0.5
            src = jnp.clip(src, 0.0, L - 1)
            i0 = jnp.floor(src).astype(jnp.int32)
            i1 = jnp.minimum(i0 + 1, L - 1)
            w = (src - i0.astype(jnp.float32))[None, :, None].astype(x.dtype)
            return x[:, i0, :] * (1 - w) + x[:, i1, :] * w
        key = jax.random.key(seed)
        ks = jax.random.split(key, 7)
        B, S, E = (1, 512, 256)
        return {'query': jax.random.normal(ks[0], (B, S, E), jnp.float32), 'in_proj_w': jax.random.normal(ks[1], (LEVELS, 3 * E, E), jnp.float32) * 0.02, 'in_proj_b': jnp.zeros((LEVELS, 3 * E), jnp.float32), 'out_w': jax.random.normal(ks[2], (LEVELS, E, E), jnp.float32) * 0.02, 'out_b': jnp.zeros((LEVELS, E), jnp.float32), 'up_w': jax.random.normal(ks[3], (LEVELS - 1, E, E), jnp.float32) * 0.02, 'up_b': jnp.zeros((LEVELS - 1, E), jnp.float32)}
    _L0_attn_all = _L0_attn_setup()
    _L0_attn_in = {k: v for k, v in _L0_attn_all.items() if k in ('in_proj_w', 'in_proj_b', 'out_w', 'out_b', 'up_w', 'up_b')}
    del _L0_attn_all

    def _L0_xattn_setup():
        import jax, jax.numpy as jnp
        import numpy as np
        D_MODEL = 256
        HEADS = 16
        DEPTH = D_MODEL // HEADS
        B, S = (4, 1024)
        EPS_K = 1e-06
        EPS_LN = 1e-06

        def _layernorm(x, g, b):
            m = jnp.mean(x, axis=-1, keepdims=True)
            var = jnp.var(x, axis=-1, keepdims=True)
            return (x - m) * jax.lax.rsqrt(var + EPS_LN) * g + b

        def _split_heads(x):
            bsz, sl, _ = x.shape
            return x.reshape(bsz, sl, HEADS, DEPTH).transpose(0, 2, 1, 3)
        key = jax.random.key(seed)
        ks = jax.random.split(key, 8)
        lecun = 1.0 / np.sqrt(D_MODEL)
        glorot = np.sqrt(2.0 / (D_MODEL + D_MODEL))
        return {'q': jax.random.normal(ks[0], (B, S, D_MODEL), jnp.float32), 'k': jax.random.normal(ks[1], (B, S, D_MODEL), jnp.float32), 'v': jax.random.normal(ks[2], (B, S, D_MODEL), jnp.float32), 'mask': jnp.ones((B, S), jnp.float32), 'wq': jax.random.normal(ks[3], (D_MODEL, D_MODEL), jnp.float32) * lecun, 'wk': jax.random.normal(ks[4], (D_MODEL, D_MODEL), jnp.float32) * lecun, 'wv': jax.random.normal(ks[5], (D_MODEL, D_MODEL), jnp.float32) * lecun, 'ln_gamma': jnp.ones((D_MODEL,), jnp.float32), 'ln_beta': jnp.zeros((D_MODEL,), jnp.float32), 'dense_w': jax.random.normal(ks[6], (D_MODEL, D_MODEL), jnp.float32) * glorot, 'dense_b': jnp.zeros((D_MODEL,), jnp.float32)}
    _L0_xattn_all = _L0_xattn_setup()
    _L0_xattn_in = {k: v for k, v in _L0_xattn_all.items() if k in ('wq', 'wk', 'wv', 'ln_gamma', 'ln_beta', 'dense_w', 'dense_b')}
    del _L0_xattn_all

    def _L0_ffn_setup():
        import jax, jax.numpy as jnp
        import numpy as np
        LN_EPS = 1e-12
        key = jax.random.key(seed)
        ks = jax.random.split(key, 8)
        B, S, H, I, E = (4, 512, 256, 1024, 8)
        sH = 1.0 / np.sqrt(H)
        sI = 1.0 / np.sqrt(I)
        return {'hidden_states': jax.random.normal(ks[0], (B, S, H), dtype=jnp.float32), 'Wr': jax.random.uniform(ks[1], (E, H), jnp.float32, -sH, sH), 'W1': jax.random.uniform(ks[2], (E, H, I), jnp.float32, -sH, sH), 'b1': jax.random.uniform(ks[3], (E, I), jnp.float32, -sH, sH), 'Wo': jax.random.uniform(ks[4], (I, H), jnp.float32, -sI, sI), 'bo': jax.random.uniform(ks[5], (H,), jnp.float32, -sI, sI), 'gamma': jnp.ones((H,), jnp.float32), 'beta': jnp.zeros((H,), jnp.float32)}
    _L0_ffn_all = _L0_ffn_setup()
    _L0_ffn_in = {k: v for k, v in _L0_ffn_all.items() if k in ('Wr', 'W1', 'b1', 'Wo', 'bo', 'gamma', 'beta')}
    del _L0_ffn_all

    def _L1_attn_setup():
        import jax, jax.numpy as jnp
        import numpy as np
        B, N, C, H = (4, 2048, 256, 16)
        D = C // H
        EPS = 1e-05
        key = jax.random.key(seed)
        ks = jax.random.split(key, 10)
        s = 1.0 / np.sqrt(C)
        return {'x': jax.random.normal(ks[0], (B, N, C), jnp.float32), 'Wq': jax.random.uniform(ks[1], (C, C), jnp.float32, -s, s), 'bq': jax.random.uniform(ks[2], (C,), jnp.float32, -s, s), 'Wk': jax.random.uniform(ks[3], (C, C), jnp.float32, -s, s), 'bk': jax.random.uniform(ks[4], (C,), jnp.float32, -s, s), 'Wv': jax.random.uniform(ks[5], (C, C), jnp.float32, -s, s), 'bv': jax.random.uniform(ks[6], (C,), jnp.float32, -s, s), 'Wo': jax.random.uniform(ks[7], (C, C), jnp.float32, -s, s), 'bo': jax.random.uniform(ks[8], (C,), jnp.float32, -s, s), 'ln_g': jnp.ones((C,), jnp.float32), 'ln_b': jnp.zeros((C,), jnp.float32)}
    _L1_attn_all = _L1_attn_setup()
    _L1_attn_in = {k: v for k, v in _L1_attn_all.items() if k in ('Wq', 'bq', 'Wk', 'bk', 'Wv', 'bv', 'Wo', 'bo', 'ln_g', 'ln_b')}
    del _L1_attn_all

    def _L1_xattn_setup():
        import jax, jax.numpy as jnp
        import numpy as np
        import math
        D_MODEL = 256
        NUM_HEADS = 16
        D_K = D_MODEL // NUM_HEADS
        SCALE = math.sqrt(D_K)

        def _xavier(key, shape):
            fan_in, fan_out = (shape[1], shape[0])
            a = math.sqrt(6.0 / (fan_in + fan_out))
            return jax.random.uniform(key, shape, jnp.float32, -a, a)
        key = jax.random.key(seed)
        ks = jax.random.split(key, 7)
        B, S = (2, 512)
        return {'query': jax.random.normal(ks[0], (B, S, D_MODEL), jnp.float32), 'key': jax.random.normal(ks[1], (B, S, D_MODEL), jnp.float32), 'value': jax.random.normal(ks[2], (B, S, D_MODEL), jnp.float32), 'wq': _xavier(ks[3], (D_MODEL, D_MODEL)), 'wk': _xavier(ks[4], (D_MODEL, D_MODEL)), 'wv': _xavier(ks[5], (D_MODEL, D_MODEL)), 'wo': _xavier(ks[6], (D_MODEL, D_MODEL)), 'bq': jnp.zeros((D_MODEL,), jnp.float32), 'bk': jnp.zeros((D_MODEL,), jnp.float32), 'bv': jnp.zeros((D_MODEL,), jnp.float32), 'bo': jnp.zeros((D_MODEL,), jnp.float32)}
    _L1_xattn_all = _L1_xattn_setup()
    _L1_xattn_in = {k: v for k, v in _L1_xattn_all.items() if k in ('wq', 'wk', 'wv', 'wo', 'bq', 'bk', 'bv', 'bo')}
    del _L1_xattn_all

    def _L1_ffn_setup():
        import jax, jax.numpy as jnp
        import numpy as np
        B, S, D, H, E = (8, 512, 256, 1024, 16)
        key = jax.random.key(seed)
        ks = jax.random.split(key, 4)
        sd = 1.0 / np.sqrt(D).astype(np.float32)
        sh = 1.0 / np.sqrt(H).astype(np.float32)
        return {'x': jax.random.normal(ks[0], (B, S, D), jnp.float32), 'Wg': jax.random.normal(ks[1], (D, E), jnp.float32) * sd, 'bg': jnp.zeros((E,), jnp.float32), 'W1': jax.random.normal(ks[2], (E, D, H), jnp.float32) * sd, 'b1': jnp.zeros((E, H), jnp.float32), 'W2': jax.random.normal(ks[3], (E, H, D), jnp.float32) * sh, 'b2': jnp.zeros((E, D), jnp.float32)}
    _L1_ffn_all = _L1_ffn_setup()
    _L1_ffn_in = {k: v for k, v in _L1_ffn_all.items() if k in ('Wg', 'bg', 'W1', 'b1', 'W2', 'b2')}
    del _L1_ffn_all

    def _L2_attn_setup():
        import jax, jax.numpy as jnp
        import numpy as np
        DIM = 256
        HEADS = 16
        HEAD_DIM = DIM // HEADS
        SCALE = HEAD_DIM ** (-0.5)
        key = jax.random.key(seed)
        k1, k2, k3, k4 = jax.random.split(key, 4)
        x = jax.random.normal(k1, (4, 512, DIM), dtype=jnp.float32)
        w_qkv = jax.random.normal(k2, (3 * DIM, DIM), dtype=jnp.float32) * DIM ** (-0.5)
        w_proj = jax.random.normal(k3, (DIM, DIM), dtype=jnp.float32) * DIM ** (-0.5)
        b_proj = jax.random.normal(k4, (DIM,), dtype=jnp.float32) * 0.02
        return {'x': x, 'w_qkv': w_qkv, 'w_proj': w_proj, 'b_proj': b_proj}
    _L2_attn_all = _L2_attn_setup()
    _L2_attn_in = {k: v for k, v in _L2_attn_all.items() if k in ('w_qkv', 'w_proj', 'b_proj')}
    del _L2_attn_all

    def _L2_xattn_setup():
        import jax, jax.numpy as jnp
        import numpy as np
        EPS = 1e-05

        def layer_norm(x, g, b):
            mu = jnp.mean(x, axis=-1, keepdims=True)
            var = jnp.var(x, axis=-1, keepdims=True)
            return (x - mu) * jax.lax.rsqrt(var + EPS) * g + b
        key = jax.random.key(seed)
        ks = jax.random.split(key, 8)
        dim, heads, dim_head = (256, 16, 64)
        inner = heads * dim_head
        b, n, m = (8, 1024, 64)
        s = dim ** (-0.5)
        return {'x': jax.random.normal(ks[0], (b, n, dim), jnp.float32), 'latents': jax.random.normal(ks[1], (b, m, dim), jnp.float32), 'ln_m_g': jnp.ones((dim,), jnp.float32), 'ln_m_b': jnp.zeros((dim,), jnp.float32), 'ln_l_g': jnp.ones((dim,), jnp.float32), 'ln_l_b': jnp.zeros((dim,), jnp.float32), 'Wq': jax.random.normal(ks[2], (dim, inner), jnp.float32) * s, 'Wkv': jax.random.normal(ks[3], (dim, 2 * inner), jnp.float32) * s, 'Wout': jax.random.normal(ks[4], (inner, dim), jnp.float32) * s}
    _L2_xattn_all = _L2_xattn_setup()
    _L2_xattn_in = {k: v for k, v in _L2_xattn_all.items() if k in ('ln_m_g', 'ln_m_b', 'ln_l_g', 'ln_l_b', 'Wq', 'Wkv', 'Wout')}
    del _L2_xattn_all

    def _L2_ffn_setup():
        import jax, jax.numpy as jnp
        import numpy as np
        B, S, H, F, G = (8, 512, 256, 1024, 128)
        EPS = 1e-05

        def _dequant(q, scales, g):
            K, N = q.shape
            w = (q.astype(jnp.float32) - 128.0).reshape(K // g, g, N) * scales[:, None, :]
            return w.reshape(K, N)
        key = jax.random.key(seed)
        ks = jax.random.split(key, 8)
        x = jax.random.normal(ks[0], (B, S, H), dtype=jnp.float32)
        ln_gamma = jnp.ones((H,), jnp.float32)
        ln_beta = jnp.zeros((H,), jnp.float32)
        fc1_q = jax.random.randint(ks[1], (H, F), 0, 64, dtype=jnp.int32)
        fc2_q = jax.random.randint(ks[2], (F, H), 0, 64, dtype=jnp.int32)
        fc1_scales = jax.random.uniform(ks[3], (H // G, F), jnp.float32) * 0.02 + 0.001
        fc2_scales = jax.random.uniform(ks[4], (F // G, H), jnp.float32) * 0.02 + 0.001
        fc1_bias = jax.random.normal(ks[5], (F,), jnp.float32) * 0.02
        fc2_bias = jax.random.normal(ks[6], (H,), jnp.float32) * 0.02
        return {'x': x, 'ln_gamma': ln_gamma, 'ln_beta': ln_beta, 'fc1_q': fc1_q, 'fc1_scales': fc1_scales, 'fc1_bias': fc1_bias, 'fc2_q': fc2_q, 'fc2_scales': fc2_scales, 'fc2_bias': fc2_bias}
    _L2_ffn_all = _L2_ffn_setup()
    _L2_ffn_in = {k: v for k, v in _L2_ffn_all.items() if k in ('ln_gamma', 'ln_beta', 'fc1_q', 'fc1_scales', 'fc1_bias', 'fc2_q', 'fc2_scales', 'fc2_bias')}
    del _L2_ffn_all

    def _L3_attn_setup():
        import jax, jax.numpy as jnp
        import numpy as np
        import math
        EMBED_DIM = 256
        NUM_HEADS = 16
        HEAD_DIM = EMBED_DIM // NUM_HEADS

        def alibi_slopes(num_heads: int) -> np.ndarray:

            def slopes_pow2(n):
                start = 2.0 ** (-2.0 ** (-(math.log2(n) - 3)))
                return [start * start ** i for i in range(n)]
            if math.log2(num_heads).is_integer():
                return np.array(slopes_pow2(num_heads), dtype=np.float32)
            closest = 2 ** math.floor(math.log2(num_heads))
            extra = slopes_pow2(2 * closest)[closest:]
            return np.array(slopes_pow2(closest) + extra[:num_heads - closest], dtype=np.float32)
        key = jax.random.key(seed)
        ks = jax.random.split(key, 9)
        B, S, E = (2, 512, EMBED_DIM)
        scale = 1.0 / math.sqrt(E)
        x = jax.random.normal(ks[0], (B, S, E), dtype=jnp.float32)
        Wq = jax.random.normal(ks[1], (E, E), dtype=jnp.float32) * scale
        Wk = jax.random.normal(ks[2], (E, E), dtype=jnp.float32) * scale
        Wv = jax.random.normal(ks[3], (E, E), dtype=jnp.float32) * scale
        Wo = jax.random.normal(ks[4], (E, E), dtype=jnp.float32) * scale
        bq = jax.random.normal(ks[5], (E,), dtype=jnp.float32) * 0.01
        bk = jax.random.normal(ks[6], (E,), dtype=jnp.float32) * 0.01
        bv = jax.random.normal(ks[7], (E,), dtype=jnp.float32) * 0.01
        bo = jax.random.normal(ks[8], (E,), dtype=jnp.float32) * 0.01
        return {'x': x, 'Wq': Wq, 'bq': bq, 'Wk': Wk, 'bk': bk, 'Wv': Wv, 'bv': bv, 'Wo': Wo, 'bo': bo}
    _L3_attn_all = _L3_attn_setup()
    _L3_attn_in = {k: v for k, v in _L3_attn_all.items() if k in ('Wq', 'bq', 'Wk', 'bk', 'Wv', 'bv', 'Wo', 'bo')}
    del _L3_attn_all

    def _L3_xattn_setup():
        import jax, jax.numpy as jnp
        import numpy as np
        HIDDEN = 256
        HEADS = 16
        N, T1, T2 = (2, 512, 512)

        def _split_heads(x):
            n, t, e = x.shape
            return x.reshape(n, t, HEADS, e // HEADS).transpose(0, 2, 1, 3)
        key = jax.random.key(seed)
        k1, k2, k3, k4 = jax.random.split(key, 4)
        q = jax.random.normal(k1, (N, T1, HIDDEN), dtype=jnp.float32)
        encoder_k = jax.random.normal(k2, (N, T2, HIDDEN), dtype=jnp.float32)
        encoder_v = jax.random.normal(k3, (N, T2, HIDDEN), dtype=jnp.float32)
        encoder_attention_mask = jnp.zeros((N, 1, T2, T2), dtype=jnp.float32)
        wo_w = jax.random.normal(k4, (HIDDEN, HIDDEN), dtype=jnp.float32) * (1.0 / np.sqrt(HIDDEN))
        wo_b = jnp.zeros((HIDDEN,), dtype=jnp.float32)
        return {'q': q, 'encoder_k': encoder_k, 'encoder_v': encoder_v, 'encoder_attention_mask': encoder_attention_mask, 'wo_w': wo_w, 'wo_b': wo_b}
    _L3_xattn_all = _L3_xattn_setup()
    _L3_xattn_in = {k: v for k, v in _L3_xattn_all.items() if k in ('wo_w', 'wo_b')}
    del _L3_xattn_all

    def _L3_ffn_setup():
        import jax, jax.numpy as jnp
        import numpy as np
        DIM = 256

        def _reference_tuple_inner(x, W_r, W_k, W_v, mu_r, mu_k):
            B, T, C = x.shape
            x_prev = jnp.concatenate([jnp.zeros((B, 1, C), x.dtype), x[:, :-1, :]], axis=1)
            xr = mu_r * x + (1.0 - mu_r) * x_prev
            xk = mu_k * x + (1.0 - mu_k) * x_prev
            r = jax.nn.sigmoid(jnp.einsum('btc,dc->btd', xr, W_r))
            k = jnp.einsum('btc,dc->btd', xk, W_k)
            k_act = jnp.square(jax.nn.relu(k))
            out = r * jnp.einsum('btc,dc->btd', k_act, W_v)
            new_state = x[:, -1, :]
            return (out, new_state)
        key = jax.random.key(seed)
        ks = jax.random.split(key, 6)
        B, T, C = (8, 512, DIM)
        x = jax.random.normal(ks[0], (B, T, C), dtype=jnp.float32)
        s = 1.0 / np.sqrt(C)
        W_r = jax.random.uniform(ks[1], (C, C), jnp.float32, -s, s)
        W_k = jax.random.uniform(ks[2], (C, C), jnp.float32, -s, s)
        W_v = jax.random.uniform(ks[3], (C, C), jnp.float32, -s, s)
        mu_r = jax.random.uniform(ks[4], (C,), jnp.float32)
        mu_k = jax.random.uniform(ks[5], (C,), jnp.float32)
        return {'x': x, 'W_r': W_r, 'W_k': W_k, 'W_v': W_v, 'mu_r': mu_r, 'mu_k': mu_k}
    _L3_ffn_all = _L3_ffn_setup()
    _L3_ffn_in = {k: v for k, v in _L3_ffn_all.items() if k in ('W_r', 'W_k', 'W_v', 'mu_r', 'mu_k')}
    del _L3_ffn_all
    return {'x': x, 'ctx_1024': ctx_1024, 'mask_BxS2_ff1': mask_BxS2_ff1, 'mask_Bx1xSxS2_ff0': mask_Bx1xSxS2_ff0, 'L0_attn_in_proj_w': _L0_attn_in['in_proj_w'], 'L0_attn_in_proj_b': _L0_attn_in['in_proj_b'], 'L0_attn_out_w': _L0_attn_in['out_w'], 'L0_attn_out_b': _L0_attn_in['out_b'], 'L0_attn_up_w': _L0_attn_in['up_w'], 'L0_attn_up_b': _L0_attn_in['up_b'], 'L0_xattn_wq': _L0_xattn_in['wq'], 'L0_xattn_wk': _L0_xattn_in['wk'], 'L0_xattn_wv': _L0_xattn_in['wv'], 'L0_xattn_ln_gamma': _L0_xattn_in['ln_gamma'], 'L0_xattn_ln_beta': _L0_xattn_in['ln_beta'], 'L0_xattn_dense_w': _L0_xattn_in['dense_w'], 'L0_xattn_dense_b': _L0_xattn_in['dense_b'], 'L0_ffn_Wr': _L0_ffn_in['Wr'], 'L0_ffn_W1': _L0_ffn_in['W1'], 'L0_ffn_b1': _L0_ffn_in['b1'], 'L0_ffn_Wo': _L0_ffn_in['Wo'], 'L0_ffn_bo': _L0_ffn_in['bo'], 'L0_ffn_gamma': _L0_ffn_in['gamma'], 'L0_ffn_beta': _L0_ffn_in['beta'], 'L1_attn_Wq': _L1_attn_in['Wq'], 'L1_attn_bq': _L1_attn_in['bq'], 'L1_attn_Wk': _L1_attn_in['Wk'], 'L1_attn_bk': _L1_attn_in['bk'], 'L1_attn_Wv': _L1_attn_in['Wv'], 'L1_attn_bv': _L1_attn_in['bv'], 'L1_attn_Wo': _L1_attn_in['Wo'], 'L1_attn_bo': _L1_attn_in['bo'], 'L1_attn_ln_g': _L1_attn_in['ln_g'], 'L1_attn_ln_b': _L1_attn_in['ln_b'], 'L1_xattn_wq': _L1_xattn_in['wq'], 'L1_xattn_wk': _L1_xattn_in['wk'], 'L1_xattn_wv': _L1_xattn_in['wv'], 'L1_xattn_wo': _L1_xattn_in['wo'], 'L1_xattn_bq': _L1_xattn_in['bq'], 'L1_xattn_bk': _L1_xattn_in['bk'], 'L1_xattn_bv': _L1_xattn_in['bv'], 'L1_xattn_bo': _L1_xattn_in['bo'], 'L1_ffn_Wg': _L1_ffn_in['Wg'], 'L1_ffn_bg': _L1_ffn_in['bg'], 'L1_ffn_W1': _L1_ffn_in['W1'], 'L1_ffn_b1': _L1_ffn_in['b1'], 'L1_ffn_W2': _L1_ffn_in['W2'], 'L1_ffn_b2': _L1_ffn_in['b2'], 'L2_attn_w_qkv': _L2_attn_in['w_qkv'], 'L2_attn_w_proj': _L2_attn_in['w_proj'], 'L2_attn_b_proj': _L2_attn_in['b_proj'], 'L2_xattn_ln_m_g': _L2_xattn_in['ln_m_g'], 'L2_xattn_ln_m_b': _L2_xattn_in['ln_m_b'], 'L2_xattn_ln_l_g': _L2_xattn_in['ln_l_g'], 'L2_xattn_ln_l_b': _L2_xattn_in['ln_l_b'], 'L2_xattn_Wq': _L2_xattn_in['Wq'], 'L2_xattn_Wkv': _L2_xattn_in['Wkv'], 'L2_xattn_Wout': _L2_xattn_in['Wout'], 'L2_ffn_ln_gamma': _L2_ffn_in['ln_gamma'], 'L2_ffn_ln_beta': _L2_ffn_in['ln_beta'], 'L2_ffn_fc1_q': _L2_ffn_in['fc1_q'], 'L2_ffn_fc1_scales': _L2_ffn_in['fc1_scales'], 'L2_ffn_fc1_bias': _L2_ffn_in['fc1_bias'], 'L2_ffn_fc2_q': _L2_ffn_in['fc2_q'], 'L2_ffn_fc2_scales': _L2_ffn_in['fc2_scales'], 'L2_ffn_fc2_bias': _L2_ffn_in['fc2_bias'], 'L3_attn_Wq': _L3_attn_in['Wq'], 'L3_attn_bq': _L3_attn_in['bq'], 'L3_attn_Wk': _L3_attn_in['Wk'], 'L3_attn_bk': _L3_attn_in['bk'], 'L3_attn_Wv': _L3_attn_in['Wv'], 'L3_attn_bv': _L3_attn_in['bv'], 'L3_attn_Wo': _L3_attn_in['Wo'], 'L3_attn_bo': _L3_attn_in['bo'], 'L3_xattn_wo_w': _L3_xattn_in['wo_w'], 'L3_xattn_wo_b': _L3_xattn_in['wo_b'], 'L3_ffn_W_r': _L3_ffn_in['W_r'], 'L3_ffn_W_k': _L3_ffn_in['W_k'], 'L3_ffn_W_v': _L3_ffn_in['W_v'], 'L3_ffn_mu_r': _L3_ffn_in['mu_r'], 'L3_ffn_mu_k': _L3_ffn_in['mu_k']}

def reference(x, ctx_1024, mask_BxS2_ff1, mask_Bx1xSxS2_ff0, L0_attn_in_proj_w, L0_attn_in_proj_b, L0_attn_out_w, L0_attn_out_b, L0_attn_up_w, L0_attn_up_b, L0_xattn_wq, L0_xattn_wk, L0_xattn_wv, L0_xattn_ln_gamma, L0_xattn_ln_beta, L0_xattn_dense_w, L0_xattn_dense_b, L0_ffn_Wr, L0_ffn_W1, L0_ffn_b1, L0_ffn_Wo, L0_ffn_bo, L0_ffn_gamma, L0_ffn_beta, L1_attn_Wq, L1_attn_bq, L1_attn_Wk, L1_attn_bk, L1_attn_Wv, L1_attn_bv, L1_attn_Wo, L1_attn_bo, L1_attn_ln_g, L1_attn_ln_b, L1_xattn_wq, L1_xattn_wk, L1_xattn_wv, L1_xattn_wo, L1_xattn_bq, L1_xattn_bk, L1_xattn_bv, L1_xattn_bo, L1_ffn_Wg, L1_ffn_bg, L1_ffn_W1, L1_ffn_b1, L1_ffn_W2, L1_ffn_b2, L2_attn_w_qkv, L2_attn_w_proj, L2_attn_b_proj, L2_xattn_ln_m_g, L2_xattn_ln_m_b, L2_xattn_ln_l_g, L2_xattn_ln_l_b, L2_xattn_Wq, L2_xattn_Wkv, L2_xattn_Wout, L2_ffn_ln_gamma, L2_ffn_ln_beta, L2_ffn_fc1_q, L2_ffn_fc1_scales, L2_ffn_fc1_bias, L2_ffn_fc2_q, L2_ffn_fc2_scales, L2_ffn_fc2_bias, L3_attn_Wq, L3_attn_bq, L3_attn_Wk, L3_attn_bk, L3_attn_Wv, L3_attn_bv, L3_attn_Wo, L3_attn_bo, L3_xattn_wo_w, L3_xattn_wo_b, L3_ffn_W_r, L3_ffn_W_k, L3_ffn_W_v, L3_ffn_mu_r, L3_ffn_mu_k):
    import jax
    import jax.numpy as jnp

    def _L0_attn_ref(query, in_proj_w, in_proj_b, out_w, out_b, up_w, up_b):
        import jax, jax.numpy as jnp
        import numpy as np
        NUM_HEADS = 16
        LEVELS = 4

        def _mha(x, w_in, b_in, w_out, b_out):
            B, S, E = x.shape
            H = NUM_HEADS
            hd = E // H
            qkv = x @ w_in.T + b_in
            q, k, v = jnp.split(qkv, 3, axis=-1)
            split = lambda t: t.reshape(B, S, H, hd).transpose(0, 2, 1, 3)
            q, k, v = (split(q), split(k), split(v))
            scores = jnp.einsum('bhqd,bhkd->bhqk', q, k) / jnp.sqrt(jnp.asarray(hd, x.dtype))
            attn = jax.nn.softmax(scores, axis=-1)
            out = jnp.einsum('bhqk,bhkd->bhqd', attn, v)
            out = out.transpose(0, 2, 1, 3).reshape(B, S, E)
            return out @ w_out.T + b_out

        def _upsample_linear(x, target):
            B, L, E = x.shape
            src = (jnp.arange(target, dtype=jnp.float32) + 0.5) * (L / target) - 0.5
            src = jnp.clip(src, 0.0, L - 1)
            i0 = jnp.floor(src).astype(jnp.int32)
            i1 = jnp.minimum(i0 + 1, L - 1)
            w = (src - i0.astype(jnp.float32))[None, :, None].astype(x.dtype)
            return x[:, i0, :] * (1 - w) + x[:, i1, :] * w
        B, S, E = query.shape
        outs = []
        for lvl in range(LEVELS):
            stride = 2 ** lvl
            x = query[:, ::stride, :]
            outs.append(_mha(x, in_proj_w[lvl], in_proj_b[lvl], out_w[lvl], out_b[lvl]))
        current = outs[-1]
        for lvl in range(LEVELS - 2, -1, -1):
            fine = outs[lvl]
            if current.shape[1] != fine.shape[1]:
                current = _upsample_linear(current, fine.shape[1])
            current = current @ up_w[lvl].T + up_b[lvl]
            current = current + fine
        return current

    def _L0_xattn_ref(q, k, v, mask, wq, wk, wv, ln_gamma, ln_beta, dense_w, dense_b):
        import jax, jax.numpy as jnp
        import numpy as np
        D_MODEL = 256
        HEADS = 16
        DEPTH = D_MODEL // HEADS
        B, S = (4, 1024)
        EPS_K = 1e-06
        EPS_LN = 1e-06

        def _layernorm(x, g, b):
            m = jnp.mean(x, axis=-1, keepdims=True)
            var = jnp.var(x, axis=-1, keepdims=True)
            return (x - m) * jax.lax.rsqrt(var + EPS_LN) * g + b

        def _split_heads(x):
            bsz, sl, _ = x.shape
            return x.reshape(bsz, sl, HEADS, DEPTH).transpose(0, 2, 1, 3)
        bsz = q.shape[0]
        em = mask[:, None, :, None]
        qh = _split_heads(_layernorm(q @ wq, ln_gamma, ln_beta))
        kh = _split_heads(_layernorm(k @ wk, ln_gamma, ln_beta))
        vh = _split_heads(_layernorm(v @ wv, ln_gamma, ln_beta))
        q_prime = jax.nn.relu(qh) + EPS_K
        k_prime = (jax.nn.relu(kh) + EPS_K) * em
        vh = vh * em
        kv = jnp.einsum('bhnd,bhne->bhde', k_prime, vh)
        z = 1.0 / (jnp.einsum('bhnd,bhd->bhn', q_prime, k_prime.sum(axis=-2)) + EPS_K)
        att = jnp.einsum('bhnd,bhde,bhn->bhne', q_prime, kv, z)
        att = att.reshape(bsz, -1, D_MODEL)
        out = att @ dense_w + dense_b
        return _layernorm(out, ln_gamma, ln_beta)

    def _L0_ffn_ref(hidden_states, Wr, W1, b1, Wo, bo, gamma, beta):
        import jax, jax.numpy as jnp
        import numpy as np
        LN_EPS = 1e-12
        B, S, H = hidden_states.shape
        E = Wr.shape[0]
        x = hidden_states.reshape(-1, H)
        router_logits = x @ Wr.T
        expert_idx = jnp.argmax(jax.nn.softmax(router_logits, axis=-1), axis=-1)
        inter = jnp.zeros((x.shape[0], W1.shape[2]), dtype=x.dtype)
        for e in range(E):
            mask = (expert_idx == e)[:, None].astype(x.dtype)
            inter = inter + mask * jax.nn.gelu(x @ W1[e] + b1[e], approximate=False)
        y = inter @ Wo + bo + x
        mu = jnp.mean(y, axis=-1, keepdims=True)
        var = jnp.mean(jnp.square(y - mu), axis=-1, keepdims=True)
        out = (y - mu) * jax.lax.rsqrt(var + LN_EPS) * gamma + beta
        return out.reshape(B, S, H)

    def _L1_attn_ref(x, Wq, bq, Wk, bk, Wv, bv, Wo, bo, ln_g, ln_b):
        import jax, jax.numpy as jnp
        import numpy as np
        B, N, C, H = (4, 2048, 256, 16)
        D = C // H
        EPS = 1e-05
        b, n, c = x.shape
        q = x @ Wq.T + bq
        k = x @ Wk.T + bk
        v = x @ Wv.T + bv
        split = lambda z: z.reshape(b, n, H, D).transpose(0, 2, 1, 3)
        q, k, v = (split(q), split(k), split(v))
        q = jax.nn.softmax(q, axis=-1)
        k = jax.nn.softmax(k, axis=-2)
        state = jnp.einsum('bhnd,bhne->bhde', k, v)
        out = jnp.einsum('bhnd,bhde->bhne', q, state)
        out = out.transpose(0, 2, 1, 3).reshape(b, n, c)
        mu = out.mean(-1, keepdims=True)
        var = out.var(-1, keepdims=True)
        out = (out - mu) * jax.lax.rsqrt(var + EPS) * ln_g + ln_b
        return out @ Wo.T + bo

    def _L1_xattn_ref(query, key, value, wq, wk, wv, wo, bq, bk, bv, bo):
        import jax, jax.numpy as jnp
        import numpy as np
        import math
        D_MODEL = 256
        NUM_HEADS = 16
        D_K = D_MODEL // NUM_HEADS
        SCALE = math.sqrt(D_K)

        def _xavier(key, shape):
            fan_in, fan_out = (shape[1], shape[0])
            a = math.sqrt(6.0 / (fan_in + fan_out))
            return jax.random.uniform(key, shape, jnp.float32, -a, a)
        B, Sq, _ = query.shape
        Sk = key.shape[1]
        q = (query @ wq.T + bq).reshape(B, Sq, NUM_HEADS, D_K).transpose(0, 2, 1, 3)
        k = (key @ wk.T + bk).reshape(B, Sk, NUM_HEADS, D_K).transpose(0, 2, 1, 3)
        v = (value @ wv.T + bv).reshape(B, Sk, NUM_HEADS, D_K).transpose(0, 2, 1, 3)
        scores = jnp.einsum('bhqd,bhkd->bhqk', q, k) / SCALE
        attn = jax.nn.softmax(scores, axis=-1)
        out = jnp.einsum('bhqk,bhkd->bhqd', attn, v)
        out = out.transpose(0, 2, 1, 3).reshape(B, Sq, D_MODEL)
        return out @ wo.T + bo

    def _L1_ffn_ref(x, Wg, bg, W1, b1, W2, b2):
        import jax, jax.numpy as jnp
        import numpy as np
        B, S, D, H, E = (8, 512, 256, 1024, 16)
        d = x.shape[-1]
        xf = x.reshape(-1, d)
        n_tok = xf.shape[0]
        n_exp = Wg.shape[1]
        cap = -(-n_tok // n_exp)
        score = jax.nn.softmax(xf @ Wg + bg, axis=-1)
        gate = jnp.max(score, axis=-1)
        idx = jnp.argmax(score, axis=-1)
        onehot = jax.nn.one_hot(idx, n_exp, dtype=jnp.int32)
        pos = jnp.sum((jnp.cumsum(onehot, axis=0) - 1) * onehot, axis=-1)
        keep = pos < cap
        safe_pos = jnp.where(keep, pos, cap - 1)
        buf = jnp.zeros((n_exp, cap, d), x.dtype).at[idx, safe_pos].add(jnp.where(keep[:, None], xf, 0.0))
        h = jax.nn.relu(jnp.einsum('ecd,edh->ech', buf, W1) + b1[:, None, :])
        y = jnp.einsum('ech,ehd->ecd', h, W2) + b2[:, None, :]
        out = y[idx, safe_pos] * gate[:, None]
        out = jnp.where(keep[:, None], out, 0.0)
        return out.reshape(x.shape)

    def _L2_attn_ref(x, w_qkv, w_proj, b_proj):
        import jax, jax.numpy as jnp
        import numpy as np
        DIM = 256
        HEADS = 16
        HEAD_DIM = DIM // HEADS
        SCALE = HEAD_DIM ** (-0.5)
        b, n, c = x.shape
        qkv = jnp.einsum('bnc,oc->bno', x, w_qkv)
        q, k, v = jnp.split(qkv, 3, axis=-1)

        def to_heads(t):
            return t.reshape(b, n, HEADS, HEAD_DIM).transpose(0, 2, 1, 3)
        q, k, v = (to_heads(q), to_heads(k), to_heads(v))
        attn = jnp.einsum('bhqd,bhkd->bhqk', q, k) * SCALE
        attn = jax.nn.softmax(attn, axis=-1)
        out = jnp.einsum('bhqk,bhkd->bhqd', attn, v)
        out = out.transpose(0, 2, 1, 3).reshape(b, n, c)
        out = jnp.einsum('bnc,oc->bno', out, w_proj) + b_proj
        return out

    def _L2_xattn_ref(x, latents, ln_m_g, ln_m_b, ln_l_g, ln_l_b, Wq, Wkv, Wout):
        import jax, jax.numpy as jnp
        import numpy as np
        EPS = 1e-05

        def layer_norm(x, g, b):
            mu = jnp.mean(x, axis=-1, keepdims=True)
            var = jnp.var(x, axis=-1, keepdims=True)
            return (x - mu) * jax.lax.rsqrt(var + EPS) * g + b
        heads, dim_head = (16, 64)
        scale = dim_head ** (-0.5)
        x = layer_norm(x, ln_m_g, ln_m_b)
        lat = layer_norm(latents, ln_l_g, ln_l_b)
        b, m, _ = lat.shape
        q = lat @ Wq
        kv_input = jnp.concatenate([x, lat], axis=1)
        kv = kv_input @ Wkv
        k, v = jnp.split(kv, 2, axis=-1)

        def split_heads(t):
            return t.reshape(t.shape[0], t.shape[1], heads, dim_head).transpose(0, 2, 1, 3)
        q, k, v = (split_heads(q), split_heads(k), split_heads(v))
        dots = jnp.einsum('bhid,bhjd->bhij', q, k) * scale
        attn = jax.nn.softmax(dots, axis=-1)
        out = jnp.einsum('bhij,bhjd->bhid', attn, v)
        out = out.transpose(0, 2, 1, 3).reshape(b, m, heads * dim_head)
        return out @ Wout

    def _L2_ffn_ref(x, ln_gamma, ln_beta, fc1_q, fc1_scales, fc1_bias, fc2_q, fc2_scales, fc2_bias):
        import jax, jax.numpy as jnp
        import numpy as np
        B, S, H, F, G = (8, 512, 256, 1024, 128)
        EPS = 1e-05

        def _dequant(q, scales, g):
            K, N = q.shape
            w = (q.astype(jnp.float32) - 128.0).reshape(K // g, g, N) * scales[:, None, :]
            return w.reshape(K, N)
        residual = x
        mu = jnp.mean(x, axis=-1, keepdims=True)
        var = jnp.mean(jnp.square(x - mu), axis=-1, keepdims=True)
        h = (x - mu) * jax.lax.rsqrt(var + EPS) * ln_gamma + ln_beta
        hf = h.reshape(-1, H)
        w1 = _dequant(fc1_q, fc1_scales, G)
        y = hf @ w1 + fc1_bias
        y = jax.nn.silu(y)
        w2 = _dequant(fc2_q, fc2_scales, G)
        z = y @ w2 + fc2_bias
        return residual + 0.5 * z.reshape(residual.shape)

    def _L3_attn_ref(x, Wq, bq, Wk, bk, Wv, bv, Wo, bo):
        import jax, jax.numpy as jnp
        import numpy as np
        import math
        EMBED_DIM = 256
        NUM_HEADS = 16
        HEAD_DIM = EMBED_DIM // NUM_HEADS

        def alibi_slopes(num_heads: int) -> np.ndarray:

            def slopes_pow2(n):
                start = 2.0 ** (-2.0 ** (-(math.log2(n) - 3)))
                return [start * start ** i for i in range(n)]
            if math.log2(num_heads).is_integer():
                return np.array(slopes_pow2(num_heads), dtype=np.float32)
            closest = 2 ** math.floor(math.log2(num_heads))
            extra = slopes_pow2(2 * closest)[closest:]
            return np.array(slopes_pow2(closest) + extra[:num_heads - closest], dtype=np.float32)
        B, S, E = x.shape
        H, D = (NUM_HEADS, HEAD_DIM)
        q = (x @ Wq.T + bq).reshape(B, S, H, D).transpose(0, 2, 1, 3)
        k = (x @ Wk.T + bk).reshape(B, S, H, D).transpose(0, 2, 1, 3)
        v = (x @ Wv.T + bv).reshape(B, S, H, D).transpose(0, 2, 1, 3)
        slopes = jnp.asarray(alibi_slopes(H))
        pos = jnp.arange(S, dtype=jnp.float32)
        rel = jnp.abs(pos[None, :] - pos[:, None])
        bias = -slopes[:, None, None] * rel[None, :, :]
        scores = jnp.einsum('bhqd,bhkd->bhqk', q, k) / math.sqrt(D)
        scores = scores + bias[None]
        causal = jnp.tril(jnp.ones((S, S), dtype=bool))
        scores = jnp.where(causal[None, None], scores, -jnp.inf)
        probs = jax.nn.softmax(scores, axis=-1)
        out = jnp.einsum('bhqk,bhkd->bhqd', probs, v)
        out = out.transpose(0, 2, 1, 3).reshape(B, S, E)
        return out @ Wo.T + bo

    def _L3_xattn_ref(q, encoder_k, encoder_v, encoder_attention_mask, wo_w, wo_b):
        import jax, jax.numpy as jnp
        import numpy as np
        HIDDEN = 256
        HEADS = 16
        N, T1, T2 = (2, 512, 512)

        def _split_heads(x):
            n, t, e = x.shape
            return x.reshape(n, t, HEADS, e // HEADS).transpose(0, 2, 1, 3)
        qh = _split_heads(q)
        kh = _split_heads(encoder_k)
        vh = _split_heads(encoder_v)
        scores = jnp.einsum('bhqd,bhkd->bhqk', qh, kh) + encoder_attention_mask
        weights = jax.nn.softmax(scores, axis=-1)
        ctx = jnp.einsum('bhqk,bhkd->bhqd', weights, vh)
        ctx = ctx.transpose(0, 2, 1, 3).reshape(q.shape[0], q.shape[1], -1)
        return jax.nn.relu(ctx @ wo_w.T + wo_b)

    def _L3_ffn_ref(x, W_r, W_k, W_v, mu_r, mu_k):
        import jax, jax.numpy as jnp
        import numpy as np
        DIM = 256

        def _reference_tuple_inner(x, W_r, W_k, W_v, mu_r, mu_k):
            B, T, C = x.shape
            x_prev = jnp.concatenate([jnp.zeros((B, 1, C), x.dtype), x[:, :-1, :]], axis=1)
            xr = mu_r * x + (1.0 - mu_r) * x_prev
            xk = mu_k * x + (1.0 - mu_k) * x_prev
            r = jax.nn.sigmoid(jnp.einsum('btc,dc->btd', xr, W_r))
            k = jnp.einsum('btc,dc->btd', xk, W_k)
            k_act = jnp.square(jax.nn.relu(k))
            out = r * jnp.einsum('btc,dc->btd', k_act, W_v)
            new_state = x[:, -1, :]
            return (out, new_state)
        return _reference_tuple_inner(x, W_r, W_k, W_v, mu_r, mu_k)[0]
    x = _layernorm(x + _L0_attn_ref(x, L0_attn_in_proj_w, L0_attn_in_proj_b, L0_attn_out_w, L0_attn_out_b, L0_attn_up_w, L0_attn_up_b), axis=-1)
    x = _layernorm(x + _L0_xattn_ref(x, ctx_1024, ctx_1024, mask_BxS2_ff1, L0_xattn_wq, L0_xattn_wk, L0_xattn_wv, L0_xattn_ln_gamma, L0_xattn_ln_beta, L0_xattn_dense_w, L0_xattn_dense_b), axis=-1)
    x = _layernorm(x + _L0_ffn_ref(x, L0_ffn_Wr, L0_ffn_W1, L0_ffn_b1, L0_ffn_Wo, L0_ffn_bo, L0_ffn_gamma, L0_ffn_beta), axis=-1)
    x = _layernorm(x + _L1_attn_ref(x, L1_attn_Wq, L1_attn_bq, L1_attn_Wk, L1_attn_bk, L1_attn_Wv, L1_attn_bv, L1_attn_Wo, L1_attn_bo, L1_attn_ln_g, L1_attn_ln_b), axis=-1)
    x = _layernorm(x + _L1_xattn_ref(x, ctx_1024, ctx_1024, L1_xattn_wq, L1_xattn_wk, L1_xattn_wv, L1_xattn_wo, L1_xattn_bq, L1_xattn_bk, L1_xattn_bv, L1_xattn_bo), axis=-1)
    x = _layernorm(x + _L1_ffn_ref(x, L1_ffn_Wg, L1_ffn_bg, L1_ffn_W1, L1_ffn_b1, L1_ffn_W2, L1_ffn_b2), axis=-1)
    x = _layernorm(x + _L2_attn_ref(x, L2_attn_w_qkv, L2_attn_w_proj, L2_attn_b_proj), axis=-1)
    x = _layernorm(x + _L2_xattn_ref(ctx_1024, x, L2_xattn_ln_m_g, L2_xattn_ln_m_b, L2_xattn_ln_l_g, L2_xattn_ln_l_b, L2_xattn_Wq, L2_xattn_Wkv, L2_xattn_Wout), axis=-1)
    x = _layernorm(x + _L2_ffn_ref(x, L2_ffn_ln_gamma, L2_ffn_ln_beta, L2_ffn_fc1_q, L2_ffn_fc1_scales, L2_ffn_fc1_bias, L2_ffn_fc2_q, L2_ffn_fc2_scales, L2_ffn_fc2_bias), axis=-1)
    x = _layernorm(x + _L3_attn_ref(x, L3_attn_Wq, L3_attn_bq, L3_attn_Wk, L3_attn_bk, L3_attn_Wv, L3_attn_bv, L3_attn_Wo, L3_attn_bo), axis=-1)
    x = _layernorm(x + _L3_xattn_ref(x, ctx_1024, ctx_1024, mask_Bx1xSxS2_ff0, L3_xattn_wo_w, L3_xattn_wo_b), axis=-1)
    x = _layernorm(x + _L3_ffn_ref(x, L3_ffn_W_r, L3_ffn_W_k, L3_ffn_W_v, L3_ffn_mu_r, L3_ffn_mu_k), axis=-1)
    return x

_drawn_inputs = setup_inputs


def setup_inputs(seed=0):
    import zlib

    import numpy as np

    out = dict(_drawn_inputs(seed))
    spreads = {'L0_attn_in_proj_b': (0.0, 0.8),
     'L0_attn_out_b': (0.0, 0.461),
     'L0_attn_up_b': (0.0, 0.426),
     'L0_xattn_ln_gamma': (1.0, 0.6),
     'L0_xattn_ln_beta': (0.0, 0.391),
     'L0_xattn_dense_b': (0.0, 0.1),
     'L0_ffn_gamma': (1.0, 0.6),
     'L0_ffn_beta': (0.0, 0.541),
     'L1_attn_ln_g': (1.0, 0.6),
     'L1_attn_ln_b': (0.0, 0.8),
     'L1_xattn_bq': (0.0, 0.8),
     'L1_xattn_bk': (0.0, 2.0),
     'L1_xattn_bv': (0.0, 0.6),
     'L1_xattn_bo': (0.0, 0.465),
     'L1_ffn_bg': (0.0, 0.8),
     'L1_ffn_b1': (0.0, 2.0),
     'L1_ffn_b2': (0.0, 2.0),
     'L2_xattn_ln_m_g': (1.0, 0.6),
     'L2_xattn_ln_m_b': (0.0, 0.1),
     'L2_xattn_ln_l_g': (1.0, 0.6),
     'L2_xattn_ln_l_b': (0.0, 0.8),
     'L2_ffn_ln_gamma': (1.0, 0.2),
     'L2_ffn_ln_beta': (0.0, 0.267),
     'L3_xattn_wo_b': (0.0, 0.1)}
    factors = {'L0_attn_in_proj_w': 8.0,
     'L0_attn_out_w': 6.406,
     'L0_attn_up_w': 3.8,
     'L0_xattn_wq': 5.453,
     'L0_xattn_wk': 3.984,
     'L0_ffn_Wr': 7.592,
     'L0_ffn_W1': 7.41,
     'L0_ffn_b1': 8.0,
     'L0_ffn_Wo': 4.209,
     'L0_ffn_bo': 23.442,
     'L1_attn_Wq': 8.0,
     'L1_attn_bq': 8.0,
     'L1_attn_Wk': 5.593,
     'L1_attn_bk': 200.0,
     'L1_attn_bo': 8.0,
     'L1_xattn_wk': 3.259,
     'L1_ffn_Wg': 4.77,
     'L1_ffn_W1': 6.381,
     'L1_ffn_W2': 4.787,
     'L2_attn_b_proj': 8.0,
     'L2_ffn_fc1_bias': 55.501,
     'L2_ffn_fc2_bias': 200.0,
     'L3_attn_Wq': 8.0,
     'L3_attn_bq': 200.0,
     'L3_attn_Wk': 8.0,
     'L3_attn_bk': 200.0,
     'L3_attn_bv': 8.0,
     'L3_attn_bo': 7.459,
     'L3_ffn_mu_r': 25.782,
     'L3_ffn_mu_k': 8.0}
    for name, (base, spread) in spreads.items():
        noise = np.random.default_rng([zlib.crc32(name.encode()), seed]).standard_normal(out[name].shape)
        drawn = base * np.exp(spread * noise) if base else spread * noise
        out[name] = jnp.asarray(drawn.astype(out[name].dtype))
    for name, factor in factors.items():
        out[name] = (out[name] * factor).astype(out[name].dtype)
    return out
```

```python
from contextlib import ExitStack, contextmanager

import numpy as np

import concourse.bass as bass
from concourse import mybir

F32 = mybir.dt.float32
BF16 = mybir.dt.bfloat16
I32 = mybir.dt.int32
U32 = mybir.dt.uint32
ALU = mybir.AluOpType
ACT = mybir.ActivationFunctionType
AX = mybir.AxisListType.X

P = 128
B, S, C = 4, 512, 256
SC = 1024
T, TC = B * S, B * SC
NT, NTC = T // P, TC // P
CH = C // P
H, HD = 16, 16
QUAD = 32
HG = 4
NG = H // HG
Q_PART = (0, 0, 1, 1, 0, 2)
K_PART = (0, 1, 0, 1, 2, 0)
STACK = len(Q_PART) * HD
BANK = 512


class Program:

    FIRST_SEM, SET = 176, 38

    def __init__(self, nc, inputs):
        self.nc, self.inp = nc, inputs
        self.stages = 0

    @contextmanager
    def stage(self, *names):
        first = self.FIRST_SEM + self.SET * (self.stages % 2)
        assert len(names) <= self.SET
        self.stages += 1
        with ExitStack() as held:
            yield [held.enter_context(self.nc.semaphore(f"s{self.stages}_{name}", num=first + i))
                   for i, name in enumerate(names)]

    def clear_last_set(self, sync):
        first = self.FIRST_SEM + self.SET * (self.stages % 2)
        sync.sem_clear(range(first, first + self.SET))


def load_stage(k, pairs):
    nc = k.nc
    with k.stage("loaded") as (loaded,), nc.Block(no_gpsimd_drain=True) as block:
        @block.sync
        def _(sync):
            k.clear_last_set(sync)
            for tile, source in pairs[0::2]:
                sync.dma_start(tile, source).then_inc(loaded, 16)
            sync.wait_ge(loaded, 16 * len(pairs))

        @block.scalar
        def _(act):
            for tile, source in pairs[1::2]:
                act.dma_start(tile, source).then_inc(loaded, 16)


def project_stage(k, units, weights):
    nc = k.nc
    splits = [n for n, u in enumerate(units) if u[0] == "split"]
    with (
        nc.sbuf_tensor(f"proj_full_{k.stages}", [P, 2, BANK], F32) as full,
        nc.sbuf_tensor(f"proj_rest_{k.stages}", [P, 2, BANK], F32) as rest,
        nc.sbuf_tensor(f"proj_parts_{k.stages}", [P, 3, 3, BANK], BF16) as parts,
        nc.sbuf_tensor(f"proj_value_{k.stages}", [P, 2, H, QUAD], F32) as value,
        k.stage("weights", "ready", "evacuated", "high", "remainder", "middle", "low", "ones", "parts_stored0",
                "parts_stored1", "parts_stored2", "value_stored0", "value_stored1") as (
            weights_in, ready, evacuated, high, remainder, middle, low, ones_set, *stores),
        nc.Block() as block,
    ):
        parts_stored, value_stored = stores[0:3], stores[3:5]

        @block.sync
        def _(sync):
            k.clear_last_set(sync)
            for tile, source in weights:
                sync.dma_start(tile, source).then_inc(weights_in, 16)
            i = j = 0
            for n, unit in enumerate(units):
                if unit[0] == "split":
                    sync.wait_ge(low, i + 1)
                    sync.dma_start(unit[4], parts[:, i % 3, :, 0:unit[2]]).then_inc(parts_stored[i % 3], 16)
                    i += 1
                else:
                    sync.wait_ge(evacuated, n + 1)
                    sync.dma_start(unit[3], value[0:unit[2], j % 2].rearrange("p h d -> p (h d)")
                                   ).then_inc(value_stored[j % 2], 16)
                    j += 1
            for r in range(3):
                sync.wait_ge(parts_stored[r], 16 * len(range(r, i, 3)))
            for r in range(2):
                sync.wait_ge(value_stored[r], 16 * len(range(r, j, 2)))

        @block.tensor
        def _(pe):
            pe.wait_ge(weights_in, 16 * len(weights))
            for n, unit in enumerate(units):
                if n >= 4:
                    pe.wait_ge(evacuated, n - 3)
                rows = P if unit[0] == "split" else unit[2]
                for cols, lhsT, rhs, start, stop in unit[1]:
                    last = nc.tensor.matmul(k.ps[0:rows, n % 4, cols], lhsT, rhs, start=start, stop=stop)
                last.then_inc(ready, 1)

        @block.scalar
        def _(act):
            act.wait_ge(ones_set, 1)
            i = j = 0
            for n, unit in enumerate(units):
                act.wait_ge(ready, n + 1)
                if unit[0] == "split":
                    _, _, width, bias, _ = unit
                    if i >= 2:
                        act.wait_ge(remainder, i - 1)
                    if i == 0 and bias is not None:
                        act.wait_ge(weights_in, 16 * len(weights))
                    nc.scalar.activation(full[:, i % 2, 0:width], k.ps[:, n % 4, 0:width], ACT.Identity,
                                         bias=0.0 if bias is None else bias).then_inc(evacuated, 1)
                    i += 1
                else:
                    rows = unit[2]
                    if j >= 2:
                        act.wait_ge(value_stored[j % 2], 16 * (j // 2))
                    d = HD if unit[0] == "value" else QUAD
                    nc.scalar.activation(value[0:rows, j % 2, :, 0:d], k.ps[0:rows, n % 4, 0:H * d].rearrange("p (h d) -> p h d", h=H),
                                         ACT.Copy).then_inc(evacuated, 1)
                    j += 1

        @block.vector
        def _(dve):
            nc.vector.memset(value[:], 1.0).then_inc(ones_set, 1)
            for i, n in enumerate(splits):
                width = units[n][2]
                dve.wait_ge(evacuated, n + 1)
                if i >= 3:
                    dve.wait_ge(parts_stored[i % 3], 16 * (i // 3))
                nc.vector.tensor_copy(parts[:, i % 3, 0, 0:width], full[:, i % 2, 0:width]).then_inc(high, 1)
                if i >= 2:
                    dve.wait_ge(low, i - 1)
                dve.wait_ge(high, i + 1)
                nc.vector.tensor_tensor(rest[:, i % 2, 0:width], full[:, i % 2, 0:width],
                                        parts[:, i % 3, 0, 0:width], ALU.subtract).then_inc(remainder, 1)

        @block.gpsimd
        def _(pool):
            for i, n in enumerate(splits):
                width = units[n][2]
                pool.wait_ge(remainder, i + 1)
                nc.gpsimd.tensor_copy(parts[:, i % 3, 1, 0:width], rest[:, i % 2, 0:width]).then_inc(middle, 1)
                pool.wait_ge(middle, i + 1)
                nc.gpsimd.tensor_tensor(parts[:, i % 3, 2, 0:width], rest[:, i % 2, 0:width],
                                        parts[:, i % 3, 1, 0:width], ALU.subtract).then_inc(low, 1)


def split_units(source, width, weight, bias, store):
    tiles = store.shape[2] // width
    return [("split", [(slice(0, width), weight[:, c, m * P:(m + 1) * P], source(c, t), c == 0, c == CH - 1)
                       for c in range(CH)], width, None if bias is None else bias[:, m:m + 1],
             store[:, m * P:(m + 1) * P, t * width:(t + 1) * width].rearrange("a p n -> p a n"))
            for t in range(tiles) for m in range(CH)]


def value_units(source, rows, weight, store):
    return [("value", [(slice(0, C), source(c, t), weight[:, c, :], c == 0, c == CH - 1) for c in range(CH)],
             rows, store[t]) for t in range(store.shape[0])]


def attention_stage(k, name, q_parts, k_parts, values, nq, nk, scale, att, head_dim=HD, slopes=None, mask=None):
    nc = k.nc
    causal, small = slopes is not None, head_dim == HD
    heads = HG if small else 2
    groups, strip = H // heads, P // heads
    qt, kt, wide = min(P, nq), min(P, nk), min(BANK, nk)
    nqt, nkt, nwide = nq // qt, nk // kt, nk // wide
    rows_a = STACK + (3 if causal else 0)
    rows_b = rows_a + 3
    chunks = [(qi, j, c) for qi in range(nqt) for j in range(heads) for c in range(nwide)]
    steps = [(i, pair) for i in range(nkt) for pair in range(heads // 2)]
    NCH, NS = len(chunks), len(steps)
    slots = heads * nqt
    turn_step, sums_step = (1, 4) if NS >= 8 else (0, 1)
    per_step = [chunks[s * NCH // NS:(s + 1) * NCH // NS] for s in range(NS)]
    A0, B0, ACC, SIDE = 0, 2, 6, 7

    with ExitStack() as held:
        def sb(what, shape, dt):
            return held.enter_context(nc.sbuf_tensor(f"{name}_{what}", shape, dt))

        RING, V_RING = 4, 2
        if small:
            q_stack = [sb(f"q{r}", [rows_b, heads, nq], BF16) for r in range(RING)]
            k_stack = [sb(f"k{r}", [rows_b, heads, nk], BF16) for r in range(RING)]
        else:
            q_stack = [sb(f"q{r}", [P, 3, heads, nq], BF16) for r in range(RING)]
            k_stack = [sb(f"k{r}", [P, 2, heads, nk], BF16) for r in range(RING)]
            top_rows = [sb(f"top_rows{r}", [3, heads, nq], BF16) for r in range(RING)]
            weight_sums = sb("weight_sums", [kt, 2, heads, nq], F32)
        v_tile = [sb(f"v{r}", [P, nkt, P], F32) for r in range(V_RING)]
        weights = sb("weights", [P, 4, 2, nq], F32)
        part_max = sb("part_max", [qt, 2, slots, nwide], F32)
        row_max = sb("row_max", [P, 2, slots], F32)
        negative = sb("negative", [slots, 2, qt], F32)
        max_parts = sb("max_parts", [slots, 3, qt], BF16)
        sums = sb("sums", [P, nq], F32)
        inverse = sb("inverse", [P, nq], F32)
        names = ["row_in", "row_made", "a_ready", "a_taken", "max_ready", "turned", "s_ready", "exp_done", "pv_done", "acc_copied",
                 "sums_ready", "inverted", "normed", "set_up", "negated", "max_split", "added", "masked", "a_masked"]
        if mask is not None:
            mask_q, mask_k = sb("mask_q", [P, nqt, nk], F32), sb("mask_k", [P, nkt, nq], F32)
            masked_scores, with_mask = sb("masked_scores", [P, 2, 2, nq], F32), sb("with_mask", [P, 2, wide], F32)
        all_names = names + [f"loaded{r}" for r in range(RING)] + [f"v_loaded{r}" for r in range(V_RING)] + ([f"mask_q{i}" for i in range(nqt)] + [f"mask_k{i}" for i in range(nkt)]
                                                                   if mask is not None else [])
        (row_in, row_made, a_ready, a_taken, max_ready, turned, s_ready, exp_done, pv_done, acc_copied, sums_ready, inverted, normed,
         set_up, negated, max_split, added, masked, a_masked, *more) = held.enter_context(k.stage(*all_names))
        loaded, v_loaded, more = more[:RING], more[RING:RING + V_RING], more[RING + V_RING:]
        mask_q_in, mask_k_in = more[:nqt], more[nqt:]
        block = held.enter_context(nc.Block(no_gpsimd_drain=True))

        def at(b, g, per_group, n):
            return b * (groups * per_group) + (g * per_group + n)

        def first(b, g, n=1):
            return isinstance(b, int) and b * groups + g < n

        def later(b, g, ahead):
            return b + (g + ahead) // groups, (g + ahead) % groups

        def keys_of(qi, c):
            return slice(0, (qi + 1) * P) if causal else slice(c * wide, (c + 1) * wide)

        def queries_of(i):
            return slice(i * P if causal else 0, nq)

        def for_batches(engine, body):
            with engine.Fori(0, B - 1) as b:
                body(b, True)
            body(B - 1, False)

        def loads_of(b, g):
            r, head = g % RING, slice(g * heads * head_dim, (g + 1) * heads * head_dim)

            def part(parts, which, n):
                return parts[which, head, bass.ds(b * n, n)].rearrange("(j d) n -> d j n", d=head_dim)

            out = []
            if small:
                for stack, parts, order, n in ((q_stack[r], q_parts, Q_PART, nq), (k_stack[r], k_parts, K_PART, nk)):
                    out += [(stack[t * HD:(t + 1) * HD, :, :], part(parts, p, n)) for t, p in enumerate(order)]
            else:
                for stack, parts, order, n in ((q_stack[r], q_parts, (0, 0, 1, 1, 0, 2), nq), (k_stack[r], k_parts, (0, 1, 2, 0), nk)):
                    out += [(stack[(t % 2) * head_dim:(t % 2 + 1) * head_dim, t // 2, :, :], part(parts, p, n)) for t, p in enumerate(order)]
            if causal:
                out.append((k_stack[r][STACK:rows_a, :, :], slopes[:, g * heads:(g + 1) * heads, :]))
            return out

        n_loads = len(loads_of(0, 0))

        def loads_done(b, g):
            return 16 * n_loads * (b * (groups // RING) + (g // RING + 1))

        def v_done(b, g):
            return 16 * (b * (groups // V_RING) + (g // V_RING + 1))

        @block.sync
        def _(sync):
            k.clear_last_set(sync)

            def load_group(b, g):
                for tile, source in loads_of(b, g):
                    sync.dma_start(tile, source).then_inc(loaded[g % RING], 16)

            def load_values(b, g):
                sync.dma_start(v_tile[g % V_RING][0:kt, :, :], values[bass.ds(b * nkt, nkt), :, g * P:(g + 1) * P].rearrange("i p c -> p i c")
                               ).then_inc(v_loaded[g % V_RING], 16)

            def load_mask_q(b, qi):
                sync.dma_start(mask_q[:, qi, :], mask[0][bass.ds(b, 1), qi * P:(qi + 1) * P, :].rearrange("o p n -> p (o n)")).then_inc(mask_q_in[qi], 16)

            def load_mask_k(b, i):
                sync.dma_start(mask_k[:, i, :], mask[1][bass.ds(b, 1), i * P:(i + 1) * P, :].rearrange("o p n -> p (o n)")).then_inc(mask_k_in[i], 16)

            sync.wait_ge(set_up, 1)
            for g in range(2):
                load_group(0, g)
                load_values(0, g)
            if mask is not None:
                for qi in range(nqt):
                    load_mask_q(0, qi)
                for i in range(nkt):
                    load_mask_k(0, i)
            for g in range(2, RING):
                load_group(0, g)

            def row(b, g):
                sync.wait_ge(row_made, at(b, g, 1, 1))
                for p in range(3):
                    dst = q_stack[g % RING][rows_a + p:rows_a + p + 1, :, :] if small else top_rows[g % RING][p:p + 1, :, :]
                    sync.dma_start(dst.rearrange("o j (i t) -> o (j i) t", t=qt), max_parts[:, p, :]).then_inc(row_in, 16)

            row(0, 0)

            def batch(b, ahead):
                for g in range(groups):
                    if ahead or g < groups - 1:
                        row(*later(b, g, 1))
                    if mask is not None and ahead and g == groups - 3:
                        for qi in range(nqt):
                            sync.wait_ge(a_taken, at(b, groups - 1, NCH, (qi + 1) * NCH // nqt))
                            load_mask_q(b + 1, qi)
                    if mask is not None and ahead and g == groups - 1:
                        for i in range(nkt):
                            sync.wait_ge(masked, at(b, g, NS, (i + 1) * NS // nkt + 2))
                            load_mask_k(b + 1, i)
                    if ahead or g < groups - V_RING:
                        sync.wait_ge(pv_done, at(b, g, NS, NS + 4))
                        load_values(*later(b, g, V_RING))
                    if ahead or g < groups - RING:
                        load_group(*later(b, g, RING))

            for_batches(sync, batch)

        @block.tensor
        def _(pe):
            def pass_a(b, g, some, n0):
                r = g % RING
                if n0 == 0:
                    pe.wait_ge(loaded[r], loads_done(b, g))
                for n, (qi, j, c) in enumerate(some, n0):
                    if not (first(b, g) and n < 2):
                        pe.wait_ge(a_taken, at(b, g, NCH, n - 1))
                    keys, qs = keys_of(qi, c), slice(qi * qt, (qi + 1) * qt)
                    out = k.ps[0:qt, A0 + (g * NCH + n) % 2, 0:keys.stop - keys.start]
                    if small:
                        mm = nc.tensor.matmul(out, q_stack[r][0:rows_a, j, qs], k_stack[r][0:rows_a, j, keys], start=True, stop=not causal)
                    else:
                        mm = nc.tensor.matmul(out, q_stack[r][:, 0, j, qs], k_stack[r][:, 0, j, keys], start=True, stop=True)
                    if causal:
                        mm = nc.tensor.matmul(out[:, qi * P:(qi + 1) * P], k.ident_bf[:, :], k.above_q[:, :], start=False, stop=True)
                    mm.then_inc(a_ready, 1)

            def turn(b, g):
                pe.wait_ge(max_ready, at(b, g, 1, 1))
                if not first(b, g):
                    pb, pg = later(b, g, -1)
                    pe.wait_ge(normed, at(pb, pg, 1, 2 if pg == 0 else 1))
                nc.tensor.transpose(k.ps[0:slots, SIDE, 0:P], row_max[:, g % 2, :], k.ident[:, :]).then_inc(turned, 1)

            def spread(b, g, last_turned):
                pe.wait_ge(acc_copied, at(b, g, 1, 2))
                pe.wait_ge(negated, last_turned)
                pe.wait_ge(normed, at(b, g, 1, 2))
                if small:
                    mm = nc.tensor.matmul(k.ps[:, SIDE, 0:nq], k.spread[:, :], sums[:, :], start=True, stop=True)
                else:
                    pe.wait_ge(added, at(b, g, NS, NS + 4))
                    for j in range(heads):
                        mm = nc.tensor.matmul(k.ps[strip * j:strip * (j + 1), SIDE, 0:nq], k.ones[:, 0:strip], weight_sums[:, g % 2, j, :],
                                              start=True, stop=True, tile_position=(0, strip * j))
                mm.then_inc(sums_ready, 1)

            def weigh(b, g, s):
                i, pair = steps[s]
                pe.wait_ge(exp_done, at(b, g, NS, s + 3))
                if s == 0:
                    pe.wait_ge(v_loaded[g % V_RING], v_done(b, g))
                    pe.wait_ge(acc_copied, at(b, g, 1, 1))
                qs = queries_of(i)
                for jj in range(2):
                    j = 2 * pair + jj
                    mm = nc.tensor.matmul(k.ps[strip * j:strip * (j + 1), ACC, qs], v_tile[g % V_RING][:, i, strip * j:strip * (j + 1)],
                                          weights[:, (g * NS + s) % 4, jj, qs], start=i == 0, stop=i == nkt - 1,
                                          tile_position=(0, strip * j), skip_group_check=causal)
                mm.then_inc(pv_done, 1)

            pe.wait_ge(set_up, 1)
            pass_a(0, 0, chunks, 0)
            turn(0, 0)
            pass_a(0, 1, chunks, 0)

            def batch(b, ahead):
                for g in range(groups):
                    r = g % RING
                    pe.wait_ge(row_in, 48 * at(b, g, 1, 1))
                    n = 0
                    for s, (i, pair) in enumerate(steps):
                        if mask is None:
                            pe.wait_ge(exp_done, at(b, g, NS, s + 1))
                        else:
                            pe.wait_ge(masked, at(b, g, NS, s - 1 + 2))
                        qs, ks = queries_of(i), slice(i * kt, (i + 1) * kt)
                        for jj in range(2):
                            j = 2 * pair + jj
                            out = k.ps[0:kt, B0 + 2 * (s % 2) + jj, qs]
                            if small:
                                mm = nc.tensor.matmul(out, k_stack[r][0:rows_b, j, ks], q_stack[r][0:rows_b, j, qs], start=True, stop=not causal)
                            else:
                                for p, kp in enumerate((0, 0, 1)):
                                    nc.tensor.matmul(out, k_stack[r][:, kp, j, ks], q_stack[r][:, p, j, qs], start=p == 0, stop=False)
                                mm = nc.tensor.matmul(out, k.ones_bf[0:3, :], top_rows[r][:, j, qs], start=False, stop=True)
                            if causal:
                                mm = nc.tensor.matmul(out[:, 0:P], k.ident_bf[:, :], k.above_k[:, :], start=False, stop=True)
                        mm.then_inc(s_ready, 1)
                        if ahead or g < groups - 2:
                            pass_a(*later(b, g, 2), per_step[s], n)
                            n += len(per_step[s])
                        if s:
                            weigh(b, g, s - 1)
                        elif g:
                            weigh(b, g - 1, NS - 1)
                        if s == turn_step and (ahead or g < groups - 1):
                            turn(*later(b, g, 1))
                        if s == sums_step and g:
                            spread(b, g - 1, at(b, g, 1, 2 if ahead or g < groups - 1 else 1))
                weigh(b, groups - 1, NS - 1)
                spread(b, groups - 1, at(b, groups - 1, 1, 2 if ahead else 1))

            for_batches(pe, batch)

        @block.scalar
        def _(act):
            act.sem_inc(exp_done, 2)

            def batch(b, ahead):
                for g in range(groups):
                    for s, (i, pair) in enumerate(steps):
                        qs = queries_of(i)
                        act.wait_ge(pv_done, at(b, g, NS, s + 1))
                        if not small:
                            act.wait_ge(added, at(b, g, NS, s + 1))
                        if mask is None:
                            act.wait_ge(s_ready, at(b, g, NS, s + 1))
                            src = k.ps[0:kt, B0 + 2 * (s % 2):B0 + 2 * (s % 2) + 2, qs]
                        else:
                            act.wait_ge(masked, at(b, g, NS, s + 1 + 2))
                            src = masked_scores[:, s % 2, :, :]
                        nc.scalar.activation(weights[0:kt, (g * NS + s) % 4, :, qs], src, ACT.Exp, scale=scale).then_inc(exp_done, 1)

            for_batches(act, batch)

        @block.vector
        def _(dve):
            if small:
                for r in range(RING):
                    nc.vector.memset(q_stack[r][STACK:, :, :], 1.0)
                    last = nc.vector.memset(k_stack[r][STACK:, :, :], 1.0)
                if kt < P:
                    for tile in (weights, row_max, *v_tile):
                        last = nc.vector.memset(tile[kt:], 0.0)
                last.then_inc(set_up, 1)
            else:
                dve.sem_inc(set_up, 1)
            dve.sem_inc(pv_done, 4)
            dve.sem_inc(acc_copied, 1)
            dve.sem_inc(normed, 2)
            dve.sem_inc(sums_ready, 1)
            dve.sem_inc(masked, 2)

            def maxima(b, g, some, n0):
                if n0 == 0 and not first(b, g, 2):
                    dve.wait_ge(turned, at(b, g, 1, -1))
                for n, (qi, j, c) in enumerate(some, n0):
                    dve.wait_ge(a_ready, at(b, g, NCH, n + 1))
                    keys, slot = keys_of(qi, c), j * nqt + qi
                    out = part_max[:, g % 2, slot, c:c + 1] if nwide > 1 else row_max[0:qt, g % 2, slot:slot + 1]
                    scores = k.ps[0:qt, A0 + (g * NCH + n) % 2, 0:keys.stop - keys.start]
                    if mask is None:
                        nc.vector.reduce_max(out, scores, AX).then_inc(a_taken, 1)
                    else:
                        if n % (NCH // nqt) == 0:
                            dve.wait_ge(mask_q_in[qi], 16 * (b + 1))
                        if not (first(b, g) and n < 2):
                            dve.wait_ge(a_taken, at(b, g, NCH, n - 1))
                        nc.vector.tensor_tensor(with_mask[:, n % 2, :], scores, mask_q[:, qi, keys], ALU.add).then_inc(a_masked, 1)
                        dve.wait_ge(a_masked, at(b, g, NCH, n + 1))
                        nc.vector.reduce_max(out, with_mask[:, n % 2, :], AX).then_inc(a_taken, 1)
                if n0 + len(some) == NCH:
                    dve.wait_ge(a_taken, at(b, g, NCH, NCH))
                    if nwide > 1:
                        nc.vector.reduce_max(row_max[0:qt, g % 2, :], part_max[:, g % 2, :, :], AX).then_inc(max_ready, 1)
                    else:
                        dve.sem_inc(max_ready, 1)

            def negate(b, g):
                dve.wait_ge(turned, at(b, g, 1, 1))
                if not first(b, g):
                    dve.wait_ge(row_in, 48 * at(b, g, 1, 0))
                nc.vector.tensor_scalar(max_parts[:, 0, :], k.ps[0:slots, SIDE, 0:qt], -1.0, None, ALU.mult)
                nc.vector.tensor_scalar(negative[:, g % 2, :], k.ps[0:slots, SIDE, 0:qt], -1.0, None, ALU.mult).then_inc(negated, 1)

            def add_mask(b, g, s):
                i, pair = steps[s]
                dve.wait_ge(s_ready, at(b, g, NS, s + 1))
                dve.wait_ge(exp_done, at(b, g, NS, s - 1 + 2))
                if g == 0 and pair == 0:
                    dve.wait_ge(mask_k_in[i], 16 * (b + 1))
                nc.vector.tensor_tensor(masked_scores[:, s % 2, :, :], k.ps[:, B0 + 2 * (s % 2):B0 + 2 * (s % 2) + 2, :],
                                        mask_k[:, i, :].unsqueeze(1).broadcast_to((P, 2, nq)), ALU.add).then_inc(masked, 1)

            def copy_sums(b, g):
                dve.wait_ge(pv_done, at(b, g, NS, NS + 4))
                dve.wait_ge(sums_ready, at(b, g, 1, 1))
                dve.wait_ge(normed, at(b, g, 1, 2))
                nc.vector.tensor_copy(sums[:, :], k.ps[:, ACC, 0:nq]).then_inc(acc_copied, 1)

            def normalise(b, g):
                dve.wait_ge(sums_ready, at(b, g, 1, 2))
                nc.vector.reciprocal(inverse[:, :], k.ps[:, SIDE, 0:nq]).then_inc(inverted, 1)
                dve.wait_ge(inverted, at(b, g, 1, 1))
                nc.vector.tensor_tensor(att(g)[:, bass.ds(b * nq, nq)], sums[:, :], inverse[:, :], ALU.mult).then_inc(normed, 1)

            dve.wait_ge(set_up, 1)
            maxima(0, 0, chunks, 0)
            negate(0, 0)
            maxima(0, 1, chunks, 0)

            def batch(b, ahead):
                for g in range(groups):
                    n = 0
                    for s in range(NS):
                        if mask is not None:
                            add_mask(b, g, s)
                        if ahead or g < groups - 2:
                            maxima(*later(b, g, 2), per_step[s], n)
                            n += len(per_step[s])
                        if s == 0 and g:
                            copy_sums(b, g - 1)
                        if s == turn_step and (ahead or g < groups - 1):
                            negate(*later(b, g, 1))
                        if s == sums_step and g:
                            normalise(b, g - 1)
                copy_sums(b, groups - 1)
                normalise(b, groups - 1)

            for_batches(dve, batch)

        @block.gpsimd
        def _(pool):
            pool.sem_inc(added, 4)

            def split_max(b, g):
                own = negative[:, g % 2, :]
                pool.wait_ge(negated, at(b, g, 1, 1))
                nc.gpsimd.tensor_tensor(max_parts[:, 1, :], own, max_parts[:, 0, :], ALU.subtract).then_inc(max_split, 1)
                nc.gpsimd.tensor_tensor(own, own, max_parts[:, 0, :], ALU.subtract).then_inc(max_split, 1)
                pool.wait_ge(max_split, at(b, g, 2, 2))
                nc.gpsimd.tensor_tensor(max_parts[:, 2, :], own, max_parts[:, 1, :], ALU.subtract).then_inc(row_made, 1)

            def add_weights(b, g, s):
                pool.wait_ge(exp_done, at(b, g, NS, s + 3))
                total, own, before = weight_sums[:, g % 2, :, :], weights[:, (g * NS + s) % 4, :, :], weights[:, (g * NS + s - 1) % 4, :, :]
                if s == 1:
                    pool.wait_ge(normed, at(b, g, 1, 1))
                    nc.gpsimd.tensor_tensor(total, before, own, ALU.add).then_inc(added, 2)
                else:
                    pool.wait_ge(added, at(b, g, NS, s + 4))
                    nc.gpsimd.tensor_tensor(total, total, own, ALU.add).then_inc(added, 1)

            split_max(0, 0)

            def batch(b, ahead):
                for g in range(groups):
                    for s in range(NS):
                        if s and not small:
                            add_weights(b, g, s)
                        if s == turn_step and (ahead or g < groups - 1):
                            split_max(*later(b, g, 1))

            for_batches(pool, batch)


def residual_norm_stage(k, products, bias=None, weights=(), x_scale=1.0, y_scale=1.0, value_bias=None, out=None, rows=None, relu=False):
    nc = k.nc
    n = k.stages
    with (
        nc.sbuf_tensor(f"rn_z_{n}", [P, NT, C], F32) as z,
        nc.sbuf_tensor(f"rn_stats_{n}", [P, NT, 6], F32) as stats,
        nc.sbuf_tensor(f"rn_mean_var_{n}", [P, NT, 2], F32) as mean_var,
        nc.sbuf_tensor(f"rn_rstd_{n}", [P, 2, NT], F32) as rstd,
        k.stage("weights", "biased", "prepared", "y_ready", "z_ready", "stats", "aggregated", "deviation", "inverse",
                "normed", "turned", "copied", "stored") as (
            weights_in, biased, prepared, y_ready, z_ready, stats_ready, aggregated, deviation, inverted, normed,
            turned, copied, stored),
        nc.Block() as block,
    ):
        @block.sync
        def _(sync):
            k.clear_last_set(sync)
            for tile, source in weights:
                sync.dma_start(tile, source).then_inc(weights_in, 16)
            if out is not None:
                for t in range(0, NT, 4):
                    sync.wait_ge(normed, t + 4)
                    sync.dma_start(out[t * P:(t + 4) * P, :].rearrange("(t p) c -> p t c", p=P), k.X[:, t:t + 4, :]).then_inc(stored, 16)
                sync.wait_ge(stored, 16 * (NT // 4))

        @block.gpsimd
        def _(pool):
            if bias is not None:
                pool.wait_ge(weights_in, 16 * len(weights))
            for t in range(NT if not relu else 0):
                if x_scale != 1.0:
                    nc.gpsimd.tensor_scalar(z[:, t, :], k.X[:, t, :], x_scale, None, ALU.mult).then_inc(biased, 1)
                    pool.wait_ge(biased, t + 1)
                    ins = nc.gpsimd.tensor_tensor(z[:, t, :], z[:, t, :], bias, ALU.add)
                elif bias is not None:
                    ins = nc.gpsimd.tensor_tensor(z[:, t, :], k.X[:, t, :], bias, ALU.add)
                elif rows is not None:
                    ins = nc.gpsimd.tensor_tensor(z[:, t, :], k.X[:, t, :], rows(t), ALU.add)
                else:
                    ins = nc.gpsimd.tensor_copy(z[:, t, :], k.X[:, t, :])
                ins.then_inc(prepared, 1)

        @block.tensor
        def _(pe):
            pe.wait_ge(weights_in, 16 * len(weights))
            if value_bias is not None:
                pe.wait_ge(biased, NG)
            for t in range(NT if rows is None else 0):
                if t >= 4:
                    pe.wait_ge(z_ready, t - 3)
                for i, (lhsT, rhs) in enumerate(products):
                    mm = nc.tensor.matmul(k.ps[:, t % 4, 0:C], lhsT(t), rhs, start=i == 0, stop=i == len(products) - 1)
                mm.then_inc(y_ready, 1)
            if out is None:
                for t in range(NT):
                    pe.wait_ge(normed, t + 1)
                    if t >= 4:
                        pe.wait_ge(copied, t - 3)
                    for c in range(CH):
                        tr = nc.tensor.transpose(k.ps[:, 4 + t % 4, c * P:(c + 1) * P], k.X[:, t, c * P:(c + 1) * P], k.ident[:, :])
                    tr.then_inc(turned, 1)

        @block.vector
        def _(dve):
            if value_bias is not None:
                dve.wait_ge(weights_in, 16 * len(weights))
                for g in range(NG):
                    nc.vector.tensor_scalar(value_bias[0][:, g, :], value_bias[0][:, g, :], value_bias[1][:, g:g + 1], None,
                                            ALU.add).then_inc(biased, 1)
            for t in range(NT + 2):
                if t < NT and relu:
                    if t == 0:
                        dve.wait_ge(weights_in, 16 * len(weights))
                    dve.wait_ge(y_ready, t + 1)
                    nc.vector.tensor_tensor(z[:, t, :], k.ps[:, t % 4, 0:C], bias, ALU.add).then_inc(prepared, 1)
                    dve.wait_ge(prepared, t + 1)
                    nc.vector.scalar_tensor_tensor(z[:, t, :], z[:, t, :], 0.0, k.X[:, t, :], ALU.max, ALU.add).then_inc(z_ready, 1)
                elif t < NT and rows is None:
                    dve.wait_ge(prepared, t + 1)
                    dve.wait_ge(y_ready, t + 1)
                    nc.vector.scalar_tensor_tensor(z[:, t, :], k.ps[:, t % 4, 0:C], y_scale, z[:, t, :], ALU.mult, ALU.add).then_inc(z_ready, 1)
                if 1 <= t <= NT:
                    if rows is None:
                        dve.wait_ge(z_ready, t)
                    else:
                        dve.wait_ge(prepared, t)
                    nc.vector.bn_stats(stats[:, t - 1, :], z[:, t - 1, :]).then_inc(stats_ready, 1)
                if t >= 2:
                    dve.wait_ge(stats_ready, t - 1)
                    nc.vector.bn_aggr(mean_var[:, t - 2, :], stats[:, t - 2, :]).then_inc(aggregated, 1)
            dve.wait_ge(deviation, 1)
            nc.vector.reciprocal(rstd[:, 1, :], rstd[:, 0, :]).then_inc(inverted, 1)
            dve.wait_ge(inverted, 1)
            for t in range(NT):
                nc.vector.tensor_scalar(k.X[:, t, :], z[:, t, :], mean_var[:, t, 0:1], rstd[:, 1, t:t + 1], ALU.subtract,
                                        ALU.mult).then_inc(normed, 1)

        @block.scalar
        def _(act):
            act.wait_ge(aggregated, NT)
            nc.scalar.activation(rstd[:, 0, :], mean_var[:, :, 1], ACT.Sqrt, bias=k.eps[0]).then_inc(deviation, 1)
            if out is None:
                for t in range(NT):
                    act.wait_ge(turned, t + 1)
                    nc.scalar.activation(k.xT[:, :, t * P:(t + 1) * P], k.ps[:, 4 + t % 4, 0:C].rearrange("p (c n) -> p c n", c=CH),
                                         ACT.Copy).then_inc(copied, 1)


def merge_levels_stage(k, lvl, att, up, out_w, up_w, out_b, up_b, up_next, weights, value_bias):
    nc = k.nc
    s_l = S >> lvl
    n = B * s_l
    wide = min(n, BANK)
    parts = [(m, w) for m in range(CH) for w in range(n // wide)]
    with (
        nc.sbuf_tensor(f"current_{lvl}", [P, CH, B, s_l], F32) as current,
        nc.sbuf_tensor(f"quarter_{lvl}", [P, CH * B, s_l], F32) as quarter,
        nc.sbuf_tensor(f"level_bias_{lvl}", [P, CH], F32) as level_bias,
        k.stage("weights", "values_biased", "bias_sum", "ready", "summed", "quartered", "upsampled") as (
            weights_in, values_biased, bias_sum, ready, summed, quartered, upsampled),
        nc.Block(no_gpsimd_drain=True) as block,
    ):
        flat = current[:].rearrange("p c b s -> p c (b s)")
        rows = current[:].rearrange("p c b s -> p (c b) s")
        fine = up_next[:].rearrange("p c b (s two) -> p (c b) s two", two=2)

        @block.sync
        def _(sync):
            k.clear_last_set(sync)
            for tile, source in weights:
                sync.dma_start(tile, source).then_inc(weights_in, 16)

        @block.tensor
        def _(pe):
            pe.wait_ge(weights_in, 16 * len(weights))
            pe.wait_ge(values_biased, NG)
            for i, (m, w) in enumerate(parts):
                cols, chan = slice(w * wide, (w + 1) * wide), slice(m * P, (m + 1) * P)
                terms = [(out_w[:, g, chan], att[:, g, cols]) for g in range(NG)]
                if up is not None:
                    terms += [(up_w[:, c, chan], up[:].rearrange("p c b s -> p c (b s)")[:, c, cols]) for c in range(CH)]
                for a, (lhsT, rhs) in enumerate(terms):
                    mm = nc.tensor.matmul(k.ps[:, i, 0:wide], lhsT, rhs, start=a == 0, stop=a == len(terms) - 1)
                mm.then_inc(ready, 1)

        @block.vector
        def _(dve):
            dve.wait_ge(weights_in, 16 * len(weights))
            for g in range(NG):
                nc.vector.tensor_scalar(att[:, g, :], att[:, g, :], value_bias[:, g:g + 1], None, ALU.add).then_inc(values_biased, 1)
            if up is None:
                nc.vector.tensor_copy(level_bias[:], out_b).then_inc(bias_sum, 1)
            else:
                nc.vector.tensor_tensor(level_bias[:], out_b, up_b, ALU.add).then_inc(bias_sum, 1)
            dve.wait_ge(bias_sum, 1)
            for i, (m, w) in enumerate(parts):
                dve.wait_ge(ready, i + 1)
                nc.vector.tensor_scalar(flat[:, m, w * wide:(w + 1) * wide], k.ps[:, i, 0:wide], level_bias[:, m:m + 1], None,
                                        ALU.add).then_inc(summed, 1)
            dve.wait_ge(summed, len(parts))
            nc.vector.tensor_scalar(quarter[:], rows, 0.25, None, ALU.mult).then_inc(quartered, 1)
            nc.vector.tensor_copy(fine[:, :, 0:1, 0], rows[:, :, 0:1])
            nc.vector.tensor_copy(fine[:, :, s_l - 1:s_l, 1], rows[:, :, s_l - 1:s_l])
            dve.wait_ge(quartered, 1)
            nc.vector.scalar_tensor_tensor(fine[:, :, 1:s_l, 0], rows[:, :, 1:s_l], 0.75, quarter[:, :, 0:s_l - 1], ALU.mult, ALU.add)
            nc.vector.scalar_tensor_tensor(fine[:, :, 0:s_l - 1, 1], rows[:, :, 0:s_l - 1], 0.75, quarter[:, :, 1:s_l], ALU.mult,
                                           ALU.add).then_inc(upsampled, 1)


def pyramid_attention(k):
    nc, inp = k.nc, k.inp
    with ExitStack() as held:
        def sb(what, shape, dt=F32):
            return held.enter_context(nc.sbuf_tensor(f"pyr_{what}", shape, dt))

        att = [sb(f"att{lvl}", [P, NG, T >> lvl]) for lvl in range(4)]
        bias = sb("bias", [P, 4, 3 * CH])
        vbias = sb("vbias", [P, 4, NG])
        for lvl in range(4):
            s_l, n = S >> lvl, T >> lvl
            with nc.sbuf_tensor(f"pyr_wqkv{lvl}", [P, CH, 3 * C], F32) as w:
                if lvl == 0:
                    loads = [(w[:], inp["L0_in_w"][lvl]), (bias[:], inp["L0_in_b"]), (vbias[:], inp["L0_v_b"])]
                else:
                    loads = [(w[:], inp["L0_in_w"][lvl])]
                per = min(BANK // s_l, B)
                xs = k.xT[:].rearrange("p c (b s) -> p c b s", b=B)

                def wide(c, t):
                    return xs[:, c, t * per:(t + 1) * per, ::1 << lvl]

                kt = min(P, s_l)

                def rows(c, t):
                    b, i = divmod(t, s_l // kt)
                    return xs[:, c, b, (i * kt) << lvl:((i + 1) * kt) << lvl:1 << lvl]

                q_parts, k_parts, values = k.q_parts[:, :, 0:n], k.k_parts[:, :, 0:n], k.values_of(n // kt, kt)
                project_stage(k, split_units(wide, per * s_l, w[:, :, 0:C], bias[:, lvl, 0:CH], q_parts)
                              + split_units(wide, per * s_l, w[:, :, C:2 * C], bias[:, lvl, CH:2 * CH], k_parts)
                              + value_units(rows, kt, w[:, :, 2 * C:], values), loads)
            attention_stage(k, f"pyr_core{lvl}", q_parts, k_parts, values, s_l, s_l, HD ** -0.5,
                            lambda g, lvl=lvl: att[lvl][:, g, :])
        up = [None] + [sb(f"up{lvl}", [P, CH, B, S >> (lvl - 1)]) for lvl in (3, 2, 1)]
        out_b, up_b = sb("out_b", [P, 4, CH]), sb("up_b", [P, 3, CH])
        for i, lvl in enumerate((3, 2, 1)):
            with nc.sbuf_tensor(f"pyr_out_w{lvl}", [P, NG, C], F32) as ow, nc.sbuf_tensor(f"pyr_up_w{lvl}", [P, CH, C], F32) as uw:
                loads = [(ow[:], inp["L0_out_w"][lvl])]
                if lvl < 3:
                    loads.append((uw[:], inp["L0_up_w"][lvl]))
                else:
                    loads += [(out_b[:], inp["L0_out_b"]), (up_b[:], inp["L0_up_b"])]
                merge_levels_stage(k, lvl, att[lvl], up[i], ow, uw, out_b[:, lvl, :], up_b[:, min(lvl, 2), :], up[i + 1],
                                   loads, vbias[:, lvl, :])
        with nc.sbuf_tensor("pyr_out_w0", [P, NG, C], F32) as ow, nc.sbuf_tensor("pyr_up_w0", [P, CH, C], F32) as uw, \
                nc.sbuf_tensor("pyr_rows", [P, 2, C], F32) as rows:
            add_rows_stage(k, rows, inp["L0_out_b0_up_b0"])
            fine = up[3][:].rearrange("p c b s -> p c (b s)")
            products = [(lambda t, g=g: att[0][:, g, t * P:(t + 1) * P], ow[:, g, :]) for g in range(NG)]
            products += [(lambda t, c=c: fine[:, c, t * P:(t + 1) * P], uw[:, c, :]) for c in range(CH)]
            residual_norm_stage(k, products, rows[:, 0, :], [(ow[:], inp["L0_out_w"][0]), (uw[:], inp["L0_up_w"][0])],
                                value_bias=(att[0], vbias[:, 0, :]))


def add_rows_stage(k, rows, source):
    nc = k.nc
    with k.stage("loaded", "added") as (loaded, added), nc.Block(no_gpsimd_drain=True) as block:
        @block.sync
        def _(sync):
            k.clear_last_set(sync)
            sync.dma_start(rows[:], source.partition_broadcast(P)).then_inc(loaded, 16)

        @block.vector
        def _(dve):
            dve.wait_ge(loaded, 16)
            nc.vector.tensor_tensor(rows[:, 0, :], rows[:, 0, :], rows[:, 1, :], ALU.add).then_inc(added, 1)


def self_or_cross_attention(k, name, source, weights, nk, slopes=None):
    nc, inp = k.nc, k.inp
    w_name, b_name, out_name, out_b, v_b = weights
    with nc.sbuf_tensor(f"{name}_att", [P, NG, T], F32) as att, nc.sbuf_tensor(f"{name}_vb", [P, NG], F32) as vb:
        q_parts, k_parts, values = k.q_parts[:, :, 0:T], k.k_parts[:, :, 0:B * nk], k.values_of(B * nk // P, P)
        with nc.sbuf_tensor(f"{name}_w", [P, CH, 3 * C], F32) as w, nc.sbuf_tensor(f"{name}_b", [P, 2 * CH], F32) as bias, \
                nc.sbuf_tensor(f"{name}_src", [P, CH, TC if source is None else 1], F32) as ctxT:
            loads = [(w[:], inp[w_name])]
            if source is None:
                source = ctxT
                loads.append((ctxT[:], inp["ctxT"]))
            if b_name:
                loads += [(bias[:], inp[b_name]), (vb[:], inp[v_b])]
            project_stage(
                k, split_units(lambda c, t: k.xT[:, c, t * BANK:(t + 1) * BANK], BANK, w[:, :, 0:C],
                               bias[:, 0:CH] if b_name else None, q_parts)
                + split_units(lambda c, t: source[:, c, t * BANK:(t + 1) * BANK], BANK, w[:, :, C:2 * C],
                              bias[:, CH:] if b_name else None, k_parts)
                + value_units(lambda c, t: source[:, c, t * P:(t + 1) * P], P, w[:, :, 2 * C:], values), loads)
        attention_stage(k, f"{name}_core", q_parts, k_parts, values, S, nk, HD ** -0.5, lambda g: att[:, g, :], slopes=slopes)
        with nc.sbuf_tensor(f"{name}_ow", [P, NG, C], F32) as ow, nc.sbuf_tensor(f"{name}_ob", [P, C], F32) as ob:
            residual_norm_stage(k, [(lambda t, g=g: att[:, g, t * P:(t + 1) * P], ow[:, g, :]) for g in range(NG)], ob[:],
                                [(ow[:], inp[out_name]), (ob[:], inp[out_b].partition_broadcast(P))],
                                value_bias=(att, vb) if b_name else None)


def norm_rows_stage(k, tiles, dest, gamma, beta, eps, products=None, source=None, add=None, relu_eps=None, row_scale=None,
                    destT=None, weights=()):
    nc = k.nc
    n = k.stages
    with (
        nc.sbuf_tensor(f"nr_z_{n}", [P, tiles if source is None else 1, C], F32) as z,
        nc.sbuf_tensor(f"nr_stats_{n}", [P, tiles, 6], F32) as stats,
        nc.sbuf_tensor(f"nr_mean_var_{n}", [P, tiles, 2], F32) as mean_var,
        nc.sbuf_tensor(f"nr_rstd_{n}", [P, 2, tiles], F32) as rstd,
        k.stage("weights", "y_ready", "z_ready", "stats", "aggregated", "deviation", "inverse", "centred", "normed",
                "clipped", "scaled", "turned", "copied") as (
            weights_in, y_ready, z_ready, stats_ready, aggregated, deviation, inverted, centred, normed, clipped, scaled,
            turned, copied),
        nc.Block() as block,
    ):
        def rows(t):
            return z[:, t, :] if source is None else source(t)

        done = scaled if row_scale is not None else clipped if relu_eps is not None else normed

        @block.sync
        def _(sync):
            k.clear_last_set(sync)
            for tile, src in weights:
                sync.dma_start(tile, src).then_inc(weights_in, 16)

        @block.tensor
        def _(pe):
            if products is not None:
                pe.wait_ge(weights_in, 16 * len(weights))
                for t in range(tiles):
                    if t >= 4:
                        pe.wait_ge(z_ready, t - 3)
                    for i, (lhsT, rhs) in enumerate(products):
                        mm = nc.tensor.matmul(k.ps[:, t % 4, 0:C], lhsT(t), rhs, start=i == 0, stop=i == len(products) - 1)
                    mm.then_inc(y_ready, 1)
            if destT is not None:
                for t in range(tiles):
                    pe.wait_ge(done, t + 1)
                    if t >= 4:
                        pe.wait_ge(copied, t - 3)
                    for c in range(CH):
                        tr = nc.tensor.transpose(k.ps[:, 4 + t % 4, c * P:(c + 1) * P], dest(t)[:, c * P:(c + 1) * P], k.ident[:, :])
                    tr.then_inc(turned, 1)

        @block.vector
        def _(dve):
            dve.wait_ge(weights_in, 16 * len(weights))
            for t in range(tiles + 2):
                if t < tiles and products is not None:
                    dve.wait_ge(y_ready, t + 1)
                    if add is None:
                        nc.vector.tensor_copy(z[:, t, :], k.ps[:, t % 4, 0:C]).then_inc(z_ready, 1)
                    else:
                        nc.vector.tensor_tensor(z[:, t, :], k.ps[:, t % 4, 0:C], add(t), ALU.add).then_inc(z_ready, 1)
                if 1 <= t <= tiles:
                    if products is not None:
                        dve.wait_ge(z_ready, t)
                    nc.vector.bn_stats(stats[:, t - 1, :], rows(t - 1)).then_inc(stats_ready, 1)
                if t >= 2:
                    dve.wait_ge(stats_ready, t - 1)
                    nc.vector.bn_aggr(mean_var[:, t - 2, :], stats[:, t - 2, :]).then_inc(aggregated, 1)
            dve.wait_ge(deviation, 1)
            nc.vector.reciprocal(rstd[:, 1, :], rstd[:, 0, :]).then_inc(inverted, 1)
            dve.wait_ge(inverted, 1)
            for t in range(tiles + 1):
                if t < tiles:
                    nc.vector.scalar_tensor_tensor(dest(t), rows(t), mean_var[:, t, 0:1], gamma, ALU.subtract, ALU.mult).then_inc(centred, 1)
                if t:
                    dve.wait_ge(centred, t)
                    nc.vector.scalar_tensor_tensor(dest(t - 1), dest(t - 1), rstd[:, 1, t - 1:t], beta, ALU.mult, ALU.add).then_inc(normed, 1)

        @block.scalar
        def _(act):
            act.wait_ge(aggregated, tiles)
            nc.scalar.activation(rstd[:, 0, :], mean_var[:, :, 1], ACT.Sqrt, bias=eps).then_inc(deviation, 1)
            if destT is not None:
                for t in range(tiles):
                    act.wait_ge(turned, t + 1)
                    nc.scalar.activation(destT(t), k.ps[:, 4 + t % 4, 0:C].rearrange("p (c n) -> p c n", c=CH), ACT.Copy).then_inc(copied, 1)

        @block.gpsimd
        def _(pool):
            if row_scale is not None:
                pool.wait_ge(weights_in, 16 * len(weights))
            for t in range(tiles):
                if relu_eps is not None:
                    pool.wait_ge(normed, t + 1)
                    nc.gpsimd.tensor_scalar(dest(t), dest(t), 0.0, relu_eps, ALU.max, ALU.add).then_inc(clipped, 1)
                if row_scale is not None:
                    if relu_eps is not None:
                        pool.wait_ge(clipped, t + 1)
                    else:
                        pool.wait_ge(normed, t + 1)
                    nc.gpsimd.tensor_scalar(dest(t), dest(t), row_scale(t), None, ALU.mult).then_inc(scaled, 1)


def linear_attention_stage(k, keys, values, queryT, att, key_tiles, den_eps=None, attT=None, regroup=None):
    nc = k.nc
    n = k.stages
    with (
        nc.sbuf_tensor(f"la_state_{n}", [P, B, CH, P], F32) as state,
        nc.sbuf_tensor(f"la_sums_{n}", [P, B, CH, 2], F32) as sums,
        nc.sbuf_tensor(f"la_sum_cols_{n}", [P, B, CH, H], F32) as sum_cols,
        nc.sbuf_tensor(f"la_den_{n}", [P, NT, 2, H], F32) as den,
        k.stage("state_ready", "summed", "state_taken", "ready", "shifted", "inverse", "taken", "turned", "copied", "stored",
                "regrouped") as (state_ready, summed, state_taken, ready, shifted, inverted, taken, turned, copied, stored, regrouped),
        nc.Block(no_gpsimd_drain=True) as block,
    ):
        pairs = [(b, m) for b in range(B) for m in range(CH)]
        per_pair = 1 if den_eps is None else 2

        @block.sync
        def _(sync):
            k.clear_last_set(sync)
            if regroup is not None:
                per = NT // B
                for t in range(NT):
                    sync.wait_ge(taken, t + 1)
                    sync.dma_start(regroup[t // per, :, t % per * P:(t % per + 1) * P, :].rearrange("h n e -> n h e"),
                                   att(t).rearrange("p (h e) -> p h e", h=H)).then_inc(stored, 16)
                sync.wait_ge(stored, 16 * NT)
                flat = regroup.rearrange("b h n e -> (b h n e)").rearrange("(t p c) -> t p c", p=P, c=C)
                for t in range(NT):
                    sync.dma_start(att(t), flat[t]).then_inc(regrouped, 16)

        @block.tensor
        def _(pe):
            for n, (b, m) in enumerate(pairs):
                if n >= 4:
                    pe.wait_ge(state_taken, per_pair * (n - 3))
                for i in range(key_tiles):
                    t = b * key_tiles + i
                    mm = nc.tensor.matmul(k.ps[:, n % 4, 0:C + 1], keys(t)[:, m * P:(m + 1) * P], values(t), start=i == 0,
                                          stop=i == key_tiles - 1)
                mm.then_inc(state_ready, 1)
            pe.wait_ge(state_taken, per_pair * len(pairs))
            for t in range(NT):
                b = t // (NT // B)
                if t >= 4:
                    pe.wait_ge(taken, t - 3)
                for m in range(CH):
                    q = queryT[:, m, t * P:(t + 1) * P]
                    mm = nc.tensor.matmul(k.ps[:, 4 + t % 4, m * P:(m + 1) * P], q, state[:, b, m, :], start=m == 0, stop=den_eps is None,
                                          skip_group_check=True)
                    if den_eps is not None:
                        mm = nc.tensor.matmul(k.ps[:, 4 + t % 4, C:C + H], q, sum_cols[:, b, m, :], start=False, stop=m == CH - 1,
                                              skip_group_check=True)
                mm.then_inc(ready, 1)
            if attT is not None:
                if regroup is not None:
                    pe.wait_ge(regrouped, 16 * NT)
                for t in range(NT):
                    pe.wait_ge(taken, t + 1)
                    if t >= 4:
                        pe.wait_ge(copied, t - 3)
                    for c in range(CH):
                        tr = nc.tensor.transpose(k.ps[:, t % 4, c * P:(c + 1) * P], att(t)[:, c * P:(c + 1) * P], k.ident[:, :])
                    tr.then_inc(turned, 1)

        @block.vector
        def _(dve):
            for n, (b, m) in enumerate(pairs):
                dve.wait_ge(state_ready, n + 1)
                nc.vector.tensor_copy(sums[:, b, m, 0:1], k.ps[:, n % 4, C:C + 1]).then_inc(summed, 1)
                dve.wait_ge(summed, 2 * n + 1)
                if den_eps is None:
                    nc.vector.reciprocal(sums[:, b, m, 1:2], sums[:, b, m, 0:1]).then_inc(summed, 1)
                    dve.wait_ge(summed, 2 * n + 2)
                    nc.vector.scalar_tensor_tensor(state[:, b, m, :], k.ps[:, n % 4, m * P:(m + 1) * P], sums[:, b, m, 1:2],
                                                   k.head_blocks[:, :], ALU.mult, ALU.mult).then_inc(state_taken, 1)
                else:
                    nc.vector.tensor_scalar(sum_cols[:, b, m, :], k.head_cols[:, m, :], sums[:, b, m, 0:1], None, ALU.mult).then_inc(summed, 1)
                    nc.vector.tensor_tensor(state[:, b, m, :], k.ps[:, n % 4, m * P:(m + 1) * P], k.head_blocks[:, :], ALU.mult).then_inc(state_taken, 2)
            if den_eps is not None:
                dve.wait_ge(summed, 2 * len(pairs))
            for t in range(NT):
                dve.wait_ge(ready, t + 1)
                if den_eps is None:
                    nc.vector.tensor_copy(att(t), k.ps[:, 4 + t % 4, 0:C]).then_inc(taken, 1)
                else:
                    nc.vector.tensor_scalar(den[:, t, 0, :], k.ps[:, 4 + t % 4, C:C + H], den_eps, None, ALU.add).then_inc(shifted, 1)
                    dve.wait_ge(shifted, t + 1)
                    nc.vector.reciprocal(den[:, t, 1, :], den[:, t, 0, :]).then_inc(inverted, 1)
                    dve.wait_ge(inverted, t + 1)
                    nc.vector.tensor_tensor(att(t).rearrange("p (h d) -> p h d", h=H), k.ps[:, 4 + t % 4, 0:C].rearrange("p (h d) -> p h d", h=H),
                                            den[:, t, 1, :].unsqueeze(2).broadcast_to((P, H, HD)), ALU.mult).then_inc(taken, 1)

        @block.scalar
        def _(act):
            if attT is not None:
                for t in range(NT):
                    act.wait_ge(turned, t + 1)
                    nc.scalar.activation(attT(t), k.ps[:, t % 4, 0:C].rearrange("p (c n) -> p c n", c=CH), ACT.Copy).then_inc(copied, 1)


def memset_stage(k, *tiles):
    nc = k.nc
    with k.stage("filled") as (filled,), nc.Block(no_gpsimd_drain=True) as block:
        @block.sync
        def _(sync):
            k.clear_last_set(sync)

        @block.vector
        def _(dve):
            for tile, value in tiles:
                nc.vector.memset(tile, value).then_inc(filled, 1)


def add_norm_stage(k, y):
    residual_norm_stage(k, None, rows=y)


def relu_kernel_attention(k):
    nc, inp = k.nc, k.inp
    with ExitStack() as held:
        def sb(what, shape):
            return held.enter_context(nc.sbuf_tensor(f"rk_{what}", shape, F32))

        gain, mask = sb("gain", [P, 3, C]), sb("mask", [P, NTC])
        w = sb("w", [P, 4, CH, C])
        qT, y = sb("qT", [P, CH, T]), sb("y", [P, NT, C])
        gamma, beta = gain[:, 0, :], gain[:, 1, :]
        with nc.sbuf_tensor("rk_keys", [P, NTC, C], F32) as keys, nc.sbuf_tensor("rk_values", [P, NTC, C + 1], F32) as values, \
                nc.sbuf_tensor("rk_ctxT", [P, CH, TC], F32) as ctxT:
            loads = [(ctxT[:], inp["ctxT"]), (w[:], inp["L0x_w"]), (gain[:], inp["L0x_rows"].partition_broadcast(P)), (mask[:], inp["mask_tokens"])]

            def ctx(c):
                return lambda t: ctxT[:, c, t * P:(t + 1) * P]

            memset_stage(k, (values[:, :, C:C + 1], 1.0))
            norm_rows_stage(k, NTC, lambda t: keys[:, t, :], gamma, beta, k.eps[1], [(ctx(c), w[:, 1, c, :]) for c in range(CH)],
                            relu_eps=1e-6, row_scale=lambda t: mask[:, t:t + 1], weights=loads)
            norm_rows_stage(k, NTC, lambda t: values[:, t, 0:C], gamma, beta, k.eps[1], [(ctx(c), w[:, 2, c, :]) for c in range(CH)],
                            row_scale=lambda t: mask[:, t:t + 1])
            norm_rows_stage(k, NT, lambda t: y[:, t, :], gamma, beta, k.eps[1],
                            [(lambda t, c=c: k.xT[:, c, t * P:(t + 1) * P], w[:, 0, c, :]) for c in range(CH)],
                            relu_eps=1e-6, destT=lambda t: qT[:, :, t * P:(t + 1) * P])
            linear_attention_stage(k, lambda t: keys[:, t, :], lambda t: values[:, t, :], qT, lambda t: y[:, t, :], NTC // B,
                                   den_eps=1e-6, attT=lambda t: qT[:, :, t * P:(t + 1) * P], regroup=k.regroup)
        norm_rows_stage(k, NT, lambda t: y[:, t, :], gamma, beta, k.eps[1],
                        [(lambda t, c=c: qT[:, c, t * P:(t + 1) * P], w[:, 3, c, :]) for c in range(CH)], add=lambda t: gain[:, 2, :])
        add_norm_stage(k, lambda t: y[:, t, :])


def softmax_features_stage(k, w, rows, k_bias, queries, qT, keys, values, loads):
    nc = k.nc
    n_k = CH * B
    with (
        nc.sbuf_tensor("sf_keysT", [P, CH, T], F32) as keysT,
        nc.sbuf_tensor("sf_top", [P, 2, n_k], F32) as top,
        nc.sbuf_tensor("sf_head", [P, 3, NT * H], F32) as head,
        k.stage("weights", "ready", "taken", "k_top", "k_exp", "q_top", "q_shifted", "q_exp", "q_sum", "q_inverse",
                "q_done", "turned", "copied") as (weights_in, ready, taken, k_top, k_exp, q_top, q_shifted, q_exp, q_sum, q_inverse,
                                                  q_done, turned, copied),
        nc.Block() as block,
    ):
        units = [("q", t) for t in range(NT)] + [("k", u) for u in range(n_k)] + [("v", t) for t in range(NT)]
        heads = queries[:].rearrange("p t (h d) -> p (t h) d", d=HD)
        turns = [("q", t) for t in range(NT)] + [("k", t) for t in range(NT)]

        def spread(i):
            return head[:, i, :].unsqueeze(2).broadcast_to((P, NT * H, HD))

        @block.sync
        def _(sync):
            k.clear_last_set(sync)
            for tile, src in loads:
                sync.dma_start(tile, src).then_inc(weights_in, 16)

        @block.tensor
        def _(pe):
            pe.wait_ge(weights_in, 16 * len(loads))
            for n, (kind, i) in enumerate(units):
                if n >= 4:
                    pe.wait_ge(taken, n - 3)
                for c in range(CH):
                    if kind == "k":
                        m, b = divmod(i, B)
                        out, lhsT, rhs = k.ps[:, n % 4, :], w[:, 1, c, m * P:(m + 1) * P], k.xT[:, c, b * S:(b + 1) * S]
                    else:
                        out, lhsT = k.ps[:, n % 4, 0:C], k.xT[:, c, i * P:(i + 1) * P]
                        rhs = w[:, 0 if kind == "q" else 2, c, :]
                    mm = nc.tensor.matmul(out, lhsT, rhs, start=c == 0, stop=c == CH - 1)
                mm.then_inc(ready, 1)
            pe.wait_ge(q_done, 1)
            for n, (kind, t) in enumerate(turns):
                if kind == "k" and t == 0:
                    pe.wait_ge(k_exp, n_k)
                if n >= 4:
                    pe.wait_ge(copied, n - 3)
                for c in range(CH):
                    src = queries[:, t, c * P:(c + 1) * P] if kind == "q" else keysT[:, c, t * P:(t + 1) * P]
                    tr = nc.tensor.transpose(k.ps[:, 4 + n % 4, c * P:(c + 1) * P], src, k.ident[:, :])
                tr.then_inc(turned, 1)

        @block.vector
        def _(dve):
            dve.wait_ge(weights_in, 16 * len(loads))
            for n, (kind, i) in enumerate(units):
                dve.wait_ge(ready, n + 1)
                if kind == "q":
                    ins = nc.vector.tensor_tensor(queries[:, i, :], k.ps[:, n % 4, 0:C], rows[:, 0, :], ALU.add)
                elif kind == "k":
                    m, b = divmod(i, B)
                    ins = nc.vector.tensor_scalar(keysT[:, m, b * S:(b + 1) * S], k.ps[:, n % 4, :], k_bias[:, m:m + 1], None, ALU.add)
                else:
                    ins = nc.vector.tensor_tensor(values[:, i, 0:C], k.ps[:, n % 4, 0:C], rows[:, 1, :], ALU.add)
                ins.then_inc(taken, 1)
                if n == NT:
                    dve.wait_ge(taken, NT)
                    nc.vector.reduce_max(head[:, 0, :], heads, AX).then_inc(q_top, 1)
                if n == NT + n_k:
                    dve.wait_ge(taken, NT + n_k)
                    nc.vector.reduce_max(top[:, 0, :], keysT[:].rearrange("p c (b s) -> p (c b) s", b=B), AX).then_inc(k_top, 1)
                    dve.wait_ge(k_top, 1)
                    nc.vector.tensor_scalar(top[:, 1, :], top[:, 0, :], -1.0, None, ALU.mult).then_inc(k_top, 1)
            dve.wait_ge(q_exp, 1)
            nc.vector.reduce_sum(head[:, 1, :], heads, AX).then_inc(q_sum, 1)
            dve.wait_ge(q_sum, 1)
            nc.vector.reciprocal(head[:, 2, :], head[:, 1, :]).then_inc(q_inverse, 1)
            dve.wait_ge(q_inverse, 1)
            nc.vector.tensor_tensor(heads, heads, spread(2), ALU.mult).then_inc(q_done, 1)

        @block.gpsimd
        def _(pool):
            pool.wait_ge(q_top, 1)
            nc.gpsimd.tensor_tensor(heads, heads, spread(0), ALU.subtract).then_inc(q_shifted, 1)

        @block.scalar
        def _(act):
            act.wait_ge(q_shifted, 1)
            nc.scalar.activation(queries[:], queries[:], ACT.Exp).then_inc(q_exp, 1)
            act.wait_ge(k_top, 2)
            for u in range(n_k):
                m, b = divmod(u, B)
                part = keysT[:, m, b * S:(b + 1) * S]
                nc.scalar.activation(part, part, ACT.Exp, bias=top[:, 1, u:u + 1]).then_inc(k_exp, 1)
            for n, (kind, t) in enumerate(turns):
                act.wait_ge(turned, n + 1)
                dst = qT[:, :, t * P:(t + 1) * P] if kind == "q" else keys[:, t, :].rearrange("p (c n) -> p c n", c=CH)
                nc.scalar.activation(dst, k.ps[:, 4 + n % 4, 0:C].rearrange("p (c n) -> p c n", c=CH), ACT.Copy).then_inc(copied, 1)


def softmax_linear_attention(k):
    nc, inp = k.nc, k.inp
    with ExitStack() as held:
        def sb(what, shape):
            return held.enter_context(nc.sbuf_tensor(f"sl_{what}", shape, F32))

        w, rows, k_bias = sb("w", [P, 4, CH, C]), sb("rows", [P, 5, C]), sb("k_bias", [P, CH])
        qT, att = sb("qT", [P, CH, T]), sb("att", [P, NT, C])
        with nc.sbuf_tensor("sl_keys", [P, NT, C], F32) as keys, nc.sbuf_tensor("sl_values", [P, NT, C + 1], F32) as values:
            memset_stage(k, (values[:, :, C:C + 1], 1.0))
            softmax_features_stage(k, w, rows, k_bias, att, qT, keys, values,
                                   [(w[:], inp["L1a_w"]), (rows[:], inp["L1a_rows"].partition_broadcast(P)), (k_bias[:], inp["L1a_bk"])])
            linear_attention_stage(k, lambda t: keys[:, t, :], lambda t: values[:, t, :], qT, lambda t: att[:, t, :], NT // B)
        norm_rows_stage(k, NT, lambda t: att[:, t, :], rows[:, 2, :], rows[:, 3, :], k.eps[0], source=lambda t: att[:, t, :],
                        destT=lambda t: qT[:, :, t * P:(t + 1) * P])
        residual_norm_stage(k, [(lambda t, c=c: qT[:, c, t * P:(t + 1) * P], w[:, 3, c, :]) for c in range(CH)], rows[:, 4, :])


def context_attention(k):
    self_or_cross_attention(k, "l1x", None, ("L1x_w", "L1x_b", "L1x_out_w", "L1x_out_b", "L1x_v_b"), SC)


def plain_attention(k):
    self_or_cross_attention(k, "l2a", k.xT, ("L2a_w", None, "L2a_out_w", "L2a_out_b", None), S)


def alibi_attention(k):
    self_or_cross_attention(k, "l3a", k.xT, ("L3a_w", "L3a_b", "L3a_out_w", "L3a_out_b", "L3a_v_b"), S, slopes=k.inp["slopes"])


def first_of_maxima(nc, dve, done, count, e, top, rank, onehot, order):
    n = e.shape[2]

    def wide(col):
        return col.unsqueeze(2).broadcast_to((P, e.shape[1], n))

    nc.vector.reduce_max(top, e, AX).then_inc(done, 1)
    dve.wait_ge(done, count + 1)
    nc.vector.tensor_tensor(rank, e, wide(top), ALU.is_equal).then_inc(done, 1)
    dve.wait_ge(done, count + 2)
    nc.vector.tensor_tensor(rank, rank, order, ALU.mult).then_inc(done, 1)
    dve.wait_ge(done, count + 3)
    nc.vector.reduce_max(top, rank, AX).then_inc(done, 1)
    dve.wait_ge(done, count + 4)
    nc.vector.tensor_tensor(onehot, rank, wide(top), ALU.is_equal).then_inc(done, 1)
    dve.wait_ge(done, count + 5)
    return count + 5


def top1_ffn(k):
    nc, inp = k.nc, k.inp
    E, F = 8, 1024
    FCH = F // P
    CHUNK = 256
    with ExitStack() as held:
        def sb(what, shape, dt=F32):
            return held.enter_context(nc.sbuf_tensor(f"t1_{what}", shape, dt))

        z = sb("z", [P, NT, C])
        rows = sb("rows", [P, 3, C])
        with ExitStack() as inner:
            def sbi(what, shape, dt=F32):
                return inner.enter_context(nc.sbuf_tensor(f"t1_{what}", shape, dt))

            w1, w2, wr = sbi("w1", [P, E, CH, F]), sbi("w2", [P, FCH, C]), sbi("wr", [P, CH, E])
            b1 = sbi("b1", [E, F])
            order = sbi("order", [P, NT, E])
            e, rank, onehot, top = sbi("e", [P, NT, E]), sbi("rank", [P, NT, E]), sbi("onehot", [P, NT, E]), sbi("top", [P, NT])
            diag = sbi("diag", [P, E, P], BF16)
            ones = sbi("ones", [P, P], BF16)
            own_x = sbi("own_x", [P, CH, E, CHUNK])
            own = sbi("own", [E, CHUNK])
            hidden = sbi("hidden", [P, FCH, CHUNK])
            (router_in, weights_in, logits, centred, exped, picked, filled, diag_done, spread, own_made, own_ready, own_taken,
             hid_ready, hid_done, z_ready, z_done) = inner.enter_context(k.stage(
                 "router", "weights", "logits", "centred", "exped", "picked", "filled", "diag", "spread", "own_made", "own_ready",
                 "own_taken", "hid_ready", "hid_done", "z_ready", "z_done"))
            block = inner.enter_context(nc.Block(no_gpsimd_drain=True))
            TPC = CHUNK // P
            n_chunks = T // CHUNK
            halves = 2

            @block.sync
            def _(sync):
                k.clear_last_set(sync)
                sync.dma_start(wr[:], inp["L0f_wr"]).then_inc(router_in, 16)
                sync.dma_start(order[:], inp["order8"].partition_broadcast(P)).then_inc(router_in, 16)
                sync.dma_start(b1[:], inp["L0f_b1"]).then_inc(weights_in, 16)
                for x in range(E):
                    sync.dma_start(w1[:, x], inp["L0f_w1"][x]).then_inc(weights_in, 16)
                sync.dma_start(w2[:], inp["L0f_w2"]).then_inc(weights_in, 16)
                sync.dma_start(rows[:], inp["L0f_rows"].partition_broadcast(P)).then_inc(weights_in, 16)

            N_W = E + 3

            @block.tensor
            def _(pe):
                pe.wait_ge(router_in, 32)
                for t in range(NT):
                    for c in range(CH):
                        mm = nc.tensor.matmul(k.ps[:, 0, t * E:(t + 1) * E], k.xT[:, c, t * P:(t + 1) * P], wr[:, c, :], start=c == 0,
                                              stop=c == CH - 1)
                mm.then_inc(logits, 1)
                h = 0
                for q in range(n_chunks):
                    for tt in range(TPC):
                        t = q * TPC + tt
                        pe.wait_ge(diag_done, t + 1)
                        for half in range(halves):
                            u = t * halves + half
                            if u >= 2:
                                pe.wait_ge(own_made, u - 1)
                            nc.tensor.matmul(k.ps[:, 1 + u % 2, :], ones[:, :], diag[:, half * HG:(half + 1) * HG, :].rearrange("p e n -> p (e n)"),
                                             start=True, stop=True).then_inc(spread, 1)
                        nc.tensor.transpose(k.ps[0:E, 3, tt * P:(tt + 1) * P], onehot[:, t, :], k.ident[:, :]).then_inc(own_ready, 1)
                    pe.wait_ge(own_made, (q + 1) * TPC * halves)
                    pe.wait_ge(own_taken, q + 1)
                    pe.wait_ge(weights_in, 16 * N_W)
                    for f in range(FCH):
                        if h >= 2:
                            pe.wait_ge(hid_done, h - 1)
                        out = k.ps[:, 4 + h % 2, 0:CHUNK]
                        for x in range(E):
                            for c in range(CH):
                                nc.tensor.matmul(out, w1[:, x, c, f * P:(f + 1) * P], own_x[:, c, x, :], start=x + c == 0, stop=False)
                        nc.tensor.matmul(out, b1[:, f * P:(f + 1) * P], own[:, :], start=False, stop=True).then_inc(hid_ready, 1)
                        h += 1
                    pe.wait_ge(hid_done, h)
                    for tt in range(TPC):
                        t = q * TPC + tt
                        if t >= 2:
                            pe.wait_ge(z_done, t - 1)
                        for f in range(FCH):
                            mm = nc.tensor.matmul(k.ps[:, 6 + t % 2, 0:C], hidden[:, f, tt * P:(tt + 1) * P], w2[:, f, :], start=f == 0, stop=f == FCH - 1)
                        mm.then_inc(z_ready, 1)

            @block.scalar
            def _(act):
                act.wait_ge(centred, 1)
                nc.scalar.activation(e[:], rank[:], ACT.Exp).then_inc(exped, 1)
                for h in range(n_chunks * FCH):
                    q = h // FCH
                    act.wait_ge(hid_ready, h + 1)
                    if q:
                        act.wait_ge(z_ready, q * TPC)
                    nc.scalar.activation(hidden[:, h % FCH, :], k.ps[:, 4 + h % 2, 0:CHUNK], ACT.Gelu).then_inc(hid_done, 1)

            @block.vector
            def _(dve):
                nc.vector.memset(ones[:], 1.0).then_inc(filled, 1)
                dve.wait_ge(logits, 1)
                view = k.ps[:, 0, 0:NT * E].rearrange("p (t e) -> p t e", e=E)
                nc.vector.reduce_max(top[:], view, AX).then_inc(picked, 1)
                dve.wait_ge(picked, 1)
                nc.vector.tensor_tensor(rank[:], view, top[:].unsqueeze(2).broadcast_to((P, NT, E)), ALU.subtract).then_inc(centred, 1)
                dve.wait_ge(exped, 1)
                dve.wait_ge(router_in, 32)
                first_of_maxima(nc, dve, picked, 1, e[:], top[:], rank[:], onehot[:], order[:])
                dve.wait_ge(weights_in, 16 * N_W)
                for q in range(n_chunks):
                    for tt in range(TPC):
                        t = q * TPC + tt
                        if t:
                            dve.wait_ge(spread, t * halves)
                        for x in range(E):
                            d = nc.vector.tensor_scalar(diag[:, x, :], k.ident[:, :], onehot[:, t, x:x + 1], None, ALU.mult)
                        d.then_inc(diag_done, 1)
                        if q and tt == 0:
                            dve.wait_ge(hid_ready, q * FCH)
                        for half in range(halves):
                            u = t * halves + half
                            dve.wait_ge(spread, u + 1)
                            for c in range(CH):
                                ins = nc.vector.tensor_tensor(
                                    own_x[:, c, half * HG:(half + 1) * HG, tt * P:(tt + 1) * P],
                                    k.ps[:, 1 + u % 2, :].rearrange("p (e n) -> p e n", e=HG),
                                    k.xT[:, c, t * P:(t + 1) * P].unsqueeze(1).broadcast_to((P, HG, P)), ALU.mult)
                            ins.then_inc(own_made, 1)
                    dve.wait_ge(own_ready, (q + 1) * TPC)
                    nc.vector.tensor_copy(own[:, :], k.ps[0:E, 3, 0:CHUNK]).then_inc(own_taken, 1)
                    for tt in range(TPC):
                        t = q * TPC + tt
                        dve.wait_ge(z_ready, t + 1)
                        nc.vector.tensor_tensor(z[:, t, :], k.ps[:, 6 + t % 2, 0:C], k.X[:, t, :], ALU.add).then_inc(picked, 1)
                        dve.wait_ge(picked, 6 + t + 1)
                        nc.vector.tensor_tensor(z[:, t, :], z[:, t, :], rows[:, 0, :], ALU.add).then_inc(z_done, 1)
        norm_rows_stage(k, NT, lambda t: z[:, t, :], rows[:, 1, :], rows[:, 2, :], k.eps[2], source=lambda t: z[:, t, :])
        add_norm_stage(k, lambda t: z[:, t, :])


def capacity_ffn(k):
    nc, inp = k.nc, k.inp
    E, F = 16, 1024
    FCH, CAP = F // P, -(-T // 16)
    ROWS = E * CAP
    with ExitStack() as held:
        def sb(what, shape, dt=F32):
            return held.enter_context(nc.sbuf_tensor(f"cf_{what}", shape, dt))

        scattered, gathered = (held.enter_context(nc.semaphore(n)) for n in ("scattered", "gathered"))
        slot_to, slot_from, gate = sb("slot_to", [P, NT], U32), sb("slot_from", [P, NT], U32), sb("gate", [P, NT])
        y = sb("y", [P, NT, C])
        with ExitStack() as inner:
            def sbi(what, shape, dt=F32):
                return inner.enter_context(nc.sbuf_tensor(f"cf_{what}", shape, dt))

            wg, bg, order = sbi("wg", [P, CH, E]), sbi("bg", [P, E]), sbi("order", [P, NT, E])
            number, token = sbi("number", [P, NT, E]), sbi("token", [P, NT])
            upto, ones = sbi("upto", [P, P]), sbi("ones", [P, P])
            e, rank, onehot, before = (sbi(n, [P, NT, E]) for n in ("e", "rank", "onehot", "before"))
            top, total, pos, slot, keep = (sbi(n, [P, NT]) for n in ("top", "total", "pos", "slot", "keep"))
            zeros = sbi("zeros", [P, ROWS // P, C])
            loaded, zeroed, cleared, logits, centred, exped, step, counted, placed = inner.enter_context(k.stage(
                "loaded", "zeroed", "cleared", "logits", "centred", "exped", "step", "counted", "placed"))
            block = inner.enter_context(nc.Block())
            loads = [(wg[:], inp["L1f_wg"]), (bg[:], inp["L1f_bg"].partition_broadcast(P)), (order[:], inp["order16"].partition_broadcast(P)),
                     (number[:], inp["expert16"].partition_broadcast(P)), (token[:], inp["token"]), (upto[:], inp["upto"])]

            @block.sync
            def _(sync):
                k.clear_last_set(sync)
                for tile, src in loads:
                    sync.dma_start(tile, src).then_inc(loaded, 16)
                sync.wait_ge(zeroed, 1)
                sync.dma_start(k.slots_in[0:ROWS, :].rearrange("(t p) c -> p t c", p=P), zeros[:]).then_inc(cleared, 16)
                sync.wait_ge(cleared, 16)

            @block.gpsimd
            def _(pool):
                nc.gpsimd.memset(zeros[:], 0.0).then_inc(zeroed, 1)
                pool.wait_ge(cleared, 16)
                pool.wait_ge(placed, 1)
                for t in range(NT):
                    pool.indirect_dma_start(k.slots_in, bass.IndirectOffsetOnAxis(ap=slot_to[:, t:t + 1], axis=0), k.X[:, t, :], None).then_inc(scattered, 16)
                pool.wait_ge(scattered, 16 * NT)

            @block.tensor
            def _(pe):
                pe.wait_ge(loaded, 16 * len(loads))
                for t in range(NT):
                    for c in range(CH):
                        mm = nc.tensor.matmul(k.ps[:, 0, t * E:(t + 1) * E], k.xT[:, c, t * P:(t + 1) * P], wg[:, c, :], start=c == 0,
                                              stop=c == CH - 1)
                mm.then_inc(logits, 1)
                pe.wait_ge(counted, NT)
                flat = "p t e -> p (t e)"
                nc.tensor.matmul(k.ps[:, 1, 0:NT * E], upto[:, :], onehot[:].rearrange(flat), start=True, stop=False)
                nc.tensor.matmul(k.ps[:, 1, 0:NT * E], ones[:, :], before[:].rearrange(flat), start=False, stop=True).then_inc(logits, 1)

            @block.scalar
            def _(act):
                act.wait_ge(centred, 1)
                nc.scalar.activation(e[:], rank[:], ACT.Exp).then_inc(exped, 1)

            @block.vector
            def _(dve):
                def wide(col):
                    return col.unsqueeze(2).broadcast_to((P, NT, E))

                n = 0

                def then(ins):
                    nonlocal n
                    n += 1
                    ins.then_inc(step, 1)
                    dve.wait_ge(step, n)

                nc.vector.memset(ones[:], 1.0)
                then(nc.vector.memset(before[:, 0, :], 0.0))
                dve.wait_ge(loaded, 16 * len(loads))
                dve.wait_ge(logits, 1)
                view = k.ps[:, 0, 0:NT * E].rearrange("p (t e) -> p t e", e=E)
                then(nc.vector.tensor_tensor(rank[:], view, bg[:].unsqueeze(1).broadcast_to((P, NT, E)), ALU.add))
                then(nc.vector.reduce_max(top[:], rank[:], AX))
                nc.vector.tensor_tensor(rank[:], rank[:], wide(top[:]), ALU.subtract).then_inc(centred, 1)
                dve.wait_ge(exped, 1)
                then(nc.vector.reduce_sum(total[:], e[:], AX))
                then(nc.vector.reciprocal(total[:], total[:]))
                then(nc.vector.tensor_tensor(e[:], e[:], wide(total[:]), ALU.mult))
                then(nc.vector.reduce_max(gate[:], e[:], AX))
                n = first_of_maxima(nc, dve, step, n, e[:], top[:], rank[:], onehot[:], order[:])
                for t in range(1, NT):
                    nc.vector.tensor_tensor(before[:, t, :], before[:, t - 1, :], onehot[:, t - 1, :], ALU.add).then_inc(counted, 1)
                    dve.wait_ge(counted, t)
                then(nc.vector.tensor_tensor(rank[:], onehot[:], number[:], ALU.mult))
                then(nc.vector.reduce_sum(slot[:], rank[:], AX))
                dve.sem_inc(counted, 1)
                dve.wait_ge(logits, 2)
                then(nc.vector.tensor_tensor(rank[:], k.ps[:, 1, 0:NT * E].rearrange("p (t e) -> p t e", e=E), onehot[:], ALU.mult))
                then(nc.vector.reduce_sum(pos[:], rank[:], AX))
                then(nc.vector.tensor_scalar(keep[:], pos[:], float(CAP), None, ALU.is_le))
                then(nc.vector.scalar_tensor_tensor(slot[:], slot[:], float(CAP), pos[:], ALU.mult, ALU.add))
                then(nc.vector.scalar_tensor_tensor(slot[:], slot[:], -1.0, keep[:], ALU.add, ALU.mult))
                nc.vector.tensor_copy(slot_from[:], slot[:])
                then(nc.vector.tensor_tensor(gate[:], gate[:], keep[:], ALU.mult))
                then(nc.vector.tensor_scalar(keep[:], keep[:], -1.0, 1.0, ALU.mult, ALU.add))
                then(nc.vector.tensor_tensor(token[:], token[:], keep[:], ALU.mult))
                then(nc.vector.tensor_tensor(slot[:], slot[:], token[:], ALU.add))
                nc.vector.tensor_copy(slot_to[:], slot[:]).then_inc(placed, 1)

        with ExitStack() as inner:
            def sbi(what, shape, dt=F32):
                return inner.enter_context(nc.sbuf_tensor(f"cf_{what}", shape, dt))

            DEEP = 3
            w1 = [sbi(f"w1_{i}", [P, CH, F]) for i in range(DEEP)]
            w2 = [sbi(f"w2_{i}", [P, FCH, C]) for i in range(DEEP)]
            xe = [sbi(f"x_{i}", [CAP, C]) for i in range(DEEP)]
            b1, b2 = sbi("b1", [P, E, FCH]), sbi("b2", [P, E, C])
            xeT, hidden, ye = sbi("xT", [P, 2, CH, CAP]), sbi("hidden", [P, 2, FCH, CAP]), sbi("ye", [CAP, 2, C])
            (*loaded, bias_in, turned, x_copied, hid_ready, hid_done, y_ready, y_done, stored0, stored1) = inner.enter_context(k.stage(
                "loaded0", "loaded1", "loaded2", "bias", "turned", "x_copied", "hid_ready", "hid_done", "y_ready", "y_done", "stored0", "stored1"))
            stored = (stored0, stored1)

            def store(sync, x):
                sync.wait_ge(y_done, x + 1)
                sync.dma_start(k.slots_out[x * CAP:(x + 1) * CAP, :], ye[:, x % 2, :]).then_inc(stored[x % 2], 16)

            block = inner.enter_context(nc.Block(no_gpsimd_drain=True))

            @block.sync
            def _(sync):
                k.clear_last_set(sync)
                sync.dma_start(b1[:], inp["L1f_b1"]).then_inc(bias_in, 16)
                sync.dma_start(b2[:], inp["L1f_b2"].partition_broadcast(P)).then_inc(bias_in, 16)
                for x in range(E):
                    i = x % DEEP
                    if x >= DEEP:
                        store(sync, x - DEEP)
                    sync.dma_start(xe[i][:], k.slots_in[x * CAP:(x + 1) * CAP, :]).then_inc(loaded[i], 16)
                    sync.dma_start(w1[i][:], inp["L1f_w1"][x]).then_inc(loaded[i], 16)
                    sync.dma_start(w2[i][:], inp["L1f_w2"][x]).then_inc(loaded[i], 16)
                for x in range(E - DEEP, E):
                    store(sync, x)
                for i in range(2):
                    sync.wait_ge(stored[i], 16 * E // 2)

            @block.tensor
            def _(pe):
                for x in range(E):
                    i = x % DEEP
                    pe.wait_ge(loaded[i], 48 * (x // DEEP + 1))
                    if x >= 2:
                        pe.wait_ge(x_copied, x - 1)
                    for c in range(CH):
                        tr = nc.tensor.transpose(k.ps[:, x % 2, c * P:(c + 1) * P], xe[i][:, c * P:(c + 1) * P], k.ident[:, :])
                    tr.then_inc(turned, 1)
                    pe.wait_ge(x_copied, x + 1)
                    for f in range(FCH):
                        h = x * FCH + f
                        if h >= 4:
                            pe.wait_ge(hid_done, h - 3)
                        for c in range(CH):
                            mm = nc.tensor.matmul(k.ps[:, 2 + h % 4, 0:CAP], w1[i][:, c, f * P:(f + 1) * P], xeT[:, x % 2, c, :], start=c == 0,
                                                  stop=c == CH - 1)
                        mm.then_inc(hid_ready, 1)
                    if x >= 2:
                        pe.wait_ge(y_done, x - 1)
                    for f in range(FCH):
                        pe.wait_ge(hid_done, x * FCH + f + 1)
                        mm = nc.tensor.matmul(k.ps[0:CAP, 6 + x % 2, 0:C], hidden[:, x % 2, f, :], w2[i][:, f, :], start=f == 0, stop=f == FCH - 1)
                    mm.then_inc(y_ready, 1)

            @block.scalar
            def _(act):
                act.wait_ge(bias_in, 32)
                for x in range(E):
                    act.wait_ge(turned, x + 1)
                    nc.scalar.activation(xeT[:, x % 2, :, :], k.ps[:, x % 2, 0:C].rearrange("p (c n) -> p c n", c=CH), ACT.Copy).then_inc(x_copied, 1)
                    if x >= 2:
                        act.wait_ge(y_ready, x - 1)
                    for f in range(FCH):
                        h = x * FCH + f
                        act.wait_ge(hid_ready, h + 1)
                        nc.scalar.activation(hidden[:, x % 2, f, :], k.ps[:, 2 + h % 4, 0:CAP], ACT.Relu, bias=b1[:, x, f:f + 1]).then_inc(hid_done, 1)

            @block.vector
            def _(dve):
                dve.wait_ge(bias_in, 32)
                for x in range(E):
                    dve.wait_ge(y_ready, x + 1)
                    if x >= 2:
                        dve.wait_ge(stored[x % 2], 16 * (x // 2))
                    nc.vector.tensor_tensor(ye[:, x % 2, :], k.ps[0:CAP, 6 + x % 2, 0:C], b2[:, x, :], ALU.add).then_inc(y_done, 1)

        with nc.sbuf_tensor("cf_back", [P, NT, C], F32) as back, k.stage("scaled") as (scaled,), nc.Block() as block:
            @block.sync
            def _(sync):
                k.clear_last_set(sync)

            @block.gpsimd
            def _(pool):
                for t in range(NT):
                    pool.indirect_dma_start(back[:, t, :], None, k.slots_out, bass.IndirectOffsetOnAxis(ap=slot_from[:, t:t + 1], axis=0)).then_inc(gathered, 16)

            @block.vector
            def _(dve):
                dve.wait_ge(gathered, 16 * NT)
                for t in range(NT):
                    nc.vector.tensor_scalar(y[:, t, :], back[:, t, :], gate[:, t:t + 1], None, ALU.mult).then_inc(scaled, 1)
        add_norm_stage(k, lambda t: y[:, t, :])


def quantised_ffn(k):
    nc, inp = k.nc, k.inp
    F = 1024
    FCH = F // P
    with ExitStack() as held:
        def sb(what, shape, dt=F32):
            return held.enter_context(nc.sbuf_tensor(f"qf_{what}", shape, dt))

        w2, rows = sb("w2", [P, FCH, C]), sb("rows", [P, 3, C])
        hidden = sb("hidden", [P, FCH, T])
        with ExitStack() as inner:
            def sbi(what, shape, dt=F32):
                return inner.enter_context(nc.sbuf_tensor(f"qf_{what}", shape, dt))

            hT, h = sbi("hT", [P, CH, T]), sbi("h", [P, NT, C])
            norm_rows_stage(k, NT, lambda t: h[:, t, :], rows[:, 0, :], rows[:, 1, :], k.eps[0], source=lambda t: k.X[:, t, :],
                            destT=lambda t: hT[:, :, t * P:(t + 1) * P], weights=[(rows[:], inp["L2f_rows"].partition_broadcast(P))])
            q1, q2 = sbi("q1", [P, CH, F], I32), sbi("q2", [P, FCH, C], I32)
            w1, b1 = sbi("w1", [P, CH, F]), sbi("b1", [P, FCH])
            loaded, weights, ready, done = inner.enter_context(k.stage("loaded", "weights", "ready", "done"))
            block = inner.enter_context(nc.Block(no_gpsimd_drain=True))
            loads = [(q1[:], inp["L2f_q1"]), (w1[:], inp["L2f_s1"].partition_broadcast(P)), (q2[:], inp["L2f_q2"]),
                     (w2[:], inp["L2f_s2"].partition_broadcast(P)), (b1[:], inp["L2f_b1"])]
            units = [(q, f) for q in range(T // BANK) for f in range(FCH)]

            @block.sync
            def _(sync):
                k.clear_last_set(sync)
                for tile, src in loads:
                    sync.dma_start(tile, src).then_inc(loaded, 16)

            @block.vector
            def _(dve):
                dve.wait_ge(loaded, 16 * len(loads))
                for w, q in ((w1, q1), (w2, q2)):
                    flat = "p a b -> p (a b)"
                    nc.vector.scalar_tensor_tensor(w[:].rearrange(flat), q[:].rearrange(flat), -128.0, w[:].rearrange(flat), ALU.add,
                                                   ALU.mult).then_inc(weights, 1)
                nc.vector.tensor_scalar(rows[:, 2, :], rows[:, 2, :], 0.5, None, ALU.mult).then_inc(weights, 1)

            @block.tensor
            def _(pe):
                pe.wait_ge(weights, 1)
                for n, (q, f) in enumerate(units):
                    if n >= 4:
                        pe.wait_ge(done, n - 3)
                    for c in range(CH):
                        mm = nc.tensor.matmul(k.ps[:, n % 4, :], w1[:, c, f * P:(f + 1) * P], hT[:, c, q * BANK:(q + 1) * BANK], start=c == 0,
                                              stop=c == CH - 1)
                    mm.then_inc(ready, 1)

            @block.scalar
            def _(act):
                act.wait_ge(loaded, 16 * len(loads))
                for n, (q, f) in enumerate(units):
                    act.wait_ge(ready, n + 1)
                    nc.scalar.activation(hidden[:, f, q * BANK:(q + 1) * BANK], k.ps[:, n % 4, :], ACT.Silu, bias=b1[:, f:f + 1]).then_inc(done, 1)
        residual_norm_stage(k, [(lambda t, f=f: hidden[:, f, t * P:(t + 1) * P], w2[:, f, :]) for f in range(FCH)], rows[:, 2, :],
                            x_scale=2.0, y_scale=0.5)


def shifted_ffn(k):
    nc, inp = k.nc, k.inp
    with ExitStack() as held:
        def sb(what, shape, dt=F32):
            return held.enter_context(nc.sbuf_tensor(f"sh_{what}", shape, dt))

        y = sb("y", [P, NT, C])
        with ExitStack() as inner:
            def sbi(what, shape, dt=F32):
                return inner.enter_context(nc.sbuf_tensor(f"sh_{what}", shape, dt))

            w, mu, rest = sbi("w", [P, 3, CH, C]), sbi("mu", [P, 2, CH]), sbi("rest", [P, 2, CH])
            mixed = sbi("mixed", [P, 2, CH, T])
            keys, squares, gate = sbi("keys", [P, CH, T]), sbi("squares", [P, CH, T]), sbi("gate", [P, NT, C])
            loaded, others, scaled, mixed_done, k_ready, k_relu, squared, g_ready, g_done, v_ready, v_done = inner.enter_context(k.stage(
                "loaded", "others", "scaled", "mixed", "k_ready", "k_relu", "squared", "g_ready", "g_done", "v_ready", "v_done"))
            block = inner.enter_context(nc.Block())
            parts = [(b, c) for b in range(B) for c in range(CH)]

            @block.sync
            def _(sync):
                k.clear_last_set(sync)
                sync.dma_start(mu[:], inp["L3f_mu"]).then_inc(loaded, 16)
                sync.dma_start(w[:], inp["L3f_w"]).then_inc(loaded, 16)

            @block.vector
            def _(dve):
                dve.wait_ge(loaded, 32)
                nc.vector.tensor_scalar(rest[:], mu[:], -1.0, 1.0, ALU.mult, ALU.add).then_inc(others, 1)
                dve.wait_ge(others, 1)
                for i, which in enumerate((1, 0)):
                    for n, (b, c) in enumerate(parts):
                        part = mixed[:, which, c, b * S:(b + 1) * S]
                        nc.vector.tensor_scalar(part, k.xT[:, c, b * S:(b + 1) * S], mu[:, which, c:c + 1], None, ALU.mult).then_inc(scaled, 1)
                        dve.wait_ge(scaled, i * len(parts) + n + 1)
                        nc.vector.scalar_tensor_tensor(part[:, 1:], k.xT[:, c, b * S:(b + 1) * S - 1], rest[:, which, c:c + 1], part[:, 1:],
                                                       ALU.mult, ALU.add).then_inc(mixed_done, 1)
                for t in range(NT):
                    dve.wait_ge(v_ready, t + 1)
                    dve.wait_ge(g_done, t + 1)
                    nc.vector.tensor_tensor(y[:, t, :], k.ps[:, 6 + t % 2, 0:C], gate[:, t, :], ALU.mult).then_inc(v_done, 1)

            @block.tensor
            def _(pe):
                pe.wait_ge(loaded, 32)
                for n, (b, m) in enumerate(parts):
                    pe.wait_ge(mixed_done, CH * (b + 1))
                    if n >= 2:
                        pe.wait_ge(k_relu, n - 1)
                    for c in range(CH):
                        mm = nc.tensor.matmul(k.ps[:, n % 2, :], w[:, 1, c, m * P:(m + 1) * P], mixed[:, 1, c, b * S:(b + 1) * S], start=c == 0,
                                              stop=c == CH - 1)
                    mm.then_inc(k_ready, 1)
                for t in range(NT):
                    b = t // (NT // B)
                    pe.wait_ge(mixed_done, CH * (B + b + 1))
                    if t >= 2:
                        pe.wait_ge(g_done, t - 1)
                    for c in range(CH):
                        mm = nc.tensor.matmul(k.ps[:, 4 + t % 2, 0:C], mixed[:, 0, c, t * P:(t + 1) * P], w[:, 0, c, :], start=c == 0, stop=c == CH - 1)
                    mm.then_inc(g_ready, 1)
                for t in range(NT):
                    b = t // (NT // B)
                    pe.wait_ge(squared, CH * (b + 1))
                    if t >= 2:
                        pe.wait_ge(v_done, t - 1)
                    for c in range(CH):
                        mm = nc.tensor.matmul(k.ps[:, 6 + t % 2, 0:C], squares[:, c, t * P:(t + 1) * P], w[:, 2, c, :], start=c == 0, stop=c == CH - 1)
                    mm.then_inc(v_ready, 1)

            @block.scalar
            def _(act):
                for n, (b, m) in enumerate(parts):
                    act.wait_ge(k_ready, n + 1)
                    nc.scalar.activation(keys[:, m, b * S:(b + 1) * S], k.ps[:, n % 2, :], ACT.Relu).then_inc(k_relu, 1)
                for t in range(NT):
                    act.wait_ge(g_ready, t + 1)
                    nc.scalar.activation(gate[:, t, :], k.ps[:, 4 + t % 2, 0:C], ACT.Sigmoid).then_inc(g_done, 1)

            @block.gpsimd
            def _(pool):
                for n, (b, m) in enumerate(parts):
                    pool.wait_ge(k_relu, n + 1)
                    part = keys[:, m, b * S:(b + 1) * S]
                    nc.gpsimd.tensor_tensor(squares[:, m, b * S:(b + 1) * S], part, part, ALU.mult).then_inc(squared, 1)
        residual_norm_stage(k, None, rows=lambda t: y[:, t, :], out=k.out)


def masked_attention(k):
    nc, inp = k.nc, k.inp
    with nc.sbuf_tensor("l3x_att", [P, NG, T], F32) as att:
        q_parts, k_parts, values = k.q_parts, k.k_parts, k.values_of(NTC, P)
        with nc.sbuf_tensor("l3x_ctxT", [P, CH, TC], F32) as ctxT:
            def as_is(src, store):
                return [("split", [(slice(0, BANK), k.ident[:, :], src[:, m, t * BANK:(t + 1) * BANK], True, True)], BANK, None,
                         store[:, m * P:(m + 1) * P, t * BANK:(t + 1) * BANK].rearrange("a p n -> p a n"))
                        for t in range(store.shape[2] // BANK) for m in range(CH)]

            turned = [("value", [(slice(m * P, (m + 1) * P), ctxT[:, m, t * P:(t + 1) * P], k.ident[:, :], True, True) for m in range(CH)],
                       P, values[t]) for t in range(NTC)]
            project_stage(k, as_is(k.xT, q_parts) + as_is(ctxT, k_parts) + turned, [(ctxT[:], inp["ctxT"])])
        attention_stage(k, "l3x_core", q_parts, k_parts, values, S, SC, 1.0, lambda g: att[:, g, :], mask=(inp["mask_q"], inp["mask_k"]))
        with nc.sbuf_tensor("l3x_ow", [P, NG, C], F32) as ow, nc.sbuf_tensor("l3x_ob", [P, C], F32) as ob:
            residual_norm_stage(k, [(lambda t, g=g: att[:, g, t * P:(t + 1) * P], ow[:, g, :]) for g in range(NG)], ob[:],
                                [(ow[:], inp["L3x_out_w"]), (ob[:], inp["L3x_out_b"].partition_broadcast(P))], relu=True)


def latent_attention(k):
    nc, inp = k.nc, k.inp
    D = 64
    INNER, NK = H * D, SC + S
    ICH = INNER // P
    q_parts = nc.dram_tensor("latent_q_parts", [3, INNER, T], BF16, kind="Internal").ap()
    k_parts = nc.dram_tensor("latent_k_parts", [3, INNER, B * NK], BF16, kind="Internal").ap()
    values = nc.dram_tensor("latent_values", [B * NK // P, P, INNER], F32, kind="Internal").ap()
    with nc.sbuf_tensor("la_latT", [P, CH, T], F32) as latT, nc.sbuf_tensor("la_ctxT", [P, CH, TC], F32) as ctxT:
        with nc.sbuf_tensor("la_rows", [P, 4, C], F32) as rows, nc.sbuf_tensor("la_ctx", [P, NTC, C], F32) as ctx, \
                nc.sbuf_tensor("la_lat", [P, NT, C], F32) as lat:
            norm_rows_stage(k, NTC, lambda t: ctx[:, t, :], rows[:, 0, :], rows[:, 1, :], k.eps[0], source=lambda t: ctx[:, t, :],
                            destT=lambda t: ctxT[:, :, t * P:(t + 1) * P],
                            weights=[(rows[:], inp["L2x_rows"].partition_broadcast(P)), (ctx[:], inp["ctx"])])
            norm_rows_stage(k, NT, lambda t: lat[:, t, :], rows[:, 2, :], rows[:, 3, :], k.eps[0], source=lambda t: k.X[:, t, :],
                            destT=lambda t: latT[:, :, t * P:(t + 1) * P])
        with nc.sbuf_tensor("la_w", [P, CH, 3 * INNER], F32) as w:
            def keyT(b, i, n):
                at = i * n
                return (lambda c: ctxT[:, c, b * SC + at:b * SC + at + n]) if at < SC else (lambda c: latT[:, c, b * S + at - SC:b * S + at - SC + n])

            def split(src, col, m, store):
                return ("split", [(slice(0, BANK), w[:, c, col + m * P:col + (m + 1) * P], src(c), c == 0, c == CH - 1) for c in range(CH)],
                        BANK, None, store.rearrange("a p n -> p a n"))

            units = [split(lambda c: latT[:, c, t * BANK:(t + 1) * BANK], 0, m, q_parts[:, m * P:(m + 1) * P, t * BANK:(t + 1) * BANK])
                     for t in range(T // BANK) for m in range(ICH)]
            for b in range(B):
                for i in range(NK // BANK):
                    col = b * NK + i * BANK
                    units += [split(keyT(b, i, BANK), INNER, m, k_parts[:, m * P:(m + 1) * P, col:col + BANK]) for m in range(ICH)]
                for i in range(NK // P):
                    src = keyT(b, i, P)
                    units += [("plain", [(slice(0, BANK), src(c), w[:, c, 2 * INNER + v * BANK:2 * INNER + (v + 1) * BANK], c == 0, c == CH - 1)
                                         for c in range(CH)], P, values[b * NK // P + i, :, v * BANK:(v + 1) * BANK]) for v in range(INNER // BANK)]
            project_stage(k, units, [(w[:], inp["L2x_w"])])
    with nc.sbuf_tensor("la_att", [P, ICH - CH, T], F32) as att:
        def att_of(g):
            return k.xT[:, g, :] if g < CH else att[:, g - CH, :]

        attention_stage(k, "la_core", q_parts, k_parts, values, S, NK, D ** -0.5, att_of, head_dim=D)
        with nc.sbuf_tensor("la_ow", [P, ICH, C], F32) as ow:
            residual_norm_stage(k, [(lambda t, g=g: att_of(g)[:, t * P:(t + 1) * P], ow[:, g, :]) for g in range(ICH)], None,
                                [(ow[:], inp["L2x_out_w"])])


SUBLAYERS = (pyramid_attention, relu_kernel_attention, top1_ffn, softmax_linear_attention, context_attention, capacity_ffn, plain_attention,
             latent_attention, quantised_ffn, alibi_attention, masked_attention, shifted_ffn)


def decoder(nc, inp, out):
    k = Program(nc, inp)
    with ExitStack() as held:
        def sb(name, shape, dt=F32):
            return held.enter_context(nc.sbuf_tensor(name, shape, dt))

        k.ps = held.enter_context(nc.psum_tensor("ps", [P, 8, BANK], F32))
        k.X, k.xT = sb("X", [P, NT, C]), sb("xT", [P, CH, T])
        k.ident, k.spread = sb("ident", [P, P]), sb("spread", [P, P])
        k.ident_bf, k.above_q, k.above_k = (sb(n, [P, P], BF16) for n in ("ident_bf", "above_q", "above_k"))
        eps = sb("eps", [P, 4])
        k.ones, k.ones_bf = sb("ones", [P, P]), sb("ones_bf", [3, P], BF16)
        k.eps = [eps[:, i:i + 1] for i in range(3)]
        k.head_blocks, k.head_cols = sb("head_blocks", [P, P]), sb("head_cols", [P, CH, H])
        k.q_parts = nc.dram_tensor("q_parts", [3, C, T], BF16, kind="Internal").ap()
        k.k_parts = nc.dram_tensor("k_parts", [3, C, TC], BF16, kind="Internal").ap()
        store = nc.dram_tensor("values", [NTC, P, H * QUAD], F32, kind="Internal").ap()
        k.slots_in = nc.dram_tensor("slots_in", [2 * T, C], F32, kind="Internal").ap()
        k.slots_out = nc.dram_tensor("slots_out", [T, C], F32, kind="Internal").ap()
        k.out = out
        k.regroup = nc.dram_tensor("regroup", [B, H, S, HD], F32, kind="Internal").ap()
        k.values_of = lambda tiles, rows: store[0:tiles, 0:rows, :]
        load_stage(k, [(k.X[:], inp["x"]), (k.xT[:], inp["xT"]), (k.ident[:], inp["ident"]), (k.spread[:], inp["spread"]),
                       (k.ident_bf[:], inp["ident_bf"]), (k.above_q[:], inp["above_q"]), (k.above_k[:], inp["above_k"]),
                       (eps[:], inp["eps"].partition_broadcast(P)), (k.head_blocks[:], inp["head_blocks"]),
                       (k.head_cols[:], inp["head_cols"])])
        memset_stage(k, (k.ones[:], 1.0), (k.ones_bf[:], 1.0))

        for sublayer in SUBLAYERS:
            sublayer(k)


def lay_out(a):
    f = {n: np.ascontiguousarray(v) for n, v in a.items()}
    bf16 = mybir.dt.np(BF16)

    def rows_in(w, chunks=CH):
        return w.reshape(chunks, P, w.shape[1]).transpose(1, 0, 2)

    def column(v):
        return v.reshape(-1, P).T

    def strips(w):
        z = np.zeros((H, QUAD, w.shape[1]), w.dtype)
        z[:, :HD] = w.reshape(H, HD, -1)
        return z.reshape(NG, P, -1).transpose(1, 0, 2)

    def strip_column(v):
        return strips(v[:, None])[:, :, 0]

    i = np.arange(P)
    exact = 2.0 ** (-0.5 * (np.arange(H)[:, None] + 1)) * np.arange(S) * HD ** 0.5
    parts = []
    for _ in range(3):
        parts.append((exact - sum(p.astype(np.float64) for p in parts)).astype(np.float32).astype(bf16))
    slopes = np.stack(parts)
    d = {
        "x": f["x"].reshape(NT, P, C).transpose(1, 0, 2),
        "xT": f["x"].reshape(T, CH, P).transpose(2, 1, 0),
        "ident": np.eye(P, dtype=np.float32),
        "spread": ((i[:, None] % QUAD == HD) & (i[:, None] // QUAD == i[None, :] // QUAD)).astype(np.float32),
        "ident_bf": np.eye(P).astype(bf16),
        "above_q": np.where(i[None, :] > i[:, None], -1e30, 0.0).astype(bf16),
        "above_k": np.where(i[None, :] < i[:, None], -1e30, 0.0).astype(bf16),
        "eps": np.array([1e-5, 1e-6, 1e-12, 0.0], np.float32),
        "ctxT": f["ctx_1024"].reshape(TC, CH, P).transpose(2, 1, 0),
        "head_blocks": (i[:, None] // HD == i[None, :] // HD).astype(np.float32),
        "head_cols": ((i[:, None, None] + P * np.arange(CH)[:, None]) // HD == np.arange(H)).astype(np.float32),
        "mask_tokens": f["mask_BxS2_ff1"].reshape(NTC, P).T,
        "L0x_w": np.stack([rows_in(f[f"L0_xattn_{n}"]) for n in ("wq", "wk", "wv", "dense_w")], 1),
        "L0x_rows": np.stack([f["L0_xattn_ln_gamma"], f["L0_xattn_ln_beta"], f["L0_xattn_dense_b"]]),
        "order8": np.tile(np.arange(8, 0, -1, dtype=np.float32), (NT, 1)),
        "L0f_wr": rows_in(f["L0_ffn_Wr"].T),
        "L0f_w1": np.stack([rows_in(w) for w in f["L0_ffn_W1"]]),
        "L0f_b1": f["L0_ffn_b1"],
        "L0f_w2": rows_in(f["L0_ffn_Wo"], 8),
        "L0f_rows": np.stack([f[f"L0_ffn_{n}"] for n in ("bo", "gamma", "beta")]),
        "L1a_w": np.stack([rows_in(f[f"L1_attn_{n}"].T) for n in ("Wq", "Wk", "Wv", "Wo")], 1),
        "L1a_rows": np.stack([f[f"L1_attn_{n}"] for n in ("bq", "bv", "ln_g", "ln_b", "bo")]),
        "L1a_bk": column(f["L1_attn_bk"]),
        "L1x_w": np.concatenate([rows_in(f[f"L1_xattn_{n}"].T) for n in ("wq", "wk", "wv")], 2),
        "L1x_b": np.concatenate([column(f["L1_xattn_bq"]), column(f["L1_xattn_bk"])], 1),
        "L1x_v_b": strip_column(f["L1_xattn_bv"]),
        "L1x_out_w": strips(f["L1_xattn_wo"].T),
        "L1x_out_b": f["L1_xattn_bo"],
        "L2a_w": rows_in(f["L2_attn_w_qkv"].T),
        "L2a_out_w": strips(f["L2_attn_w_proj"].T),
        "L2a_out_b": f["L2_attn_b_proj"],
        "L3a_w": np.concatenate([rows_in(f[f"L3_attn_{n}"].T) for n in ("Wq", "Wk", "Wv")], 2),
        "L3a_b": np.concatenate([column(f["L3_attn_bq"]), column(f["L3_attn_bk"])], 1),
        "L3a_v_b": strip_column(f["L3_attn_bv"]),
        "L3a_out_w": strips(f["L3_attn_Wo"].T),
        "L3a_out_b": f["L3_attn_bo"],
        "slopes": slopes,
        "order16": np.tile(np.arange(16, 0, -1, dtype=np.float32), (NT, 1)),
        "expert16": np.tile(np.arange(16, dtype=np.float32), (NT, 1)),
        "token": (T + np.arange(T, dtype=np.float32)).reshape(NT, P).T,
        "upto": (i[:, None] <= i[None, :]).astype(np.float32),
        "L1f_wg": rows_in(f["L1_ffn_Wg"]),
        "L1f_bg": f["L1_ffn_bg"],
        "L1f_w1": np.stack([rows_in(w) for w in f["L1_ffn_W1"]]),
        "L1f_w2": np.stack([rows_in(w, 8) for w in f["L1_ffn_W2"]]),
        "L1f_b1": f["L1_ffn_b1"].reshape(16, 8, P).transpose(2, 0, 1),
        "L1f_b2": f["L1_ffn_b2"],
        "L2f_rows": np.stack([f[f"L2_ffn_{n}"] for n in ("ln_gamma", "ln_beta", "fc2_bias")]),
        "L2f_q1": rows_in(f["L2_ffn_fc1_q"]),
        "L2f_q2": rows_in(f["L2_ffn_fc2_q"], 8),
        "L2f_s1": f["L2_ffn_fc1_scales"],
        "L2f_s2": f["L2_ffn_fc2_scales"],
        "L2f_b1": column(f["L2_ffn_fc1_bias"]),
        "L3f_w": np.stack([rows_in(f[f"L3_ffn_W_{n}"].T) for n in "rkv"], 1),
        "L3f_mu": np.stack([column(f[f"L3_ffn_mu_{n}"]) for n in "rk"], 1),
        "ctx": f["ctx_1024"].reshape(NTC, P, C).transpose(1, 0, 2),
        "mask_q": f["mask_Bx1xSxS2_ff0"][:, 0],
        "mask_k": f["mask_Bx1xSxS2_ff0"][:, 0].transpose(0, 2, 1),
        "L3x_out_w": strips(f["L3_xattn_wo_w"].T),
        "L3x_out_b": f["L3_xattn_wo_b"],
        "L2x_rows": np.stack([f[f"L2_xattn_{n}"] for n in ("ln_m_g", "ln_m_b", "ln_l_g", "ln_l_b")]),
        "L2x_w": np.concatenate([rows_in(f["L2_xattn_Wq"]), rows_in(f["L2_xattn_Wkv"])], 2),
        "L2x_out_w": rows_in(f["L2_xattn_Wout"], 8),
        "L0_in_w": np.stack([rows_in(w.T) for w in f["L0_attn_in_proj_w"]]),
        "L0_in_b": np.stack([column(b) for b in f["L0_attn_in_proj_b"]], 1),
        "L0_v_b": np.stack([strip_column(b[2 * C:]) for b in f["L0_attn_in_proj_b"]], 1),
        "L0_out_w": np.stack([strips(w.T) for w in f["L0_attn_out_w"]]),
        "L0_out_b": np.stack([column(b) for b in f["L0_attn_out_b"]], 1),
        "L0_up_w": np.stack([rows_in(w.T) for w in f["L0_attn_up_w"]]),
        "L0_up_b": np.stack([column(b) for b in f["L0_attn_up_b"]], 1),
        "L0_out_b0_up_b0": np.stack([f["L0_attn_out_b"][0], f["L0_attn_up_b"][0]]),
    }
    return {n: np.ascontiguousarray(v) for n, v in d.items()}


def build(nc, arrays):
    inp = {n: nc.dram_tensor(f"in_{n}", v.shape, mybir.dt.from_np(v.dtype), kind="ExternalInput").ap() for n, v in arrays.items()}
    decoder(nc, inp, nc.dram_tensor("out_x", [T, C], F32, kind="ExternalOutput").ap())


def kernel(**inputs):
    import concourse.bacc as bacc
    from concourse.bass_utils import run_bass_kernel_spmd

    arrays = lay_out({n: np.asarray(v) for n, v in inputs.items()})
    nc = bacc.Bacc("TRN2", target_bir_lowering=False, num_devices=1)
    build(nc, arrays)
    result = run_bass_kernel_spmd(nc, [{f"in_{n}": v for n, v in arrays.items()}], core_ids=[0])
    return result.results[0]["out_x"].reshape(B, S, C)
```

```python
from contextlib import ExitStack, contextmanager

import numpy as np

import concourse.bass as bass
from concourse import mybir

F32 = mybir.dt.float32
BF16 = mybir.dt.bfloat16
I32 = mybir.dt.int32
U32 = mybir.dt.uint32
ALU = mybir.AluOpType
ACT = mybir.ActivationFunctionType
AX = mybir.AxisListType.X

P = 128
B, S, C = 4, 512, 256
SC = 1024
T, TC = B * S, B * SC
NT, NTC = T // P, TC // P
CH = C // P
H, HD = 16, 16
QUAD = 32
HG = 4
NG = H // HG
Q_PART = (0, 0, 0, 1, 1, 2)
K_PART = (0, 1, 2, 0, 1, 0)
STACK = len(Q_PART) * HD
BANK = 512


class Program:

    FIRST_SEM, SET = 176, 38

    def __init__(self, nc, inputs):
        self.nc, self.inp = nc, inputs
        self.stages = 0

    @contextmanager
    def stage(self, *names):
        first = self.FIRST_SEM + self.SET * (self.stages % 2)
        assert len(names) <= self.SET
        self.stages += 1
        with ExitStack() as held:
            yield [held.enter_context(self.nc.semaphore(f"s{self.stages}_{name}", num=first + i))
                   for i, name in enumerate(names)]

    def clear_last_set(self, sync):
        first = self.FIRST_SEM + self.SET * (self.stages % 2)
        sync.sem_clear(range(first, first + self.SET))


def load_stage(k, pairs):
    nc = k.nc
    with k.stage("loaded") as (loaded,), nc.Block(no_gpsimd_drain=True) as block:
        @block.sync
        def _(sync):
            k.clear_last_set(sync)
            for tile, source in pairs[0::2]:
                sync.dma_start(tile, source).then_inc(loaded, 16)
            sync.wait_ge(loaded, 16 * len(pairs))

        @block.scalar
        def _(act):
            for tile, source in pairs[1::2]:
                act.dma_start(tile, source).then_inc(loaded, 16)


def project_stage(k, units, weights, stores=()):
    nc = k.nc
    splits = [n for n, u in enumerate(units) if u[0] == "split"]
    stored_by = []
    for i, n in enumerate(splits):
        stored_by.append((stored_by[i - 3] if i >= 3 else 0) + 16 * len(units[n][4]))
    with (
        nc.sbuf_tensor(f"proj_full_{k.stages}", [P, 2, BANK], F32) as full,
        nc.sbuf_tensor(f"proj_rest_{k.stages}", [P, 2, BANK], F32) as rest,
        nc.sbuf_tensor(f"proj_parts_{k.stages}", [P, 3, 3, BANK], BF16) as parts,
        nc.sbuf_tensor(f"proj_value_{k.stages}", [P, 2, H, QUAD], F32) as value,
        k.stage("weights", "ready", "evacuated", "high", "remainder", "middle", "low", "ones", "parts_stored0",
                "parts_stored1", "parts_stored2", "value_stored0", "value_stored1", "others_stored") as (
            weights_in, ready, evacuated, high, remainder, middle, low, ones_set, *stored, others_stored),
        nc.Block() as block,
    ):
        parts_stored, value_stored = stored[0:3], stored[3:5]

        @block.sync
        def _(sync):
            k.clear_last_set(sync)
            for tile, source in weights:
                sync.dma_start(tile, source).then_inc(weights_in, 16)
            for destination, source in stores:
                sync.dma_start(destination, source).then_inc(others_stored, 16)
            i = j = 0
            for n, unit in enumerate(units):
                if unit[0] == "split":
                    sync.wait_ge(low, i + 1)
                    for destination, taken in unit[4]:
                        sync.dma_start(destination, taken(parts[:, i % 3, :, 0:unit[2]])).then_inc(parts_stored[i % 3], 16)
                    i += 1
                else:
                    sync.wait_ge(evacuated, n + 1)
                    sync.dma_start(unit[3], value[0:unit[2], j % 2].rearrange("p h d -> p (h d)")
                                   ).then_inc(value_stored[j % 2], 16)
                    j += 1
            for r in range(min(3, i)):
                sync.wait_ge(parts_stored[(i - 1 - r) % 3], stored_by[i - 1 - r])
            if stores:
                sync.wait_ge(others_stored, 16 * len(stores))
            for r in range(min(2, j)):
                sync.wait_ge(value_stored[r], 16 * len(range(r, j, 2)))

        @block.tensor
        def _(pe):
            pe.wait_ge(weights_in, 16 * len(weights))
            for n, unit in enumerate(units):
                if n >= 8:
                    pe.wait_ge(evacuated, n - 7)
                rows = P if unit[0] == "split" else unit[2]
                for cols, lhsT, rhs, start, stop in unit[1]:
                    last = nc.tensor.matmul(k.ps[0:rows, n % 8, cols], lhsT, rhs, start=start, stop=stop)
                last.then_inc(ready, 1)

        @block.scalar
        def _(act):
            act.wait_ge(ones_set, 1)

            def take_middle(i):
                width = units[splits[i]][2]
                act.wait_ge(remainder, i + 1)
                nc.scalar.activation(parts[:, i % 3, 1, 0:width], rest[:, i % 2, 0:width], ACT.Copy).then_inc(middle, 1)

            i = j = 0
            for n, unit in enumerate(units):
                act.wait_ge(ready, n + 1)
                if unit[0] == "split":
                    _, _, width, bias, _ = unit
                    if i >= 2:
                        act.wait_ge(remainder, i - 1)
                    if i == 0 and bias is not None:
                        act.wait_ge(weights_in, 16 * len(weights))
                    for cols, column in bias if isinstance(bias, list) else [(slice(0, width), 0.0 if bias is None else bias)]:
                        ins = nc.scalar.activation(full[:, i % 2, cols], k.ps[:, n % 8, cols], ACT.Identity, bias=column)
                    ins.then_inc(evacuated, 1)
                    i += 1
                else:
                    rows = unit[2]
                    if j >= 2:
                        act.wait_ge(value_stored[j % 2], 16 * (j // 2))
                    d = HD if unit[0] == "value" else QUAD
                    nc.scalar.activation(value[0:rows, j % 2, :, 0:d], k.ps[0:rows, n % 8, 0:H * d].rearrange("p (h d) -> p h d", h=H),
                                         ACT.Copy).then_inc(evacuated, 1)
                    j += 1
                if n and units[n - 1][0] == "split":
                    take_middle(splits.index(n - 1))
            if units[-1][0] == "split":
                take_middle(len(splits) - 1)

        @block.vector
        def _(dve):
            nc.vector.memset(value[:], 1.0).then_inc(ones_set, 1)
            for i, n in enumerate(splits):
                width = units[n][2]
                dve.wait_ge(evacuated, n + 1)
                if i >= 3:
                    dve.wait_ge(parts_stored[i % 3], stored_by[i - 3])
                nc.vector.tensor_copy(parts[:, i % 3, 0, 0:width], full[:, i % 2, 0:width]).then_inc(high, 1)
                if i >= 2:
                    dve.wait_ge(low, i - 1)
                dve.wait_ge(high, i + 1)
                nc.vector.tensor_tensor(rest[:, i % 2, 0:width], full[:, i % 2, 0:width],
                                        parts[:, i % 3, 0, 0:width], ALU.subtract).then_inc(remainder, 1)

        @block.gpsimd
        def _(pool):
            for i, n in enumerate(splits):
                width = units[n][2]
                pool.wait_ge(middle, i + 1)
                nc.gpsimd.tensor_tensor(parts[:, i % 3, 2, 0:width], rest[:, i % 2, 0:width],
                                        parts[:, i % 3, 1, 0:width], ALU.subtract).then_inc(low, 1)


def stacked(store, order):
    n = store.shape[2]
    at, out = 0, []
    for part, times in enumerate((3, 2, 1)):
        if order == Q_PART:
            out.append((store[:, at:at + times, :], lambda p, part=part, times=times: p[:, part:part + 1, :].broadcast_to((P, times, n))))
        else:
            out.append((store[:, at:at + times, :], lambda p, times=times: p[:, 0:times, :]))
        at += times
    return out


def split_units(source, width, weight, bias, store, order):
    return [("split", [(slice(0, width), weight[:, c, m * P:(m + 1) * P], source(c, t), c == 0, c == CH - 1) for c in range(CH)],
             width, None if bias is None else bias[:, m:m + 1], stacked(store[m * P:(m + 1) * P, :, t * width:(t + 1) * width], order))
            for t in range(store.shape[2] // width) for m in range(CH)]


def value_units(source, rows, weight, store):
    return [("value", [(slice(0, C), source(c, t), weight[:, c, :], c == 0, c == CH - 1) for c in range(CH)],
             rows, store[t]) for t in range(len(store) if isinstance(store, list) else store.shape[0])]


def attention_stage(k, name, q_store, k_store, values, nq, nk, scale, att, head_dim=HD, slopes=None, mask=None, spans=None):
    nc = k.nc
    causal, small = slopes is not None, head_dim == HD
    heads = HG if small else 2
    groups, strip = H // heads, P // heads
    nqt, nkt, wide = nq // P, nk // P, min(BANK, nk)
    nwide = nk // wide
    rows_a = STACK + (3 if causal else 0)
    rows_b = rows_a + 3
    chunks = [(qi, j, c) for qi in range(nqt) for j in range(heads) for c in range(nwide)]
    NCH, NS = len(chunks), nkt * heads
    slots = heads * nqt
    A0, B0, ACC, SIDE = 0, 3, 6, 7
    WEIGHTS = 8
    ahead_tiles = WEIGHTS // heads
    spread_at = 1
    QUARTER = nq // 4
    SUMS = 2
    inverse_at = [(2 + p, 0) for p in range(4)]

    def chunks_of(i):
        some = list(range(i * NCH // nkt, (i + 1) * NCH // nkt))
        return [some[len(some) * j // heads:len(some) * (j + 1) // heads] for j in range(heads)]

    with ExitStack() as held:
        def sb(what, shape, dt):
            return held.enter_context(nc.sbuf_tensor(f"{name}_{what}", shape, dt))

        RING, V_RING = 4, 2
        if small:
            q_stack = [sb(f"q{r}", [rows_b, heads, nq], BF16) for r in range(RING)]
            k_stack = [sb(f"k{r}", [rows_b, heads, nk], BF16) for r in range(RING)]
        else:
            q_stack = [sb(f"q{r}", [P, 3, heads, nq], BF16) for r in range(RING)]
            k_stack = [sb(f"k{r}", [P, 2, heads, nk], BF16) for r in range(RING)]
            top_rows = [sb(f"top_rows{r}", [3, heads, nq], BF16) for r in range(RING)]
            weight_sums = sb("weight_sums", [P, 2, heads, nq], F32)
        v_tile = [sb(f"v{r}", [P, nkt, P], F32) for r in range(V_RING)]
        weights = sb("weights", [P, WEIGHTS, nq], F32)
        part_max = sb("part_max", [P, 2, slots, nwide], F32)
        row_max = sb("row_max", [P, 2, slots], F32)
        negative = sb("negative", [slots, 2, P], F32)
        max_parts = sb("max_parts", [slots, 3, P], BF16)
        if small:
            inverse = sb("inverse", [P, groups, nq], F32)
            dense, dense_inverse = (sb(what, [P, H * nq // P], F32) for what in ("dense", "dense_inverse"))
        else:
            sums, inverse = sb("sums", [P, SUMS, nq], F32), sb("inverse", [P, nq], F32)
        names = ["row_in", "row_made", "a_ready", "a_taken", "turned", "s_ready", "exp_done", "pv_done", "acc_copied",
                 "sums_ready", "inverted", "normed", "set_up", "negated", "max_split", "added", "masked", "sums_out", "dense_in",
                 "inverses_out", "inverses_in"]
        if mask is not None:
            mask_q, mask_k = sb("mask_q", [P, nqt, nk], F32), sb("mask_k", [P, nkt, nq], F32)
            masked_scores, unused = sb("masked_scores", [P, 3, nq], F32), sb("unused", [P, 2, wide], F32)
            held_back = sb("held_back", [1, 2], F32)
        all_names = names + [f"loaded{r}" for r in range(RING)] + [f"v_loaded{r}" for r in range(V_RING)] + (
            [f"mask_q{i}" for i in range(nqt)] + [f"mask_k{i}" for i in range(nkt // 2)] if mask is not None else [])
        (row_in, row_made, a_ready, a_taken, turned, s_ready, exp_done, pv_done, acc_copied, sums_ready, inverted, normed,
         set_up, negated, max_split, added, masked, sums_out, dense_in, inverses_out, inverses_in, *more) = held.enter_context(k.stage(*all_names))
        loaded, v_loaded, more = more[:RING], more[RING:RING + V_RING], more[RING + V_RING:]
        mask_q_in, mask_k_in = more[:nqt], more[nqt:]
        block = held.enter_context(nc.Block())

        def at(b, g, per_group, n):
            return b * (groups * per_group) + (g * per_group + n)

        def index(b, g):
            return b * groups + g if isinstance(b, int) else None

        def first(b, g, n=1):
            return index(b, g) is not None and index(b, g) < n

        def exists(b, g):
            return index(b, g) is None or 0 <= index(b, g) < B * groups

        def later(b, g, ahead):
            return b + (g + ahead) // groups, (g + ahead) % groups

        def keys_of(qi, c):
            if spans:
                return spans[qi]
            return slice(0, (qi + 1) * P) if causal else slice(c * wide, (c + 1) * wide)

        def queries_of(i):
            if spans:
                tiles = [qi for qi, keys in enumerate(spans) if keys.start <= i * P < keys.stop]
                return slice(tiles[0] * P, (tiles[-1] + 1) * P)
            return slice(i * P if causal else 0, nq)

        def opens(i):
            return i == 0 or (spans is not None and queries_of(i - 1) != queries_of(i))

        def for_groups(engine, body, lead=2, turns=B - 1):
            for g in range(lead):
                body(0, g)
            with engine.Fori(0, turns) as b:
                for g in range(lead, groups + lead):
                    body(b + g // groups, g % groups)
            for n in range(lead + turns * groups, B * groups):
                body(n // groups, n % groups)

        def loads_of(b, g):
            r, rows = g % RING, slice(g * heads * head_dim, (g + 1) * heads * head_dim)
            out = []
            if small:
                for stack, store, n in ((q_stack[r], q_store, nq), (k_stack[r], k_store, nk)):
                    out.append((stack[0:STACK, :, :], store[rows, :, bass.ds(b * n, n)].rearrange("(j d) t n -> (d t) j n", d=head_dim)))
            else:
                for stack, store, order, n in ((q_stack[r], q_store, (0, 0, 1, 1, 0, 2), nq), (k_stack[r], k_store, (0, 1, 2, 0), nk)):
                    out += [(stack[(t % 2) * head_dim:(t % 2 + 1) * head_dim, t // 2, :, :],
                             store[p, rows, bass.ds(b * n, n)].rearrange("(j d) n -> d j n", d=head_dim)) for t, p in enumerate(order)]
            if causal:
                out.append((k_stack[r][STACK:rows_a, :, :], slopes[:, g * heads:(g + 1) * heads, :]))
            return out

        n_loads = len(loads_of(0, 0))
        n_ones = RING * (2 if causal else 1)

        def loads_done(b, g):
            return 16 * n_loads * (b * (groups // RING) + (g // RING + 1))

        def v_done(b, g):
            return 16 * (b * (groups // V_RING) + (g // V_RING + 1))

        @block.sync
        def _(sync):
            k.clear_last_set(sync)

            def load_group(b, g):
                for tile, source in loads_of(b, g):
                    sync.dma_start(tile, source).then_inc(loaded[g % RING], 16)

            def load_values(b, g):
                sync.dma_start(v_tile[g % V_RING][:, :, :], values[bass.ds(b * nkt, nkt), :, g * P:(g + 1) * P].rearrange("i p c -> p i c")
                               ).then_inc(v_loaded[g % V_RING], 16)

            def load_mask_q(b, qi):
                sync.dma_start(mask_q[:, qi, :], mask[0][bass.ds(b, 1), qi * P:(qi + 1) * P, :].rearrange("o p n -> p (o n)")).then_inc(mask_q_in[qi], 16)

            def load_mask_k(b, i):
                sync.dma_start(mask_k[:, 2 * i:2 * i + 2, :], mask[1][bass.ds(b, 1), 2 * i * P:2 * (i + 1) * P, :].rearrange("o (i p) n -> p (o i) n", p=P)
                               ).then_inc(mask_k_in[i], 16)

            for g in range(2):
                load_group(0, g)
            if mask is not None:
                for qi in range(nqt):
                    load_mask_q(0, qi)
            for g in range(2):
                load_values(0, g)
            if mask is not None:
                for i in range(nkt // 2):
                    load_mask_k(0, i)
            for g in range(2, RING):
                load_group(0, g)

            def row(b, g):
                sync.wait_ge(row_made, at(b, g, 1, 1))
                for p in range(3):
                    dst = q_stack[g % RING][rows_a + p:rows_a + p + 1, :, :] if small else top_rows[g % RING][p:p + 1, :, :]
                    sync.dma_start(dst.rearrange("o j (i t) -> o (j i) t", t=P), max_parts[:, p, :]).then_inc(row_in, 16)

            def gather_sums(b):
                sync.wait_ge(acc_copied, at(b, groups, 1, 1))
                sync.dma_start(k.sums_of_weights, att[HD::QUAD, :, bass.ds(b * nq, nq)]).then_inc(sums_out, 16)
                sync.wait_ge(sums_out, 16 * (b + 1))
                sync.dma_start(dense[:, :], k.sums_of_weights.rearrange("j g (s n) -> (j g s) n", n=H * nq // P)).then_inc(dense_in, 16)

            def return_inverses(b):
                sync.wait_ge(normed, at(b, 0, 1, SUMS))
                sync.wait_ge(inverses_in, 16 * heads * b + 1)
                sync.wait_ge(inverted, b + 1)
                sync.dma_start(k.inverse_sums.rearrange("j g (s n) -> (j g s) n", n=H * nq // P), dense_inverse[:, :]).then_inc(inverses_out, 16)
                sync.wait_ge(inverses_out, 16 * (b + 1))
                for j in range(heads):
                    sync.dma_start(inverse[strip * j:strip * (j + 1), :, :], k.inverse_sums[j, :, :].partition_broadcast(strip)).then_inc(inverses_in, 16)

            row(0, 0)

            def group(b, g):
                before = later(b, g, -1)
                if exists(*before):
                    sync.wait_ge(pv_done, at(*before, nkt, nkt + ahead_tiles))
                    if exists(*later(b, g, 1)):
                        load_values(*later(b, g, 1))
                    if exists(*later(b, g, RING - 1)):
                        load_group(*later(b, g, RING - 1))
                if exists(*later(b, g, 1)):
                    row(*later(b, g, 1))
                if small and g == 0 and exists(b - 1, 0):
                    gather_sums(b - 1)
                if small and g == 1 and exists(b - 1, 0):
                    return_inverses(b - 1)
                if mask is not None and g == groups - 3 and exists(b + 1, 0):
                    for qi in range(nqt):
                        sync.wait_ge(a_taken, at(b, groups - 1, NCH + 1, (qi + 1) * NCH // nqt))
                        load_mask_q(b + 1, qi)
                if mask is not None and g == groups - 1 and exists(b + 1, 0):
                    for i in range(nkt // 2):
                        sync.wait_ge(masked, at(b, g, NS, 2 * (i + 1) * heads + 3))
                        load_mask_k(b + 1, i)

            for_groups(sync, group, lead=groups, turns=B - 2)
            if small:
                gather_sums(B - 1)
                return_inverses(B - 1)

        @block.tensor
        def _(pe):
            def pass_a(b, g, some):
                r = g % RING
                for n in some:
                    qi, j, c = chunks[n]
                    if n == 0:
                        pe.wait_ge(loaded[r], loads_done(b, g))
                    if not (first(b, g) and n < 3):
                        pe.wait_ge(a_taken, at(b, g, NCH + 1, 0 if n < 2 else n - 2))
                    keys, qs = keys_of(qi, c), slice(qi * P, (qi + 1) * P)
                    out = k.ps[:, A0 + (g * NCH + n) % 3, 0:keys.stop - keys.start]
                    if small:
                        mm = nc.tensor.matmul(out, q_stack[r][0:rows_a, j, qs], k_stack[r][0:rows_a, j, keys], start=True, stop=not causal)
                    else:
                        mm = nc.tensor.matmul(out, q_stack[r][:, 0, j, qs], k_stack[r][:, 0, j, keys], start=True, stop=True)
                    if causal:
                        mm = nc.tensor.matmul(out[:, qi * P:(qi + 1) * P], k.ident_bf[:, :], k.above_q[:, :], start=False, stop=True)
                    mm.then_inc(a_ready, 1 if n < NCH - 1 else 2)

            def turn(b, g):
                pe.wait_ge(a_taken, at(b, g, NCH + 1, NCH + 1))
                if not first(b, g):
                    pe.wait_ge(negated, at(b, g, 1, 0))
                if not small and not first(b, g, 3):
                    pe.wait_ge(inverted, at(b, g, 4, -4))
                nc.tensor.transpose(k.ps[0:slots, SIDE, 0:P], row_max[:, g % 2, :], k.ident[:, :]).then_inc(turned, 1)

            def spread(b, g, last_turned):
                pe.wait_ge(acc_copied, at(b, g, 1, 2))
                pe.wait_ge(negated, last_turned)
                pe.wait_ge(inverted, at(b, g, 4, 4))
                pe.wait_ge(added, at(b, g, nkt, nkt + 4))
                for j in range(heads):
                    mm = nc.tensor.matmul(k.ps[strip * j:strip * (j + 1), SIDE, 0:nq], k.ones[:, 0:strip], weight_sums[:, g % 2, j, :],
                                          start=True, stop=True, tile_position=(0, strip * j))
                mm.then_inc(sums_ready, 1)

            def weigh(b, g, i):
                pe.wait_ge(exp_done, at(b, g, NS, (i + 1) * heads + 3))
                if i == 0:
                    pe.wait_ge(v_loaded[g % V_RING], v_done(b, g))
                    pe.wait_ge(acc_copied, at(b, g, 1, 1))
                qs = queries_of(i)
                for j in range(heads):
                    mm = nc.tensor.matmul(k.ps[strip * j:strip * (j + 1), ACC, qs], v_tile[g % V_RING][:, i, strip * j:strip * (j + 1)],
                                          weights[:, (g * NS + i * heads + j) % WEIGHTS, qs], start=opens(i), stop=i == nkt - 1,
                                          tile_position=(0, strip * j), skip_group_check=causal or spans is not None)
                mm.then_inc(pv_done, 1)

            if small:
                pe.wait_ge(set_up, 16 * n_ones)
            pass_a(0, 0, range(NCH))
            turn(0, 0)
            pass_a(0, 1, range(NCH))

            def group(b, g):
                r = g % RING
                pe.wait_ge(row_in, 48 * at(b, g, 1, 1))
                for i in range(nkt):
                    more = chunks_of(i) if exists(*later(b, g, 2)) else [()] * heads
                    qs, ks = queries_of(i), slice(i * P, (i + 1) * P)
                    for j in range(heads):
                        s = i * heads + j
                        pe.wait_ge(exp_done if mask is None else masked, at(b, g, NS, 3 if g == s == 0 else s + 1))
                        out = k.ps[:, B0 + (g * NS + s) % 3, qs]
                        if small:
                            mm = nc.tensor.matmul(out, k_stack[r][0:rows_b, j, ks], q_stack[r][0:rows_b, j, qs], start=True, stop=not causal)
                        else:
                            for p, kp in enumerate((0, 0, 1)):
                                nc.tensor.matmul(out, k_stack[r][:, kp, j, ks], q_stack[r][:, p, j, qs], start=p == 0, stop=False)
                            mm = nc.tensor.matmul(out, k.ones_bf[0:3, :], top_rows[r][:, j, qs], start=False, stop=True)
                        if causal:
                            mm = nc.tensor.matmul(out[:, 0:P], k.ident_bf[:, :], k.above_k[:, :], start=False, stop=True)
                        mm.then_inc(s_ready, 1)
                        pass_a(*later(b, g, 2), more[j])
                    if i:
                        weigh(b, g, i - 1)
                    elif exists(*later(b, g, -1)):
                        weigh(*later(b, g, -1), nkt - 1)
                    if i == 0 and exists(*later(b, g, 1)):
                        turn(*later(b, g, 1))
                    if i == spread_at and not small and exists(*later(b, g, -1)):
                        spread(*later(b, g, -1), at(b, g, 1, 2 if exists(*later(b, g, 1)) else 1))

            for_groups(pe, group)
            weigh(B - 1, groups - 1, nkt - 1)
            if not small:
                spread(B - 1, groups - 1, B * groups)

        @block.scalar
        def _(act):
            act.sem_inc(exp_done, 3)
            for r in range(RING if small else 0):
                act.dma_start(k_stack[r][rows_a:rows_b, :, :], k.rows_of_ones[:, :, 0:nk]).then_inc(set_up, 16)
                if causal:
                    act.dma_start(q_stack[r][STACK:rows_a, :, :], k.rows_of_ones[:, :, 0:nq]).then_inc(set_up, 16)

            def copy_sums(b, g):
                act.wait_ge(pv_done, at(b, g, nkt, nkt + ahead_tiles))
                if small:
                    out = att[:, g, bass.ds(b * nq, nq)]
                else:
                    act.wait_ge(normed, at(b, g, 1, 1))
                    out = sums[:, g % SUMS, :]
                nc.scalar.activation(out, k.ps[:, ACC, 0:nq], ACT.Copy).then_inc(acc_copied, 1)

            def group(b, g):
                for s in range(NS):
                    i = s // heads
                    qs = queries_of(i)
                    if s % heads == 0:
                        act.wait_ge(pv_done, at(b, g, nkt, i + 1))
                        if not small:
                            act.wait_ge(added, at(b, g, nkt, i + 1))
                    if mask is None:
                        act.wait_ge(s_ready, at(b, g, NS, s + 1))
                        src = k.ps[:, B0 + (g * NS + s) % 3, qs]
                    else:
                        act.wait_ge(masked, at(b, g, NS, s + 1 + 3))
                        src = masked_scores[:, (g * NS + s) % 3, :]
                    nc.scalar.activation(weights[:, (g * NS + s) % WEIGHTS, qs], src, ACT.Exp, scale=scale).then_inc(exp_done, 1)
                    if s == heads - 1 and exists(*later(b, g, -1)):
                        copy_sums(*later(b, g, -1))

            for_groups(act, group)
            copy_sums(B - 1, groups - 1)

        @block.vector
        def _(dve):
            dve.sem_inc(pv_done, ahead_tiles)
            dve.sem_inc(acc_copied, 1)
            if small:
                dve.sem_inc(inverses_in, 1)
            else:
                dve.sem_inc(inverted, 4)
            dve.sem_inc(normed, SUMS)
            dve.sem_inc(masked, 3)

            def maxima(b, g, some):
                for n in some:
                    qi, j, c = chunks[n]
                    if n == 0 and not first(b, g, 2):
                        dve.wait_ge(turned, at(b, g, 1, -1))
                    keys, slot = keys_of(qi, c), j * nqt + qi
                    out = part_max[:, g % 2, slot, c:c + 1] if nwide > 1 else row_max[:, g % 2, slot:slot + 1]
                    scores = k.ps[:, A0 + (g * NCH + n) % 3, 0:keys.stop - keys.start]
                    if mask is not None:
                        if n % (NCH // nqt) == 0:
                            dve.wait_ge(mask_q_in[qi], 16 * (b + 1))
                        if not (first(b, g) and n < 2):
                            dve.wait_ge(a_taken, at(b, g, NCH + 1, max(n - 1, 0)))
                        dve.wait_ge(a_ready, at(b, g, NCH + 1, n + 1))
                        nc.vector.memset(held_back[:, n % 2:n % 2 + 1], 0.0)
                        nc.vector.tensor_tensor_reduce(unused[:, n % 2, :], scores, mask_q[:, qi, keys], 1.0, -3.0e38, ALU.add, ALU.max,
                                                       out).then_inc(a_taken, 1)
                    else:
                        dve.wait_ge(a_ready, at(b, g, NCH + 1, n + 1))
                        nc.vector.reduce_max(out, scores, AX).then_inc(a_taken, 1)
                    if n == NCH - 1:
                        dve.wait_ge(a_taken, at(b, g, NCH + 1, NCH))
                        if nwide > 1:
                            nc.vector.reduce_max(row_max[:, g % 2, :], part_max[:, g % 2, :, :], AX).then_inc(a_taken, 1)
                        else:
                            dve.sem_inc(a_taken, 1)

            def negate(b, g):
                dve.wait_ge(turned, at(b, g, 1, 1))
                if not first(b, g):
                    dve.wait_ge(row_made, at(b, g, 1, 0))
                    dve.wait_ge(row_in, 48 * at(b, g, 1, 0))
                nc.vector.tensor_scalar(max_parts[:, 0, :], k.ps[0:slots, SIDE, 0:P], -1.0, None, ALU.mult)
                nc.vector.tensor_scalar(negative[:, g % 2, :], k.ps[0:slots, SIDE, 0:P], -1.0, None, ALU.mult).then_inc(negated, 1)

            def add_mask(b, g, s):
                i, j = divmod(s, heads)
                if g == 0 and j == 0 and i % 2 == 0:
                    dve.wait_ge(mask_k_in[i // 2], 16 * (b + 1))
                dve.wait_ge(s_ready, at(b, g, NS, s + 1))
                dve.wait_ge(exp_done, at(b, g, NS, 3 if g == s == 0 else s + 1))
                nc.vector.tensor_tensor(masked_scores[:, (g * NS + s) % 3, :], k.ps[:, B0 + (g * NS + s) % 3, :], mask_k[:, i, :],
                                        ALU.add).then_inc(masked, 1)

            def invert_dense(b):
                dve.wait_ge(dense_in, 16 * (b + 1))
                dve.wait_ge(inverses_in, 16 * heads * b + 1)
                nc.vector.reciprocal(dense_inverse[:, :], dense[:, :]).then_inc(inverted, 1)

            def invert(b, g, quarter):
                if quarter == 0:
                    dve.wait_ge(sums_ready, at(b, g, 1, 1))
                    dve.wait_ge(normed, at(b, g, 1, SUMS))
                own = slice(quarter * QUARTER, (quarter + 1) * QUARTER)
                nc.vector.reciprocal(inverse[:, own], k.ps[:, SIDE, own]).then_inc(inverted, 1)

            maxima(0, 0, range(NCH))
            negate(0, 0)
            maxima(0, 1, range(NCH))

            def group(b, g):
                before = later(b, g, -1)
                for i in range(nkt):
                    more = chunks_of(i) if exists(*later(b, g, 2)) else [()] * heads
                    for j in range(heads):
                        if mask is not None:
                            add_mask(b, g, i * heads + j)
                        maxima(*later(b, g, 2), more[j])
                        if (i, j) in inverse_at and not small and exists(*before):
                            invert(*before, inverse_at.index((i, j)))
                    if i == 0 and exists(*later(b, g, 1)):
                        negate(*later(b, g, 1))
                    if i == 0 and g == 1 and small and exists(b - 1, 0):
                        invert_dense(b - 1)

            for_groups(dve, group, lead=2)
            if small:
                invert_dense(B - 1)
            else:
                for quarter in range(4):
                    invert(B - 1, groups - 1, quarter)

        @block.gpsimd
        def _(pool):
            pool.sem_inc(added, 4)

            def split_max(b, g):
                own = negative[:, g % 2, :]
                pool.wait_ge(negated, at(b, g, 1, 1))
                nc.gpsimd.tensor_tensor(max_parts[:, 1, :], own, max_parts[:, 0, :], ALU.subtract).then_inc(max_split, 1)
                nc.gpsimd.tensor_tensor(own, own, max_parts[:, 0, :], ALU.subtract).then_inc(max_split, 1)
                pool.wait_ge(max_split, at(b, g, 2, 2))
                nc.gpsimd.tensor_tensor(max_parts[:, 2, :], own, max_parts[:, 1, :], ALU.subtract).then_inc(row_made, 1)

            def add_weights(b, g, i):
                pool.wait_ge(exp_done, at(b, g, NS, (i + 1) * heads + 3))
                total = weight_sums[:, g % 2, :, :]
                own, before = (weights[:, x:x + heads, :] for x in ((g * NS + i * heads) % WEIGHTS, (g * NS + (i - 1) * heads) % WEIGHTS))
                if i == 1:
                    pool.wait_ge(normed, at(b, g, 1, SUMS - 1))
                    nc.gpsimd.tensor_tensor(total, before, own, ALU.add).then_inc(added, 2)
                else:
                    pool.wait_ge(added, at(b, g, nkt, i + 4))
                    nc.gpsimd.tensor_tensor(total, total, own, ALU.add).then_inc(added, 1)

            def normalise(b, g):
                if small:
                    own, sums_of, inverse_of = att[:, g, bass.ds(b * nq, nq)], att[:, g, bass.ds(b * nq, nq)], inverse[:, g, :]
                    pool.wait_ge(inverses_in, 16 * heads * (b + 1) + 1)
                else:
                    own, sums_of, inverse_of = att(g)[:, bass.ds(b * nq, nq)], sums[:, g % SUMS, :], inverse[:, :]
                    pool.wait_ge(inverted, at(b, g, 4, 8))
                nc.gpsimd.tensor_tensor(own, sums_of, inverse_of, ALU.mult).then_inc(normed, 1)

            split_max(0, 0)

            def group(b, g):
                for i in range(nkt):
                    if i and not small:
                        add_weights(b, g, i)
                    if i == 0 and exists(*later(b, g, 1)):
                        split_max(*later(b, g, 1))
                    if not small and i == 5 and exists(*later(b, g, -1)):
                        normalise(*later(b, g, -1))
                if small and g >= 2 and exists(b - 1, 0):
                    normalise(b - 1, 2 * g - 4)
                    normalise(b - 1, 2 * g - 3)

            for_groups(pool, group, lead=groups, turns=B - 2)
            for g in range(groups if small else 1):
                normalise(*(B - 1, g) if small else (B - 1, groups - 1))


def residual_norm_stage(k, products, bias=None, weights=(), x_scale=1.0, y_scale=1.0, value_bias=None, out=None, rows=None, relu=False):
    nc = k.nc
    n = k.stages
    with (
        nc.sbuf_tensor(f"rn_z_{n}", [P, NT, C], F32) as z,
        nc.sbuf_tensor(f"rn_stats_{n}", [P, NT, 6], F32) as stats,
        nc.sbuf_tensor(f"rn_mean_var_{n}", [P, NT, 2], F32) as mean_var,
        nc.sbuf_tensor(f"rn_rstd_{n}", [P, 2, NT], F32) as rstd,
        k.stage("weights", "biased", "prepared", "y_ready", "z_ready", "stats", "aggregated", "deviation", "inverse",
                "normed", "turned", "copied", "stored") as (
            weights_in, biased, prepared, y_ready, z_ready, stats_ready, aggregated, deviation, inverted, normed,
            turned, copied, stored),
        nc.Block() as block,
    ):
        @block.sync
        def _(sync):
            k.clear_last_set(sync)
            for tile, source in weights:
                sync.dma_start(tile, source).then_inc(weights_in, 16)
            if out is not None:
                for t in range(0, NT, 4):
                    sync.wait_ge(normed, t + 4)
                    sync.dma_start(out[t * P:(t + 4) * P, :].rearrange("(t p) c -> p t c", p=P), k.X[:, t:t + 4, :]).then_inc(stored, 16)
                sync.wait_ge(stored, 16 * (NT // 4))

        @block.gpsimd
        def _(pool):
            if bias is not None:
                pool.wait_ge(weights_in, 16 * len(weights))
            for t in range(NT if not relu else 0):
                if x_scale != 1.0:
                    nc.gpsimd.tensor_scalar(z[:, t, :], k.X[:, t, :], x_scale, None, ALU.mult).then_inc(biased, 1)
                    pool.wait_ge(biased, t + 1)
                    ins = nc.gpsimd.tensor_tensor(z[:, t, :], z[:, t, :], bias, ALU.add)
                elif bias is not None:
                    ins = nc.gpsimd.tensor_tensor(z[:, t, :], k.X[:, t, :], bias, ALU.add)
                elif rows is not None:
                    ins = nc.gpsimd.tensor_tensor(z[:, t, :], k.X[:, t, :], rows(t), ALU.add)
                else:
                    ins = nc.gpsimd.tensor_copy(z[:, t, :], k.X[:, t, :])
                ins.then_inc(prepared, 1)

        @block.tensor
        def _(pe):
            pe.wait_ge(weights_in, 16 * len(weights))
            if value_bias is not None:
                pe.wait_ge(biased, NG)
            for t in range(NT if rows is None else 0):
                if t >= 4:
                    pe.wait_ge(z_ready, t - 3)
                for i, (lhsT, rhs) in enumerate(products):
                    mm = nc.tensor.matmul(k.ps[:, t % 4, 0:C], lhsT(t), rhs, start=i == 0, stop=i == len(products) - 1)
                mm.then_inc(y_ready, 1)
            if out is None:
                for t in range(NT):
                    pe.wait_ge(normed, t + 1)
                    if t >= 4:
                        pe.wait_ge(copied, t - 3)
                    for c in range(CH):
                        tr = nc.tensor.transpose(k.ps[:, 4 + t % 4, c * P:(c + 1) * P], k.X[:, t, c * P:(c + 1) * P], k.ident[:, :])
                    tr.then_inc(turned, 1)

        @block.vector
        def _(dve):
            if value_bias is not None:
                dve.wait_ge(weights_in, 16 * len(weights))
                for g in range(NG):
                    nc.vector.tensor_scalar(value_bias[0][:, g, :], value_bias[0][:, g, :], value_bias[1][:, g:g + 1], None,
                                            ALU.add).then_inc(biased, 1)
            for t in range(NT + 2):
                if t < NT and relu:
                    if t == 0:
                        dve.wait_ge(weights_in, 16 * len(weights))
                    dve.wait_ge(y_ready, t + 1)
                    nc.vector.tensor_tensor(z[:, t, :], k.ps[:, t % 4, 0:C], bias, ALU.add).then_inc(prepared, 1)
                    dve.wait_ge(prepared, t + 1)
                    nc.vector.scalar_tensor_tensor(z[:, t, :], z[:, t, :], 0.0, k.X[:, t, :], ALU.max, ALU.add).then_inc(z_ready, 1)
                elif t < NT and rows is None:
                    dve.wait_ge(prepared, t + 1)
                    dve.wait_ge(y_ready, t + 1)
                    nc.vector.scalar_tensor_tensor(z[:, t, :], k.ps[:, t % 4, 0:C], y_scale, z[:, t, :], ALU.mult, ALU.add).then_inc(z_ready, 1)
                if 1 <= t <= NT:
                    if rows is None:
                        dve.wait_ge(z_ready, t)
                    else:
                        dve.wait_ge(prepared, t)
                    nc.vector.bn_stats(stats[:, t - 1, :], z[:, t - 1, :]).then_inc(stats_ready, 1)
                if t >= 2:
                    dve.wait_ge(stats_ready, t - 1)
                    nc.vector.bn_aggr(mean_var[:, t - 2, :], stats[:, t - 2, :]).then_inc(aggregated, 1)
            dve.wait_ge(deviation, 1)
            nc.vector.reciprocal(rstd[:, 1, :], rstd[:, 0, :]).then_inc(inverted, 1)
            dve.wait_ge(inverted, 1)
            for t in range(NT):
                nc.vector.tensor_scalar(k.X[:, t, :], z[:, t, :], mean_var[:, t, 0:1], rstd[:, 1, t:t + 1], ALU.subtract,
                                        ALU.mult).then_inc(normed, 1)

        @block.scalar
        def _(act):
            act.wait_ge(aggregated, NT)
            nc.scalar.activation(rstd[:, 0, :], mean_var[:, :, 1], ACT.Sqrt, bias=k.eps[0]).then_inc(deviation, 1)
            if out is None:
                for t in range(NT):
                    act.wait_ge(turned, t + 1)
                    nc.scalar.activation(k.xT[:, :, t * P:(t + 1) * P], k.ps[:, 4 + t % 4, 0:C].rearrange("p (c n) -> p c n", c=CH),
                                         ACT.Copy).then_inc(copied, 1)


def merge_levels_stage(k, lvl, att, up, out_w, up_w, out_b, up_b, up_next, weights, value_bias):
    nc = k.nc
    s_l = S >> lvl
    n = B * s_l
    wide = min(n, BANK)
    parts = [(m, w) for m in range(CH) for w in range(n // wide)]
    with (
        nc.sbuf_tensor(f"current_{lvl}", [P, CH, B, s_l], F32) as current,
        nc.sbuf_tensor(f"quarter_{lvl}", [P, CH * B, s_l], F32) as quarter,
        nc.sbuf_tensor(f"level_bias_{lvl}", [P, CH], F32) as level_bias,
        k.stage("weights", "values_biased", "bias_sum", "ready", "summed", "quartered", "upsampled") as (
            weights_in, values_biased, bias_sum, ready, summed, quartered, upsampled),
        nc.Block(no_gpsimd_drain=True) as block,
    ):
        flat = current[:].rearrange("p c b s -> p c (b s)")
        rows = current[:].rearrange("p c b s -> p (c b) s")
        fine = up_next[:].rearrange("p c b (s two) -> p (c b) s two", two=2)

        @block.sync
        def _(sync):
            k.clear_last_set(sync)
            for tile, source in weights:
                sync.dma_start(tile, source).then_inc(weights_in, 16)

        @block.tensor
        def _(pe):
            pe.wait_ge(weights_in, 16 * len(weights))
            pe.wait_ge(values_biased, NG)
            for i, (m, w) in enumerate(parts):
                cols, chan = slice(w * wide, (w + 1) * wide), slice(m * P, (m + 1) * P)
                batches = slice(w * wide // s_l, (w + 1) * wide // s_l)
                terms = [(out_w[:, g, chan], att[:, g, batches, :]) for g in range(NG)]
                if up is not None:
                    terms += [(up_w[:, c, chan], up[:].rearrange("p c b s -> p c (b s)")[:, c, cols]) for c in range(CH)]
                for a, (lhsT, rhs) in enumerate(terms):
                    mm = nc.tensor.matmul(k.ps[:, i, 0:wide], lhsT, rhs, start=a == 0, stop=a == len(terms) - 1)
                mm.then_inc(ready, 1)

        @block.vector
        def _(dve):
            dve.wait_ge(weights_in, 16 * len(weights))
            for g in range(NG):
                nc.vector.tensor_scalar(att[:, g, :, :], att[:, g, :, :], value_bias[:, g:g + 1], None, ALU.add).then_inc(values_biased, 1)
            if up is None:
                nc.vector.tensor_copy(level_bias[:], out_b).then_inc(bias_sum, 1)
            else:
                nc.vector.tensor_tensor(level_bias[:], out_b, up_b, ALU.add).then_inc(bias_sum, 1)
            dve.wait_ge(bias_sum, 1)
            for i, (m, w) in enumerate(parts):
                dve.wait_ge(ready, i + 1)
                nc.vector.tensor_scalar(flat[:, m, w * wide:(w + 1) * wide], k.ps[:, i, 0:wide], level_bias[:, m:m + 1], None,
                                        ALU.add).then_inc(summed, 1)
            dve.wait_ge(summed, len(parts))
            nc.vector.tensor_scalar(quarter[:], rows, 0.25, None, ALU.mult).then_inc(quartered, 1)
            nc.vector.tensor_copy(fine[:, :, 0:1, 0], rows[:, :, 0:1])
            nc.vector.tensor_copy(fine[:, :, s_l - 1:s_l, 1], rows[:, :, s_l - 1:s_l])
            dve.wait_ge(quartered, 1)
            nc.vector.scalar_tensor_tensor(fine[:, :, 1:s_l, 0], rows[:, :, 1:s_l], 0.75, quarter[:, :, 0:s_l - 1], ALU.mult, ALU.add)
            nc.vector.scalar_tensor_tensor(fine[:, :, 0:s_l - 1, 1], rows[:, :, 0:s_l - 1], 0.75, quarter[:, :, 1:s_l], ALU.mult,
                                           ALU.add).then_inc(upsampled, 1)


def pyramid_attention(k):
    nc, inp = k.nc, k.inp
    with ExitStack() as held:
        def sb(what, shape, dt=F32):
            return held.enter_context(nc.sbuf_tensor(f"pyr_{what}", shape, dt))

        att, att_coarse = sb("att", [P, NG, T]), sb("att_coarse", [P, NG, T])
        place = {1: 0, 2: 256, 3: 384}
        bias = sb("bias", [P, 4, 3 * CH])
        vbias = sb("vbias", [P, 4, NG])
        q_coarse, k_coarse = (nc.dram_tensor(n, [C, 6, T], BF16, kind="Internal").ap() for n in ("q_coarse", "k_coarse"))
        v_coarse = nc.dram_tensor("v_coarse", [B * 4, P, H * QUAD], F32, kind="Internal").ap()
        q_parts, k_parts, values = k.q_parts[:, :, 0:T], k.k_parts[:, :, 0:T], k.values_of(NT, P)
        xs = k.xT[:].rearrange("p c (b s) -> p c b s", b=B)
        with nc.sbuf_tensor("pyr_wqkv", [P, 4, CH, 3 * C], F32) as w, nc.sbuf_tensor("pyr_zeros", [P, H * QUAD], F32) as zeros:
            memset_stage(k, (zeros[:], 0.0))
            units = []
            for store, col, order in ((q_parts, 0, Q_PART), (k_parts, C, K_PART)):
                units += split_units(lambda c, t: k.xT[:, c, t * BANK:(t + 1) * BANK], BANK, w[:, 0, :, col:col + C], bias[:, 0, col // P:col // P + CH],
                                     store, order)
            units += value_units(lambda c, t: k.xT[:, c, t * P:(t + 1) * P], P, w[:, 0, :, 2 * C:], values)
            levels = (1, 2, 3)
            cols = {lvl: slice(place[lvl], place[lvl] + max(S >> lvl, P)) for lvl in levels}

            def tokens(lvl, c, b):
                own = xs[:, c, b, ::1 << lvl]
                return own if S >> lvl >= P else own.unsqueeze(1).broadcast_to((P, P // (S >> lvl), S >> lvl))

            for store, col, order in ((q_coarse, 0, Q_PART), (k_coarse, C, K_PART)):
                units += [("split", [(cols[lvl], w[:, lvl, c, col + m * P:col + (m + 1) * P], tokens(lvl, c, b), c == 0, c == CH - 1)
                                     for lvl in levels for c in range(CH)], S,
                           [(cols[lvl], bias[:, lvl, col // P + m:col // P + m + 1]) for lvl in levels],
                           stacked(store[m * P:(m + 1) * P, :, b * S:(b + 1) * S], order)) for b in range(B) for m in range(CH)]
            for lvl in levels:
                n = min(S >> lvl, P)

                def rows(c, t, lvl=lvl, n=n):
                    b, i = divmod(t, (S >> lvl) // n)
                    return xs[:, c, b, (i * n) << lvl:((i + 1) * n) << lvl:1 << lvl]

                tiles = [v_coarse[b * 4 + place[lvl] // P + i, 0:n, :] for b in range(B) for i in range((S >> lvl) // n)]
                units += value_units(rows, n, w[:, lvl, :, 2 * C:], tiles)
            project_stage(k, units, [(w[:, 0], inp["L0_in_w"][0]), (bias[:], inp["L0_in_b"]), (vbias[:], inp["L0_v_b"])]
                          + [(w[:, lvl], inp["L0_in_w"][lvl]) for lvl in (1, 2, 3)],
                          [(v_coarse[b * 4 + 3, S >> 3:P, :], zeros[S >> 3:P, :]) for b in range(B)])
        attention_stage(k, "pyr_core", q_parts, k_parts, values, S, S, HD ** -0.5, att)
        attention_stage(k, "pyr_coarse", q_coarse, k_coarse, v_coarse, S, S, HD ** -0.5, att_coarse,
                        spans=[slice(0, 256), slice(0, 256), slice(256, 384), slice(384, 512)])
        coarse = att_coarse[:].rearrange("p g (b s) -> p g b s", b=B)
        up = [None] + [sb(f"up{lvl}", [P, CH, B, S >> (lvl - 1)]) for lvl in (3, 2, 1)]
        out_b, up_b = sb("out_b", [P, 4, CH]), sb("up_b", [P, 3, CH])
        for i, lvl in enumerate((3, 2, 1)):
            with nc.sbuf_tensor(f"pyr_out_w{lvl}", [P, NG, C], F32) as ow, nc.sbuf_tensor(f"pyr_up_w{lvl}", [P, CH, C], F32) as uw:
                loads = [(ow[:], inp["L0_out_w"][lvl])]
                if lvl < 3:
                    loads.append((uw[:], inp["L0_up_w"][lvl]))
                else:
                    loads += [(out_b[:], inp["L0_out_b"]), (up_b[:], inp["L0_up_b"])]
                merge_levels_stage(k, lvl, coarse[:, :, :, place[lvl]:place[lvl] + (S >> lvl)], up[i], ow, uw, out_b[:, lvl, :], up_b[:, min(lvl, 2), :], up[i + 1],
                                   loads, vbias[:, lvl, :])
        with nc.sbuf_tensor("pyr_out_w0", [P, NG, C], F32) as ow, nc.sbuf_tensor("pyr_up_w0", [P, CH, C], F32) as uw, \
                nc.sbuf_tensor("pyr_rows", [P, 2, C], F32) as rows:
            add_rows_stage(k, rows, inp["L0_out_b0_up_b0"])
            fine = up[3][:].rearrange("p c b s -> p c (b s)")
            products = [(lambda t, g=g: att[:, g, t * P:(t + 1) * P], ow[:, g, :]) for g in range(NG)]
            products += [(lambda t, c=c: fine[:, c, t * P:(t + 1) * P], uw[:, c, :]) for c in range(CH)]
            residual_norm_stage(k, products, rows[:, 0, :], [(ow[:], inp["L0_out_w"][0]), (uw[:], inp["L0_up_w"][0])],
                                value_bias=(att, vbias[:, 0, :]))


def add_rows_stage(k, rows, source):
    nc = k.nc
    with k.stage("loaded", "added") as (loaded, added), nc.Block(no_gpsimd_drain=True) as block:
        @block.sync
        def _(sync):
            k.clear_last_set(sync)
            sync.dma_start(rows[:], source.partition_broadcast(P)).then_inc(loaded, 16)

        @block.vector
        def _(dve):
            dve.wait_ge(loaded, 16)
            nc.vector.tensor_tensor(rows[:, 0, :], rows[:, 0, :], rows[:, 1, :], ALU.add).then_inc(added, 1)


def self_or_cross_attention(k, name, source, weights, nk, slopes=None):
    nc, inp = k.nc, k.inp
    w_name, b_name, out_name, out_b, v_b = weights
    with nc.sbuf_tensor(f"{name}_att", [P, NG, T], F32) as att, nc.sbuf_tensor(f"{name}_vb", [P, NG], F32) as vb:
        q_parts, k_parts, values = k.q_parts[:, :, 0:T], k.k_parts[:, :, 0:B * nk], k.values_of(B * nk // P, P)
        with nc.sbuf_tensor(f"{name}_w", [P, CH, 3 * C], F32) as w, nc.sbuf_tensor(f"{name}_b", [P, 2 * CH], F32) as bias, \
                nc.sbuf_tensor(f"{name}_src", [P, CH, TC if source is None else 1], F32) as ctxT:
            loads = [(w[:], inp[w_name])]
            if source is None:
                source = ctxT
                loads.append((ctxT[:], inp["ctxT"]))
            if b_name:
                loads += [(bias[:], inp[b_name]), (vb[:], inp[v_b])]
            project_stage(
                k, split_units(lambda c, t: k.xT[:, c, t * BANK:(t + 1) * BANK], BANK, w[:, :, 0:C],
                               bias[:, 0:CH] if b_name else None, q_parts, Q_PART)
                + split_units(lambda c, t: source[:, c, t * BANK:(t + 1) * BANK], BANK, w[:, :, C:2 * C],
                              bias[:, CH:] if b_name else None, k_parts, K_PART)
                + value_units(lambda c, t: source[:, c, t * P:(t + 1) * P], P, w[:, :, 2 * C:], values), loads)
        attention_stage(k, f"{name}_core", q_parts, k_parts, values, S, nk, HD ** -0.5, att, slopes=slopes)
        with nc.sbuf_tensor(f"{name}_ow", [P, NG, C], F32) as ow, nc.sbuf_tensor(f"{name}_ob", [P, C], F32) as ob:
            residual_norm_stage(k, [(lambda t, g=g: att[:, g, t * P:(t + 1) * P], ow[:, g, :]) for g in range(NG)], ob[:],
                                [(ow[:], inp[out_name]), (ob[:], inp[out_b].partition_broadcast(P))],
                                value_bias=(att, vb) if b_name else None)


def norm_rows_stage(k, tiles, dest, gamma, beta, eps, products=None, source=None, add=None, relu_eps=None, row_scale=None,
                    destT=None, weights=()):
    nc = k.nc
    n = k.stages
    with (
        nc.sbuf_tensor(f"nr_z_{n}", [P, tiles if source is None else 1, C], F32) as z,
        nc.sbuf_tensor(f"nr_stats_{n}", [P, tiles, 6], F32) as stats,
        nc.sbuf_tensor(f"nr_mean_var_{n}", [P, tiles, 2], F32) as mean_var,
        nc.sbuf_tensor(f"nr_rstd_{n}", [P, 2, tiles], F32) as rstd,
        k.stage("weights", "y_ready", "z_ready", "stats", "aggregated", "deviation", "inverse", "centred", "normed",
                "clipped", "scaled", "turned", "copied") as (
            weights_in, y_ready, z_ready, stats_ready, aggregated, deviation, inverted, centred, normed, clipped, scaled,
            turned, copied),
        nc.Block() as block,
    ):
        def rows(t):
            return z[:, t, :] if source is None else source(t)

        done = scaled if row_scale is not None else clipped if relu_eps is not None else normed

        @block.sync
        def _(sync):
            k.clear_last_set(sync)
            for tile, src in weights:
                sync.dma_start(tile, src).then_inc(weights_in, 16)

        @block.tensor
        def _(pe):
            if products is not None:
                pe.wait_ge(weights_in, 16 * len(weights))
                for t in range(tiles):
                    if t >= 4:
                        pe.wait_ge(z_ready, t - 3)
                    for i, (lhsT, rhs) in enumerate(products):
                        mm = nc.tensor.matmul(k.ps[:, t % 4, 0:C], lhsT(t), rhs, start=i == 0, stop=i == len(products) - 1)
                    mm.then_inc(y_ready, 1)
            if destT is not None:
                for t in range(tiles):
                    pe.wait_ge(done, t + 1)
                    if t >= 4:
                        pe.wait_ge(copied, t - 3)
                    for c in range(CH):
                        tr = nc.tensor.transpose(k.ps[:, 4 + t % 4, c * P:(c + 1) * P], dest(t)[:, c * P:(c + 1) * P], k.ident[:, :])
                    tr.then_inc(turned, 1)

        @block.vector
        def _(dve):
            dve.wait_ge(weights_in, 16 * len(weights))
            for t in range(tiles + 2):
                if t < tiles and products is not None:
                    dve.wait_ge(y_ready, t + 1)
                    if add is None:
                        nc.vector.tensor_copy(z[:, t, :], k.ps[:, t % 4, 0:C]).then_inc(z_ready, 1)
                    else:
                        nc.vector.tensor_tensor(z[:, t, :], k.ps[:, t % 4, 0:C], add(t), ALU.add).then_inc(z_ready, 1)
                if 1 <= t <= tiles:
                    if products is not None:
                        dve.wait_ge(z_ready, t)
                    nc.vector.bn_stats(stats[:, t - 1, :], rows(t - 1)).then_inc(stats_ready, 1)
                if t >= 2:
                    dve.wait_ge(stats_ready, t - 1)
                    nc.vector.bn_aggr(mean_var[:, t - 2, :], stats[:, t - 2, :]).then_inc(aggregated, 1)
            dve.wait_ge(deviation, 1)
            nc.vector.reciprocal(rstd[:, 1, :], rstd[:, 0, :]).then_inc(inverted, 1)
            dve.wait_ge(inverted, 1)
            for t in range(tiles + 1):
                if t < tiles:
                    nc.vector.scalar_tensor_tensor(dest(t), rows(t), mean_var[:, t, 0:1], gamma, ALU.subtract, ALU.mult).then_inc(centred, 1)
                if t:
                    dve.wait_ge(centred, t)
                    nc.vector.scalar_tensor_tensor(dest(t - 1), dest(t - 1), rstd[:, 1, t - 1:t], beta, ALU.mult, ALU.add).then_inc(normed, 1)

        @block.scalar
        def _(act):
            act.wait_ge(aggregated, tiles)
            nc.scalar.activation(rstd[:, 0, :], mean_var[:, :, 1], ACT.Sqrt, bias=eps).then_inc(deviation, 1)
            if destT is not None:
                for t in range(tiles):
                    act.wait_ge(turned, t + 1)
                    nc.scalar.activation(destT(t), k.ps[:, 4 + t % 4, 0:C].rearrange("p (c n) -> p c n", c=CH), ACT.Copy).then_inc(copied, 1)

        @block.gpsimd
        def _(pool):
            if row_scale is not None:
                pool.wait_ge(weights_in, 16 * len(weights))
            for t in range(tiles):
                if relu_eps is not None:
                    pool.wait_ge(normed, t + 1)
                    nc.gpsimd.tensor_scalar(dest(t), dest(t), 0.0, relu_eps, ALU.max, ALU.add).then_inc(clipped, 1)
                if row_scale is not None:
                    if relu_eps is not None:
                        pool.wait_ge(clipped, t + 1)
                    else:
                        pool.wait_ge(normed, t + 1)
                    nc.gpsimd.tensor_scalar(dest(t), dest(t), row_scale(t), None, ALU.mult).then_inc(scaled, 1)


def linear_attention_stage(k, keys, values, queryT, att, key_tiles, den_eps=None, attT=None, regroup=None):
    nc = k.nc
    n = k.stages
    with (
        nc.sbuf_tensor(f"la_state_{n}", [P, B, CH, P], F32) as state,
        nc.sbuf_tensor(f"la_sums_{n}", [P, B, CH, 2], F32) as sums,
        nc.sbuf_tensor(f"la_sum_cols_{n}", [P, B, CH, H], F32) as sum_cols,
        nc.sbuf_tensor(f"la_den_{n}", [P, NT, 2, H], F32) as den,
        k.stage("state_ready", "summed", "state_taken", "ready", "shifted", "inverse", "taken", "turned", "copied", "stored",
                "regrouped") as (state_ready, summed, state_taken, ready, shifted, inverted, taken, turned, copied, stored, regrouped),
        nc.Block(no_gpsimd_drain=True) as block,
    ):
        pairs = [(b, m) for b in range(B) for m in range(CH)]
        per_pair = 1 if den_eps is None else 2

        @block.sync
        def _(sync):
            k.clear_last_set(sync)
            if regroup is not None:
                per = NT // B
                for t in range(NT):
                    sync.wait_ge(taken, t + 1)
                    sync.dma_start(regroup[t // per, :, t % per * P:(t % per + 1) * P, :].rearrange("h n e -> n h e"),
                                   att(t).rearrange("p (h e) -> p h e", h=H)).then_inc(stored, 16)
                sync.wait_ge(stored, 16 * NT)
                flat = regroup.rearrange("b h n e -> (b h n e)").rearrange("(t p c) -> t p c", p=P, c=C)
                for t in range(NT):
                    sync.dma_start(att(t), flat[t]).then_inc(regrouped, 16)

        @block.tensor
        def _(pe):
            for n, (b, m) in enumerate(pairs):
                if n >= 4:
                    pe.wait_ge(state_taken, per_pair * (n - 3))
                for i in range(key_tiles):
                    t = b * key_tiles + i
                    mm = nc.tensor.matmul(k.ps[:, n % 4, 0:C + 1], keys(t)[:, m * P:(m + 1) * P], values(t), start=i == 0,
                                          stop=i == key_tiles - 1)
                mm.then_inc(state_ready, 1)
            pe.wait_ge(state_taken, per_pair * len(pairs))
            for t in range(NT):
                b = t // (NT // B)
                if t >= 4:
                    pe.wait_ge(taken, t - 3)
                for m in range(CH):
                    q = queryT[:, m, t * P:(t + 1) * P]
                    mm = nc.tensor.matmul(k.ps[:, 4 + t % 4, m * P:(m + 1) * P], q, state[:, b, m, :], start=m == 0, stop=den_eps is None,
                                          skip_group_check=True)
                    if den_eps is not None:
                        mm = nc.tensor.matmul(k.ps[:, 4 + t % 4, C:C + H], q, sum_cols[:, b, m, :], start=False, stop=m == CH - 1,
                                              skip_group_check=True)
                mm.then_inc(ready, 1)
            if attT is not None:
                if regroup is not None:
                    pe.wait_ge(regrouped, 16 * NT)
                for t in range(NT):
                    pe.wait_ge(taken, t + 1)
                    if t >= 4:
                        pe.wait_ge(copied, t - 3)
                    for c in range(CH):
                        tr = nc.tensor.transpose(k.ps[:, t % 4, c * P:(c + 1) * P], att(t)[:, c * P:(c + 1) * P], k.ident[:, :])
                    tr.then_inc(turned, 1)

        @block.vector
        def _(dve):
            for n, (b, m) in enumerate(pairs):
                dve.wait_ge(state_ready, n + 1)
                nc.vector.tensor_copy(sums[:, b, m, 0:1], k.ps[:, n % 4, C:C + 1]).then_inc(summed, 1)
                dve.wait_ge(summed, 2 * n + 1)
                if den_eps is None:
                    nc.vector.reciprocal(sums[:, b, m, 1:2], sums[:, b, m, 0:1]).then_inc(summed, 1)
                    dve.wait_ge(summed, 2 * n + 2)
                    nc.vector.scalar_tensor_tensor(state[:, b, m, :], k.ps[:, n % 4, m * P:(m + 1) * P], sums[:, b, m, 1:2],
                                                   k.head_blocks[:, :], ALU.mult, ALU.mult).then_inc(state_taken, 1)
                else:
                    nc.vector.tensor_scalar(sum_cols[:, b, m, :], k.head_cols[:, m, :], sums[:, b, m, 0:1], None, ALU.mult).then_inc(summed, 1)
                    nc.vector.tensor_tensor(state[:, b, m, :], k.ps[:, n % 4, m * P:(m + 1) * P], k.head_blocks[:, :], ALU.mult).then_inc(state_taken, 2)
            if den_eps is not None:
                dve.wait_ge(summed, 2 * len(pairs))
            for t in range(NT):
                dve.wait_ge(ready, t + 1)
                if den_eps is None:
                    nc.vector.tensor_copy(att(t), k.ps[:, 4 + t % 4, 0:C]).then_inc(taken, 1)
                else:
                    nc.vector.tensor_scalar(den[:, t, 0, :], k.ps[:, 4 + t % 4, C:C + H], den_eps, None, ALU.add).then_inc(shifted, 1)
                    dve.wait_ge(shifted, t + 1)
                    nc.vector.reciprocal(den[:, t, 1, :], den[:, t, 0, :]).then_inc(inverted, 1)
                    dve.wait_ge(inverted, t + 1)
                    nc.vector.tensor_tensor(att(t).rearrange("p (h d) -> p h d", h=H), k.ps[:, 4 + t % 4, 0:C].rearrange("p (h d) -> p h d", h=H),
                                            den[:, t, 1, :].unsqueeze(2).broadcast_to((P, H, HD)), ALU.mult).then_inc(taken, 1)

        @block.scalar
        def _(act):
            if attT is not None:
                for t in range(NT):
                    act.wait_ge(turned, t + 1)
                    nc.scalar.activation(attT(t), k.ps[:, t % 4, 0:C].rearrange("p (c n) -> p c n", c=CH), ACT.Copy).then_inc(copied, 1)


def memset_stage(k, *tiles):
    nc = k.nc
    with k.stage("filled") as (filled,), nc.Block(no_gpsimd_drain=True) as block:
        @block.sync
        def _(sync):
            k.clear_last_set(sync)

        @block.vector
        def _(dve):
            for tile, value in tiles:
                nc.vector.memset(tile, value).then_inc(filled, 1)


def add_norm_stage(k, y):
    residual_norm_stage(k, None, rows=y)


def relu_kernel_attention(k):
    nc, inp = k.nc, k.inp
    with ExitStack() as held:
        def sb(what, shape):
            return held.enter_context(nc.sbuf_tensor(f"rk_{what}", shape, F32))

        gain, mask = sb("gain", [P, 3, C]), sb("mask", [P, NTC])
        w = sb("w", [P, 4, CH, C])
        qT, y = sb("qT", [P, CH, T]), sb("y", [P, NT, C])
        gamma, beta = gain[:, 0, :], gain[:, 1, :]
        with nc.sbuf_tensor("rk_keys", [P, NTC, C], F32) as keys, nc.sbuf_tensor("rk_values", [P, NTC, C + 1], F32) as values, \
                nc.sbuf_tensor("rk_ctxT", [P, CH, TC], F32) as ctxT:
            loads = [(ctxT[:], inp["ctxT"]), (w[:], inp["L0x_w"]), (gain[:], inp["L0x_rows"].partition_broadcast(P)), (mask[:], inp["mask_tokens"])]

            def ctx(c):
                return lambda t: ctxT[:, c, t * P:(t + 1) * P]

            memset_stage(k, (values[:, :, C:C + 1], 1.0))
            norm_rows_stage(k, NTC, lambda t: keys[:, t, :], gamma, beta, k.eps[1], [(ctx(c), w[:, 1, c, :]) for c in range(CH)],
                            relu_eps=1e-6, row_scale=lambda t: mask[:, t:t + 1], weights=loads)
            norm_rows_stage(k, NTC, lambda t: values[:, t, 0:C], gamma, beta, k.eps[1], [(ctx(c), w[:, 2, c, :]) for c in range(CH)],
                            row_scale=lambda t: mask[:, t:t + 1])
            norm_rows_stage(k, NT, lambda t: y[:, t, :], gamma, beta, k.eps[1],
                            [(lambda t, c=c: k.xT[:, c, t * P:(t + 1) * P], w[:, 0, c, :]) for c in range(CH)],
                            relu_eps=1e-6, destT=lambda t: qT[:, :, t * P:(t + 1) * P])
            linear_attention_stage(k, lambda t: keys[:, t, :], lambda t: values[:, t, :], qT, lambda t: y[:, t, :], NTC // B,
                                   den_eps=1e-6, attT=lambda t: qT[:, :, t * P:(t + 1) * P], regroup=k.regroup)
        norm_rows_stage(k, NT, lambda t: y[:, t, :], gamma, beta, k.eps[1],
                        [(lambda t, c=c: qT[:, c, t * P:(t + 1) * P], w[:, 3, c, :]) for c in range(CH)], add=lambda t: gain[:, 2, :])
        add_norm_stage(k, lambda t: y[:, t, :])


def softmax_features_stage(k, w, rows, k_bias, queries, qT, keys, values, loads):
    nc = k.nc
    n_k = CH * B
    with (
        nc.sbuf_tensor("sf_keysT", [P, CH, T], F32) as keysT,
        nc.sbuf_tensor("sf_top", [P, 2, n_k], F32) as top,
        nc.sbuf_tensor("sf_head", [P, 3, NT * H], F32) as head,
        k.stage("weights", "ready", "taken", "k_top", "k_exp", "q_top", "q_shifted", "q_exp", "q_sum", "q_inverse",
                "q_done", "turned", "copied") as (weights_in, ready, taken, k_top, k_exp, q_top, q_shifted, q_exp, q_sum, q_inverse,
                                                  q_done, turned, copied),
        nc.Block() as block,
    ):
        units = [("q", t) for t in range(NT)] + [("k", u) for u in range(n_k)] + [("v", t) for t in range(NT)]
        heads = queries[:].rearrange("p t (h d) -> p (t h) d", d=HD)
        turns = [("q", t) for t in range(NT)] + [("k", t) for t in range(NT)]

        def spread(i):
            return head[:, i, :].unsqueeze(2).broadcast_to((P, NT * H, HD))

        @block.sync
        def _(sync):
            k.clear_last_set(sync)
            for tile, src in loads:
                sync.dma_start(tile, src).then_inc(weights_in, 16)

        @block.tensor
        def _(pe):
            pe.wait_ge(weights_in, 16 * len(loads))
            for n, (kind, i) in enumerate(units):
                if n >= 4:
                    pe.wait_ge(taken, n - 3)
                for c in range(CH):
                    if kind == "k":
                        m, b = divmod(i, B)
                        out, lhsT, rhs = k.ps[:, n % 4, :], w[:, 1, c, m * P:(m + 1) * P], k.xT[:, c, b * S:(b + 1) * S]
                    else:
                        out, lhsT = k.ps[:, n % 4, 0:C], k.xT[:, c, i * P:(i + 1) * P]
                        rhs = w[:, 0 if kind == "q" else 2, c, :]
                    mm = nc.tensor.matmul(out, lhsT, rhs, start=c == 0, stop=c == CH - 1)
                mm.then_inc(ready, 1)
            pe.wait_ge(q_done, 1)
            for n, (kind, t) in enumerate(turns):
                if kind == "k" and t == 0:
                    pe.wait_ge(k_exp, n_k)
                if n >= 4:
                    pe.wait_ge(copied, n - 3)
                for c in range(CH):
                    src = queries[:, t, c * P:(c + 1) * P] if kind == "q" else keysT[:, c, t * P:(t + 1) * P]
                    tr = nc.tensor.transpose(k.ps[:, 4 + n % 4, c * P:(c + 1) * P], src, k.ident[:, :])
                tr.then_inc(turned, 1)

        @block.vector
        def _(dve):
            dve.wait_ge(weights_in, 16 * len(loads))
            for n, (kind, i) in enumerate(units):
                dve.wait_ge(ready, n + 1)
                if kind == "q":
                    ins = nc.vector.tensor_tensor(queries[:, i, :], k.ps[:, n % 4, 0:C], rows[:, 0, :], ALU.add)
                elif kind == "k":
                    m, b = divmod(i, B)
                    ins = nc.vector.tensor_scalar(keysT[:, m, b * S:(b + 1) * S], k.ps[:, n % 4, :], k_bias[:, m:m + 1], None, ALU.add)
                else:
                    ins = nc.vector.tensor_tensor(values[:, i, 0:C], k.ps[:, n % 4, 0:C], rows[:, 1, :], ALU.add)
                ins.then_inc(taken, 1)
                if n == NT:
                    dve.wait_ge(taken, NT)
                    nc.vector.reduce_max(head[:, 0, :], heads, AX).then_inc(q_top, 1)
                if n == NT + n_k:
                    dve.wait_ge(taken, NT + n_k)
                    nc.vector.reduce_max(top[:, 0, :], keysT[:].rearrange("p c (b s) -> p (c b) s", b=B), AX).then_inc(k_top, 1)
                    dve.wait_ge(k_top, 1)
                    nc.vector.tensor_scalar(top[:, 1, :], top[:, 0, :], -1.0, None, ALU.mult).then_inc(k_top, 1)
            dve.wait_ge(q_exp, 1)
            nc.vector.reduce_sum(head[:, 1, :], heads, AX).then_inc(q_sum, 1)
            dve.wait_ge(q_sum, 1)
            nc.vector.reciprocal(head[:, 2, :], head[:, 1, :]).then_inc(q_inverse, 1)
            dve.wait_ge(q_inverse, 1)
            nc.vector.tensor_tensor(heads, heads, spread(2), ALU.mult).then_inc(q_done, 1)

        @block.gpsimd
        def _(pool):
            pool.wait_ge(q_top, 1)
            nc.gpsimd.tensor_tensor(heads, heads, spread(0), ALU.subtract).then_inc(q_shifted, 1)

        @block.scalar
        def _(act):
            act.wait_ge(q_shifted, 1)
            nc.scalar.activation(queries[:], queries[:], ACT.Exp).then_inc(q_exp, 1)
            act.wait_ge(k_top, 2)
            for u in range(n_k):
                m, b = divmod(u, B)
                part = keysT[:, m, b * S:(b + 1) * S]
                nc.scalar.activation(part, part, ACT.Exp, bias=top[:, 1, u:u + 1]).then_inc(k_exp, 1)
            for n, (kind, t) in enumerate(turns):
                act.wait_ge(turned, n + 1)
                dst = qT[:, :, t * P:(t + 1) * P] if kind == "q" else keys[:, t, :].rearrange("p (c n) -> p c n", c=CH)
                nc.scalar.activation(dst, k.ps[:, 4 + n % 4, 0:C].rearrange("p (c n) -> p c n", c=CH), ACT.Copy).then_inc(copied, 1)


def softmax_linear_attention(k):
    nc, inp = k.nc, k.inp
    with ExitStack() as held:
        def sb(what, shape):
            return held.enter_context(nc.sbuf_tensor(f"sl_{what}", shape, F32))

        w, rows, k_bias = sb("w", [P, 4, CH, C]), sb("rows", [P, 5, C]), sb("k_bias", [P, CH])
        qT, att = sb("qT", [P, CH, T]), sb("att", [P, NT, C])
        with nc.sbuf_tensor("sl_keys", [P, NT, C], F32) as keys, nc.sbuf_tensor("sl_values", [P, NT, C + 1], F32) as values:
            memset_stage(k, (values[:, :, C:C + 1], 1.0))
            softmax_features_stage(k, w, rows, k_bias, att, qT, keys, values,
                                   [(w[:], inp["L1a_w"]), (rows[:], inp["L1a_rows"].partition_broadcast(P)), (k_bias[:], inp["L1a_bk"])])
            linear_attention_stage(k, lambda t: keys[:, t, :], lambda t: values[:, t, :], qT, lambda t: att[:, t, :], NT // B)
        norm_rows_stage(k, NT, lambda t: att[:, t, :], rows[:, 2, :], rows[:, 3, :], k.eps[0], source=lambda t: att[:, t, :],
                        destT=lambda t: qT[:, :, t * P:(t + 1) * P])
        residual_norm_stage(k, [(lambda t, c=c: qT[:, c, t * P:(t + 1) * P], w[:, 3, c, :]) for c in range(CH)], rows[:, 4, :])


def context_attention(k):
    self_or_cross_attention(k, "l1x", None, ("L1x_w", "L1x_b", "L1x_out_w", "L1x_out_b", "L1x_v_b"), SC)


def plain_attention(k):
    self_or_cross_attention(k, "l2a", k.xT, ("L2a_w", None, "L2a_out_w", "L2a_out_b", None), S)


def alibi_attention(k):
    self_or_cross_attention(k, "l3a", k.xT, ("L3a_w", "L3a_b", "L3a_out_w", "L3a_out_b", "L3a_v_b"), S, slopes=k.inp["slopes"])


def first_of_maxima(nc, dve, done, count, e, top, rank, onehot, order):
    n = e.shape[2]

    def wide(col):
        return col.unsqueeze(2).broadcast_to((P, e.shape[1], n))

    nc.vector.reduce_max(top, e, AX).then_inc(done, 1)
    dve.wait_ge(done, count + 1)
    nc.vector.tensor_tensor(rank, e, wide(top), ALU.is_equal).then_inc(done, 1)
    dve.wait_ge(done, count + 2)
    nc.vector.tensor_tensor(rank, rank, order, ALU.mult).then_inc(done, 1)
    dve.wait_ge(done, count + 3)
    nc.vector.reduce_max(top, rank, AX).then_inc(done, 1)
    dve.wait_ge(done, count + 4)
    nc.vector.tensor_tensor(onehot, rank, wide(top), ALU.is_equal).then_inc(done, 1)
    dve.wait_ge(done, count + 5)
    return count + 5


def top1_ffn(k):
    nc, inp = k.nc, k.inp
    E, F = 8, 1024
    FCH = F // P
    CHUNK = 256
    with ExitStack() as held:
        def sb(what, shape, dt=F32):
            return held.enter_context(nc.sbuf_tensor(f"t1_{what}", shape, dt))

        z = sb("z", [P, NT, C])
        rows = sb("rows", [P, 3, C])
        with ExitStack() as inner:
            def sbi(what, shape, dt=F32):
                return inner.enter_context(nc.sbuf_tensor(f"t1_{what}", shape, dt))

            w1, w2, wr = sbi("w1", [P, E, CH, F]), sbi("w2", [P, FCH, C]), sbi("wr", [P, CH, E])
            b1 = sbi("b1", [E, F])
            order = sbi("order", [P, NT, E])
            e, rank, onehot, top = sbi("e", [P, NT, E]), sbi("rank", [P, NT, E]), sbi("onehot", [P, NT, E]), sbi("top", [P, NT])
            diag = sbi("diag", [P, E, P], BF16)
            ones = sbi("ones", [P, P], BF16)
            own_x = sbi("own_x", [P, CH, E, CHUNK])
            own = sbi("own", [E, CHUNK])
            hidden = sbi("hidden", [P, FCH, CHUNK])
            (router_in, weights_in, logits, centred, exped, picked, filled, diag_done, spread, own_made, own_ready, own_taken,
             hid_ready, hid_done, z_ready, z_done) = inner.enter_context(k.stage(
                 "router", "weights", "logits", "centred", "exped", "picked", "filled", "diag", "spread", "own_made", "own_ready",
                 "own_taken", "hid_ready", "hid_done", "z_ready", "z_done"))
            block = inner.enter_context(nc.Block(no_gpsimd_drain=True))
            TPC = CHUNK // P
            n_chunks = T // CHUNK
            halves = 2

            @block.sync
            def _(sync):
                k.clear_last_set(sync)
                sync.dma_start(wr[:], inp["L0f_wr"]).then_inc(router_in, 16)
                sync.dma_start(order[:], inp["order8"].partition_broadcast(P)).then_inc(router_in, 16)
                sync.dma_start(b1[:], inp["L0f_b1"]).then_inc(weights_in, 16)
                for x in range(E):
                    sync.dma_start(w1[:, x], inp["L0f_w1"][x]).then_inc(weights_in, 16)
                sync.dma_start(w2[:], inp["L0f_w2"]).then_inc(weights_in, 16)
                sync.dma_start(rows[:], inp["L0f_rows"].partition_broadcast(P)).then_inc(weights_in, 16)

            N_W = E + 3

            @block.tensor
            def _(pe):
                pe.wait_ge(router_in, 32)
                for t in range(NT):
                    for c in range(CH):
                        mm = nc.tensor.matmul(k.ps[:, 0, t * E:(t + 1) * E], k.xT[:, c, t * P:(t + 1) * P], wr[:, c, :], start=c == 0,
                                              stop=c == CH - 1)
                mm.then_inc(logits, 1)
                h = 0
                for q in range(n_chunks):
                    for tt in range(TPC):
                        t = q * TPC + tt
                        pe.wait_ge(diag_done, t + 1)
                        for half in range(halves):
                            u = t * halves + half
                            if u >= 2:
                                pe.wait_ge(own_made, u - 1)
                            nc.tensor.matmul(k.ps[:, 1 + u % 2, :], ones[:, :], diag[:, half * HG:(half + 1) * HG, :].rearrange("p e n -> p (e n)"),
                                             start=True, stop=True).then_inc(spread, 1)
                        nc.tensor.transpose(k.ps[0:E, 3, tt * P:(tt + 1) * P], onehot[:, t, :], k.ident[:, :]).then_inc(own_ready, 1)
                    pe.wait_ge(own_made, (q + 1) * TPC * halves)
                    pe.wait_ge(own_taken, q + 1)
                    pe.wait_ge(weights_in, 16 * N_W)
                    for f in range(FCH):
                        if h >= 2:
                            pe.wait_ge(hid_done, h - 1)
                        out = k.ps[:, 4 + h % 2, 0:CHUNK]
                        for x in range(E):
                            for c in range(CH):
                                nc.tensor.matmul(out, w1[:, x, c, f * P:(f + 1) * P], own_x[:, c, x, :], start=x + c == 0, stop=False)
                        nc.tensor.matmul(out, b1[:, f * P:(f + 1) * P], own[:, :], start=False, stop=True).then_inc(hid_ready, 1)
                        h += 1
                    pe.wait_ge(hid_done, h)
                    for tt in range(TPC):
                        t = q * TPC + tt
                        if t >= 2:
                            pe.wait_ge(z_done, t - 1)
                        for f in range(FCH):
                            mm = nc.tensor.matmul(k.ps[:, 6 + t % 2, 0:C], hidden[:, f, tt * P:(tt + 1) * P], w2[:, f, :], start=f == 0, stop=f == FCH - 1)
                        mm.then_inc(z_ready, 1)

            @block.scalar
            def _(act):
                act.wait_ge(centred, 1)
                nc.scalar.activation(e[:], rank[:], ACT.Exp).then_inc(exped, 1)
                for h in range(n_chunks * FCH):
                    q = h // FCH
                    act.wait_ge(hid_ready, h + 1)
                    if q:
                        act.wait_ge(z_ready, q * TPC)
                    nc.scalar.activation(hidden[:, h % FCH, :], k.ps[:, 4 + h % 2, 0:CHUNK], ACT.Gelu).then_inc(hid_done, 1)

            @block.vector
            def _(dve):
                nc.vector.memset(ones[:], 1.0).then_inc(filled, 1)
                dve.wait_ge(logits, 1)
                view = k.ps[:, 0, 0:NT * E].rearrange("p (t e) -> p t e", e=E)
                nc.vector.reduce_max(top[:], view, AX).then_inc(picked, 1)
                dve.wait_ge(picked, 1)
                nc.vector.tensor_tensor(rank[:], view, top[:].unsqueeze(2).broadcast_to((P, NT, E)), ALU.subtract).then_inc(centred, 1)
                dve.wait_ge(exped, 1)
                dve.wait_ge(router_in, 32)
                first_of_maxima(nc, dve, picked, 1, e[:], top[:], rank[:], onehot[:], order[:])
                dve.wait_ge(weights_in, 16 * N_W)
                for q in range(n_chunks):
                    for tt in range(TPC):
                        t = q * TPC + tt
                        if t:
                            dve.wait_ge(spread, t * halves)
                        for x in range(E):
                            d = nc.vector.tensor_scalar(diag[:, x, :], k.ident[:, :], onehot[:, t, x:x + 1], None, ALU.mult)
                        d.then_inc(diag_done, 1)
                        if q and tt == 0:
                            dve.wait_ge(hid_ready, q * FCH)
                        for half in range(halves):
                            u = t * halves + half
                            dve.wait_ge(spread, u + 1)
                            for c in range(CH):
                                ins = nc.vector.tensor_tensor(
                                    own_x[:, c, half * HG:(half + 1) * HG, tt * P:(tt + 1) * P],
                                    k.ps[:, 1 + u % 2, :].rearrange("p (e n) -> p e n", e=HG),
                                    k.xT[:, c, t * P:(t + 1) * P].unsqueeze(1).broadcast_to((P, HG, P)), ALU.mult)
                            ins.then_inc(own_made, 1)
                    dve.wait_ge(own_ready, (q + 1) * TPC)
                    nc.vector.tensor_copy(own[:, :], k.ps[0:E, 3, 0:CHUNK]).then_inc(own_taken, 1)
                    for tt in range(TPC):
                        t = q * TPC + tt
                        dve.wait_ge(z_ready, t + 1)
                        nc.vector.tensor_tensor(z[:, t, :], k.ps[:, 6 + t % 2, 0:C], k.X[:, t, :], ALU.add).then_inc(picked, 1)
                        dve.wait_ge(picked, 6 + t + 1)
                        nc.vector.tensor_tensor(z[:, t, :], z[:, t, :], rows[:, 0, :], ALU.add).then_inc(z_done, 1)
        norm_rows_stage(k, NT, lambda t: z[:, t, :], rows[:, 1, :], rows[:, 2, :], k.eps[2], source=lambda t: z[:, t, :])
        add_norm_stage(k, lambda t: z[:, t, :])


def capacity_ffn(k):
    nc, inp = k.nc, k.inp
    E, F = 16, 1024
    FCH, CAP = F // P, -(-T // 16)
    ROWS = E * CAP
    with ExitStack() as held:
        def sb(what, shape, dt=F32):
            return held.enter_context(nc.sbuf_tensor(f"cf_{what}", shape, dt))

        scattered, gathered = (held.enter_context(nc.semaphore(n)) for n in ("scattered", "gathered"))
        slot_to, slot_from, gate = sb("slot_to", [P, NT], U32), sb("slot_from", [P, NT], U32), sb("gate", [P, NT])
        y = sb("y", [P, NT, C])
        with ExitStack() as inner:
            def sbi(what, shape, dt=F32):
                return inner.enter_context(nc.sbuf_tensor(f"cf_{what}", shape, dt))

            wg, bg, order = sbi("wg", [P, CH, E]), sbi("bg", [P, E]), sbi("order", [P, NT, E])
            number, token = sbi("number", [P, NT, E]), sbi("token", [P, NT])
            upto, ones = sbi("upto", [P, P]), sbi("ones", [P, P])
            e, rank, onehot, before = (sbi(n, [P, NT, E]) for n in ("e", "rank", "onehot", "before"))
            top, total, pos, slot, keep = (sbi(n, [P, NT]) for n in ("top", "total", "pos", "slot", "keep"))
            zeros = sbi("zeros", [P, ROWS // P, C])
            loaded, zeroed, cleared, logits, centred, exped, step, counted, placed = inner.enter_context(k.stage(
                "loaded", "zeroed", "cleared", "logits", "centred", "exped", "step", "counted", "placed"))
            block = inner.enter_context(nc.Block())
            loads = [(wg[:], inp["L1f_wg"]), (bg[:], inp["L1f_bg"].partition_broadcast(P)), (order[:], inp["order16"].partition_broadcast(P)),
                     (number[:], inp["expert16"].partition_broadcast(P)), (token[:], inp["token"]), (upto[:], inp["upto"])]

            @block.sync
            def _(sync):
                k.clear_last_set(sync)
                for tile, src in loads:
                    sync.dma_start(tile, src).then_inc(loaded, 16)
                sync.wait_ge(zeroed, 1)
                sync.dma_start(k.slots_in[0:ROWS, :].rearrange("(t p) c -> p t c", p=P), zeros[:]).then_inc(cleared, 16)
                sync.wait_ge(cleared, 16)

            @block.gpsimd
            def _(pool):
                nc.gpsimd.memset(zeros[:], 0.0).then_inc(zeroed, 1)
                pool.wait_ge(cleared, 16)
                pool.wait_ge(placed, 1)
                for t in range(NT):
                    pool.indirect_dma_start(k.slots_in, bass.IndirectOffsetOnAxis(ap=slot_to[:, t:t + 1], axis=0), k.X[:, t, :], None).then_inc(scattered, 16)
                pool.wait_ge(scattered, 16 * NT)

            @block.tensor
            def _(pe):
                pe.wait_ge(loaded, 16 * len(loads))
                for t in range(NT):
                    for c in range(CH):
                        mm = nc.tensor.matmul(k.ps[:, 0, t * E:(t + 1) * E], k.xT[:, c, t * P:(t + 1) * P], wg[:, c, :], start=c == 0,
                                              stop=c == CH - 1)
                mm.then_inc(logits, 1)
                pe.wait_ge(counted, NT)
                flat = "p t e -> p (t e)"
                nc.tensor.matmul(k.ps[:, 1, 0:NT * E], upto[:, :], onehot[:].rearrange(flat), start=True, stop=False)
                nc.tensor.matmul(k.ps[:, 1, 0:NT * E], ones[:, :], before[:].rearrange(flat), start=False, stop=True).then_inc(logits, 1)

            @block.scalar
            def _(act):
                act.wait_ge(centred, 1)
                nc.scalar.activation(e[:], rank[:], ACT.Exp).then_inc(exped, 1)

            @block.vector
            def _(dve):
                def wide(col):
                    return col.unsqueeze(2).broadcast_to((P, NT, E))

                n = 0

                def then(ins):
                    nonlocal n
                    n += 1
                    ins.then_inc(step, 1)
                    dve.wait_ge(step, n)

                nc.vector.memset(ones[:], 1.0)
                then(nc.vector.memset(before[:, 0, :], 0.0))
                dve.wait_ge(loaded, 16 * len(loads))
                dve.wait_ge(logits, 1)
                view = k.ps[:, 0, 0:NT * E].rearrange("p (t e) -> p t e", e=E)
                then(nc.vector.tensor_tensor(rank[:], view, bg[:].unsqueeze(1).broadcast_to((P, NT, E)), ALU.add))
                then(nc.vector.reduce_max(top[:], rank[:], AX))
                nc.vector.tensor_tensor(rank[:], rank[:], wide(top[:]), ALU.subtract).then_inc(centred, 1)
                dve.wait_ge(exped, 1)
                then(nc.vector.reduce_sum(total[:], e[:], AX))
                then(nc.vector.reciprocal(total[:], total[:]))
                then(nc.vector.tensor_tensor(e[:], e[:], wide(total[:]), ALU.mult))
                then(nc.vector.reduce_max(gate[:], e[:], AX))
                n = first_of_maxima(nc, dve, step, n, e[:], top[:], rank[:], onehot[:], order[:])
                for t in range(1, NT):
                    nc.vector.tensor_tensor(before[:, t, :], before[:, t - 1, :], onehot[:, t - 1, :], ALU.add).then_inc(counted, 1)
                    dve.wait_ge(counted, t)
                then(nc.vector.tensor_tensor(rank[:], onehot[:], number[:], ALU.mult))
                then(nc.vector.reduce_sum(slot[:], rank[:], AX))
                dve.sem_inc(counted, 1)
                dve.wait_ge(logits, 2)
                then(nc.vector.tensor_tensor(rank[:], k.ps[:, 1, 0:NT * E].rearrange("p (t e) -> p t e", e=E), onehot[:], ALU.mult))
                then(nc.vector.reduce_sum(pos[:], rank[:], AX))
                then(nc.vector.tensor_scalar(keep[:], pos[:], float(CAP), None, ALU.is_le))
                then(nc.vector.scalar_tensor_tensor(slot[:], slot[:], float(CAP), pos[:], ALU.mult, ALU.add))
                then(nc.vector.scalar_tensor_tensor(slot[:], slot[:], -1.0, keep[:], ALU.add, ALU.mult))
                nc.vector.tensor_copy(slot_from[:], slot[:])
                then(nc.vector.tensor_tensor(gate[:], gate[:], keep[:], ALU.mult))
                then(nc.vector.tensor_scalar(keep[:], keep[:], -1.0, 1.0, ALU.mult, ALU.add))
                then(nc.vector.tensor_tensor(token[:], token[:], keep[:], ALU.mult))
                then(nc.vector.tensor_tensor(slot[:], slot[:], token[:], ALU.add))
                nc.vector.tensor_copy(slot_to[:], slot[:]).then_inc(placed, 1)

        with ExitStack() as inner:
            def sbi(what, shape, dt=F32):
                return inner.enter_context(nc.sbuf_tensor(f"cf_{what}", shape, dt))

            DEEP = 3
            w1 = [sbi(f"w1_{i}", [P, CH, F]) for i in range(DEEP)]
            w2 = [sbi(f"w2_{i}", [P, FCH, C]) for i in range(DEEP)]
            xe = [sbi(f"x_{i}", [CAP, C]) for i in range(DEEP)]
            b1, b2 = sbi("b1", [P, E, FCH]), sbi("b2", [P, E, C])
            xeT, hidden, ye = sbi("xT", [P, 2, CH, CAP]), sbi("hidden", [P, 2, FCH, CAP]), sbi("ye", [CAP, 2, C])
            (*loaded, bias_in, turned, x_copied, hid_ready, hid_done, y_ready, y_done, stored0, stored1) = inner.enter_context(k.stage(
                "loaded0", "loaded1", "loaded2", "bias", "turned", "x_copied", "hid_ready", "hid_done", "y_ready", "y_done", "stored0", "stored1"))
            stored = (stored0, stored1)

            def store(sync, x):
                sync.wait_ge(y_done, x + 1)
                sync.dma_start(k.slots_out[x * CAP:(x + 1) * CAP, :], ye[:, x % 2, :]).then_inc(stored[x % 2], 16)

            block = inner.enter_context(nc.Block(no_gpsimd_drain=True))

            @block.sync
            def _(sync):
                k.clear_last_set(sync)
                sync.dma_start(b1[:], inp["L1f_b1"]).then_inc(bias_in, 16)
                sync.dma_start(b2[:], inp["L1f_b2"].partition_broadcast(P)).then_inc(bias_in, 16)
                for x in range(E):
                    i = x % DEEP
                    if x >= DEEP:
                        store(sync, x - DEEP)
                    sync.dma_start(xe[i][:], k.slots_in[x * CAP:(x + 1) * CAP, :]).then_inc(loaded[i], 16)
                    sync.dma_start(w1[i][:], inp["L1f_w1"][x]).then_inc(loaded[i], 16)
                    sync.dma_start(w2[i][:], inp["L1f_w2"][x]).then_inc(loaded[i], 16)
                for x in range(E - DEEP, E):
                    store(sync, x)
                for i in range(2):
                    sync.wait_ge(stored[i], 16 * E // 2)

            @block.tensor
            def _(pe):
                for x in range(E):
                    i = x % DEEP
                    pe.wait_ge(loaded[i], 48 * (x // DEEP + 1))
                    if x >= 2:
                        pe.wait_ge(x_copied, x - 1)
                    for c in range(CH):
                        tr = nc.tensor.transpose(k.ps[:, x % 2, c * P:(c + 1) * P], xe[i][:, c * P:(c + 1) * P], k.ident[:, :])
                    tr.then_inc(turned, 1)
                    pe.wait_ge(x_copied, x + 1)
                    for f in range(FCH):
                        h = x * FCH + f
                        if h >= 4:
                            pe.wait_ge(hid_done, h - 3)
                        for c in range(CH):
                            mm = nc.tensor.matmul(k.ps[:, 2 + h % 4, 0:CAP], w1[i][:, c, f * P:(f + 1) * P], xeT[:, x % 2, c, :], start=c == 0,
                                                  stop=c == CH - 1)
                        mm.then_inc(hid_ready, 1)
                    if x >= 2:
                        pe.wait_ge(y_done, x - 1)
                    for f in range(FCH):
                        pe.wait_ge(hid_done, x * FCH + f + 1)
                        mm = nc.tensor.matmul(k.ps[0:CAP, 6 + x % 2, 0:C], hidden[:, x % 2, f, :], w2[i][:, f, :], start=f == 0, stop=f == FCH - 1)
                    mm.then_inc(y_ready, 1)

            @block.scalar
            def _(act):
                act.wait_ge(bias_in, 32)
                for x in range(E):
                    act.wait_ge(turned, x + 1)
                    nc.scalar.activation(xeT[:, x % 2, :, :], k.ps[:, x % 2, 0:C].rearrange("p (c n) -> p c n", c=CH), ACT.Copy).then_inc(x_copied, 1)
                    if x >= 2:
                        act.wait_ge(y_ready, x - 1)
                    for f in range(FCH):
                        h = x * FCH + f
                        act.wait_ge(hid_ready, h + 1)
                        nc.scalar.activation(hidden[:, x % 2, f, :], k.ps[:, 2 + h % 4, 0:CAP], ACT.Relu, bias=b1[:, x, f:f + 1]).then_inc(hid_done, 1)

            @block.vector
            def _(dve):
                dve.wait_ge(bias_in, 32)
                for x in range(E):
                    dve.wait_ge(y_ready, x + 1)
                    if x >= 2:
                        dve.wait_ge(stored[x % 2], 16 * (x // 2))
                    nc.vector.tensor_tensor(ye[:, x % 2, :], k.ps[0:CAP, 6 + x % 2, 0:C], b2[:, x, :], ALU.add).then_inc(y_done, 1)

        with nc.sbuf_tensor("cf_back", [P, NT, C], F32) as back, k.stage("scaled") as (scaled,), nc.Block() as block:
            @block.sync
            def _(sync):
                k.clear_last_set(sync)

            @block.gpsimd
            def _(pool):
                for t in range(NT):
                    pool.indirect_dma_start(back[:, t, :], None, k.slots_out, bass.IndirectOffsetOnAxis(ap=slot_from[:, t:t + 1], axis=0)).then_inc(gathered, 16)

            @block.vector
            def _(dve):
                dve.wait_ge(gathered, 16 * NT)
                for t in range(NT):
                    nc.vector.tensor_scalar(y[:, t, :], back[:, t, :], gate[:, t:t + 1], None, ALU.mult).then_inc(scaled, 1)
        add_norm_stage(k, lambda t: y[:, t, :])


def quantised_ffn(k):
    nc, inp = k.nc, k.inp
    F = 1024
    FCH = F // P
    with ExitStack() as held:
        def sb(what, shape, dt=F32):
            return held.enter_context(nc.sbuf_tensor(f"qf_{what}", shape, dt))

        w2, rows = sb("w2", [P, FCH, C]), sb("rows", [P, 3, C])
        hidden = sb("hidden", [P, FCH, T])
        with ExitStack() as inner:
            def sbi(what, shape, dt=F32):
                return inner.enter_context(nc.sbuf_tensor(f"qf_{what}", shape, dt))

            hT, h = sbi("hT", [P, CH, T]), sbi("h", [P, NT, C])
            norm_rows_stage(k, NT, lambda t: h[:, t, :], rows[:, 0, :], rows[:, 1, :], k.eps[0], source=lambda t: k.X[:, t, :],
                            destT=lambda t: hT[:, :, t * P:(t + 1) * P], weights=[(rows[:], inp["L2f_rows"].partition_broadcast(P))])
            q1, q2 = sbi("q1", [P, CH, F], I32), sbi("q2", [P, FCH, C], I32)
            w1, b1 = sbi("w1", [P, CH, F]), sbi("b1", [P, FCH])
            loaded, weights, ready, done = inner.enter_context(k.stage("loaded", "weights", "ready", "done"))
            block = inner.enter_context(nc.Block(no_gpsimd_drain=True))
            loads = [(q1[:], inp["L2f_q1"]), (w1[:], inp["L2f_s1"].partition_broadcast(P)), (q2[:], inp["L2f_q2"]),
                     (w2[:], inp["L2f_s2"].partition_broadcast(P)), (b1[:], inp["L2f_b1"])]
            units = [(q, f) for q in range(T // BANK) for f in range(FCH)]

            @block.sync
            def _(sync):
                k.clear_last_set(sync)
                for tile, src in loads:
                    sync.dma_start(tile, src).then_inc(loaded, 16)

            @block.vector
            def _(dve):
                dve.wait_ge(loaded, 16 * len(loads))
                for w, q in ((w1, q1), (w2, q2)):
                    flat = "p a b -> p (a b)"
                    nc.vector.scalar_tensor_tensor(w[:].rearrange(flat), q[:].rearrange(flat), -128.0, w[:].rearrange(flat), ALU.add,
                                                   ALU.mult).then_inc(weights, 1)
                nc.vector.tensor_scalar(rows[:, 2, :], rows[:, 2, :], 0.5, None, ALU.mult).then_inc(weights, 1)

            @block.tensor
            def _(pe):
                pe.wait_ge(weights, 1)
                for n, (q, f) in enumerate(units):
                    if n >= 4:
                        pe.wait_ge(done, n - 3)
                    for c in range(CH):
                        mm = nc.tensor.matmul(k.ps[:, n % 4, :], w1[:, c, f * P:(f + 1) * P], hT[:, c, q * BANK:(q + 1) * BANK], start=c == 0,
                                              stop=c == CH - 1)
                    mm.then_inc(ready, 1)

            @block.scalar
            def _(act):
                act.wait_ge(loaded, 16 * len(loads))
                for n, (q, f) in enumerate(units):
                    act.wait_ge(ready, n + 1)
                    nc.scalar.activation(hidden[:, f, q * BANK:(q + 1) * BANK], k.ps[:, n % 4, :], ACT.Silu, bias=b1[:, f:f + 1]).then_inc(done, 1)
        residual_norm_stage(k, [(lambda t, f=f: hidden[:, f, t * P:(t + 1) * P], w2[:, f, :]) for f in range(FCH)], rows[:, 2, :],
                            x_scale=2.0, y_scale=0.5)


def shifted_ffn(k):
    nc, inp = k.nc, k.inp
    with ExitStack() as held:
        def sb(what, shape, dt=F32):
            return held.enter_context(nc.sbuf_tensor(f"sh_{what}", shape, dt))

        y = sb("y", [P, NT, C])
        with ExitStack() as inner:
            def sbi(what, shape, dt=F32):
                return inner.enter_context(nc.sbuf_tensor(f"sh_{what}", shape, dt))

            w, mu, rest = sbi("w", [P, 3, CH, C]), sbi("mu", [P, 2, CH]), sbi("rest", [P, 2, CH])
            mixed = sbi("mixed", [P, 2, CH, T])
            keys, squares, gate = sbi("keys", [P, CH, T]), sbi("squares", [P, CH, T]), sbi("gate", [P, NT, C])
            loaded, others, scaled, mixed_done, k_ready, k_relu, squared, g_ready, g_done, v_ready, v_done = inner.enter_context(k.stage(
                "loaded", "others", "scaled", "mixed", "k_ready", "k_relu", "squared", "g_ready", "g_done", "v_ready", "v_done"))
            block = inner.enter_context(nc.Block())
            parts = [(b, c) for b in range(B) for c in range(CH)]

            @block.sync
            def _(sync):
                k.clear_last_set(sync)
                sync.dma_start(mu[:], inp["L3f_mu"]).then_inc(loaded, 16)
                sync.dma_start(w[:], inp["L3f_w"]).then_inc(loaded, 16)

            @block.vector
            def _(dve):
                dve.wait_ge(loaded, 32)
                nc.vector.tensor_scalar(rest[:], mu[:], -1.0, 1.0, ALU.mult, ALU.add).then_inc(others, 1)
                dve.wait_ge(others, 1)
                for i, which in enumerate((1, 0)):
                    for n, (b, c) in enumerate(parts):
                        part = mixed[:, which, c, b * S:(b + 1) * S]
                        nc.vector.tensor_scalar(part, k.xT[:, c, b * S:(b + 1) * S], mu[:, which, c:c + 1], None, ALU.mult).then_inc(scaled, 1)
                        dve.wait_ge(scaled, i * len(parts) + n + 1)
                        nc.vector.scalar_tensor_tensor(part[:, 1:], k.xT[:, c, b * S:(b + 1) * S - 1], rest[:, which, c:c + 1], part[:, 1:],
                                                       ALU.mult, ALU.add).then_inc(mixed_done, 1)
                for t in range(NT):
                    dve.wait_ge(v_ready, t + 1)
                    dve.wait_ge(g_done, t + 1)
                    nc.vector.tensor_tensor(y[:, t, :], k.ps[:, 6 + t % 2, 0:C], gate[:, t, :], ALU.mult).then_inc(v_done, 1)

            @block.tensor
            def _(pe):
                pe.wait_ge(loaded, 32)
                for n, (b, m) in enumerate(parts):
                    pe.wait_ge(mixed_done, CH * (b + 1))
                    if n >= 2:
                        pe.wait_ge(k_relu, n - 1)
                    for c in range(CH):
                        mm = nc.tensor.matmul(k.ps[:, n % 2, :], w[:, 1, c, m * P:(m + 1) * P], mixed[:, 1, c, b * S:(b + 1) * S], start=c == 0,
                                              stop=c == CH - 1)
                    mm.then_inc(k_ready, 1)
                for t in range(NT):
                    b = t // (NT // B)
                    pe.wait_ge(mixed_done, CH * (B + b + 1))
                    if t >= 2:
                        pe.wait_ge(g_done, t - 1)
                    for c in range(CH):
                        mm = nc.tensor.matmul(k.ps[:, 4 + t % 2, 0:C], mixed[:, 0, c, t * P:(t + 1) * P], w[:, 0, c, :], start=c == 0, stop=c == CH - 1)
                    mm.then_inc(g_ready, 1)
                for t in range(NT):
                    b = t // (NT // B)
                    pe.wait_ge(squared, CH * (b + 1))
                    if t >= 2:
                        pe.wait_ge(v_done, t - 1)
                    for c in range(CH):
                        mm = nc.tensor.matmul(k.ps[:, 6 + t % 2, 0:C], squares[:, c, t * P:(t + 1) * P], w[:, 2, c, :], start=c == 0, stop=c == CH - 1)
                    mm.then_inc(v_ready, 1)

            @block.scalar
            def _(act):
                for n, (b, m) in enumerate(parts):
                    act.wait_ge(k_ready, n + 1)
                    nc.scalar.activation(keys[:, m, b * S:(b + 1) * S], k.ps[:, n % 2, :], ACT.Relu).then_inc(k_relu, 1)
                for t in range(NT):
                    act.wait_ge(g_ready, t + 1)
                    nc.scalar.activation(gate[:, t, :], k.ps[:, 4 + t % 2, 0:C], ACT.Sigmoid).then_inc(g_done, 1)

            @block.gpsimd
            def _(pool):
                for n, (b, m) in enumerate(parts):
                    pool.wait_ge(k_relu, n + 1)
                    part = keys[:, m, b * S:(b + 1) * S]
                    nc.gpsimd.tensor_tensor(squares[:, m, b * S:(b + 1) * S], part, part, ALU.mult).then_inc(squared, 1)
        residual_norm_stage(k, None, rows=lambda t: y[:, t, :], out=k.out)


def masked_attention(k):
    nc, inp = k.nc, k.inp
    with nc.sbuf_tensor("l3x_att", [P, NG, T], F32) as att:
        q_parts, k_parts, values = k.q_parts, k.k_parts, k.values_of(NTC, P)
        with nc.sbuf_tensor("l3x_ctxT", [P, CH, TC], F32) as ctxT:
            def as_is(src, store, order):
                return [("split", [(slice(0, BANK), k.ident[:, :], src[:, m, t * BANK:(t + 1) * BANK], True, True)], BANK, None,
                         stacked(store[m * P:(m + 1) * P, :, t * BANK:(t + 1) * BANK], order))
                        for t in range(store.shape[2] // BANK) for m in range(CH)]

            turned = [("value", [(slice(m * P, (m + 1) * P), ctxT[:, m, t * P:(t + 1) * P], k.ident[:, :], True, True) for m in range(CH)],
                       P, values[t]) for t in range(NTC)]
            project_stage(k, as_is(k.xT, q_parts, Q_PART) + as_is(ctxT, k_parts, K_PART) + turned, [(ctxT[:], inp["ctxT"])])
        attention_stage(k, "l3x_core", q_parts, k_parts, values, S, SC, 1.0, att, mask=(inp["mask_q"], inp["mask_k"]))
        with nc.sbuf_tensor("l3x_ow", [P, NG, C], F32) as ow, nc.sbuf_tensor("l3x_ob", [P, C], F32) as ob:
            residual_norm_stage(k, [(lambda t, g=g: att[:, g, t * P:(t + 1) * P], ow[:, g, :]) for g in range(NG)], ob[:],
                                [(ow[:], inp["L3x_out_w"]), (ob[:], inp["L3x_out_b"].partition_broadcast(P))], relu=True)


def latent_attention(k):
    nc, inp = k.nc, k.inp
    D = 64
    INNER, NK = H * D, SC + S
    ICH = INNER // P
    q_parts = nc.dram_tensor("latent_q_parts", [3, INNER, T], BF16, kind="Internal").ap()
    k_parts = nc.dram_tensor("latent_k_parts", [3, INNER, B * NK], BF16, kind="Internal").ap()
    values = nc.dram_tensor("latent_values", [B * NK // P, P, INNER], F32, kind="Internal").ap()
    with nc.sbuf_tensor("la_latT", [P, CH, T], F32) as latT, nc.sbuf_tensor("la_ctxT", [P, CH, TC], F32) as ctxT:
        with nc.sbuf_tensor("la_rows", [P, 4, C], F32) as rows, nc.sbuf_tensor("la_ctx", [P, NTC, C], F32) as ctx, \
                nc.sbuf_tensor("la_lat", [P, NT, C], F32) as lat:
            norm_rows_stage(k, NTC, lambda t: ctx[:, t, :], rows[:, 0, :], rows[:, 1, :], k.eps[0], source=lambda t: ctx[:, t, :],
                            destT=lambda t: ctxT[:, :, t * P:(t + 1) * P],
                            weights=[(rows[:], inp["L2x_rows"].partition_broadcast(P)), (ctx[:], inp["ctx"])])
            norm_rows_stage(k, NT, lambda t: lat[:, t, :], rows[:, 2, :], rows[:, 3, :], k.eps[0], source=lambda t: k.X[:, t, :],
                            destT=lambda t: latT[:, :, t * P:(t + 1) * P])
        with nc.sbuf_tensor("la_w", [P, CH, 3 * INNER], F32) as w:
            def keyT(b, i, n):
                at = i * n
                return (lambda c: ctxT[:, c, b * SC + at:b * SC + at + n]) if at < SC else (lambda c: latT[:, c, b * S + at - SC:b * S + at - SC + n])

            def split(src, col, m, store):
                return ("split", [(slice(0, BANK), w[:, c, col + m * P:col + (m + 1) * P], src(c), c == 0, c == CH - 1) for c in range(CH)],
                        BANK, None, [(store.rearrange("a p n -> p a n"), lambda parts: parts)])

            units = [split(lambda c: latT[:, c, t * BANK:(t + 1) * BANK], 0, m, q_parts[:, m * P:(m + 1) * P, t * BANK:(t + 1) * BANK])
                     for t in range(T // BANK) for m in range(ICH)]
            for b in range(B):
                for i in range(NK // BANK):
                    col = b * NK + i * BANK
                    units += [split(keyT(b, i, BANK), INNER, m, k_parts[:, m * P:(m + 1) * P, col:col + BANK]) for m in range(ICH)]
                for i in range(NK // P):
                    src = keyT(b, i, P)
                    units += [("plain", [(slice(0, BANK), src(c), w[:, c, 2 * INNER + v * BANK:2 * INNER + (v + 1) * BANK], c == 0, c == CH - 1)
                                         for c in range(CH)], P, values[b * NK // P + i, :, v * BANK:(v + 1) * BANK]) for v in range(INNER // BANK)]
            project_stage(k, units, [(w[:], inp["L2x_w"])])
    with nc.sbuf_tensor("la_att", [P, ICH - CH, T], F32) as att:
        def att_of(g):
            return k.xT[:, g, :] if g < CH else att[:, g - CH, :]

        attention_stage(k, "la_core", q_parts, k_parts, values, S, NK, D ** -0.5, att_of, head_dim=D)
        with nc.sbuf_tensor("la_ow", [P, ICH, C], F32) as ow:
            residual_norm_stage(k, [(lambda t, g=g: att_of(g)[:, t * P:(t + 1) * P], ow[:, g, :]) for g in range(ICH)], None,
                                [(ow[:], inp["L2x_out_w"])])


SUBLAYERS = (pyramid_attention, relu_kernel_attention, top1_ffn, softmax_linear_attention, context_attention, capacity_ffn, plain_attention,
             latent_attention, quantised_ffn, alibi_attention, masked_attention, shifted_ffn)


def decoder(nc, inp, out):
    k = Program(nc, inp)
    with ExitStack() as held:
        def sb(name, shape, dt=F32):
            return held.enter_context(nc.sbuf_tensor(name, shape, dt))

        k.ps = held.enter_context(nc.psum_tensor("ps", [P, 8, BANK], F32))
        k.X, k.xT = sb("X", [P, NT, C]), sb("xT", [P, CH, T])
        k.ident, k.spread = sb("ident", [P, P]), sb("spread", [P, P])
        k.ident_bf, k.above_q, k.above_k = (sb(n, [P, P], BF16) for n in ("ident_bf", "above_q", "above_k"))
        eps = sb("eps", [P, 4])
        k.ones, k.ones_bf = sb("ones", [P, P]), sb("ones_bf", [3, P], BF16)
        k.eps = [eps[:, i:i + 1] for i in range(3)]
        k.head_blocks, k.head_cols = sb("head_blocks", [P, P]), sb("head_cols", [P, CH, H])
        k.q_parts = nc.dram_tensor("q_parts", [C, 6, T], BF16, kind="Internal").ap()
        k.k_parts = nc.dram_tensor("k_parts", [C, 6, TC], BF16, kind="Internal").ap()
        store = nc.dram_tensor("values", [NTC, P, H * QUAD], F32, kind="Internal").ap()
        k.slots_in = nc.dram_tensor("slots_in", [2 * T, C], F32, kind="Internal").ap()
        k.slots_out = nc.dram_tensor("slots_out", [T, C], F32, kind="Internal").ap()
        k.rows_of_ones = inp["rows_of_ones"]
        k.out = out
        k.sums_of_weights, k.inverse_sums = (nc.dram_tensor(n, [HG, NG, S], F32, kind="Internal").ap() for n in ("sums_of_weights", "inverse_sums"))
        k.regroup = nc.dram_tensor("regroup", [B, H, S, HD], F32, kind="Internal").ap()
        k.values_of = lambda tiles, rows: store[0:tiles, 0:rows, :]
        load_stage(k, [(k.X[:], inp["x"]), (k.xT[:], inp["xT"]), (k.ident[:], inp["ident"]), (k.spread[:], inp["spread"]),
                       (k.ident_bf[:], inp["ident_bf"]), (k.above_q[:], inp["above_q"]), (k.above_k[:], inp["above_k"]),
                       (eps[:], inp["eps"].partition_broadcast(P)), (k.head_blocks[:], inp["head_blocks"]),
                       (k.head_cols[:], inp["head_cols"])])
        memset_stage(k, (k.ones[:], 1.0), (k.ones_bf[:], 1.0))

        for sublayer in SUBLAYERS:
            sublayer(k)


def lay_out(a):
    f = {n: np.ascontiguousarray(v) for n, v in a.items()}
    bf16 = mybir.dt.np(BF16)

    def rows_in(w, chunks=CH):
        return w.reshape(chunks, P, w.shape[1]).transpose(1, 0, 2)

    def column(v):
        return v.reshape(-1, P).T

    def strips(w):
        z = np.zeros((H, QUAD, w.shape[1]), w.dtype)
        z[:, :HD] = w.reshape(H, HD, -1)
        return z.reshape(NG, P, -1).transpose(1, 0, 2)

    def strip_column(v):
        return strips(v[:, None])[:, :, 0]

    i = np.arange(P)
    exact = 2.0 ** (-0.5 * (np.arange(H)[:, None] + 1)) * np.arange(S) * HD ** 0.5
    parts = []
    for _ in range(3):
        parts.append((exact - sum(p.astype(np.float64) for p in parts)).astype(np.float32).astype(bf16))
    slopes = np.stack(parts)
    d = {
        "x": f["x"].reshape(NT, P, C).transpose(1, 0, 2),
        "xT": f["x"].reshape(T, CH, P).transpose(2, 1, 0),
        "ident": np.eye(P, dtype=np.float32),
        "spread": ((i[:, None] % QUAD == HD) & (i[:, None] // QUAD == i[None, :] // QUAD)).astype(np.float32),
        "ident_bf": np.eye(P).astype(bf16),
        "above_q": np.where(i[None, :] > i[:, None], -1e30, 0.0).astype(bf16),
        "above_k": np.where(i[None, :] < i[:, None], -1e30, 0.0).astype(bf16),
        "eps": np.array([1e-5, 1e-6, 1e-12, 0.0], np.float32),
        "ctxT": f["ctx_1024"].reshape(TC, CH, P).transpose(2, 1, 0),
        "head_blocks": (i[:, None] // HD == i[None, :] // HD).astype(np.float32),
        "head_cols": ((i[:, None, None] + P * np.arange(CH)[:, None]) // HD == np.arange(H)).astype(np.float32),
        "mask_tokens": f["mask_BxS2_ff1"].reshape(NTC, P).T,
        "L0x_w": np.stack([rows_in(f[f"L0_xattn_{n}"]) for n in ("wq", "wk", "wv", "dense_w")], 1),
        "L0x_rows": np.stack([f["L0_xattn_ln_gamma"], f["L0_xattn_ln_beta"], f["L0_xattn_dense_b"]]),
        "order8": np.tile(np.arange(8, 0, -1, dtype=np.float32), (NT, 1)),
        "L0f_wr": rows_in(f["L0_ffn_Wr"].T),
        "L0f_w1": np.stack([rows_in(w) for w in f["L0_ffn_W1"]]),
        "L0f_b1": f["L0_ffn_b1"],
        "L0f_w2": rows_in(f["L0_ffn_Wo"], 8),
        "L0f_rows": np.stack([f[f"L0_ffn_{n}"] for n in ("bo", "gamma", "beta")]),
        "L1a_w": np.stack([rows_in(f[f"L1_attn_{n}"].T) for n in ("Wq", "Wk", "Wv", "Wo")], 1),
        "L1a_rows": np.stack([f[f"L1_attn_{n}"] for n in ("bq", "bv", "ln_g", "ln_b", "bo")]),
        "L1a_bk": column(f["L1_attn_bk"]),
        "L1x_w": np.concatenate([rows_in(f[f"L1_xattn_{n}"].T) for n in ("wq", "wk", "wv")], 2),
        "L1x_b": np.concatenate([column(f["L1_xattn_bq"]), column(f["L1_xattn_bk"])], 1),
        "L1x_v_b": strip_column(f["L1_xattn_bv"]),
        "L1x_out_w": strips(f["L1_xattn_wo"].T),
        "L1x_out_b": f["L1_xattn_bo"],
        "L2a_w": rows_in(f["L2_attn_w_qkv"].T),
        "L2a_out_w": strips(f["L2_attn_w_proj"].T),
        "L2a_out_b": f["L2_attn_b_proj"],
        "L3a_w": np.concatenate([rows_in(f[f"L3_attn_{n}"].T) for n in ("Wq", "Wk", "Wv")], 2),
        "L3a_b": np.concatenate([column(f["L3_attn_bq"]), column(f["L3_attn_bk"])], 1),
        "L3a_v_b": strip_column(f["L3_attn_bv"]),
        "L3a_out_w": strips(f["L3_attn_Wo"].T),
        "L3a_out_b": f["L3_attn_bo"],
        "slopes": slopes,
        "rows_of_ones": np.ones((3, HG, SC), bf16),
        "order16": np.tile(np.arange(16, 0, -1, dtype=np.float32), (NT, 1)),
        "expert16": np.tile(np.arange(16, dtype=np.float32), (NT, 1)),
        "token": (T + np.arange(T, dtype=np.float32)).reshape(NT, P).T,
        "upto": (i[:, None] <= i[None, :]).astype(np.float32),
        "L1f_wg": rows_in(f["L1_ffn_Wg"]),
        "L1f_bg": f["L1_ffn_bg"],
        "L1f_w1": np.stack([rows_in(w) for w in f["L1_ffn_W1"]]),
        "L1f_w2": np.stack([rows_in(w, 8) for w in f["L1_ffn_W2"]]),
        "L1f_b1": f["L1_ffn_b1"].reshape(16, 8, P).transpose(2, 0, 1),
        "L1f_b2": f["L1_ffn_b2"],
        "L2f_rows": np.stack([f[f"L2_ffn_{n}"] for n in ("ln_gamma", "ln_beta", "fc2_bias")]),
        "L2f_q1": rows_in(f["L2_ffn_fc1_q"]),
        "L2f_q2": rows_in(f["L2_ffn_fc2_q"], 8),
        "L2f_s1": f["L2_ffn_fc1_scales"],
        "L2f_s2": f["L2_ffn_fc2_scales"],
        "L2f_b1": column(f["L2_ffn_fc1_bias"]),
        "L3f_w": np.stack([rows_in(f[f"L3_ffn_W_{n}"].T) for n in "rkv"], 1),
        "L3f_mu": np.stack([column(f[f"L3_ffn_mu_{n}"]) for n in "rk"], 1),
        "ctx": f["ctx_1024"].reshape(NTC, P, C).transpose(1, 0, 2),
        "mask_q": f["mask_Bx1xSxS2_ff0"][:, 0],
        "mask_k": f["mask_Bx1xSxS2_ff0"][:, 0].transpose(0, 2, 1),
        "L3x_out_w": strips(f["L3_xattn_wo_w"].T),
        "L3x_out_b": f["L3_xattn_wo_b"],
        "L2x_rows": np.stack([f[f"L2_xattn_{n}"] for n in ("ln_m_g", "ln_m_b", "ln_l_g", "ln_l_b")]),
        "L2x_w": np.concatenate([rows_in(f["L2_xattn_Wq"]), rows_in(f["L2_xattn_Wkv"])], 2),
        "L2x_out_w": rows_in(f["L2_xattn_Wout"], 8),
        "L0_in_w": np.stack([rows_in(w.T) for w in f["L0_attn_in_proj_w"]]),
        "L0_in_b": np.stack([column(b) for b in f["L0_attn_in_proj_b"]], 1),
        "L0_v_b": np.stack([strip_column(b[2 * C:]) for b in f["L0_attn_in_proj_b"]], 1),
        "L0_out_w": np.stack([strips(w.T) for w in f["L0_attn_out_w"]]),
        "L0_out_b": np.stack([column(b) for b in f["L0_attn_out_b"]], 1),
        "L0_up_w": np.stack([rows_in(w.T) for w in f["L0_attn_up_w"]]),
        "L0_up_b": np.stack([column(b) for b in f["L0_attn_up_b"]], 1),
        "L0_out_b0_up_b0": np.stack([f["L0_attn_out_b"][0], f["L0_attn_up_b"][0]]),
    }
    return {n: np.ascontiguousarray(v) for n, v in d.items()}


def build(nc, arrays):
    inp = {n: nc.dram_tensor(f"in_{n}", v.shape, mybir.dt.from_np(v.dtype), kind="ExternalInput").ap() for n, v in arrays.items()}
    decoder(nc, inp, nc.dram_tensor("out_x", [T, C], F32, kind="ExternalOutput").ap())


def kernel(**inputs):
    import concourse.bacc as bacc
    from concourse.bass_utils import run_bass_kernel_spmd

    arrays = lay_out({n: np.asarray(v) for n, v in inputs.items()})
    nc = bacc.Bacc("TRN2", target_bir_lowering=False, num_devices=1)
    build(nc, arrays)
    result = run_bass_kernel_spmd(nc, [{f"in_{n}": v for n, v in arrays.items()}], core_ids=[0])
    return result.results[0]["out_x"].reshape(B, S, C)
```

```python
from contextlib import ExitStack, contextmanager

import numpy as np

import concourse.bass as bass
from concourse import mybir

F32 = mybir.dt.float32
BF16 = mybir.dt.bfloat16
I32 = mybir.dt.int32
U32 = mybir.dt.uint32
ALU = mybir.AluOpType
ACT = mybir.ActivationFunctionType
AX = mybir.AxisListType.X

P = 128
B, S, C = 4, 512, 256
SC = 1024
T, TC = B * S, B * SC
NT, NTC = T // P, TC // P
CH = C // P
H, HD = 16, 16
QUAD = 32
HG = 4
NG = H // HG
Q_PART = (0, 0, 0, 1, 1, 2)
K_PART = (0, 1, 2, 0, 1, 0)
STACK = len(Q_PART) * HD
BANK = 512


class Program:

    FIRST_SEM, SET = 176, 38

    def __init__(self, nc, inputs):
        self.nc, self.inp = nc, inputs
        self.stages = 0

    @contextmanager
    def stage(self, *names):
        first = self.FIRST_SEM + self.SET * (self.stages % 2)
        assert len(names) <= self.SET
        self.stages += 1
        with ExitStack() as held:
            yield [held.enter_context(self.nc.semaphore(f"s{self.stages}_{name}", num=first + i))
                   for i, name in enumerate(names)]

    def clear_last_set(self, sync):
        first = self.FIRST_SEM + self.SET * (self.stages % 2)
        sync.sem_clear(range(first, first + self.SET))


def load_stage(k, pairs):
    nc = k.nc
    with k.stage("loaded") as (loaded,), nc.Block(no_gpsimd_drain=True) as block:
        @block.sync
        def _(sync):
            k.clear_last_set(sync)
            for tile, source in pairs[0::2]:
                sync.dma_start(tile, source).then_inc(loaded, 16)
            sync.wait_ge(loaded, 16 * len(pairs))

        @block.scalar
        def _(act):
            for tile, source in pairs[1::2]:
                act.dma_start(tile, source).then_inc(loaded, 16)


def project_stage(k, units, weights, stores=(), late=(), late_unit=0, prefetch=()):
    nc = k.nc
    splits = [n for n, u in enumerate(units) if u[0] == "split"]
    VALUES = 6
    stored_by = []
    for i, n in enumerate(splits):
        stored_by.append((stored_by[i - 3] if i >= 3 else 0) + 16 * len(units[n][4]))
    with (
        nc.sbuf_tensor(f"proj_full_{k.stages}", [P, 2, BANK], F32) as full,
        nc.sbuf_tensor(f"proj_rest_{k.stages}", [P, 2, BANK], F32) as rest,
        nc.sbuf_tensor(f"proj_parts_{k.stages}", [P, 3, 3, BANK], BF16) as parts,
        nc.sbuf_tensor(f"proj_value_{k.stages}", [P, VALUES, H, QUAD], F32) as value,
        k.stage("weights", "late", "prefetched", "ready", "evacuated", "high", "remainder", "middle", "low", "ones", "parts_stored0",
                "parts_stored1", "parts_stored2", "others_stored", *(f"value_stored{i}" for i in range(VALUES))) as (
            weights_in, late_in, prefetched, ready, evacuated, high, remainder, middle, low, ones_set, *stored),
        nc.Block() as block,
    ):
        parts_stored, others_stored, value_stored = stored[0:3], stored[3], stored[4:]

        @block.sync
        def _(sync):
            k.clear_last_set(sync)
            for tile, source in weights:
                sync.dma_start(tile, source).then_inc(weights_in, 16)
            for tile, source in late:
                sync.dma_start(tile, source).then_inc(late_in, 16)
            for tile, source in prefetch:
                sync.dma_start(tile, source).then_inc(prefetched, 16)
            for destination, source in stores:
                sync.dma_start(destination, source).then_inc(others_stored, 16)
            i = j = 0
            for n, unit in enumerate(units):
                if unit[0] == "split":
                    sync.wait_ge(low, i + 1)
                    for destination, taken in unit[4]:
                        sync.dma_start(destination, taken(parts[:, i % 3, :, 0:unit[2]])).then_inc(parts_stored[i % 3], 16)
                    i += 1
                else:
                    sync.wait_ge(evacuated, n + 1)
                    sync.dma_start(unit[3], value[0:unit[2], j % VALUES].rearrange("p h d -> p (h d)")
                                   ).then_inc(value_stored[j % VALUES], 16)
                    j += 1
            if prefetch:
                sync.wait_ge(prefetched, 16 * len(prefetch))
            for r in range(min(3, i)):
                sync.wait_ge(parts_stored[(i - 1 - r) % 3], stored_by[i - 1 - r])
            if stores:
                sync.wait_ge(others_stored, 16 * len(stores))
            for r in range(min(VALUES, j)):
                sync.wait_ge(value_stored[r], 16 * len(range(r, j, VALUES)))

        @block.tensor
        def _(pe):
            if weights:
                pe.wait_ge(weights_in, 16 * len(weights))
            for n, unit in enumerate(units):
                if late and n == late_unit:
                    pe.wait_ge(late_in, 16 * len(late))
                if n >= 8:
                    pe.wait_ge(evacuated, n - 7)
                rows = P if unit[0] == "split" else unit[2]
                for cols, lhsT, rhs, start, stop in unit[1]:
                    last = nc.tensor.matmul(k.ps[0:rows, n % 8, cols], lhsT, rhs, start=start, stop=stop)
                last.then_inc(ready, 1)

        @block.scalar
        def _(act):
            act.wait_ge(ones_set, 1)

            def take_middle(i):
                width = units[splits[i]][2]
                act.wait_ge(remainder, i + 1)
                nc.scalar.activation(parts[:, i % 3, 1, 0:width], rest[:, i % 2, 0:width], ACT.Copy).then_inc(middle, 1)

            i = j = 0
            for n, unit in enumerate(units):
                act.wait_ge(ready, n + 1)
                if unit[0] == "split":
                    _, _, width, bias, _ = unit
                    if i >= 2:
                        act.wait_ge(remainder, i - 1)
                    if i == 0 and bias is not None:
                        act.wait_ge(weights_in, 16 * len(weights))
                    for cols, column in bias if isinstance(bias, list) else [(slice(0, width), 0.0 if bias is None else bias)]:
                        ins = nc.scalar.activation(full[:, i % 2, cols], k.ps[:, n % 8, cols], ACT.Identity, bias=column)
                    ins.then_inc(evacuated, 1)
                    i += 1
                else:
                    rows = unit[2]
                    if j >= VALUES:
                        act.wait_ge(value_stored[j % VALUES], 16 * (j // VALUES))
                    d = HD if unit[0] == "value" else QUAD
                    nc.scalar.activation(value[0:rows, j % VALUES, :, 0:d], k.ps[0:rows, n % 8, 0:H * d].rearrange("p (h d) -> p h d", h=H),
                                         ACT.Copy).then_inc(evacuated, 1)
                    j += 1
                if n and units[n - 1][0] == "split":
                    take_middle(splits.index(n - 1))
            if units[-1][0] == "split":
                take_middle(len(splits) - 1)

        @block.vector
        def _(dve):
            nc.vector.memset(value[:], 1.0).then_inc(ones_set, 1)
            for i, n in enumerate(splits):
                width = units[n][2]
                dve.wait_ge(evacuated, n + 1)
                if i >= 3:
                    dve.wait_ge(parts_stored[i % 3], stored_by[i - 3])
                nc.vector.tensor_copy(parts[:, i % 3, 0, 0:width], full[:, i % 2, 0:width]).then_inc(high, 1)
                if i >= 2:
                    dve.wait_ge(low, i - 1)
                dve.wait_ge(high, i + 1)
                nc.vector.tensor_tensor(rest[:, i % 2, 0:width], full[:, i % 2, 0:width],
                                        parts[:, i % 3, 0, 0:width], ALU.subtract).then_inc(remainder, 1)

        @block.gpsimd
        def _(pool):
            for i, n in enumerate(splits):
                width = units[n][2]
                pool.wait_ge(middle, i + 1)
                nc.gpsimd.tensor_tensor(parts[:, i % 3, 2, 0:width], rest[:, i % 2, 0:width],
                                        parts[:, i % 3, 1, 0:width], ALU.subtract).then_inc(low, 1)


def stacked(store, order):
    n = store.shape[2]
    at, out = 0, []
    for part, times in enumerate((3, 2, 1)):
        if order == Q_PART:
            out.append((store[:, at:at + times, :], lambda p, part=part, times=times: p[:, part:part + 1, :].broadcast_to((P, times, n))))
        else:
            out.append((store[:, at:at + times, :], lambda p, times=times: p[:, 0:times, :]))
        at += times
    return out


def split_units(source, width, weight, bias, store, order):
    return [("split", [(slice(0, width), weight[:, c, m * P:(m + 1) * P], source(c, t), c == 0, c == CH - 1) for c in range(CH)],
             width, None if bias is None else bias[:, m:m + 1], stacked(store[m * P:(m + 1) * P, :, t * width:(t + 1) * width], order))
            for t in range(store.shape[2] // width) for m in range(CH)]


def value_units(source, rows, weight, store):
    return [("value", [(slice(0, C), source(c, t), weight[:, c, :], c == 0, c == CH - 1) for c in range(CH)],
             rows, store[t]) for t in range(len(store) if isinstance(store, list) else store.shape[0])]


def dense_rows(dense, att, tokens):
    return [(dense[odd * P // 2 + j * HD:odd * P // 2 + (j + 1) * HD, :, tokens], att[j * QUAD:j * QUAD + HD, odd::2, tokens])
            for j in range(HG) for odd in range(2)]


def attention_stage(k, name, q_store, k_store, values, nq, nk, scale, att, head_dim=HD, slopes=None, mask=None, spans=None, dense_att=None, carried=None,
                    finish=True):
    nc = k.nc
    causal, small = slopes is not None, head_dim == HD
    heads = HG if small else 2
    groups, strip = H // heads, P // heads
    nqt, nkt, wide = nq // P, nk // P, min(BANK, nk)
    nwide = nk // wide
    rows_a = STACK + (3 if causal else 0)
    rows_b = rows_a + 3
    chunks = [(qi, j, c) for qi in range(nqt) for j in range(heads) for c in range(nwide)]
    NCH, NS = len(chunks), nkt * heads
    slots = heads * nqt
    seeded = mask is not None or not small
    A_BANKS = 3 if mask is None else 2
    B_BANKS = 6 - A_BANKS
    A0, B0, ACC, SIDE = 0, A_BANKS, 6, 7
    LEAD = B_BANKS - 1
    WEIGHTS = 8
    ahead_tiles = WEIGHTS // heads
    spread_at = 1
    QUARTER = nq // 4
    SUMS = 2
    inverse_at = [(2 + p, 0) for p in range(4)]

    def chunks_of(i):
        some = list(range(i * NCH // nkt, (i + 1) * NCH // nkt))
        return [some[len(some) * j // heads:len(some) * (j + 1) // heads] for j in range(heads)]

    assert not seeded or groups * NS % B_BANKS == 0 and groups * NCH % A_BANKS == 0
    by_vector = [s for s in range(NS) if mask is not None and s % 4 == 1]
    by_scalar = [s for s in range(NS) if s not in by_vector]

    def step_after(b, g, s):
        return (b, g, s + LEAD) if s + LEAD < NS else (b + (g + 1) // groups, (g + 1) % groups, s + LEAD - NS)

    with ExitStack() as held:
        def sb(what, shape, dt):
            return held.enter_context(nc.sbuf_tensor(f"{name}_{what}", shape, dt))

        RING, V_RING = 4, 2
        if small:
            q_stack = [sb(f"q{r}", [rows_b, heads, nq], BF16) for r in range(RING)]
            k_stack = [sb(f"k{r}", [rows_b, heads, nk], BF16) for r in range(RING)]
        else:
            q_stack = [sb(f"q{r}", [P, 3, heads, nq], BF16) for r in range(RING)]
            k_stack = [sb(f"k{r}", [P, 2, heads, nk], BF16) for r in range(RING)]
            tops = sb("tops", [P, 2, heads, nq], F32)
            max_rows = nc.dram_tensor(f"{name}_max_rows", [2, slots, P], F32, kind="Internal").ap()
            weight_sums = sb("weight_sums", [P, 2, heads, nq], F32)
        v_tile = [sb(f"v{r}", [P, nkt, P], F32) for r in range(V_RING)]
        weights = sb("weights", [P, WEIGHTS, nq], F32)
        part_max = sb("part_max", [P, 2, slots, nwide], F32)
        row_max = sb("row_max", [P, 2, slots], F32)
        negative = sb("negative", [slots, 2, P], F32)
        if small:
            max_parts = sb("max_parts", [slots, 3, P], BF16)
            inverse = sb("inverse", [P, groups, nq], F32)
            dense, dense_inverse = (sb(what, [P, H * nq // P], F32) for what in ("dense", "dense_inverse"))
        else:
            sums, inverse = sb("sums", [P, SUMS, nq], F32), sb("inverse", [P, nq], F32)
        names = ["row_in", "row_made", "a_ready", "a_taken", "turned", "s_ready", "exp_done", "pv_done", "acc_copied",
                 "sums_ready", "inverted", "normed", "set_up", "negated", "max_split", "added", "sums_out", "dense_in",
                 "inverses_out", "inverses_in", "opened", "filled", "filled_by_vector", "made_dense"]
        if mask is not None:
            mask_q, mask_k = sb("mask_q", [P, nqt, nk], F32), sb("mask_k", [P, nkt, nq], F32)
            unused = sb("unused", [P, 2, wide], F32)
            held_back = sb("held_back", [1, 2], F32)
        all_names = names + [f"loaded{r}" for r in range(RING)] + [f"v_loaded{r}" for r in range(V_RING)] + (
            [f"mask_q{i}" for i in range(nqt)] + [f"mask_k{i}" for i in range(nkt // 2)] if mask is not None else [])
        (row_in, row_made, a_ready, a_taken, turned, s_ready, exp_done, pv_done, acc_copied, sums_ready, inverted, normed,
         set_up, negated, max_split, added, sums_out, dense_in, inverses_out, inverses_in, opened, filled, filled_by_vector, made_dense, *more) = held.enter_context(k.stage(*all_names))
        loaded, v_loaded, more = more[:RING], more[RING:RING + V_RING], more[RING + V_RING:]
        mask_q_in, mask_k_in = more[:nqt], more[nqt:]
        block = held.enter_context(nc.Block())

        def at(b, g, per_group, n):
            return b * (groups * per_group) + (g * per_group + n)

        def index(b, g):
            return b * groups + g if isinstance(b, int) else None

        n_carried = 0 if carried is None else 1

        def sums_of(b):
            if isinstance(b, int) and b < 0:
                return carried[0][:, :, (B - 1) * nq:B * nq]
            return att[:, :, bass.ds(b * nq, nq)]

        def to_finish(b):
            return small and (exists(b, 0) or (carried is not None and isinstance(b, int) and b == -1))

        def first(b, g, n=1):
            return index(b, g) is not None and index(b, g) < n

        def exists(b, g):
            return index(b, g) is None or 0 <= index(b, g) < B * groups

        def later(b, g, ahead):
            return b + (g + ahead) // groups, (g + ahead) % groups

        def keys_of(qi, c):
            if spans:
                return spans[qi]
            return slice(0, (qi + 1) * P) if causal else slice(c * wide, (c + 1) * wide)

        def queries_of(i):
            if spans:
                tiles = [qi for qi, keys in enumerate(spans) if keys.start <= i * P < keys.stop]
                return slice(tiles[0] * P, (tiles[-1] + 1) * P)
            return slice(i * P if causal else 0, nq)

        def opens(i):
            return i == 0 or (spans is not None and queries_of(i - 1) != queries_of(i))

        def for_groups(engine, body, lead=2, turns=B - 1):
            for g in range(lead):
                body(0, g)
            with engine.Fori(0, turns) as b:
                for g in range(lead, groups + lead):
                    body(b + g // groups, g % groups)
            for n in range(lead + turns * groups, B * groups):
                body(n // groups, n % groups)

        def loads_of(b, g):
            r, rows = g % RING, slice(g * heads * head_dim, (g + 1) * heads * head_dim)
            out = []
            if small:
                for stack, store, n in ((q_stack[r], q_store, nq), (k_stack[r], k_store, nk)):
                    out.append((stack[0:STACK, :, :], store[rows, :, bass.ds(b * n, n)].rearrange("(j d) t n -> (d t) j n", d=head_dim)))
            else:
                for stack, store, order, n in ((q_stack[r], q_store, (0, 0, 1, 1, 0, 2), nq), (k_stack[r], k_store, (0, 1, 2, 0), nk)):
                    out += [(stack[(t % 2) * head_dim:(t % 2 + 1) * head_dim, t // 2, :, :],
                             store[p, rows, bass.ds(b * n, n)].rearrange("(j d) n -> d j n", d=head_dim)) for t, p in enumerate(order)]
            if causal:
                out.append((k_stack[r][STACK:rows_a, :, :], slopes[:, g * heads:(g + 1) * heads, :]))
            return out

        n_loads = len(loads_of(0, 0))
        n_ones = RING * (2 if causal else 1)

        def loads_done(b, g):
            return 16 * n_loads * (b * (groups // RING) + (g // RING + 1))

        def v_done(b, g):
            return 16 * (b * (groups // V_RING) + (g // V_RING + 1))

        @block.sync
        def _(sync):
            k.clear_last_set(sync)

            def load_group(b, g):
                for tile, source in loads_of(b, g):
                    sync.dma_start(tile, source).then_inc(loaded[g % RING], 16)

            def load_values(b, g):
                sync.dma_start(v_tile[g % V_RING][:, :, :], values[bass.ds(b * nkt, nkt), :, g * P:(g + 1) * P].rearrange("i p c -> p i c")
                               ).then_inc(v_loaded[g % V_RING], 16)

            def load_mask_q(b, qi):
                sync.dma_start(mask_q[:, qi, :], mask[0][bass.ds(b, 1), qi * P:(qi + 1) * P, :].rearrange("o p n -> p (o n)")).then_inc(mask_q_in[qi], 16)

            def load_mask_k(b, i):
                sync.dma_start(mask_k[:, 2 * i:2 * i + 2, :], mask[1][bass.ds(b, 1), 2 * i * P:2 * (i + 1) * P, :].rearrange("o (i p) n -> p (o i) n", p=P)
                               ).then_inc(mask_k_in[i], 16)

            for g in range(2):
                load_group(0, g)
            if mask is not None:
                for qi in range(nqt):
                    load_mask_q(0, qi)
            for g in range(2):
                load_values(0, g)
            if mask is not None:
                for i in range(nkt // 2):
                    load_mask_k(0, i)
            for g in range(2, RING):
                load_group(0, g)

            def row(b, g):
                if small:
                    sync.wait_ge(row_made, at(b, g, 1, 1))
                    for p in range(3):
                        sync.dma_start(q_stack[g % RING][rows_a + p:rows_a + p + 1, :, :].rearrange("o j (i t) -> o (j i) t", t=P),
                                       max_parts[:, p, :]).then_inc(row_in, 16)
                else:
                    sync.wait_ge(negated, at(b, g, 1, 1))
                    sync.dma_start(max_rows[g % 2, :, :], negative[:, g % 2, :]).then_inc(row_made, 16)
                    sync.wait_ge(row_made, 16 * at(b, g, 1, 1))
                    sync.dma_start(tops[:, g % 2, :, :].rearrange("p j n -> p (j n)"),
                                   max_rows[g % 2, :, :].rearrange("s t -> (s t)").partition_broadcast(P)).then_inc(row_in, 16)

            def gather_sums(b):
                if exists(b, 0):
                    sync.wait_ge(acc_copied, at(b, groups, 1, 1))
                sync.dma_start(k.sums_of_weights, sums_of(b)[HD::QUAD, :, :]).then_inc(sums_out, 16)
                sync.wait_ge(sums_out, 16 * (b + n_carried + 1))
                sync.dma_start(dense[:, :], k.sums_of_weights.rearrange("j g (s n) -> (j g s) n", n=H * nq // P)).then_inc(dense_in, 16)

            def return_inverses(b):
                sync.wait_ge(normed, at(b + n_carried, 0, 1, SUMS))
                sync.wait_ge(inverses_in, 16 * heads * (b + n_carried) + 1)
                sync.wait_ge(inverted, b + n_carried + 1)
                sync.dma_start(k.inverse_sums.rearrange("j g (s n) -> (j g s) n", n=H * nq // P), dense_inverse[:, :]).then_inc(inverses_out, 16)
                sync.wait_ge(inverses_out, 16 * (b + n_carried + 1))
                for j in range(heads):
                    sync.dma_start(inverse[strip * j:strip * (j + 1), :, :], k.inverse_sums[j, :, :].partition_broadcast(strip)).then_inc(inverses_in, 16)

            def make_dense(b):
                sync.wait_ge(normed, at(b + n_carried, groups, 1, SUMS))
                if exists(b, 0):
                    pairs = dense_rows(dense_att, att, bass.ds(b * nq, nq))
                else:
                    pairs = dense_rows(carried[1], carried[0], slice((B - 1) * nq, B * nq))
                for destination, source in pairs:
                    sync.dma_start(destination, source).then_inc(made_dense, 16)

            row(0, 0)

            def group(b, g):
                before = later(b, g, -1)
                if exists(*before):
                    sync.wait_ge(pv_done, at(*before, nkt, nkt + ahead_tiles))
                    if exists(*later(b, g, 1)):
                        load_values(*later(b, g, 1))
                    if exists(*later(b, g, RING - 1)):
                        load_group(*later(b, g, RING - 1))
                if exists(*later(b, g, 1)):
                    row(*later(b, g, 1))
                if g == 0 and to_finish(b - 1):
                    gather_sums(b - 1)
                if g == 1 and to_finish(b - 1):
                    return_inverses(b - 1)
                if g == 3 and to_finish(b - 1):
                    make_dense(b - 1)
                if mask is not None and g == groups - 3 and exists(b + 1, 0):
                    for qi in range(nqt):
                        sync.wait_ge(a_taken, at(b, groups - 1, NCH + 1, (qi + 1) * NCH // nqt))
                        load_mask_q(b + 1, qi)
                if mask is not None and g == groups - 1 and exists(b + 1, 0):
                    for i in range(nkt // 2):
                        sync.wait_ge(exp_done, at(b, g, NS, 2 * (i + 1) * heads + 3))
                        load_mask_k(b + 1, i)

            for_groups(sync, group, lead=groups, turns=B - 2)
            if small and finish:
                gather_sums(B - 1)
                return_inverses(B - 1)
                make_dense(B - 1)
            if small:
                sync.wait_ge(made_dense, 16 * 2 * HG * (n_carried + (B if finish else B - 1)))

        @block.tensor
        def _(pe):
            def pass_a(b, g, some):
                r = g % RING
                for n in some:
                    qi, j, c = chunks[n]
                    if n == 0:
                        pe.wait_ge(loaded[r], loads_done(b, g))
                    if not (first(b, g) and n < A_BANKS):
                        pe.wait_ge(a_taken, at(b, g, NCH + 1, max(0, n - A_BANKS + 1)))
                    keys, qs = keys_of(qi, c), slice(qi * P, (qi + 1) * P)
                    out = k.ps[:, A0 + (g * NCH + n) % A_BANKS, 0:keys.stop - keys.start]
                    if small:
                        mm = nc.tensor.matmul(out, q_stack[r][0:rows_a, j, qs], k_stack[r][0:rows_a, j, keys], start=True, stop=not causal)
                    else:
                        mm = nc.tensor.matmul(out, q_stack[r][:, 0, j, qs], k_stack[r][:, 0, j, keys], start=True, stop=True)
                    if causal:
                        mm = nc.tensor.matmul(out[:, qi * P:(qi + 1) * P], k.ident_bf[:, :], k.above_q[:, :], start=False, stop=True)
                    mm.then_inc(a_ready, 1 if n < NCH - 1 else 2)

            def turn(b, g):
                pe.wait_ge(a_taken, at(b, g, NCH + 1, NCH + 1))
                if not first(b, g):
                    pe.wait_ge(negated, at(b, g, 1, 0))
                if not small and not first(b, g, 3):
                    pe.wait_ge(inverted, at(b, g, 4, -4))
                nc.tensor.transpose(k.ps[0:slots, SIDE, 0:P], row_max[:, g % 2, :], k.ident[:, :]).then_inc(turned, 1)

            def spread(b, g, last_turned):
                pe.wait_ge(acc_copied, at(b, g, 1, 2))
                pe.wait_ge(negated, last_turned)
                pe.wait_ge(inverted, at(b, g, 4, 4))
                pe.wait_ge(added, at(b, g, nkt, nkt + 4))
                for j in range(heads):
                    mm = nc.tensor.matmul(k.ps[strip * j:strip * (j + 1), SIDE, 0:nq], k.ones[:, 0:strip], weight_sums[:, g % 2, j, :],
                                          start=True, stop=True, tile_position=(0, strip * j))
                mm.then_inc(sums_ready, 1)

            def weigh(b, g, i):
                pe.wait_ge(exp_done, at(b, g, NS, (i + 1) * heads + 3))
                if i == 0:
                    pe.wait_ge(v_loaded[g % V_RING], v_done(b, g))
                    pe.wait_ge(acc_copied, at(b, g, 1, 1))
                qs = queries_of(i)
                for j in range(heads):
                    mm = nc.tensor.matmul(k.ps[strip * j:strip * (j + 1), ACC, qs], v_tile[g % V_RING][:, i, strip * j:strip * (j + 1)],
                                          weights[:, (g * NS + i * heads + j) % WEIGHTS, qs], start=opens(i), stop=i == nkt - 1,
                                          tile_position=(0, strip * j), skip_group_check=causal or spans is not None)
                mm.then_inc(pv_done, 1)

            if small:
                pe.wait_ge(set_up, 16 * n_ones)
            if seeded:
                pe.wait_ge(loaded[0], loads_done(0, 0))
                operands = (k_stack[0][0:STACK, 0, 0:P], q_stack[0][0:STACK, 0, :]) if small else (k_stack[0][:, 0, 0, 0:P], q_stack[0][:, 0, 0, :])
                for n in range(B_BANKS):
                    nc.tensor.matmul(k.ps[:, B0 + n, 0:nq], *operands, start=True, stop=False, skip_group_check=True).then_inc(opened, 1)
            pass_a(0, 0, range(NCH))
            turn(0, 0)
            pass_a(0, 1, range(NCH))

            def group(b, g):
                r = g % RING
                if small:
                    pe.wait_ge(row_in, 48 * at(b, g, 1, 1))
                for i in range(nkt):
                    more = chunks_of(i) if exists(*later(b, g, 2)) else [()] * heads
                    qs, ks = queries_of(i), slice(i * P, (i + 1) * P)
                    for j in range(heads):
                        s = i * heads + j
                        if s in by_vector:
                            pe.wait_ge(filled_by_vector, at(b, g, len(by_vector), by_vector.index(s) + 1))
                        elif seeded:
                            pe.wait_ge(filled, at(b, g, len(by_scalar), by_scalar.index(s) + 1))
                        else:
                            pe.wait_ge(exp_done, at(b, g, NS, 3 if g == s == 0 else s + 1))
                        out = k.ps[:, B0 + (g * NS + s) % B_BANKS, qs]
                        if small:
                            mm = nc.tensor.matmul(out, k_stack[r][0:rows_b, j, ks], q_stack[r][0:rows_b, j, qs], start=not seeded,
                                                  stop=not (causal or seeded), skip_group_check=seeded)
                        else:
                            for p, kp in enumerate((0, 0, 1)):
                                mm = nc.tensor.matmul(out, k_stack[r][:, kp, j, ks], q_stack[r][:, p, j, qs], start=False, stop=False, skip_group_check=True)
                        if causal:
                            mm = nc.tensor.matmul(out[:, 0:P], k.ident_bf[:, :], k.above_k[:, :], start=False, stop=True)
                        mm.then_inc(s_ready, 1)
                        pass_a(*later(b, g, 2), more[j])
                    if i:
                        weigh(b, g, i - 1)
                    elif exists(*later(b, g, -1)):
                        weigh(*later(b, g, -1), nkt - 1)
                    if i == 0 and exists(*later(b, g, 1)):
                        turn(*later(b, g, 1))
                    if i == spread_at and not small and exists(*later(b, g, -1)):
                        spread(*later(b, g, -1), at(b, g, 1, 2 if exists(*later(b, g, 1)) else 1))

            for_groups(pe, group)
            weigh(B - 1, groups - 1, nkt - 1)
            if not small:
                spread(B - 1, groups - 1, B * groups)

        @block.scalar
        def _(act):
            act.sem_inc(exp_done, 3)
            for r in range(RING if small else 0):
                act.dma_start(k_stack[r][rows_a:rows_b, :, :], k.rows_of_ones[:, :, 0:nk]).then_inc(set_up, 16)
                if causal:
                    act.dma_start(q_stack[r][STACK:rows_a, :, :], k.rows_of_ones[:, :, 0:nq]).then_inc(set_up, 16)

            def copy_sums(b, g):
                act.wait_ge(pv_done, at(b, g, nkt, nkt + ahead_tiles))
                if small:
                    out = att[:, g, bass.ds(b * nq, nq)]
                else:
                    act.wait_ge(normed, at(b, g, 1, 1))
                    out = sums[:, g % SUMS, :]
                nc.scalar.activation(out, k.ps[:, ACC, 0:nq], ACT.Copy).then_inc(acc_copied, 1)

            def fill(b, g, s):
                if mask is not None:
                    if g == 0:
                        act.wait_ge(mask_k_in[s // heads // 2], 16 * (b + 1))
                    seed = mask_k[:, s // heads, :]
                else:
                    if s == 0:
                        act.wait_ge(row_in, 16 * at(b, g, 1, 1))
                    seed = tops[:, g % 2, s % heads, :]
                nc.scalar.activation(k.ps[:, B0 + (g * NS + s) % B_BANKS, 0:nq], seed, ACT.Copy).then_inc(filled, 1)

            if seeded:
                act.wait_ge(opened, B_BANKS)
                for s in range(LEAD):
                    if s in by_scalar:
                        fill(0, 0, s)

            def group(b, g):
                for s in range(NS):
                    i = s // heads
                    qs = queries_of(i)
                    if s % heads == 0:
                        act.wait_ge(pv_done, at(b, g, nkt, i + 1))
                        if not small:
                            act.wait_ge(added, at(b, g, nkt, i + 1))
                    act.wait_ge(s_ready, at(b, g, NS, s + 1))
                    nc.scalar.activation(weights[:, (g * NS + s) % WEIGHTS, qs], k.ps[:, B0 + (g * NS + s) % B_BANKS, qs], ACT.Exp, scale=scale
                                         ).then_inc(exp_done, 1)
                    after = step_after(b, g, s)
                    if seeded and after[2] in by_scalar and exists(*after[:2]):
                        act.wait_ge(exp_done, at(b, g, NS, s + 3))
                        fill(*after)
                    if s == heads - 1 and exists(*later(b, g, -1)):
                        copy_sums(*later(b, g, -1))

            for_groups(act, group)
            copy_sums(B - 1, groups - 1)

        @block.vector
        def _(dve):
            dve.sem_inc(pv_done, ahead_tiles)
            dve.sem_inc(acc_copied, 1)
            if small:
                dve.sem_inc(inverses_in, 1)
            else:
                dve.sem_inc(inverted, 4)
            dve.sem_inc(normed, SUMS)

            def maxima(b, g, some):
                for n in some:
                    qi, j, c = chunks[n]
                    if n == 0 and not first(b, g, 2):
                        dve.wait_ge(turned, at(b, g, 1, -1))
                    keys, slot = keys_of(qi, c), j * nqt + qi
                    out = part_max[:, g % 2, slot, c:c + 1] if nwide > 1 else row_max[:, g % 2, slot:slot + 1]
                    scores = k.ps[:, A0 + (g * NCH + n) % A_BANKS, 0:keys.stop - keys.start]
                    if mask is not None:
                        if n % (NCH // nqt) == 0:
                            dve.wait_ge(mask_q_in[qi], 16 * (b + 1))
                        if not (first(b, g) and n < 2):
                            dve.wait_ge(a_taken, at(b, g, NCH + 1, max(n - 1, 0)))
                        dve.wait_ge(a_ready, at(b, g, NCH + 1, n + 1))
                        nc.vector.memset(held_back[:, n % 2:n % 2 + 1], 0.0)
                        nc.vector.tensor_tensor_reduce(unused[:, n % 2, :], scores, mask_q[:, qi, keys], 1.0, -3.0e38, ALU.add, ALU.max,
                                                       out).then_inc(a_taken, 1)
                    else:
                        dve.wait_ge(a_ready, at(b, g, NCH + 1, n + 1))
                        nc.vector.reduce_max(out, scores, AX).then_inc(a_taken, 1)
                    if n == NCH - 1:
                        dve.wait_ge(a_taken, at(b, g, NCH + 1, NCH))
                        if nwide > 1:
                            nc.vector.reduce_max(row_max[:, g % 2, :], part_max[:, g % 2, :, :], AX).then_inc(a_taken, 1)
                        else:
                            dve.sem_inc(a_taken, 1)

            def negate(b, g):
                dve.wait_ge(turned, at(b, g, 1, 1))
                if small:
                    if not first(b, g):
                        dve.wait_ge(row_made, at(b, g, 1, 0))
                        dve.wait_ge(row_in, 48 * at(b, g, 1, 0))
                    nc.vector.tensor_scalar(max_parts[:, 0, :], k.ps[0:slots, SIDE, 0:P], -1.0, None, ALU.mult)
                elif not first(b, g):
                    dve.wait_ge(row_in, 16 * at(b, g, 1, 0))
                nc.vector.tensor_scalar(negative[:, g % 2, :], k.ps[0:slots, SIDE, 0:P], -1.0, None, ALU.mult).then_inc(negated, 1)

            def fill(b, g, s, exponentiated):
                if g == 0:
                    dve.wait_ge(mask_k_in[s // heads // 2], 16 * (b + 1))
                dve.wait_ge(exp_done, exponentiated)
                nc.vector.tensor_copy(k.ps[:, B0 + (g * NS + s) % B_BANKS, 0:nq], mask_k[:, s // heads, :]).then_inc(filled_by_vector, 1)

            def invert_dense(b):
                dve.wait_ge(dense_in, 16 * (b + n_carried + 1))
                dve.wait_ge(inverses_in, 16 * heads * (b + n_carried) + 1)
                nc.vector.reciprocal(dense_inverse[:, :], dense[:, :]).then_inc(inverted, 1)

            def invert(b, g, quarter):
                if quarter == 0:
                    dve.wait_ge(sums_ready, at(b, g, 1, 1))
                    dve.wait_ge(normed, at(b, g, 1, SUMS))
                own = slice(quarter * QUARTER, (quarter + 1) * QUARTER)
                nc.vector.reciprocal(inverse[:, own], k.ps[:, SIDE, own]).then_inc(inverted, 1)

            if by_vector:
                dve.wait_ge(opened, B_BANKS)
                for s in range(LEAD):
                    if s in by_vector:
                        fill(0, 0, s, 1)
            maxima(0, 0, range(NCH))
            negate(0, 0)
            maxima(0, 1, range(NCH))

            def group(b, g):
                before = later(b, g, -1)
                for i in range(nkt):
                    more = chunks_of(i) if exists(*later(b, g, 2)) else [()] * heads
                    for j in range(heads):
                        after = step_after(b, g, i * heads + j)
                        if after[2] in by_vector and exists(*after[:2]):
                            fill(*after, at(b, g, NS, i * heads + j + 3))
                        maxima(*later(b, g, 2), more[j])
                        if (i, j) in inverse_at and not small and exists(*before):
                            invert(*before, inverse_at.index((i, j)))
                    if i == 0 and exists(*later(b, g, 1)):
                        negate(*later(b, g, 1))
                    if i == 0 and g == 1 and to_finish(b - 1):
                        invert_dense(b - 1)

            for_groups(dve, group, lead=2)
            if small:
                if finish:
                    invert_dense(B - 1)
            else:
                for quarter in range(4):
                    invert(B - 1, groups - 1, quarter)

        @block.gpsimd
        def _(pool):
            pool.sem_inc(added, 4)

            def split_max(b, g):
                own = negative[:, g % 2, :]
                pool.wait_ge(negated, at(b, g, 1, 1))
                nc.gpsimd.tensor_tensor(max_parts[:, 1, :], own, max_parts[:, 0, :], ALU.subtract).then_inc(max_split, 1)
                nc.gpsimd.tensor_tensor(own, own, max_parts[:, 0, :], ALU.subtract).then_inc(max_split, 1)
                pool.wait_ge(max_split, at(b, g, 2, 2))
                nc.gpsimd.tensor_tensor(max_parts[:, 2, :], own, max_parts[:, 1, :], ALU.subtract).then_inc(row_made, 1)

            def add_weights(b, g, i):
                pool.wait_ge(exp_done, at(b, g, NS, (i + 1) * heads + 3))
                total = weight_sums[:, g % 2, :, :]
                own, before = (weights[:, x:x + heads, :] for x in ((g * NS + i * heads) % WEIGHTS, (g * NS + (i - 1) * heads) % WEIGHTS))
                if i == 1:
                    pool.wait_ge(normed, at(b, g, 1, SUMS - 1))
                    nc.gpsimd.tensor_tensor(total, before, own, ALU.add).then_inc(added, 2)
                else:
                    pool.wait_ge(added, at(b, g, nkt, i + 4))
                    nc.gpsimd.tensor_tensor(total, total, own, ALU.add).then_inc(added, 1)

            def normalise(b, g):
                if small:
                    own, undivided, inverse_of = sums_of(b)[:, g, :], sums_of(b)[:, g, :], inverse[:, g, :]
                    pool.wait_ge(inverses_in, 16 * heads * (b + n_carried + 1) + 1)
                else:
                    own, undivided, inverse_of = att(g)[:, bass.ds(b * nq, nq)], sums[:, g % SUMS, :], inverse[:, :]
                    pool.wait_ge(inverted, at(b, g, 4, 8))
                nc.gpsimd.tensor_tensor(own, undivided, inverse_of, ALU.mult).then_inc(normed, 1)

            if small:
                split_max(0, 0)

            def group(b, g):
                for i in range(nkt):
                    if i and not small:
                        add_weights(b, g, i)
                    if small and i == 0 and exists(*later(b, g, 1)):
                        split_max(*later(b, g, 1))
                    if not small and i == 5 and exists(*later(b, g, -1)):
                        normalise(*later(b, g, -1))
                if g >= 2 and to_finish(b - 1):
                    normalise(b - 1, 2 * g - 4)
                    normalise(b - 1, 2 * g - 3)

            for_groups(pool, group, lead=groups, turns=B - 2)
            for g in range((groups if finish else 0) if small else 1):
                normalise(*(B - 1, g) if small else (B - 1, groups - 1))


def residual_norm_stage(k, products, bias=None, weights=(), x_scale=1.0, y_scale=1.0, value_bias=None, out=None, rows=None, relu=False, finish=None):
    nc = k.nc
    GROUP = 4
    last_batch, dense_shape = slice(T - S, T), [P, H * S // P]
    n = k.stages
    with (
        nc.sbuf_tensor(f"rn_z_{n}", [P, NT, C], F32) as z,
        nc.sbuf_tensor(f"rn_stats_{n}", [P, NT, 6], F32) as stats,
        nc.sbuf_tensor(f"rn_mean_var_{n}", [P, NT, 2], F32) as mean_var,
        nc.sbuf_tensor(f"rn_rstd_{n}", [P, 2, NT], F32) as rstd,
        nc.sbuf_tensor(f"rn_dense_{n}", dense_shape, F32) as dense,
        nc.sbuf_tensor(f"rn_dense_inverse_{n}", dense_shape, F32) as dense_inverse,
        nc.sbuf_tensor(f"rn_inverse_sums_{n}", [P, NG, S] if finish is not None else [P, 1, 1], F32) as inverse_sums,
        k.stage("weights", "biased", "prepared", "y_ready", "z_ready", "stats", "aggregated", "deviation", "inverse",
                "normed", "turned", "copied", "stored", "sums_out", "dense_in", "dense_inverted", "inverses_out", "inverses_in",
                "divided", "made_dense") as (
            weights_in, biased, prepared, y_ready, z_ready, stats_ready, aggregated, deviation, inverted, normed,
            turned, copied, stored, sums_out, dense_in, dense_inverted, inverses_out, inverses_in, divided, made_dense),
        nc.Block() as block,
    ):
        @block.sync
        def _(sync):
            k.clear_last_set(sync)
            for tile, source in weights:
                sync.dma_start(tile, source).then_inc(weights_in, 16)
            if finish is not None:
                sync.dma_start(k.sums_of_weights, finish[0][HD::QUAD, :, last_batch]).then_inc(sums_out, 16)
                sync.wait_ge(sums_out, 16)
                sync.dma_start(dense[:, :], k.sums_of_weights.rearrange("j g (s n) -> (j g s) n", n=dense_shape[1])).then_inc(dense_in, 16)
                sync.wait_ge(dense_inverted, 1)
                sync.dma_start(k.inverse_sums.rearrange("j g (s n) -> (j g s) n", n=dense_shape[1]), dense_inverse[:, :]).then_inc(inverses_out, 16)
                sync.wait_ge(inverses_out, 16)
                for j in range(HG):
                    sync.dma_start(inverse_sums[QUAD * j:QUAD * (j + 1), :, :], k.inverse_sums[j, :, :].partition_broadcast(QUAD)).then_inc(inverses_in, 16)
                sync.wait_ge(divided, NG)
                for destination, source in dense_rows(finish[1], finish[0], last_batch):
                    sync.dma_start(destination, source).then_inc(made_dense, 16)
            if out is not None:
                for t in range(0, NT, 4):
                    sync.wait_ge(normed, t + 4)
                    sync.dma_start(out[t * P:(t + 4) * P, :].rearrange("(t p) c -> p t c", p=P), k.X[:, t:t + 4, :]).then_inc(stored, 16)
                sync.wait_ge(stored, 16 * (NT // 4))

        @block.gpsimd
        def _(pool):
            if bias is not None and weights:
                pool.wait_ge(weights_in, 16 * len(weights))
            for t in range(NT if not relu else 0):
                if x_scale != 1.0:
                    nc.gpsimd.tensor_scalar(z[:, t, :], k.X[:, t, :], x_scale, None, ALU.mult).then_inc(biased, 1)
                    pool.wait_ge(biased, t + 1)
                    ins = nc.gpsimd.tensor_tensor(z[:, t, :], z[:, t, :], bias, ALU.add)
                elif bias is not None:
                    ins = nc.gpsimd.tensor_tensor(z[:, t, :], k.X[:, t, :], bias, ALU.add)
                elif rows is not None:
                    ins = nc.gpsimd.tensor_tensor(z[:, t, :], k.X[:, t, :], rows(t), ALU.add)
                else:
                    ins = nc.gpsimd.tensor_copy(z[:, t, :], k.X[:, t, :])
                ins.then_inc(prepared, 1)

        @block.tensor
        def _(pe):
            if weights:
                pe.wait_ge(weights_in, 16 * len(weights))
            for t in range(NT + GROUP):
                if t < NT and t % GROUP == 0:
                    if value_bias is not None:
                        pe.wait_ge(biased, CH * (t // GROUP + 1))
                    elif finish is not None and t == NT - GROUP:
                        pe.wait_ge(made_dense, 16 * 2 * HG)
                if t < NT and rows is None:
                    if t >= 4:
                        pe.wait_ge(z_ready, t - 3)
                    for i, (lhsT, rhs) in enumerate(products):
                        mm = nc.tensor.matmul(k.ps[:, t % 4, 0:C], lhsT(t), rhs, start=i == 0, stop=i == len(products) - 1)
                    mm.then_inc(y_ready, 1)
                if t % GROUP == GROUP - 1 and t >= GROUP and out is None:
                    for u in range(t + 1 - 2 * GROUP, t + 1 - GROUP):
                        pe.wait_ge(normed, u + 1)
                        if u >= 4:
                            pe.wait_ge(copied, u - 3)
                        for c in range(CH):
                            tr = nc.tensor.transpose(k.ps[:, 4 + u % 4, c * P:(c + 1) * P], k.X[:, u, c * P:(c + 1) * P], k.ident[:, :])
                        tr.then_inc(turned, 1)

        @block.vector
        def _(dve):
            if relu and weights:
                dve.wait_ge(weights_in, 16 * len(weights))
            for first in range(0, NT, GROUP):
                end = first + GROUP
                for t in range(first, end + 2):
                    if finish is not None and t == GROUP - 1:
                        dve.wait_ge(dense_in, 16)
                        nc.vector.reciprocal(dense_inverse[:, :], dense[:, :]).then_inc(dense_inverted, 1)
                    if t < end and relu:
                        dve.wait_ge(y_ready, t + 1)
                        nc.vector.tensor_tensor(z[:, t, :], k.ps[:, t % 4, 0:C], bias, ALU.add).then_inc(prepared, 1)
                        dve.wait_ge(prepared, t + 1)
                        nc.vector.scalar_tensor_tensor(z[:, t, :], z[:, t, :], 0.0, k.X[:, t, :], ALU.max, ALU.add).then_inc(z_ready, 1)
                    elif t < end and rows is None:
                        dve.wait_ge(prepared, t + 1)
                        dve.wait_ge(y_ready, t + 1)
                        nc.vector.scalar_tensor_tensor(z[:, t, :], k.ps[:, t % 4, 0:C], y_scale, z[:, t, :], ALU.mult, ALU.add).then_inc(z_ready, 1)
                    if first < t <= end:
                        dve.wait_ge(z_ready if rows is None else prepared, t)
                        nc.vector.bn_stats(stats[:, t - 1, :], z[:, t - 1, :]).then_inc(stats_ready, 1)
                    if t >= first + 2:
                        dve.wait_ge(stats_ready, t - 1)
                        nc.vector.bn_aggr(mean_var[:, t - 2, :], stats[:, t - 2, :]).then_inc(aggregated, 1)
                dve.wait_ge(deviation, end // GROUP)
                nc.vector.reciprocal(rstd[:, 1, first:end], rstd[:, 0, first:end]).then_inc(inverted, 1)
                dve.wait_ge(inverted, end // GROUP)
                if finish is not None and first == GROUP:
                    dve.wait_ge(inverses_in, 16 * HG)
                    for g in range(NG):
                        nc.vector.tensor_tensor(finish[0][:, g, last_batch], finish[0][:, g, last_batch], inverse_sums[:, g, :], ALU.mult
                                                ).then_inc(divided, 1)
                for t in range(first, end):
                    nc.vector.tensor_scalar(k.X[:, t, :], z[:, t, :], mean_var[:, t, 0:1], rstd[:, 1, t:t + 1], ALU.subtract,
                                            ALU.mult).then_inc(normed, 1)

        @block.scalar
        def _(act):
            def add_value_bias(b):
                if finish is not None and b == B - 1:
                    act.wait_ge(made_dense, 16 * 2 * HG)
                for g in range(CH):
                    own = value_bias[0][:, g, b * S:(b + 1) * S]
                    nc.scalar.activation(own, own, ACT.Identity, bias=value_bias[1][:, g:g + 1]).then_inc(biased, 1)

            if value_bias is not None:
                add_value_bias(0)
            for first in range(0, NT + GROUP, GROUP):
                if value_bias is not None and first // GROUP + 1 < B:
                    add_value_bias(first // GROUP + 1)
                if first < NT:
                    act.wait_ge(aggregated, first + GROUP)
                    own = slice(first, first + GROUP)
                    nc.scalar.activation(rstd[:, 0, own], mean_var[:, own, 1], ACT.Sqrt, bias=k.eps[0]).then_inc(deviation, 1)
                if first and out is None:
                    for t in range(first - GROUP, first):
                        act.wait_ge(turned, t + 1)
                        nc.scalar.activation(k.xT[:, :, t * P:(t + 1) * P], k.ps[:, 4 + t % 4, 0:C].rearrange("p (c n) -> p c n", c=CH),
                                             ACT.Copy).then_inc(copied, 1)


def merge_levels_stage(k, lvl, att, up, out_w, up_w, out_b, up_b, up_next, value_bias):
    nc = k.nc
    s_l = S >> lvl
    n = B * s_l
    wide = min(n, BANK)
    parts = [(m, w) for m in range(CH) for w in range(n // wide)]
    with (
        nc.sbuf_tensor(f"current_{lvl}", [P, CH, B, s_l], F32) as current,
        nc.sbuf_tensor(f"quarter_{lvl}", [P, CH * B, s_l], F32) as quarter,
        nc.sbuf_tensor(f"level_bias_{lvl}", [P, CH], F32) as level_bias,
        k.stage("values_biased", "bias_sum", "ready", "summed", "quartered", "upsampled") as (
            values_biased, bias_sum, ready, summed, quartered, upsampled),
        nc.Block(no_gpsimd_drain=True) as block,
    ):
        flat = current[:].rearrange("p c b s -> p c (b s)")
        rows = current[:].rearrange("p c b s -> p (c b) s")
        fine = up_next[:].rearrange("p c b (s two) -> p (c b) s two", two=2)

        @block.sync
        def _(sync):
            k.clear_last_set(sync)

        @block.tensor
        def _(pe):
            pe.wait_ge(values_biased, CH)
            for i, (m, w) in enumerate(parts):
                cols, chan = slice(w * wide, (w + 1) * wide), slice(m * P, (m + 1) * P)
                batches = slice(w * wide // s_l, (w + 1) * wide // s_l)
                terms = [(out_w[:, g, chan], att[:, g, batches, :]) for g in range(CH)]
                if up is not None:
                    terms += [(up_w[:, c, chan], up[:].rearrange("p c b s -> p c (b s)")[:, c, cols]) for c in range(CH)]
                for a, (lhsT, rhs) in enumerate(terms):
                    mm = nc.tensor.matmul(k.ps[:, i, 0:wide], lhsT, rhs, start=a == 0, stop=a == len(terms) - 1)
                mm.then_inc(ready, 1)

        @block.vector
        def _(dve):
            for g in range(CH):
                nc.vector.tensor_scalar(att[:, g, :, :], att[:, g, :, :], value_bias[:, g:g + 1], None, ALU.add).then_inc(values_biased, 1)
            if up is None:
                nc.vector.tensor_copy(level_bias[:], out_b).then_inc(bias_sum, 1)
            else:
                nc.vector.tensor_tensor(level_bias[:], out_b, up_b, ALU.add).then_inc(bias_sum, 1)
            dve.wait_ge(bias_sum, 1)
            for i, (m, w) in enumerate(parts):
                dve.wait_ge(ready, i + 1)
                nc.vector.tensor_scalar(flat[:, m, w * wide:(w + 1) * wide], k.ps[:, i, 0:wide], level_bias[:, m:m + 1], None,
                                        ALU.add).then_inc(summed, 1)
            dve.wait_ge(summed, len(parts))
            nc.vector.tensor_scalar(quarter[:], rows, 0.25, None, ALU.mult).then_inc(quartered, 1)
            nc.vector.tensor_copy(fine[:, :, 0:1, 0], rows[:, :, 0:1])
            nc.vector.tensor_copy(fine[:, :, s_l - 1:s_l, 1], rows[:, :, s_l - 1:s_l])
            dve.wait_ge(quartered, 1)
            nc.vector.scalar_tensor_tensor(fine[:, :, 1:s_l, 0], rows[:, :, 1:s_l], 0.75, quarter[:, :, 0:s_l - 1], ALU.mult, ALU.add)
            nc.vector.scalar_tensor_tensor(fine[:, :, 0:s_l - 1, 1], rows[:, :, 0:s_l - 1], 0.75, quarter[:, :, 1:s_l], ALU.mult,
                                           ALU.add).then_inc(upsampled, 1)


def pyramid_attention(k):
    nc, inp = k.nc, k.inp
    with ExitStack() as held:
        def sb(what, shape, dt=F32):
            return held.enter_context(nc.sbuf_tensor(f"pyr_{what}", shape, dt))

        att, att_coarse, dense_coarse = sb("att", [P, NG, T]), sb("att_coarse", [P, NG, T]), sb("dense_coarse", [P, CH, T])
        dense_att = k.xT
        place = {1: 0, 2: 256, 3: 384}
        bias = sb("bias", [P, 4, 3 * CH])
        vbias = sb("vbias", [P, 4, CH])
        q_coarse, k_coarse = (nc.dram_tensor(n, [C, 6, T], BF16, kind="Internal").ap() for n in ("q_coarse", "k_coarse"))
        v_coarse = nc.dram_tensor("v_coarse", [B * 4, P, H * QUAD], F32, kind="Internal").ap()
        q_parts, k_parts, values = k.q_parts[:, :, 0:T], k.k_parts[:, :, 0:T], k.values_of(NT, P)
        xs = k.xT[:].rearrange("p c (b s) -> p c b s", b=B)
        out_w, up_w, out_rows = sb("out_w", [P, 4, CH, C]), sb("up_w", [P, 3, CH, C]), sb("rows", [P, 2, C])
        out_b, up_b = sb("out_b", [P, 4, CH]), sb("up_b", [P, 3, CH])
        prefetch = [(out_w[:, lvl], inp["L0_out_w"][lvl]) for lvl in range(4)] + [(up_w[:, lvl], inp["L0_up_w"][lvl]) for lvl in range(3)]
        prefetch += [(out_rows[:], inp["L0_out_b0_up_b0"].partition_broadcast(P)), (out_b[:], inp["L0_out_b"]), (up_b[:], inp["L0_up_b"]),
                     (vbias[:], inp["L0_v_b"])]
        with nc.sbuf_tensor("pyr_wqkv", [P, 4, CH, 3 * C], F32) as w, nc.sbuf_tensor("pyr_zeros", [P, H * QUAD], F32) as zeros:
            memset_stage(k, (zeros[:], 0.0))
            units = []
            for store, col, order in ((q_parts, 0, Q_PART), (k_parts, C, K_PART)):
                units += split_units(lambda c, t: k.xT[:, c, t * BANK:(t + 1) * BANK], BANK, w[:, 0, :, col:col + C], bias[:, 0, col // P:col // P + CH],
                                     store, order)
            units += value_units(lambda c, t: k.xT[:, c, t * P:(t + 1) * P], P, w[:, 0, :, 2 * C:], values)
            fine_units = len(units)
            levels = (1, 2, 3)
            cols = {lvl: slice(place[lvl], place[lvl] + max(S >> lvl, P)) for lvl in levels}

            def tokens(lvl, c, b):
                own = xs[:, c, b, ::1 << lvl]
                return own if S >> lvl >= P else own.unsqueeze(1).broadcast_to((P, P // (S >> lvl), S >> lvl))

            for store, col, order in ((q_coarse, 0, Q_PART), (k_coarse, C, K_PART)):
                units += [("split", [(cols[lvl], w[:, lvl, c, col + m * P:col + (m + 1) * P], tokens(lvl, c, b), c == 0, c == CH - 1)
                                     for lvl in levels for c in range(CH)], S,
                           [(cols[lvl], bias[:, lvl, col // P + m:col // P + m + 1]) for lvl in levels],
                           stacked(store[m * P:(m + 1) * P, :, b * S:(b + 1) * S], order)) for b in range(B) for m in range(CH)]
            for lvl in levels:
                n = min(S >> lvl, P)

                def rows(c, t, lvl=lvl, n=n):
                    b, i = divmod(t, (S >> lvl) // n)
                    return xs[:, c, b, (i * n) << lvl:((i + 1) * n) << lvl:1 << lvl]

                tiles = [v_coarse[b * 4 + place[lvl] // P + i, 0:n, :] for b in range(B) for i in range((S >> lvl) // n)]
                units += value_units(rows, n, w[:, lvl, :, 2 * C:], tiles)
            project_stage(k, units, [(w[:, 0], inp["L0_in_w"][0]), (bias[:], inp["L0_in_b"])],
                          [(v_coarse[b * 4 + 3, S >> 3:P, :], zeros[S >> 3:P, :]) for b in range(B)],
                          late=[(w[:, lvl], inp["L0_in_w"][lvl]) for lvl in levels], late_unit=fine_units, prefetch=prefetch)
        attention_stage(k, "pyr_coarse", q_coarse, k_coarse, v_coarse, S, S, HD ** -0.5, att_coarse, dense_att=dense_coarse,
                        spans=[slice(0, 256), slice(0, 256), slice(256, 384), slice(384, 512)], finish=False)
        attention_stage(k, "pyr_core", q_parts, k_parts, values, S, S, HD ** -0.5, att, dense_att=dense_att,
                        carried=(att_coarse, dense_coarse), finish=False)
        coarse = dense_coarse[:].rearrange("p g (b s) -> p g b s", b=B)
        up = [None] + [sb(f"up{lvl}", [P, CH, B, S >> (lvl - 1)]) for lvl in (3, 2, 1)]
        for i, lvl in enumerate((3, 2, 1)):
            merge_levels_stage(k, lvl, coarse[:, :, :, place[lvl]:place[lvl] + (S >> lvl)], up[i], out_w[:, lvl], up_w[:, min(lvl, 2)], out_b[:, lvl, :],
                               up_b[:, min(lvl, 2), :], up[i + 1], vbias[:, lvl, :])
        add_rows_stage(k, out_rows)
        fine = up[3][:].rearrange("p c b s -> p c (b s)")
        products = [(lambda t, c=c: dense_att[:, c, t * P:(t + 1) * P], out_w[:, 0, c, :]) for c in range(CH)]
        products += [(lambda t, c=c: fine[:, c, t * P:(t + 1) * P], up_w[:, 0, c, :]) for c in range(CH)]
        residual_norm_stage(k, products, out_rows[:, 0, :], value_bias=(dense_att, vbias[:, 0, :]), finish=(att, dense_att))


def add_rows_stage(k, rows):
    nc = k.nc
    with k.stage("added") as (added,), nc.Block(no_gpsimd_drain=True) as block:
        @block.sync
        def _(sync):
            k.clear_last_set(sync)

        @block.vector
        def _(dve):
            nc.vector.tensor_tensor(rows[:, 0, :], rows[:, 0, :], rows[:, 1, :], ALU.add).then_inc(added, 1)


def self_or_cross_attention(k, name, source, weights, nk, slopes=None):
    nc, inp = k.nc, k.inp
    w_name, b_name, out_name, out_b, v_b = weights
    with nc.sbuf_tensor(f"{name}_att", [P, NG, T], F32) as att, nc.sbuf_tensor(f"{name}_vb", [P, CH], F32) as vb, \
            nc.sbuf_tensor(f"{name}_ow", [P, CH, C], F32) as ow, nc.sbuf_tensor(f"{name}_ob", [P, C], F32) as ob:
        q_parts, k_parts, values = k.q_parts[:, :, 0:T], k.k_parts[:, :, 0:B * nk], k.values_of(B * nk // P, P)
        with nc.sbuf_tensor(f"{name}_w", [P, CH, 3 * C], F32) as w, nc.sbuf_tensor(f"{name}_b", [P, 2 * CH], F32) as bias, \
                nc.sbuf_tensor(f"{name}_src", [P, CH, TC if source is None else 1], F32) as ctxT:
            loads = [(w[:], inp[w_name])]
            prefetch = [(ow[:], inp[out_name]), (ob[:], inp[out_b].partition_broadcast(P))]
            late = []
            if source is None:
                source = ctxT
                late = [(ctxT[:], inp["ctxT"])]
            if b_name:
                loads.append((bias[:], inp[b_name]))
                prefetch.append((vb[:], inp[v_b]))
            project_stage(
                k, split_units(lambda c, t: k.xT[:, c, t * BANK:(t + 1) * BANK], BANK, w[:, :, 0:C],
                               bias[:, 0:CH] if b_name else None, q_parts, Q_PART)
                + split_units(lambda c, t: source[:, c, t * BANK:(t + 1) * BANK], BANK, w[:, :, C:2 * C],
                              bias[:, CH:] if b_name else None, k_parts, K_PART)
                + value_units(lambda c, t: source[:, c, t * P:(t + 1) * P], P, w[:, :, 2 * C:], values), loads,
                late=late, late_unit=T // BANK * CH, prefetch=prefetch)
        dense_att = k.xT
        attention_stage(k, f"{name}_core", q_parts, k_parts, values, S, nk, HD ** -0.5, att, slopes=slopes, dense_att=dense_att, finish=False)
        residual_norm_stage(k, [(lambda t, c=c: dense_att[:, c, t * P:(t + 1) * P], ow[:, c, :]) for c in range(CH)], ob[:],
                            value_bias=(dense_att, vb) if b_name else None, finish=(att, dense_att))


def norm_rows_stage(k, tiles, dest, gamma, beta, eps, products=None, source=None, add=None, relu_eps=None, row_scale=None,
                    destT=None, weights=(), pieces=(), prefetch=()):
    nc = k.nc
    n = k.stages
    GROUP = 4
    groups = tiles // GROUP
    per_piece = tiles // len(pieces) if pieces else 0
    with (
        nc.sbuf_tensor(f"nr_z_{n}", [P, tiles if source is None else 1, C], F32) as z,
        nc.sbuf_tensor(f"nr_stats_{n}", [P, tiles, 6], F32) as stats,
        nc.sbuf_tensor(f"nr_mean_var_{n}", [P, tiles, 2], F32) as mean_var,
        nc.sbuf_tensor(f"nr_rstd_{n}", [P, 2, tiles], F32) as rstd,
        k.stage("weights", "y_ready", "z_ready", "stats", "aggregated", "deviation", "inverse", "centred", "normed",
                "rectified", "scaled", "turned", "copied", "prefetched", *(f"piece{i}" for i in range(len(pieces)))) as (
            weights_in, y_ready, z_ready, stats_ready, aggregated, deviation, inverted, centred, normed, rectified, scaled,
            turned, copied, prefetched, *piece_in),
        nc.Block() as block,
    ):
        def rows(t):
            return z[:, t, :] if source is None else source(t)

        def of(group):
            return range(group * GROUP, (group + 1) * GROUP) if 0 <= group < groups else ()

        on_pool = relu_eps is not None or row_scale is not None
        done = scaled if on_pool else normed

        @block.sync
        def _(sync):
            k.clear_last_set(sync)
            for tile, src in weights:
                sync.dma_start(tile, src).then_inc(weights_in, 16)
            for (tile, src), landed in zip(pieces, piece_in):
                sync.dma_start(tile, src).then_inc(landed, 16)
            for tile, src in prefetch:
                sync.dma_start(tile, src).then_inc(prefetched, 16)
            if prefetch:
                sync.wait_ge(prefetched, 16 * len(prefetch))

        @block.tensor
        def _(pe):
            if products is not None and weights:
                pe.wait_ge(weights_in, 16 * len(weights))
            for group in range(groups + 3):
                if products is not None:
                    for t in of(group):
                        if pieces and t % per_piece == 0:
                            pe.wait_ge(piece_in[t // per_piece], 16)
                        if t >= 4:
                            pe.wait_ge(z_ready, t - 3)
                        for i, (lhsT, rhs) in enumerate(products):
                            mm = nc.tensor.matmul(k.ps[:, t % 4, 0:C], lhsT(t), rhs, start=i == 0, stop=i == len(products) - 1)
                        mm.then_inc(y_ready, 1)
                if destT is not None:
                    for t in of(group - 3):
                        pe.wait_ge(done, t + 1)
                        if t >= 4:
                            pe.wait_ge(copied, t - 3)
                        for c in range(CH):
                            tr = nc.tensor.transpose(k.ps[:, 4 + t % 4, c * P:(c + 1) * P], dest(t)[:, c * P:(c + 1) * P], k.ident[:, :])
                        tr.then_inc(turned, 1)

        @block.vector
        def _(dve):
            if weights:
                dve.wait_ge(weights_in, 16 * len(weights))
            for group in range(groups + 1):
                own = of(group)
                for t in own:
                    if add is not None:
                        dve.wait_ge(y_ready, t + 1)
                        nc.vector.tensor_tensor(z[:, t, :], k.ps[:, t % 4, 0:C], add(t), ALU.add).then_inc(z_ready, 1)
                    if products is not None:
                        dve.wait_ge(z_ready, t + 1)
                    elif pieces and t % per_piece == 0:
                        dve.wait_ge(piece_in[t // per_piece], 16)
                    nc.vector.bn_stats(stats[:, t, :], rows(t)).then_inc(stats_ready, 1)
                for t in own:
                    dve.wait_ge(stats_ready, t + 1)
                    nc.vector.bn_aggr(mean_var[:, t, :], stats[:, t, :]).then_inc(aggregated, 1)
                last = of(group - 1)
                for t in last:
                    if t == last[0]:
                        dve.wait_ge(deviation, group)
                        nc.vector.reciprocal(rstd[:, 1, t:t + GROUP], rstd[:, 0, t:t + GROUP]).then_inc(inverted, 1)
                    nc.vector.scalar_tensor_tensor(dest(t), rows(t), mean_var[:, t, 0:1], gamma, ALU.subtract, ALU.mult).then_inc(centred, 1)
                for t in last:
                    if t == last[0]:
                        dve.wait_ge(inverted, group)
                    dve.wait_ge(centred, t + 1)
                    nc.vector.scalar_tensor_tensor(dest(t), dest(t), rstd[:, 1, t:t + 1], beta, ALU.mult, ALU.add).then_inc(normed, 1)

        @block.scalar
        def _(act):
            for group in range(groups + 3):
                if products is not None and add is None:
                    for t in of(group):
                        act.wait_ge(y_ready, t + 1)
                        nc.scalar.activation(z[:, t, :], k.ps[:, t % 4, 0:C], ACT.Copy).then_inc(z_ready, 1)
                last = of(group - 1)
                if last:
                    act.wait_ge(aggregated, last[-1] + 1)
                    nc.scalar.activation(rstd[:, 0, last[0]:last[-1] + 1], mean_var[:, last[0]:last[-1] + 1, 1], ACT.Sqrt,
                                         bias=eps).then_inc(deviation, 1)
                if relu_eps is not None:
                    for t in of(group - 2):
                        act.wait_ge(normed, t + 1)
                        nc.scalar.activation(dest(t), dest(t), ACT.Relu).then_inc(rectified, 1)
                if destT is not None:
                    for t in of(group - 3):
                        act.wait_ge(turned, t + 1)
                        nc.scalar.activation(destT(t), k.ps[:, 4 + t % 4, 0:C].rearrange("p (c n) -> p c n", c=CH), ACT.Copy).then_inc(copied, 1)

        @block.gpsimd
        def _(pool):
            if row_scale is not None and weights:
                pool.wait_ge(weights_in, 16 * len(weights))
            for t in range(tiles if on_pool else 0):
                if relu_eps is None:
                    pool.wait_ge(normed, t + 1)
                    nc.gpsimd.tensor_scalar(dest(t), dest(t), row_scale(t), None, ALU.mult).then_inc(scaled, 1)
                else:
                    pool.wait_ge(rectified, t + 1)
                    if row_scale is None:
                        nc.gpsimd.tensor_scalar(dest(t), dest(t), relu_eps, None, ALU.add).then_inc(scaled, 1)
                    else:
                        nc.gpsimd.tensor_scalar(dest(t), dest(t), relu_eps, row_scale(t), ALU.add, ALU.mult).then_inc(scaled, 1)


def linear_attention_stage(k, keys, values, queryT, att, key_tiles, den_eps=None, attT=None, regroup=None):
    nc = k.nc
    n = k.stages
    with (
        nc.sbuf_tensor(f"la_state_{n}", [P, B, CH, P], F32) as state,
        nc.sbuf_tensor(f"la_sums_{n}", [P, B, CH, 2], F32) as sums,
        nc.sbuf_tensor(f"la_sum_cols_{n}", [P, B, CH, H], F32) as sum_cols,
        nc.sbuf_tensor(f"la_den_{n}", [P, NT, 2, H], F32) as den,
        k.stage("state_ready", "summed", "state_taken", "ready", "shifted", "inverse", "taken", "turned", "copied", "stored",
                "regrouped") as (state_ready, summed, state_taken, ready, shifted, inverted, taken, turned, copied, stored, regrouped),
        nc.Block(no_gpsimd_drain=True) as block,
    ):
        pairs = [(b, m) for b in range(B) for m in range(CH)]
        per_pair = 1 if den_eps is None else 2

        @block.sync
        def _(sync):
            k.clear_last_set(sync)
            if regroup is not None:
                per = NT // B
                for t in range(NT):
                    sync.wait_ge(taken, t + 1)
                    sync.dma_start(regroup[t // per, :, t % per * P:(t % per + 1) * P, :].rearrange("h n e -> n h e"),
                                   att(t).rearrange("p (h e) -> p h e", h=H)).then_inc(stored, 16)
                sync.wait_ge(stored, 16 * NT)
                flat = regroup.rearrange("b h n e -> (b h n e)").rearrange("(t p c) -> t p c", p=P, c=C)
                for t in range(NT):
                    sync.dma_start(att(t), flat[t]).then_inc(regrouped, 16)

        @block.tensor
        def _(pe):
            for n, (b, m) in enumerate(pairs):
                if n >= 4:
                    pe.wait_ge(state_taken, per_pair * (n - 3))
                for i in range(key_tiles):
                    t = b * key_tiles + i
                    mm = nc.tensor.matmul(k.ps[:, n % 4, 0:C + 1], keys(t)[:, m * P:(m + 1) * P], values(t), start=i == 0,
                                          stop=i == key_tiles - 1)
                mm.then_inc(state_ready, 1)
            pe.wait_ge(state_taken, per_pair * len(pairs))
            for t in range(NT):
                b = t // (NT // B)
                if t >= 4:
                    pe.wait_ge(taken, t - 3)
                for m in range(CH):
                    q = queryT[:, m, t * P:(t + 1) * P]
                    mm = nc.tensor.matmul(k.ps[:, 4 + t % 4, m * P:(m + 1) * P], q, state[:, b, m, :], start=m == 0, stop=den_eps is None,
                                          skip_group_check=True)
                    if den_eps is not None:
                        mm = nc.tensor.matmul(k.ps[:, 4 + t % 4, C:C + H], q, sum_cols[:, b, m, :], start=False, stop=m == CH - 1,
                                              skip_group_check=True)
                mm.then_inc(ready, 1)
            if attT is not None:
                if regroup is not None:
                    pe.wait_ge(regrouped, 16 * NT)
                for t in range(NT):
                    pe.wait_ge(taken, t + 1)
                    if t >= 4:
                        pe.wait_ge(copied, t - 3)
                    for c in range(CH):
                        tr = nc.tensor.transpose(k.ps[:, t % 4, c * P:(c + 1) * P], att(t)[:, c * P:(c + 1) * P], k.ident[:, :])
                    tr.then_inc(turned, 1)

        @block.vector
        def _(dve):
            for n, (b, m) in enumerate(pairs):
                dve.wait_ge(state_ready, n + 1)
                nc.vector.tensor_copy(sums[:, b, m, 0:1], k.ps[:, n % 4, C:C + 1]).then_inc(summed, 1)
                dve.wait_ge(summed, 2 * n + 1)
                if den_eps is None:
                    nc.vector.reciprocal(sums[:, b, m, 1:2], sums[:, b, m, 0:1]).then_inc(summed, 1)
                    dve.wait_ge(summed, 2 * n + 2)
                    nc.vector.scalar_tensor_tensor(state[:, b, m, :], k.ps[:, n % 4, m * P:(m + 1) * P], sums[:, b, m, 1:2],
                                                   k.head_blocks[:, :], ALU.mult, ALU.mult).then_inc(state_taken, 1)
                else:
                    nc.vector.tensor_scalar(sum_cols[:, b, m, :], k.head_cols[:, m, :], sums[:, b, m, 0:1], None, ALU.mult).then_inc(summed, 1)
                    nc.vector.tensor_tensor(state[:, b, m, :], k.ps[:, n % 4, m * P:(m + 1) * P], k.head_blocks[:, :], ALU.mult).then_inc(state_taken, 2)
            if den_eps is not None:
                dve.wait_ge(summed, 2 * len(pairs))
            for t in range(NT):
                dve.wait_ge(ready, t + 1)
                if den_eps is None:
                    nc.vector.tensor_copy(att(t), k.ps[:, 4 + t % 4, 0:C]).then_inc(taken, 1)
                else:
                    nc.vector.tensor_scalar(den[:, t, 0, :], k.ps[:, 4 + t % 4, C:C + H], den_eps, None, ALU.add).then_inc(shifted, 1)
                    dve.wait_ge(shifted, t + 1)
                    nc.vector.reciprocal(den[:, t, 1, :], den[:, t, 0, :]).then_inc(inverted, 1)
                    dve.wait_ge(inverted, t + 1)
                    nc.vector.tensor_tensor(att(t).rearrange("p (h d) -> p h d", h=H), k.ps[:, 4 + t % 4, 0:C].rearrange("p (h d) -> p h d", h=H),
                                            den[:, t, 1, :].unsqueeze(2).broadcast_to((P, H, HD)), ALU.mult).then_inc(taken, 1)

        @block.scalar
        def _(act):
            if attT is not None:
                for t in range(NT):
                    act.wait_ge(turned, t + 1)
                    nc.scalar.activation(attT(t), k.ps[:, t % 4, 0:C].rearrange("p (c n) -> p c n", c=CH), ACT.Copy).then_inc(copied, 1)


def memset_stage(k, *tiles):
    nc = k.nc
    with k.stage("filled") as (filled,), nc.Block(no_gpsimd_drain=True) as block:
        @block.sync
        def _(sync):
            k.clear_last_set(sync)

        @block.vector
        def _(dve):
            for tile, value in tiles:
                nc.vector.memset(tile, value).then_inc(filled, 1)


def add_norm_stage(k, y):
    residual_norm_stage(k, None, rows=y)


def relu_kernel_attention(k):
    nc, inp = k.nc, k.inp
    with ExitStack() as held:
        def sb(what, shape):
            return held.enter_context(nc.sbuf_tensor(f"rk_{what}", shape, F32))

        gain, mask = sb("gain", [P, 3, C]), sb("mask", [P, NTC])
        w = sb("w", [P, 4, CH, C])
        qT, y = sb("qT", [P, CH, T]), sb("y", [P, NT, C])
        gamma, beta = gain[:, 0, :], gain[:, 1, :]
        with nc.sbuf_tensor("rk_keys", [P, NTC, C], F32) as keys, nc.sbuf_tensor("rk_values", [P, NTC, C + 1], F32) as values, \
                nc.sbuf_tensor("rk_ctxT", [P, CH, TC], F32) as ctxT:
            loads = [(w[:], inp["L0x_w"]), (gain[:], inp["L0x_rows"].partition_broadcast(P)), (mask[:], inp["mask_tokens"])]
            ctx_pieces = [(ctxT[:, :, i * SC:(i + 1) * SC], inp["ctxT"][:, :, i * SC:(i + 1) * SC]) for i in range(B)]

            def ctx(c):
                return lambda t: ctxT[:, c, t * P:(t + 1) * P]

            memset_stage(k, (values[:, :, C:C + 1], 1.0))
            norm_rows_stage(k, NTC, lambda t: keys[:, t, :], gamma, beta, k.eps[1], [(ctx(c), w[:, 1, c, :]) for c in range(CH)],
                            relu_eps=1e-6, row_scale=lambda t: mask[:, t:t + 1], weights=loads, pieces=ctx_pieces)
            norm_rows_stage(k, NTC, lambda t: values[:, t, 0:C], gamma, beta, k.eps[1], [(ctx(c), w[:, 2, c, :]) for c in range(CH)],
                            row_scale=lambda t: mask[:, t:t + 1])
            norm_rows_stage(k, NT, lambda t: y[:, t, :], gamma, beta, k.eps[1],
                            [(lambda t, c=c: k.xT[:, c, t * P:(t + 1) * P], w[:, 0, c, :]) for c in range(CH)],
                            relu_eps=1e-6, destT=lambda t: qT[:, :, t * P:(t + 1) * P])
            linear_attention_stage(k, lambda t: keys[:, t, :], lambda t: values[:, t, :], qT, lambda t: y[:, t, :], NTC // B,
                                   den_eps=1e-6, attT=lambda t: qT[:, :, t * P:(t + 1) * P], regroup=k.regroup)
        norm_rows_stage(k, NT, lambda t: y[:, t, :], gamma, beta, k.eps[1],
                        [(lambda t, c=c: qT[:, c, t * P:(t + 1) * P], w[:, 3, c, :]) for c in range(CH)], add=lambda t: gain[:, 2, :])
        add_norm_stage(k, lambda t: y[:, t, :])


def softmax_features_stage(k, w, rows, k_bias, queries, qT, keys, values, loads):
    nc = k.nc
    n_k = CH * B
    with (
        nc.sbuf_tensor("sf_keysT", [P, CH, T], F32) as keysT,
        nc.sbuf_tensor("sf_top", [P, 2, n_k], F32) as top,
        nc.sbuf_tensor("sf_head", [P, 3, NT * H], F32) as head,
        k.stage("weights", "ready", "taken", "k_top", "k_exp", "q_top", "q_shifted", "q_exp", "q_sum", "q_inverse",
                "q_done", "turned", "copied") as (weights_in, ready, taken, k_top, k_exp, q_top, q_shifted, q_exp, q_sum, q_inverse,
                                                  q_done, turned, copied),
        nc.Block() as block,
    ):
        units = [("q", t) for t in range(NT)] + [("k", u) for u in range(n_k)] + [("v", t) for t in range(NT)]
        heads = queries[:].rearrange("p t (h d) -> p (t h) d", d=HD)
        turns = [("q", t) for t in range(NT)] + [("k", t) for t in range(NT)]

        def spread(i):
            return head[:, i, :].unsqueeze(2).broadcast_to((P, NT * H, HD))

        @block.sync
        def _(sync):
            k.clear_last_set(sync)
            for tile, src in loads:
                sync.dma_start(tile, src).then_inc(weights_in, 16)

        @block.tensor
        def _(pe):
            pe.wait_ge(weights_in, 16 * len(loads))
            for n, (kind, i) in enumerate(units):
                if n >= 4:
                    pe.wait_ge(taken, n - 3)
                for c in range(CH):
                    if kind == "k":
                        m, b = divmod(i, B)
                        out, lhsT, rhs = k.ps[:, n % 4, :], w[:, 1, c, m * P:(m + 1) * P], k.xT[:, c, b * S:(b + 1) * S]
                    else:
                        out, lhsT = k.ps[:, n % 4, 0:C], k.xT[:, c, i * P:(i + 1) * P]
                        rhs = w[:, 0 if kind == "q" else 2, c, :]
                    mm = nc.tensor.matmul(out, lhsT, rhs, start=c == 0, stop=c == CH - 1)
                mm.then_inc(ready, 1)
            pe.wait_ge(q_done, 1)
            for n, (kind, t) in enumerate(turns):
                if kind == "k" and t == 0:
                    pe.wait_ge(k_exp, n_k)
                if n >= 4:
                    pe.wait_ge(copied, n - 3)
                for c in range(CH):
                    src = queries[:, t, c * P:(c + 1) * P] if kind == "q" else keysT[:, c, t * P:(t + 1) * P]
                    tr = nc.tensor.transpose(k.ps[:, 4 + n % 4, c * P:(c + 1) * P], src, k.ident[:, :])
                tr.then_inc(turned, 1)

        @block.vector
        def _(dve):
            dve.wait_ge(weights_in, 16 * len(loads))
            for n, (kind, i) in enumerate(units):
                dve.wait_ge(ready, n + 1)
                if kind == "q":
                    ins = nc.vector.tensor_tensor(queries[:, i, :], k.ps[:, n % 4, 0:C], rows[:, 0, :], ALU.add)
                elif kind == "k":
                    m, b = divmod(i, B)
                    ins = nc.vector.tensor_scalar(keysT[:, m, b * S:(b + 1) * S], k.ps[:, n % 4, :], k_bias[:, m:m + 1], None, ALU.add)
                else:
                    ins = nc.vector.tensor_tensor(values[:, i, 0:C], k.ps[:, n % 4, 0:C], rows[:, 1, :], ALU.add)
                ins.then_inc(taken, 1)
                if n == NT:
                    dve.wait_ge(taken, NT)
                    nc.vector.reduce_max(head[:, 0, :], heads, AX).then_inc(q_top, 1)
                if n == NT + n_k:
                    dve.wait_ge(taken, NT + n_k)
                    nc.vector.reduce_max(top[:, 0, :], keysT[:].rearrange("p c (b s) -> p (c b) s", b=B), AX).then_inc(k_top, 1)
                    dve.wait_ge(k_top, 1)
                    nc.vector.tensor_scalar(top[:, 1, :], top[:, 0, :], -1.0, None, ALU.mult).then_inc(k_top, 1)
            dve.wait_ge(q_exp, 1)
            nc.vector.reduce_sum(head[:, 1, :], heads, AX).then_inc(q_sum, 1)
            dve.wait_ge(q_sum, 1)
            nc.vector.reciprocal(head[:, 2, :], head[:, 1, :]).then_inc(q_inverse, 1)
            dve.wait_ge(q_inverse, 1)
            nc.vector.tensor_tensor(heads, heads, spread(2), ALU.mult).then_inc(q_done, 1)

        @block.gpsimd
        def _(pool):
            pool.wait_ge(q_top, 1)
            nc.gpsimd.tensor_tensor(heads, heads, spread(0), ALU.subtract).then_inc(q_shifted, 1)

        @block.scalar
        def _(act):
            act.wait_ge(q_shifted, 1)
            nc.scalar.activation(queries[:], queries[:], ACT.Exp).then_inc(q_exp, 1)
            act.wait_ge(k_top, 2)
            for u in range(n_k):
                m, b = divmod(u, B)
                part = keysT[:, m, b * S:(b + 1) * S]
                nc.scalar.activation(part, part, ACT.Exp, bias=top[:, 1, u:u + 1]).then_inc(k_exp, 1)
            for n, (kind, t) in enumerate(turns):
                act.wait_ge(turned, n + 1)
                dst = qT[:, :, t * P:(t + 1) * P] if kind == "q" else keys[:, t, :].rearrange("p (c n) -> p c n", c=CH)
                nc.scalar.activation(dst, k.ps[:, 4 + n % 4, 0:C].rearrange("p (c n) -> p c n", c=CH), ACT.Copy).then_inc(copied, 1)


def softmax_linear_attention(k):
    nc, inp = k.nc, k.inp
    with ExitStack() as held:
        def sb(what, shape):
            return held.enter_context(nc.sbuf_tensor(f"sl_{what}", shape, F32))

        w, rows, k_bias = sb("w", [P, 4, CH, C]), sb("rows", [P, 5, C]), sb("k_bias", [P, CH])
        qT, att = sb("qT", [P, CH, T]), sb("att", [P, NT, C])
        with nc.sbuf_tensor("sl_keys", [P, NT, C], F32) as keys, nc.sbuf_tensor("sl_values", [P, NT, C + 1], F32) as values:
            memset_stage(k, (values[:, :, C:C + 1], 1.0))
            softmax_features_stage(k, w, rows, k_bias, att, qT, keys, values,
                                   [(w[:], inp["L1a_w"]), (rows[:], inp["L1a_rows"].partition_broadcast(P)), (k_bias[:], inp["L1a_bk"])])
            linear_attention_stage(k, lambda t: keys[:, t, :], lambda t: values[:, t, :], qT, lambda t: att[:, t, :], NT // B)
        norm_rows_stage(k, NT, lambda t: att[:, t, :], rows[:, 2, :], rows[:, 3, :], k.eps[0], source=lambda t: att[:, t, :],
                        destT=lambda t: qT[:, :, t * P:(t + 1) * P])
        residual_norm_stage(k, [(lambda t, c=c: qT[:, c, t * P:(t + 1) * P], w[:, 3, c, :]) for c in range(CH)], rows[:, 4, :])


def context_attention(k):
    self_or_cross_attention(k, "l1x", None, ("L1x_w", "L1x_b", "L1x_out_w", "L1x_out_b", "L1x_v_b"), SC)


def plain_attention(k):
    self_or_cross_attention(k, "l2a", k.xT, ("L2a_w", None, "L2a_out_w", "L2a_out_b", None), S)


def alibi_attention(k):
    self_or_cross_attention(k, "l3a", k.xT, ("L3a_w", "L3a_b", "L3a_out_w", "L3a_out_b", "L3a_v_b"), S, slopes=k.inp["slopes"])


def first_of_maxima(nc, dve, done, count, e, top, rank, onehot, order):
    n = e.shape[2]

    def wide(col):
        return col.unsqueeze(2).broadcast_to((P, e.shape[1], n))

    nc.vector.reduce_max(top, e, AX).then_inc(done, 1)
    dve.wait_ge(done, count + 1)
    nc.vector.tensor_tensor(rank, e, wide(top), ALU.is_equal).then_inc(done, 1)
    dve.wait_ge(done, count + 2)
    nc.vector.tensor_tensor(rank, rank, order, ALU.mult).then_inc(done, 1)
    dve.wait_ge(done, count + 3)
    nc.vector.reduce_max(top, rank, AX).then_inc(done, 1)
    dve.wait_ge(done, count + 4)
    nc.vector.tensor_tensor(onehot, rank, wide(top), ALU.is_equal).then_inc(done, 1)
    dve.wait_ge(done, count + 5)
    return count + 5


def top1_ffn(k):
    nc, inp = k.nc, k.inp
    E, F = 8, 1024
    FCH = F // P
    SLOTS = NT + E - 1
    ROW = CH * F + FCH
    with ExitStack() as held:
        def sb(what, shape, dt=F32):
            return held.enter_context(nc.sbuf_tensor(f"t1_{what}", shape, dt))

        scattered, gathered, *fetched = (held.enter_context(nc.semaphore(f"t1_{n}")) for n in ("scattered", "gathered", "fetched0", "fetched1", "fetched2"))
        z = sb("z", [P, NT, C])
        rows = sb("rows", [P, 3, C])
        row_of, weights_of = sb("row_of", [P, NT], U32), sb("weights_of", [P, SLOTS], U32)
        with ExitStack() as inner:
            def sbi(what, shape, dt=F32):
                return inner.enter_context(nc.sbuf_tensor(f"t1_{what}", shape, dt))

            wr, order = sbi("wr", [P, CH, E]), sbi("order", [P, NT, E])
            upto, ones, earlier = sbi("upto", [P, P]), sbi("ones", [P, P]), sbi("earlier", [P, E, E])
            steps, numbers, partition = sbi("steps", [P, NT]), sbi("numbers", [P, SLOTS]), sbi("partition", [P, 1])
            e, rank, onehot, before = (sbi(n, [P, NT, E]) for n in ("e", "rank", "onehot", "before"))
            top, total, used, base, end = sbi("top", [P, NT]), *(sbi(n, [P, E]) for n in ("total", "used", "base", "end"))
            filled, below, passed, expert = sbi("filled", [P, E, NT]), sbi("below", [P, E, E]), sbi("passed", [P, SLOTS, E]), sbi("expert", [P, SLOTS])
            zeros = sbi("zeros", [P, SLOTS, C])
            loaded, zeroed, cleared, logits, centred, exped, step, counted, placed = inner.enter_context(k.stage(
                "loaded", "zeroed", "cleared", "logits", "centred", "exped", "step", "counted", "placed"))
            block = inner.enter_context(nc.Block())
            loads = [(wr[:], inp["L0f_wr"]), (order[:], inp["order8"].partition_broadcast(P)), (upto[:], inp["upto"]),
                     (earlier[:], inp["earlier8"].partition_broadcast(P)), (steps[:], inp["slot_steps"].partition_broadcast(P)),
                     (numbers[:], inp["slot_numbers"].partition_broadcast(P)), (partition[:], inp["partition"])]

            @block.sync
            def _(sync):
                k.clear_last_set(sync)
                for tile, src in loads:
                    sync.dma_start(tile, src).then_inc(loaded, 16)
                sync.wait_ge(zeroed, 1)
                sync.dma_start(k.slots_in[0:SLOTS * P, :].rearrange("(t p) c -> p t c", p=P), zeros[:]).then_inc(cleared, 16)
                sync.wait_ge(cleared, 16)

            @block.gpsimd
            def _(pool):
                nc.gpsimd.memset(zeros[:], 0.0).then_inc(zeroed, 1)
                pool.wait_ge(cleared, 16)
                pool.wait_ge(placed, 1)
                for t in range(NT):
                    pool.indirect_dma_start(k.slots_in, bass.IndirectOffsetOnAxis(ap=row_of[:, t:t + 1], axis=0), k.X[:, t, :], None).then_inc(scattered, 16)
                pool.wait_ge(scattered, 16 * NT)

            @block.tensor
            def _(pe):
                pe.wait_ge(loaded, 16 * len(loads))
                for t in range(NT):
                    for c in range(CH):
                        mm = nc.tensor.matmul(k.ps[:, 0, t * E:(t + 1) * E], k.xT[:, c, t * P:(t + 1) * P], wr[:, c, :], start=c == 0,
                                              stop=c == CH - 1)
                mm.then_inc(logits, 1)
                pe.wait_ge(counted, NT + 1)
                flat = "p t e -> p (t e)"
                nc.tensor.matmul(k.ps[:, 1, 0:NT * E], upto[:, :], onehot[:].rearrange(flat), start=True, stop=False)
                nc.tensor.matmul(k.ps[:, 1, 0:NT * E], ones[:, :], before[:].rearrange(flat), start=False, stop=True)
                nc.tensor.matmul(k.ps[:, 2, 0:E], ones[:, :], total[:, :], start=True, stop=True).then_inc(logits, 1)

            @block.scalar
            def _(act):
                act.wait_ge(centred, 1)
                nc.scalar.activation(e[:], rank[:], ACT.Exp).then_inc(exped, 1)

            @block.vector
            def _(dve):
                n = 0

                def then(ins):
                    nonlocal n
                    n += 1
                    ins.then_inc(step, 1)
                    dve.wait_ge(step, n)

                nc.vector.memset(ones[:], 1.0)
                then(nc.vector.memset(before[:, 0, :], 0.0))
                dve.wait_ge(loaded, 16 * len(loads))
                dve.wait_ge(logits, 1)
                view = k.ps[:, 0, 0:NT * E].rearrange("p (t e) -> p t e", e=E)
                then(nc.vector.reduce_max(top[:], view, AX))
                nc.vector.tensor_tensor(rank[:], view, top[:].unsqueeze(2).broadcast_to((P, NT, E)), ALU.subtract).then_inc(centred, 1)
                dve.wait_ge(exped, 1)
                n = first_of_maxima(nc, dve, step, n, e[:], top[:], rank[:], onehot[:], order[:])
                for t in range(1, NT):
                    nc.vector.tensor_tensor(before[:, t, :], before[:, t - 1, :], onehot[:, t - 1, :], ALU.add).then_inc(counted, 1)
                    dve.wait_ge(counted, t)
                nc.vector.tensor_tensor(total[:], before[:, NT - 1, :], onehot[:, NT - 1, :], ALU.add).then_inc(counted, 2)
                dve.wait_ge(logits, 2)
                then(nc.vector.tensor_tensor(filled[:], k.ps[:, 2, 0:E].unsqueeze(2).broadcast_to((P, E, NT)),
                                             steps[:].unsqueeze(1).broadcast_to((P, E, NT)), ALU.is_gt))
                then(nc.vector.reduce_sum(used[:], filled[:], AX))
                then(nc.vector.tensor_tensor(below[:], earlier[:], used[:].unsqueeze(1).broadcast_to((P, E, E)), ALU.mult))
                then(nc.vector.reduce_sum(base[:], below[:], AX))
                then(nc.vector.tensor_tensor(end[:], base[:], used[:], ALU.add))
                then(nc.vector.tensor_tensor(passed[:], numbers[:].unsqueeze(2).broadcast_to((P, SLOTS, E)),
                                             end[:].unsqueeze(1).broadcast_to((P, SLOTS, E)), ALU.is_ge))
                then(nc.vector.reduce_sum(expert[:], passed[:], AX))
                then(nc.vector.tensor_scalar(expert[:], expert[:], float(E - 1), float(P), ALU.min, ALU.mult))
                then(nc.vector.tensor_tensor(expert[:], expert[:], partition[:].broadcast_to((P, SLOTS)), ALU.add))
                nc.vector.tensor_copy(weights_of[:], expert[:])
                then(nc.vector.tensor_scalar(base[:], base[:], float(P), -1.0, ALU.mult, ALU.add))
                then(nc.vector.tensor_tensor(rank[:], k.ps[:, 1, 0:NT * E].rearrange("p (t e) -> p t e", e=E),
                                             base[:].unsqueeze(1).broadcast_to((P, NT, E)), ALU.add))
                then(nc.vector.tensor_tensor(rank[:], rank[:], onehot[:], ALU.mult))
                then(nc.vector.reduce_sum(top[:], rank[:], AX))
                nc.vector.tensor_copy(row_of[:], top[:]).then_inc(placed, 1)

        with ExitStack() as inner:
            def sbi(what, shape, dt=F32):
                return inner.enter_context(nc.sbuf_tensor(f"t1_{what}", shape, dt))

            DEEP = 3
            w1 = [sbi(f"w1_{i}", [P, ROW]) for i in range(DEEP)]
            xe = [sbi(f"x_{i}", [P, C]) for i in range(DEEP)]
            w2 = sbi("w2", [P, FCH, C])
            xeT, hidden, ye = sbi("xT", [P, 2, CH, P]), sbi("hidden", [P, 2, FCH, P]), sbi("ye", [P, 2, C])
            (*loaded, weights_in, turned, x_copied, hid_ready, hid_done, y_ready, y_done, stored0, stored1) = inner.enter_context(k.stage(
                "loaded0", "loaded1", "loaded2", "weights", "turned", "x_copied", "hid_ready", "hid_done", "y_ready", "y_done", "stored0", "stored1"))
            stored = (stored0, stored1)

            def store(sync, s):
                sync.wait_ge(y_done, s + 1)
                sync.dma_start(k.slots_out[s * P:(s + 1) * P, :], ye[:, s % 2, :]).then_inc(stored[s % 2], 16)

            block = inner.enter_context(nc.Block())

            @block.sync
            def _(sync):
                k.clear_last_set(sync)
                for s in range(SLOTS):
                    if s >= DEEP:
                        sync.wait_ge(turned, s - DEEP + 1)
                    sync.dma_start(xe[s % DEEP][:], k.slots_in[s * P:(s + 1) * P, :]).then_inc(loaded[s % DEEP], 16)
                    if s == 0:
                        sync.dma_start(w2[:], inp["L0f_w2"]).then_inc(weights_in, 16)
                        sync.dma_start(rows[:], inp["L0f_rows"].partition_broadcast(P)).then_inc(weights_in, 16)
                    if s >= DEEP:
                        store(sync, s - DEEP)
                for s in range(SLOTS - DEEP, SLOTS):
                    store(sync, s)
                for i in range(2):
                    sync.wait_ge(stored[i], 16 * len(range(i, SLOTS, 2)))

            @block.gpsimd
            def _(pool):
                for s in range(SLOTS):
                    if s >= DEEP:
                        pool.wait_ge(hid_done, (s - DEEP + 1) * FCH)
                    pool.indirect_dma_start(w1[s % DEEP][:], None, inp["L0f_w1"], bass.IndirectOffsetOnAxis(ap=weights_of[:, s:s + 1], axis=0)
                                            ).then_inc(fetched[s % DEEP], 16)

            @block.tensor
            def _(pe):
                def turn(s):
                    pe.wait_ge(loaded[s % DEEP], 16 * (s // DEEP + 1))
                    if s >= 2:
                        pe.wait_ge(x_copied, s - 1)
                    for c in range(CH):
                        tr = nc.tensor.transpose(k.ps[:, s % 2, c * P:(c + 1) * P], xe[s % DEEP][:, c * P:(c + 1) * P], k.ident[:, :])
                    tr.then_inc(turned, 1)

                def outputs(s):
                    if s >= 2:
                        pe.wait_ge(y_done, s - 1)
                    pe.wait_ge(hid_done, (s + 1) * FCH)
                    for f in range(FCH):
                        mm = nc.tensor.matmul(k.ps[:, 6 + s % 2, 0:C], hidden[:, s % 2, f, :], w2[:, f, :], start=f == 0, stop=f == FCH - 1)
                    mm.then_inc(y_ready, 1)

                turn(0)
                for s in range(SLOTS):
                    if s + 1 < SLOTS:
                        turn(s + 1)
                    pe.wait_ge(x_copied, s + 1)
                    pe.wait_ge(fetched[s % DEEP], 16 * (s // DEEP + 1))
                    for f in range(FCH):
                        h = s * FCH + f
                        if h >= 4:
                            pe.wait_ge(hid_done, h - 3)
                        for c in range(CH):
                            mm = nc.tensor.matmul(k.ps[:, 2 + h % 4, 0:P], w1[s % DEEP][:, c * F + f * P:c * F + (f + 1) * P], xeT[:, s % 2, c, :],
                                                  start=c == 0, stop=c == CH - 1)
                        mm.then_inc(hid_ready, 1)
                    if s == 0:
                        pe.wait_ge(weights_in, 32)
                    if s:
                        outputs(s - 1)
                outputs(SLOTS - 1)

            @block.scalar
            def _(act):
                def copy_x(s):
                    act.wait_ge(turned, s + 1)
                    if s >= 2:
                        act.wait_ge(hid_ready, (s - 1) * FCH)
                    nc.scalar.activation(xeT[:, s % 2, :, :], k.ps[:, s % 2, 0:C].rearrange("p (c n) -> p c n", c=CH), ACT.Copy).then_inc(x_copied, 1)

                copy_x(0)
                for s in range(SLOTS):
                    if s + 1 < SLOTS:
                        copy_x(s + 1)
                    act.wait_ge(fetched[s % DEEP], 16 * (s // DEEP + 1))
                    if s >= 2:
                        act.wait_ge(y_ready, s - 1)
                    for f in range(FCH):
                        act.wait_ge(hid_ready, s * FCH + f + 1)
                        nc.scalar.activation(hidden[:, s % 2, f, :], k.ps[:, 2 + (s * FCH + f) % 4, 0:P], ACT.Gelu,
                                             bias=w1[s % DEEP][:, CH * F + f:CH * F + f + 1]).then_inc(hid_done, 1)

            @block.vector
            def _(dve):
                for s in range(SLOTS):
                    dve.wait_ge(y_ready, s + 1)
                    if s >= 2:
                        dve.wait_ge(stored[s % 2], 16 * (s // 2))
                    nc.vector.tensor_copy(ye[:, s % 2, :], k.ps[:, 6 + s % 2, 0:C]).then_inc(y_done, 1)

        with nc.sbuf_tensor("t1_back", [P, NT, C], F32) as back, k.stage("with_bias", "summed") as (with_bias, summed), nc.Block() as block:
            @block.sync
            def _(sync):
                k.clear_last_set(sync)

            @block.gpsimd
            def _(pool):
                for t in range(NT):
                    pool.indirect_dma_start(back[:, t, :], None, k.slots_out[0:SLOTS * P, :], bass.IndirectOffsetOnAxis(ap=row_of[:, t:t + 1], axis=0)).then_inc(gathered, 16)

            @block.vector
            def _(dve):
                nc.vector.tensor_tensor(z[:], k.X[:], rows[:, 0, :].unsqueeze(1).broadcast_to((P, NT, C)), ALU.add).then_inc(with_bias, 1)
                dve.wait_ge(with_bias, 1)
                dve.wait_ge(gathered, 16 * NT)
                nc.vector.tensor_tensor(z[:], z[:], back[:], ALU.add).then_inc(summed, 1)
        norm_rows_stage(k, NT, lambda t: z[:, t, :], rows[:, 1, :], rows[:, 2, :], k.eps[2], source=lambda t: z[:, t, :])
        add_norm_stage(k, lambda t: z[:, t, :])


def capacity_ffn(k):
    nc, inp = k.nc, k.inp
    E, F = 16, 1024
    FCH, CAP = F // P, -(-T // 16)
    ROWS = E * CAP
    with ExitStack() as held:
        def sb(what, shape, dt=F32):
            return held.enter_context(nc.sbuf_tensor(f"cf_{what}", shape, dt))

        scattered, gathered = (held.enter_context(nc.semaphore(n)) for n in ("scattered", "gathered"))
        DEEP = 4
        w1 = [sb(f"w1_{i}", [P, CH, F]) for i in range(DEEP)]
        w2 = [sb(f"w2_{i}", [P, FCH, C]) for i in range(DEEP)]
        b1, b2 = sb("b1", [P, E, FCH]), sb("b2", [P, E, C])
        slot_to, slot_from, gate = sb("slot_to", [P, NT], U32), sb("slot_from", [P, NT], U32), sb("gate", [P, NT])
        y = sb("y", [P, NT, C])
        with ExitStack() as inner:
            def sbi(what, shape, dt=F32):
                return inner.enter_context(nc.sbuf_tensor(f"cf_{what}", shape, dt))

            wg, bg, order = sbi("wg", [P, CH, E]), sbi("bg", [P, E]), sbi("order", [P, NT, E])
            number, token = sbi("number", [P, NT, E]), sbi("token", [P, NT])
            upto, ones = sbi("upto", [P, P]), sbi("ones", [P, P])
            e, rank, onehot, before = (sbi(n, [P, NT, E]) for n in ("e", "rank", "onehot", "before"))
            top, total, pos, slot, keep = (sbi(n, [P, NT]) for n in ("top", "total", "pos", "slot", "keep"))
            zeros = sbi("zeros", [P, ROWS // P, C])
            loaded, prefetched, zeroed, cleared, logits, centred, exped, step, counted, placed = inner.enter_context(k.stage(
                "loaded", "prefetched", "zeroed", "cleared", "logits", "centred", "exped", "step", "counted", "placed"))
            block = inner.enter_context(nc.Block())
            loads = [(wg[:], inp["L1f_wg"]), (bg[:], inp["L1f_bg"].partition_broadcast(P)), (order[:], inp["order16"].partition_broadcast(P)),
                     (number[:], inp["expert16"].partition_broadcast(P)), (token[:], inp["token"]), (upto[:], inp["upto"])]

            @block.sync
            def _(sync):
                k.clear_last_set(sync)
                for tile, src in loads:
                    sync.dma_start(tile, src).then_inc(loaded, 16)
                sync.wait_ge(zeroed, 1)
                sync.dma_start(k.slots_in[0:ROWS, :].rearrange("(t p) c -> p t c", p=P), zeros[:]).then_inc(cleared, 16)
                prefetch = [(b1[:], inp["L1f_b1"]), (b2[:], inp["L1f_b2"].partition_broadcast(P))]
                prefetch += [pair for x in range(DEEP) for pair in ((w1[x][:], inp["L1f_w1"][x]), (w2[x][:], inp["L1f_w2"][x]))]
                for tile, src in prefetch:
                    sync.dma_start(tile, src).then_inc(prefetched, 16)
                sync.wait_ge(cleared, 16)
                sync.wait_ge(prefetched, 16 * len(prefetch))

            @block.gpsimd
            def _(pool):
                nc.gpsimd.memset(zeros[:], 0.0).then_inc(zeroed, 1)
                pool.wait_ge(cleared, 16)
                pool.wait_ge(placed, 1)
                for t in range(NT):
                    pool.indirect_dma_start(k.slots_in, bass.IndirectOffsetOnAxis(ap=slot_to[:, t:t + 1], axis=0), k.X[:, t, :], None).then_inc(scattered, 16)
                pool.wait_ge(scattered, 16 * NT)

            @block.tensor
            def _(pe):
                pe.wait_ge(loaded, 16 * len(loads))
                for t in range(NT):
                    for c in range(CH):
                        mm = nc.tensor.matmul(k.ps[:, 0, t * E:(t + 1) * E], k.xT[:, c, t * P:(t + 1) * P], wg[:, c, :], start=c == 0,
                                              stop=c == CH - 1)
                mm.then_inc(logits, 1)
                pe.wait_ge(counted, NT)
                flat = "p t e -> p (t e)"
                nc.tensor.matmul(k.ps[:, 1, 0:NT * E], upto[:, :], onehot[:].rearrange(flat), start=True, stop=False)
                nc.tensor.matmul(k.ps[:, 1, 0:NT * E], ones[:, :], before[:].rearrange(flat), start=False, stop=True).then_inc(logits, 1)

            @block.scalar
            def _(act):
                act.wait_ge(centred, 1)
                nc.scalar.activation(e[:], rank[:], ACT.Exp).then_inc(exped, 1)

            @block.vector
            def _(dve):
                def wide(col):
                    return col.unsqueeze(2).broadcast_to((P, NT, E))

                n = 0

                def then(ins):
                    nonlocal n
                    n += 1
                    ins.then_inc(step, 1)
                    dve.wait_ge(step, n)

                nc.vector.memset(ones[:], 1.0)
                then(nc.vector.memset(before[:, 0, :], 0.0))
                dve.wait_ge(loaded, 16 * len(loads))
                dve.wait_ge(logits, 1)
                view = k.ps[:, 0, 0:NT * E].rearrange("p (t e) -> p t e", e=E)
                then(nc.vector.tensor_tensor(rank[:], view, bg[:].unsqueeze(1).broadcast_to((P, NT, E)), ALU.add))
                then(nc.vector.reduce_max(top[:], rank[:], AX))
                nc.vector.tensor_tensor(rank[:], rank[:], wide(top[:]), ALU.subtract).then_inc(centred, 1)
                dve.wait_ge(exped, 1)
                then(nc.vector.reduce_sum(total[:], e[:], AX))
                then(nc.vector.reciprocal(total[:], total[:]))
                then(nc.vector.tensor_tensor(e[:], e[:], wide(total[:]), ALU.mult))
                then(nc.vector.reduce_max(gate[:], e[:], AX))
                n = first_of_maxima(nc, dve, step, n, e[:], top[:], rank[:], onehot[:], order[:])
                for t in range(1, NT):
                    nc.vector.tensor_tensor(before[:, t, :], before[:, t - 1, :], onehot[:, t - 1, :], ALU.add).then_inc(counted, 1)
                    dve.wait_ge(counted, t)
                then(nc.vector.tensor_tensor(rank[:], onehot[:], number[:], ALU.mult))
                then(nc.vector.reduce_sum(slot[:], rank[:], AX))
                dve.sem_inc(counted, 1)
                dve.wait_ge(logits, 2)
                then(nc.vector.tensor_tensor(rank[:], k.ps[:, 1, 0:NT * E].rearrange("p (t e) -> p t e", e=E), onehot[:], ALU.mult))
                then(nc.vector.reduce_sum(pos[:], rank[:], AX))
                then(nc.vector.tensor_scalar(keep[:], pos[:], float(CAP), None, ALU.is_le))
                then(nc.vector.scalar_tensor_tensor(slot[:], slot[:], float(CAP), pos[:], ALU.mult, ALU.add))
                then(nc.vector.scalar_tensor_tensor(slot[:], slot[:], -1.0, keep[:], ALU.add, ALU.mult))
                nc.vector.tensor_copy(slot_from[:], slot[:])
                then(nc.vector.tensor_tensor(gate[:], gate[:], keep[:], ALU.mult))
                then(nc.vector.tensor_scalar(keep[:], keep[:], -1.0, 1.0, ALU.mult, ALU.add))
                then(nc.vector.tensor_tensor(token[:], token[:], keep[:], ALU.mult))
                then(nc.vector.tensor_tensor(slot[:], slot[:], token[:], ALU.add))
                nc.vector.tensor_copy(slot_to[:], slot[:]).then_inc(placed, 1)

        with ExitStack() as inner:
            def sbi(what, shape, dt=F32):
                return inner.enter_context(nc.sbuf_tensor(f"cf_{what}", shape, dt))

            xe = [sbi(f"x_{i}", [CAP, C]) for i in range(DEEP)]
            xeT, hidden, ye = sbi("xT", [P, 2, CH, CAP]), sbi("hidden", [P, 2, FCH, CAP]), sbi("ye", [CAP, 2, C])
            (*loaded, turned, x_copied, hid_ready, hid_done, y_ready, y_done, stored0, stored1) = inner.enter_context(k.stage(
                *(f"tokens{i}" for i in range(DEEP)), *(f"weights{i}" for i in range(DEEP)), "turned", "x_copied", "hid_ready", "hid_done", "y_ready", "y_done", "stored0", "stored1"))
            tokens_in, weights_in = loaded[:DEEP], loaded[DEEP:]
            stored = (stored0, stored1)

            def store(sync, x):
                sync.wait_ge(y_done, x + 1)
                sync.dma_start(k.slots_out[x * CAP:(x + 1) * CAP, :], ye[:, x % 2, :]).then_inc(stored[x % 2], 16)

            block = inner.enter_context(nc.Block(no_gpsimd_drain=True))

            @block.sync
            def _(sync):
                k.clear_last_set(sync)
                for x in range(E):
                    i = x % DEEP
                    if x >= DEEP:
                        store(sync, x - DEEP)
                    sync.dma_start(xe[i][:], k.slots_in[x * CAP:(x + 1) * CAP, :]).then_inc(tokens_in[i], 16)
                    if x >= DEEP:
                        sync.dma_start(w1[i][:], inp["L1f_w1"][x]).then_inc(weights_in[i], 16)
                        sync.dma_start(w2[i][:], inp["L1f_w2"][x]).then_inc(weights_in[i], 16)
                for x in range(E - DEEP, E):
                    store(sync, x)
                for i in range(2):
                    sync.wait_ge(stored[i], 16 * E // 2)

            @block.tensor
            def _(pe):
                def turn(x):
                    pe.wait_ge(tokens_in[x % DEEP], 16 * (x // DEEP + 1))
                    if x >= 2:
                        pe.wait_ge(x_copied, x - 1)
                    for c in range(CH):
                        tr = nc.tensor.transpose(k.ps[:, x % 2, c * P:(c + 1) * P], xe[x % DEEP][:, c * P:(c + 1) * P], k.ident[:, :])
                    tr.then_inc(turned, 1)

                def outputs(x):
                    if x >= 2:
                        pe.wait_ge(y_done, x - 1)
                    pe.wait_ge(hid_done, (x + 1) * FCH)
                    for f in range(FCH):
                        mm = nc.tensor.matmul(k.ps[0:CAP, 6 + x % 2, 0:C], hidden[:, x % 2, f, :], w2[x % DEEP][:, f, :], start=f == 0, stop=f == FCH - 1)
                    mm.then_inc(y_ready, 1)

                turn(0)
                for x in range(E):
                    if x + 1 < E:
                        turn(x + 1)
                    pe.wait_ge(x_copied, x + 1)
                    if x >= DEEP:
                        pe.wait_ge(weights_in[x % DEEP], 32 * (x // DEEP))
                    for f in range(FCH):
                        h = x * FCH + f
                        if h >= 4:
                            pe.wait_ge(hid_done, h - 3)
                        for c in range(CH):
                            mm = nc.tensor.matmul(k.ps[:, 2 + h % 4, 0:CAP], w1[x % DEEP][:, c, f * P:(f + 1) * P], xeT[:, x % 2, c, :], start=c == 0,
                                                  stop=c == CH - 1)
                        mm.then_inc(hid_ready, 1)
                    if x:
                        outputs(x - 1)
                outputs(E - 1)

            @block.scalar
            def _(act):
                def copy_x(x):
                    act.wait_ge(turned, x + 1)
                    if x >= 2:
                        act.wait_ge(hid_ready, (x - 1) * FCH)
                    nc.scalar.activation(xeT[:, x % 2, :, :], k.ps[:, x % 2, 0:C].rearrange("p (c n) -> p c n", c=CH), ACT.Copy).then_inc(x_copied, 1)

                copy_x(0)
                for x in range(E):
                    if x + 1 < E:
                        copy_x(x + 1)
                    if x >= 2:
                        act.wait_ge(y_ready, x - 1)
                    for f in range(FCH):
                        h = x * FCH + f
                        act.wait_ge(hid_ready, h + 1)
                        nc.scalar.activation(hidden[:, x % 2, f, :], k.ps[:, 2 + h % 4, 0:CAP], ACT.Relu, bias=b1[:, x, f:f + 1]).then_inc(hid_done, 1)

            @block.vector
            def _(dve):
                for x in range(E):
                    dve.wait_ge(y_ready, x + 1)
                    if x >= 2:
                        dve.wait_ge(stored[x % 2], 16 * (x // 2))
                    nc.vector.tensor_tensor(ye[:, x % 2, :], k.ps[0:CAP, 6 + x % 2, 0:C], b2[:, x, :], ALU.add).then_inc(y_done, 1)

        with nc.sbuf_tensor("cf_back", [P, NT, C], F32) as back, k.stage("scaled") as (scaled,), nc.Block() as block:
            @block.sync
            def _(sync):
                k.clear_last_set(sync)

            @block.gpsimd
            def _(pool):
                for t in range(NT):
                    pool.indirect_dma_start(back[:, t, :], None, k.slots_out[0:ROWS, :], bass.IndirectOffsetOnAxis(ap=slot_from[:, t:t + 1], axis=0)).then_inc(gathered, 16)

            @block.vector
            def _(dve):
                dve.wait_ge(gathered, 16 * NT)
                for t in range(NT):
                    nc.vector.tensor_scalar(y[:, t, :], back[:, t, :], gate[:, t:t + 1], None, ALU.mult).then_inc(scaled, 1)
        add_norm_stage(k, lambda t: y[:, t, :])


def quantised_ffn(k):
    nc, inp = k.nc, k.inp
    F = 1024
    FCH = F // P
    with ExitStack() as held:
        def sb(what, shape, dt=F32):
            return held.enter_context(nc.sbuf_tensor(f"qf_{what}", shape, dt))

        w2, rows = sb("w2", [P, FCH, C]), sb("rows", [P, 3, C])
        hidden = sb("hidden", [P, FCH, T])
        with ExitStack() as inner:
            def sbi(what, shape, dt=F32):
                return inner.enter_context(nc.sbuf_tensor(f"qf_{what}", shape, dt))

            hT, h = sbi("hT", [P, CH, T]), sbi("h", [P, NT, C])
            q1, q2 = sbi("q1", [P, CH, F], I32), sbi("q2", [P, FCH, C], I32)
            w1, b1 = sbi("w1", [P, CH, F]), sbi("b1", [P, FCH])
            norm_rows_stage(k, NT, lambda t: h[:, t, :], rows[:, 0, :], rows[:, 1, :], k.eps[0], source=lambda t: k.X[:, t, :],
                            destT=lambda t: hT[:, :, t * P:(t + 1) * P], weights=[(rows[:], inp["L2f_rows"].partition_broadcast(P))],
                            prefetch=[(q1[:], inp["L2f_q1"]), (w1[:], inp["L2f_s1"].partition_broadcast(P)), (q2[:], inp["L2f_q2"]),
                                      (w2[:], inp["L2f_s2"].partition_broadcast(P)), (b1[:], inp["L2f_b1"])])
            weights, ready, done = inner.enter_context(k.stage("weights", "ready", "done"))
            block = inner.enter_context(nc.Block(no_gpsimd_drain=True))
            units = [(q, f) for q in range(T // BANK) for f in range(FCH)]

            @block.sync
            def _(sync):
                k.clear_last_set(sync)

            @block.vector
            def _(dve):
                for w, q in ((w1, q1), (w2, q2)):
                    flat = "p a b -> p (a b)"
                    nc.vector.scalar_tensor_tensor(w[:].rearrange(flat), q[:].rearrange(flat), -128.0, w[:].rearrange(flat), ALU.add,
                                                   ALU.mult).then_inc(weights, 1)
                nc.vector.tensor_scalar(rows[:, 2, :], rows[:, 2, :], 0.5, None, ALU.mult).then_inc(weights, 1)

            @block.tensor
            def _(pe):
                pe.wait_ge(weights, 1)
                for n, (q, f) in enumerate(units):
                    if n >= 4:
                        pe.wait_ge(done, n - 3)
                    for c in range(CH):
                        mm = nc.tensor.matmul(k.ps[:, n % 4, :], w1[:, c, f * P:(f + 1) * P], hT[:, c, q * BANK:(q + 1) * BANK], start=c == 0,
                                              stop=c == CH - 1)
                    mm.then_inc(ready, 1)

            @block.scalar
            def _(act):
                for n, (q, f) in enumerate(units):
                    act.wait_ge(ready, n + 1)
                    nc.scalar.activation(hidden[:, f, q * BANK:(q + 1) * BANK], k.ps[:, n % 4, :], ACT.Silu, bias=b1[:, f:f + 1]).then_inc(done, 1)
        residual_norm_stage(k, [(lambda t, f=f: hidden[:, f, t * P:(t + 1) * P], w2[:, f, :]) for f in range(FCH)], rows[:, 2, :],
                            x_scale=2.0, y_scale=0.5)


def shifted_ffn(k):
    nc, inp = k.nc, k.inp
    with ExitStack() as held:
        def sb(what, shape, dt=F32):
            return held.enter_context(nc.sbuf_tensor(f"sh_{what}", shape, dt))

        y = sb("y", [P, NT, C])
        with ExitStack() as inner:
            def sbi(what, shape, dt=F32):
                return inner.enter_context(nc.sbuf_tensor(f"sh_{what}", shape, dt))

            w, mu, rest = sbi("w", [P, 3, CH, C]), sbi("mu", [P, 2, CH]), sbi("rest", [P, 2, CH])
            mixed = sbi("mixed", [P, 2, CH, T])
            keys, squares, gate = sbi("keys", [P, CH, T]), sbi("squares", [P, CH, T]), sbi("gate", [P, NT, C])
            loaded, others, scaled, mixed_done, k_ready, k_relu, squared, g_ready, g_done, v_ready, v_done = inner.enter_context(k.stage(
                "loaded", "others", "scaled", "mixed", "k_ready", "k_relu", "squared", "g_ready", "g_done", "v_ready", "v_done"))
            block = inner.enter_context(nc.Block())
            parts = [(b, c) for b in range(B) for c in range(CH)]

            @block.sync
            def _(sync):
                k.clear_last_set(sync)
                sync.dma_start(mu[:], inp["L3f_mu"]).then_inc(loaded, 16)
                sync.dma_start(w[:], inp["L3f_w"]).then_inc(loaded, 16)

            @block.vector
            def _(dve):
                dve.wait_ge(loaded, 32)
                nc.vector.tensor_scalar(rest[:], mu[:], -1.0, 1.0, ALU.mult, ALU.add).then_inc(others, 1)
                dve.wait_ge(others, 1)
                for i, which in enumerate((1, 0)):
                    for n, (b, c) in enumerate(parts):
                        part = mixed[:, which, c, b * S:(b + 1) * S]
                        nc.vector.tensor_scalar(part, k.xT[:, c, b * S:(b + 1) * S], mu[:, which, c:c + 1], None, ALU.mult).then_inc(scaled, 1)
                        dve.wait_ge(scaled, i * len(parts) + n + 1)
                        nc.vector.scalar_tensor_tensor(part[:, 1:], k.xT[:, c, b * S:(b + 1) * S - 1], rest[:, which, c:c + 1], part[:, 1:],
                                                       ALU.mult, ALU.add).then_inc(mixed_done, 1)
                for t in range(NT):
                    dve.wait_ge(v_ready, t + 1)
                    dve.wait_ge(g_done, t + 1)
                    nc.vector.tensor_tensor(y[:, t, :], k.ps[:, 6 + t % 2, 0:C], gate[:, t, :], ALU.mult).then_inc(v_done, 1)

            @block.tensor
            def _(pe):
                pe.wait_ge(loaded, 32)
                for n, (b, m) in enumerate(parts):
                    pe.wait_ge(mixed_done, CH * (b + 1))
                    if n >= 2:
                        pe.wait_ge(k_relu, n - 1)
                    for c in range(CH):
                        mm = nc.tensor.matmul(k.ps[:, n % 2, :], w[:, 1, c, m * P:(m + 1) * P], mixed[:, 1, c, b * S:(b + 1) * S], start=c == 0,
                                              stop=c == CH - 1)
                    mm.then_inc(k_ready, 1)
                for t in range(NT):
                    b = t // (NT // B)
                    pe.wait_ge(mixed_done, CH * (B + b + 1))
                    if t >= 2:
                        pe.wait_ge(g_done, t - 1)
                    for c in range(CH):
                        mm = nc.tensor.matmul(k.ps[:, 4 + t % 2, 0:C], mixed[:, 0, c, t * P:(t + 1) * P], w[:, 0, c, :], start=c == 0, stop=c == CH - 1)
                    mm.then_inc(g_ready, 1)
                for t in range(NT):
                    b = t // (NT // B)
                    pe.wait_ge(squared, CH * (b + 1))
                    if t >= 2:
                        pe.wait_ge(v_done, t - 1)
                    for c in range(CH):
                        mm = nc.tensor.matmul(k.ps[:, 6 + t % 2, 0:C], squares[:, c, t * P:(t + 1) * P], w[:, 2, c, :], start=c == 0, stop=c == CH - 1)
                    mm.then_inc(v_ready, 1)

            @block.scalar
            def _(act):
                for n, (b, m) in enumerate(parts):
                    act.wait_ge(k_ready, n + 1)
                    nc.scalar.activation(keys[:, m, b * S:(b + 1) * S], k.ps[:, n % 2, :], ACT.Relu).then_inc(k_relu, 1)
                for t in range(NT):
                    act.wait_ge(g_ready, t + 1)
                    nc.scalar.activation(gate[:, t, :], k.ps[:, 4 + t % 2, 0:C], ACT.Sigmoid).then_inc(g_done, 1)

            @block.gpsimd
            def _(pool):
                for n, (b, m) in enumerate(parts):
                    pool.wait_ge(k_relu, n + 1)
                    part = keys[:, m, b * S:(b + 1) * S]
                    nc.gpsimd.tensor_tensor(squares[:, m, b * S:(b + 1) * S], part, part, ALU.mult).then_inc(squared, 1)
        residual_norm_stage(k, None, rows=lambda t: y[:, t, :], out=k.out)


def masked_attention(k):
    nc, inp = k.nc, k.inp
    with nc.sbuf_tensor("l3x_att", [P, NG, T], F32) as att, \
            nc.sbuf_tensor("l3x_ow", [P, CH, C], F32) as ow, nc.sbuf_tensor("l3x_ob", [P, C], F32) as ob:
        q_parts, k_parts, values = k.q_parts, k.k_parts, k.values_of(NTC, P)
        with nc.sbuf_tensor("l3x_ctxT", [P, CH, TC], F32) as ctxT:
            def as_is(src, store, order):
                return [("split", [(slice(0, BANK), k.ident[:, :], src[:, m, t * BANK:(t + 1) * BANK], True, True)], BANK, None,
                         stacked(store[m * P:(m + 1) * P, :, t * BANK:(t + 1) * BANK], order))
                        for t in range(store.shape[2] // BANK) for m in range(CH)]

            turned = [("value", [(slice(m * P, (m + 1) * P), ctxT[:, m, t * P:(t + 1) * P], k.ident[:, :], True, True) for m in range(CH)],
                       P, values[t]) for t in range(NTC)]
            project_stage(k, as_is(k.xT, q_parts, Q_PART) + as_is(ctxT, k_parts, K_PART) + turned, [],
                          late=[(ctxT[:], inp["ctxT"])], late_unit=T // BANK * CH,
                          prefetch=[(ow[:], inp["L3x_out_w"]), (ob[:], inp["L3x_out_b"].partition_broadcast(P))])
        dense_att = k.xT
        attention_stage(k, "l3x_core", q_parts, k_parts, values, S, SC, 1.0, att, mask=(inp["mask_q"], inp["mask_k"]), dense_att=dense_att, finish=False)
        residual_norm_stage(k, [(lambda t, c=c: dense_att[:, c, t * P:(t + 1) * P], ow[:, c, :]) for c in range(CH)], ob[:], relu=True,
                            finish=(att, dense_att))


def latent_attention(k):
    nc, inp = k.nc, k.inp
    D = 64
    INNER, NK = H * D, SC + S
    ICH = INNER // P
    q_parts = nc.dram_tensor("latent_q_parts", [3, INNER, T], BF16, kind="Internal").ap()
    k_parts = nc.dram_tensor("latent_k_parts", [3, INNER, B * NK], BF16, kind="Internal").ap()
    values = nc.dram_tensor("latent_values", [B * NK // P, P, INNER], F32, kind="Internal").ap()
    with nc.sbuf_tensor("la_latT", [P, CH, T], F32) as latT, nc.sbuf_tensor("la_ctxT", [P, CH, TC], F32) as ctxT:
        with nc.sbuf_tensor("la_rows", [P, 4, C], F32) as rows, nc.sbuf_tensor("la_ctx", [P, NTC, C], F32) as ctx, \
                nc.sbuf_tensor("la_lat", [P, NT, C], F32) as lat:
            norm_rows_stage(k, NTC, lambda t: ctx[:, t, :], rows[:, 0, :], rows[:, 1, :], k.eps[0], source=lambda t: ctx[:, t, :],
                            destT=lambda t: ctxT[:, :, t * P:(t + 1) * P],
                            weights=[(rows[:], inp["L2x_rows"].partition_broadcast(P))],
                            pieces=[(ctx[:, i * SC // P:(i + 1) * SC // P, :], inp["ctx"][:, i * SC // P:(i + 1) * SC // P, :]) for i in range(B)])
            norm_rows_stage(k, NT, lambda t: lat[:, t, :], rows[:, 2, :], rows[:, 3, :], k.eps[0], source=lambda t: k.X[:, t, :],
                            destT=lambda t: latT[:, :, t * P:(t + 1) * P])
        with nc.sbuf_tensor("la_w", [P, CH, 3 * INNER], F32) as w:
            def keyT(b, i, n):
                at = i * n
                return (lambda c: ctxT[:, c, b * SC + at:b * SC + at + n]) if at < SC else (lambda c: latT[:, c, b * S + at - SC:b * S + at - SC + n])

            def split(src, col, m, store):
                return ("split", [(slice(0, BANK), w[:, c, col + m * P:col + (m + 1) * P], src(c), c == 0, c == CH - 1) for c in range(CH)],
                        BANK, None, [(store.rearrange("a p n -> p a n"), lambda parts: parts)])

            units = [split(lambda c: latT[:, c, t * BANK:(t + 1) * BANK], 0, m, q_parts[:, m * P:(m + 1) * P, t * BANK:(t + 1) * BANK])
                     for t in range(T // BANK) for m in range(ICH)]
            for b in range(B):
                for i in range(NK // BANK):
                    col = b * NK + i * BANK
                    units += [split(keyT(b, i, BANK), INNER, m, k_parts[:, m * P:(m + 1) * P, col:col + BANK]) for m in range(ICH)]
                for i in range(NK // P):
                    src = keyT(b, i, P)
                    units += [("plain", [(slice(0, BANK), src(c), w[:, c, 2 * INNER + v * BANK:2 * INNER + (v + 1) * BANK], c == 0, c == CH - 1)
                                         for c in range(CH)], P, values[b * NK // P + i, :, v * BANK:(v + 1) * BANK]) for v in range(INNER // BANK)]
            project_stage(k, units, [(w[:], inp["L2x_w"])])
    with nc.sbuf_tensor("la_att", [P, ICH - CH, T], F32) as att:
        def att_of(g):
            return k.xT[:, g, :] if g < CH else att[:, g - CH, :]

        attention_stage(k, "la_core", q_parts, k_parts, values, S, NK, D ** -0.5, att_of, head_dim=D)
        with nc.sbuf_tensor("la_ow", [P, ICH, C], F32) as ow:
            residual_norm_stage(k, [(lambda t, g=g: att_of(g)[:, t * P:(t + 1) * P], ow[:, g, :]) for g in range(ICH)], None,
                                [(ow[:], inp["L2x_out_w"])])


SUBLAYERS = (pyramid_attention, relu_kernel_attention, top1_ffn, softmax_linear_attention, context_attention, capacity_ffn, plain_attention,
             latent_attention, quantised_ffn, alibi_attention, masked_attention, shifted_ffn)


def decoder(nc, inp, out):
    k = Program(nc, inp)
    with ExitStack() as held:
        def sb(name, shape, dt=F32):
            return held.enter_context(nc.sbuf_tensor(name, shape, dt))

        k.ps = held.enter_context(nc.psum_tensor("ps", [P, 8, BANK], F32))
        k.X, k.xT = sb("X", [P, NT, C]), sb("xT", [P, CH, T])
        k.ident, k.spread = sb("ident", [P, P]), sb("spread", [P, P])
        k.ident_bf, k.above_q, k.above_k = (sb(n, [P, P], BF16) for n in ("ident_bf", "above_q", "above_k"))
        eps = sb("eps", [P, 4])
        k.ones = sb("ones", [P, P])
        k.eps = [eps[:, i:i + 1] for i in range(3)]
        k.head_blocks, k.head_cols = sb("head_blocks", [P, P]), sb("head_cols", [P, CH, H])
        k.q_parts = nc.dram_tensor("q_parts", [C, 6, T], BF16, kind="Internal").ap()
        k.k_parts = nc.dram_tensor("k_parts", [C, 6, TC], BF16, kind="Internal").ap()
        store = nc.dram_tensor("values", [NTC, P, H * QUAD], F32, kind="Internal").ap()
        k.slots_in = nc.dram_tensor("slots_in", [2 * T, C], F32, kind="Internal").ap()
        k.slots_out = nc.dram_tensor("slots_out", [2 * T, C], F32, kind="Internal").ap()
        k.rows_of_ones = inp["rows_of_ones"]
        k.out = out
        k.sums_of_weights, k.inverse_sums = (nc.dram_tensor(n, [HG, NG, S], F32, kind="Internal").ap() for n in ("sums_of_weights", "inverse_sums"))
        k.regroup = nc.dram_tensor("regroup", [B, H, S, HD], F32, kind="Internal").ap()
        k.values_of = lambda tiles, rows: store[0:tiles, 0:rows, :]
        load_stage(k, [(k.X[:], inp["x"]), (k.xT[:], inp["xT"]), (k.ident[:], inp["ident"]), (k.spread[:], inp["spread"]),
                       (k.ident_bf[:], inp["ident_bf"]), (k.above_q[:], inp["above_q"]), (k.above_k[:], inp["above_k"]),
                       (eps[:], inp["eps"].partition_broadcast(P)), (k.head_blocks[:], inp["head_blocks"]),
                       (k.head_cols[:], inp["head_cols"])])
        memset_stage(k, (k.ones[:], 1.0))

        for sublayer in SUBLAYERS:
            sublayer(k)


def lay_out(a):
    f = {n: np.ascontiguousarray(v) for n, v in a.items()}
    bf16 = mybir.dt.np(BF16)

    def rows_in(w, chunks=CH):
        return w.reshape(chunks, P, w.shape[1]).transpose(1, 0, 2)

    def column(v):
        return v.reshape(-1, P).T

    i = np.arange(P)
    exact = 2.0 ** (-0.5 * (np.arange(H)[:, None] + 1)) * np.arange(S) * HD ** 0.5
    parts = []
    for _ in range(3):
        parts.append((exact - sum(p.astype(np.float64) for p in parts)).astype(np.float32).astype(bf16))
    slopes = np.stack(parts)
    d = {
        "x": f["x"].reshape(NT, P, C).transpose(1, 0, 2),
        "xT": f["x"].reshape(T, CH, P).transpose(2, 1, 0),
        "ident": np.eye(P, dtype=np.float32),
        "spread": ((i[:, None] % QUAD == HD) & (i[:, None] // QUAD == i[None, :] // QUAD)).astype(np.float32),
        "ident_bf": np.eye(P).astype(bf16),
        "above_q": np.where(i[None, :] > i[:, None], -1e30, 0.0).astype(bf16),
        "above_k": np.where(i[None, :] < i[:, None], -1e30, 0.0).astype(bf16),
        "eps": np.array([1e-5, 1e-6, 1e-12, 0.0], np.float32),
        "ctxT": f["ctx_1024"].reshape(TC, CH, P).transpose(2, 1, 0),
        "head_blocks": (i[:, None] // HD == i[None, :] // HD).astype(np.float32),
        "head_cols": ((i[:, None, None] + P * np.arange(CH)[:, None]) // HD == np.arange(H)).astype(np.float32),
        "mask_tokens": f["mask_BxS2_ff1"].reshape(NTC, P).T,
        "L0x_w": np.stack([rows_in(f[f"L0_xattn_{n}"]) for n in ("wq", "wk", "wv", "dense_w")], 1),
        "L0x_rows": np.stack([f["L0_xattn_ln_gamma"], f["L0_xattn_ln_beta"], f["L0_xattn_dense_b"]]),
        "order8": np.tile(np.arange(8, 0, -1, dtype=np.float32), (NT, 1)),
        "L0f_wr": rows_in(f["L0_ffn_Wr"].T),
        "L0f_w1": np.concatenate([np.stack([rows_in(w) for w in f["L0_ffn_W1"]]).reshape(8 * P, -1),
                                  f["L0_ffn_b1"].reshape(8, 8, P).transpose(0, 2, 1).reshape(8 * P, 8)], 1),
        "earlier8": np.tril(np.ones((8, 8), np.float32), -1),
        "slot_steps": np.arange(NT, dtype=np.float32) * P,
        "slot_numbers": np.arange(NT + 7, dtype=np.float32),
        "partition": i[:, None].astype(np.float32),
        "L0f_w2": rows_in(f["L0_ffn_Wo"], 8),
        "L0f_rows": np.stack([f[f"L0_ffn_{n}"] for n in ("bo", "gamma", "beta")]),
        "L1a_w": np.stack([rows_in(f[f"L1_attn_{n}"].T) for n in ("Wq", "Wk", "Wv", "Wo")], 1),
        "L1a_rows": np.stack([f[f"L1_attn_{n}"] for n in ("bq", "bv", "ln_g", "ln_b", "bo")]),
        "L1a_bk": column(f["L1_attn_bk"]),
        "L1x_w": np.concatenate([rows_in(f[f"L1_xattn_{n}"].T) for n in ("wq", "wk", "wv")], 2),
        "L1x_b": np.concatenate([column(f["L1_xattn_bq"]), column(f["L1_xattn_bk"])], 1),
        "L1x_v_b": column(f["L1_xattn_bv"]),
        "L1x_out_w": rows_in(f["L1_xattn_wo"].T),
        "L1x_out_b": f["L1_xattn_bo"],
        "L2a_w": rows_in(f["L2_attn_w_qkv"].T),
        "L2a_out_w": rows_in(f["L2_attn_w_proj"].T),
        "L2a_out_b": f["L2_attn_b_proj"],
        "L3a_w": np.concatenate([rows_in(f[f"L3_attn_{n}"].T) for n in ("Wq", "Wk", "Wv")], 2),
        "L3a_b": np.concatenate([column(f["L3_attn_bq"]), column(f["L3_attn_bk"])], 1),
        "L3a_v_b": column(f["L3_attn_bv"]),
        "L3a_out_w": rows_in(f["L3_attn_Wo"].T),
        "L3a_out_b": f["L3_attn_bo"],
        "slopes": slopes,
        "rows_of_ones": np.ones((3, HG, SC), bf16),
        "order16": np.tile(np.arange(16, 0, -1, dtype=np.float32), (NT, 1)),
        "expert16": np.tile(np.arange(16, dtype=np.float32), (NT, 1)),
        "token": (T + np.arange(T, dtype=np.float32)).reshape(NT, P).T,
        "upto": (i[:, None] <= i[None, :]).astype(np.float32),
        "L1f_wg": rows_in(f["L1_ffn_Wg"]),
        "L1f_bg": f["L1_ffn_bg"],
        "L1f_w1": np.stack([rows_in(w) for w in f["L1_ffn_W1"]]),
        "L1f_w2": np.stack([rows_in(w, 8) for w in f["L1_ffn_W2"]]),
        "L1f_b1": f["L1_ffn_b1"].reshape(16, 8, P).transpose(2, 0, 1),
        "L1f_b2": f["L1_ffn_b2"],
        "L2f_rows": np.stack([f[f"L2_ffn_{n}"] for n in ("ln_gamma", "ln_beta", "fc2_bias")]),
        "L2f_q1": rows_in(f["L2_ffn_fc1_q"]),
        "L2f_q2": rows_in(f["L2_ffn_fc2_q"], 8),
        "L2f_s1": f["L2_ffn_fc1_scales"],
        "L2f_s2": f["L2_ffn_fc2_scales"],
        "L2f_b1": column(f["L2_ffn_fc1_bias"]),
        "L3f_w": np.stack([rows_in(f[f"L3_ffn_W_{n}"].T) for n in "rkv"], 1),
        "L3f_mu": np.stack([column(f[f"L3_ffn_mu_{n}"]) for n in "rk"], 1),
        "ctx": f["ctx_1024"].reshape(NTC, P, C).transpose(1, 0, 2),
        "mask_q": f["mask_Bx1xSxS2_ff0"][:, 0],
        "mask_k": f["mask_Bx1xSxS2_ff0"][:, 0].transpose(0, 2, 1),
        "L3x_out_w": rows_in(f["L3_xattn_wo_w"].T),
        "L3x_out_b": f["L3_xattn_wo_b"],
        "L2x_rows": np.stack([f[f"L2_xattn_{n}"] for n in ("ln_m_g", "ln_m_b", "ln_l_g", "ln_l_b")]),
        "L2x_w": np.concatenate([rows_in(f["L2_xattn_Wq"]), rows_in(f["L2_xattn_Wkv"])], 2),
        "L2x_out_w": rows_in(f["L2_xattn_Wout"], 8),
        "L0_in_w": np.stack([rows_in(w.T) for w in f["L0_attn_in_proj_w"]]),
        "L0_in_b": np.stack([column(b) for b in f["L0_attn_in_proj_b"]], 1),
        "L0_v_b": np.stack([column(b[2 * C:]) for b in f["L0_attn_in_proj_b"]], 1),
        "L0_out_w": np.stack([rows_in(w.T) for w in f["L0_attn_out_w"]]),
        "L0_out_b": np.stack([column(b) for b in f["L0_attn_out_b"]], 1),
        "L0_up_w": np.stack([rows_in(w.T) for w in f["L0_attn_up_w"]]),
        "L0_up_b": np.stack([column(b) for b in f["L0_attn_up_b"]], 1),
        "L0_out_b0_up_b0": np.stack([f["L0_attn_out_b"][0], f["L0_attn_up_b"][0]]),
    }
    return {n: np.ascontiguousarray(v) for n, v in d.items()}


def build(nc, arrays):
    inp = {n: nc.dram_tensor(f"in_{n}", v.shape, mybir.dt.from_np(v.dtype), kind="ExternalInput").ap() for n, v in arrays.items()}
    decoder(nc, inp, nc.dram_tensor("out_x", [T, C], F32, kind="ExternalOutput").ap())


def kernel(**inputs):
    import concourse.bacc as bacc
    from concourse.bass_utils import run_bass_kernel_spmd

    arrays = lay_out({n: np.asarray(v) for n, v in inputs.items()})
    nc = bacc.Bacc("TRN2", target_bir_lowering=False, num_devices=1)
    build(nc, arrays)
    result = run_bass_kernel_spmd(nc, [{f"in_{n}": v for n, v in arrays.items()}], core_ids=[0])
    return result.results[0]["out_x"].reshape(B, S, C)
```
